# Optimizing a Trainium2 kernel written in Bass

```python
import numpy as np
import jax
import jax.numpy as jnp

def _softmax(x, axis=-1):
    return jax.nn.softmax(x, axis=axis)

def _gelu(x):
    return jax.nn.gelu(x, approximate=True)

def _silu(x):
    return jax.nn.silu(x)

def _sigmoid(x):
    return jax.nn.sigmoid(x)

def _layernorm(x, axis=-1, eps=1e-05):
    m = jnp.mean(x, axis=axis, keepdims=True)
    v = jnp.var(x, axis=axis, keepdims=True)
    return (x - m) / jnp.sqrt(v + eps)

def _scatter_add(tgt, idx, src, axis=0):
    return tgt.at[idx].add(src)

def _segment_sum(src, seg, n):
    return jax.ops.segment_sum(src, seg, n)
kernel_name = 'mk_gps_d2_gnn_r32_a2ef32'

def setup_inputs(seed: int=0):
    np.random.seed(seed)
    _w = jnp.asarray

    def _rec_inputs():
        import jax
        import jax.numpy as jnp
        _gk = jax.random.key(seed)
        x = -6.415e-05 + 1 * jax.random.normal(jax.random.fold_in(_gk, 1), (3125, 256), jnp.float32)
        _s = jax.random.randint(jax.random.fold_in(_gk, 2), (25000,), 0, 3125, jnp.int32)
        _d = jax.random.randint(jax.random.fold_in(_gk, 3), (25000,), 0, 3125, jnp.int32)
        _loop = jnp.arange(3125, dtype=jnp.int32)
        src = jnp.concatenate([_s, _d, _loop])
        dst = jnp.concatenate([_d, _s, _loop])
        _o = jnp.argsort(dst, stable=True)
        src = src[_o]
        dst = dst[_o]
        edge_type_2 = jax.random.randint(jax.random.fold_in(_gk, 14), (53125,), 0, 2, jnp.int32)
        edge_weight = jax.random.uniform(jax.random.fold_in(_gk, 15), (53125,), jnp.float32, 0.0, 1)
        return (x, src, dst, edge_type_2, edge_weight)
    x, src, dst, edge_type_2, edge_weight = _rec_inputs()

    def _L0_gnn_setup():
        import jax, jax.numpy as jnp
        import numpy as np
        N, E, B = (1250, 10000, 64)
        D = 256
        HID = 128
        H = 4
        SLOPE = 0.2

        def _segment_softmax(alpha, dst, n):
            amax = jax.lax.stop_gradient(jax.ops.segment_max(alpha, dst, num_segments=n))
            ex = jnp.exp(alpha - amax[dst])
            den = jax.ops.segment_sum(ex, dst, num_segments=n)
            return ex / (den[dst] + 1e-16)

        def _rgat(x, src, dst, etype, W, Q, K, b, heads, out_ch, n):
            xw = jnp.einsum('ni,rio->rno', x, W)
            out_i = xw[etype, dst]
            out_j = xw[etype, src]
            alpha = jax.nn.leaky_relu(out_i @ Q + out_j @ K, SLOPE)
            alpha = _segment_softmax(alpha, dst, n)
            msg = (out_j.reshape(-1, heads, out_ch) * alpha[..., None]).reshape(-1, heads * out_ch)
            return jax.ops.segment_sum(msg, dst, num_segments=n) + b
        key = jax.random.key(seed)
        ks = jax.random.split(key, 20)
        s = 0.05
        return {'x': jax.random.normal(ks[0], (N, D), jnp.float32), 'query': jax.random.normal(ks[1], (B, D), jnp.float32), 'edge_index': jax.random.randint(ks[2], (2, E), 0, N), 'edge_type': jax.random.randint(ks[3], (E,), 0, 2), 'batch': jnp.sort(jax.random.randint(ks[4], (N,), 0, B)), 'gate_w1': jax.random.normal(ks[5], (2 * D, D), jnp.float32) * s, 'gate_b1': jnp.zeros((D,), jnp.float32), 'gate_w2': jax.random.normal(ks[6], (D, D), jnp.float32) * s, 'gate_b2': jnp.zeros((D,), jnp.float32), 'W1': jax.random.normal(ks[7], (2, 3 * D, H * HID), jnp.float32) * s, 'q1': jax.random.normal(ks[8], (H * HID, H), jnp.float32) * s, 'k1': jax.random.normal(ks[9], (H * HID, H), jnp.float32) * s, 'b1': jnp.zeros((H * HID,), jnp.float32), 'W2': jax.random.normal(ks[10], (2, H * HID, H * HID), jnp.float32) * s, 'q2': jax.random.normal(ks[11], (H * HID, H), jnp.float32) * s, 'k2': jax.random.normal(ks[12], (H * HID, H), jnp.float32) * s, 'b2': jnp.zeros((H * HID,), jnp.float32), 'W3': jax.random.normal(ks[13], (2, H * HID, HID), jnp.float32) * s, 'q3': jax.random.normal(ks[14], (HID, 1), jnp.float32) * s, 'k3': jax.random.normal(ks[15], (HID, 1), jnp.float32) * s, 'b3': jnp.zeros((HID,), jnp.float32), 'proj_w': jax.random.normal(ks[16], (HID, D), jnp.float32) * s, 'proj_b': jnp.zeros((D,), jnp.float32)}
    _L0_gnn_all = _L0_gnn_setup()
    _L0_gnn_in = {k: v for k, v in _L0_gnn_all.items() if k in ('query', 'gate_w1', 'gate_b1', 'gate_w2', 'gate_b2', 'W1', 'q1', 'k1', 'b1', 'W2', 'q2', 'k2', 'b2', 'W3', 'q3', 'k3', 'b3', 'proj_w', 'proj_b')}
    del _L0_gnn_all

    def _L0_mix_setup():
        import jax, jax.numpy as jnp
        import numpy as np
        C_CURV = 1.0
        MIN_NORM = 1e-15
        BALL_EPS = 1e-05
        ATT_EPS = 1e-15
        DIM = 32

        def _norm(x):
            return jnp.clip(jnp.linalg.norm(x, axis=-1, keepdims=True), MIN_NORM)

        def proj(x, c):
            maxnorm = (1.0 - BALL_EPS) / jnp.sqrt(c)
            n = _norm(x)
            return jnp.where(n > maxnorm, x / n * maxnorm, x)

        def expmap0(u, c):
            sc = jnp.sqrt(c)
            n = _norm(u)
            return jnp.tanh(sc * n) * u / (sc * n)

        def logmap0(p, c):
            sc = jnp.sqrt(c)
            n = _norm(p)
            return jnp.arctanh(jnp.clip(sc * n, -1.0 + 1e-07, 1.0 - 1e-07)) * p / (sc * n)

        def mobius_add(x, y, c):
            x2 = jnp.sum(x * x, -1, keepdims=True)
            y2 = jnp.sum(y * y, -1, keepdims=True)
            xy = jnp.sum(x * y, -1, keepdims=True)
            num = (1 + 2 * c * xy + c * y2) * x + (1 - c * x2) * y
            den = 1 + 2 * c * xy + c * c * x2 * y2
            return num / jnp.clip(den, MIN_NORM)

        def conv1d(x, w, pad, groups=1):
            return jax.lax.conv_general_dilated(x, w, (1,), [(pad, pad)], dimension_numbers=('NCH', 'OIH', 'NCH'), feature_group_count=groups)

        def batchnorm(x, gamma, beta):
            mean = jnp.mean(x, axis=(0, 2), keepdims=True)
            var = jnp.var(x, axis=(0, 2), keepdims=True)
            xn = (x - mean) * jax.lax.rsqrt(var + 1e-05)
            return gamma[None, :, None] * xn + beta[None, :, None]

        def _reference_tuple_inner(x, w_qkv, bn_gamma, bn_beta, w_dw, w_pw, w_res, b_res):
            c = C_CURV
            h = logmap0(proj(x, c), c)
            h = jnp.transpose(h, (1, 2, 0))
            h = conv1d(h, w_qkv, pad=2)
            h = batchnorm(h, bn_gamma, bn_beta)
            h = jax.nn.relu(jnp.transpose(h, (2, 0, 1)))
            qkv = proj(expmap0(h, c), c)
            t = jnp.transpose(logmap0(proj(qkv, c), c), (1, 2, 0))
            s = conv1d(t, w_dw, pad=2, groups=t.shape[1])
            s = conv1d(s, w_pw, pad=0, groups=t.shape[1] // DIM)
            cat = jnp.concatenate([t, s], axis=1)
            ai = proj(expmap0(jnp.transpose(cat, (2, 0, 1)), c), c)
            t2 = logmap0(proj(ai, c), c)
            L, N, C2 = t2.shape
            g = C2 // (3 * DIM)
            qkv3 = jnp.transpose(t2, (1, 2, 0)).reshape(N, g, 3 * DIM, L)
            q, k, v = jnp.split(qkv3, 3, axis=2)
            q = jax.nn.relu(q)
            k = jax.nn.relu(k)
            vk = jnp.einsum('ngdl,ngel->ngde', v, k)
            out = jnp.einsum('ngde,ngdl->ngdl', vk, q)
            out = out / (jnp.sum(v, -1, keepdims=True) + ATT_EPS)
            out = jnp.transpose(out.reshape(N, g * DIM, L), (2, 0, 1))
            fx_h = proj(expmap0(out, c), c)
            ft = jnp.transpose(logmap0(proj(fx_h, c), c), (1, 2, 0))
            ft = conv1d(ft, w_res, pad=0) + b_res[None, :, None]
            fx = proj(expmap0(jnp.transpose(ft, (2, 0, 1)), c), c)
            residual = mobius_add(fx, x, c)
            return (fx, residual)
        key = jax.random.key(seed)
        ks = jax.random.split(key, 6)
        L, N, C, TD = (64, 16, 256, 256)
        x = jax.random.normal(ks[0], (L, N, C), jnp.float32) * 0.05
        w_qkv = jax.random.normal(ks[1], (3 * TD, C, 5), jnp.float32) / np.sqrt(C * 5)
        bn_gamma = jnp.ones((3 * TD,), jnp.float32)
        bn_beta = jnp.zeros((3 * TD,), jnp.float32)
        w_dw = jax.random.normal(ks[2], (3 * TD, 1, 5), jnp.float32) / np.sqrt(5.0)
        w_pw = jax.random.normal(ks[3], (3 * TD, DIM, 1), jnp.float32) / np.sqrt(DIM)
        w_res = jax.random.normal(ks[4], (C, 2 * TD, 1), jnp.float32) / np.sqrt(2 * TD)
        b_res = jnp.zeros((C,), jnp.float32)
        return {'x': x, 'w_qkv': w_qkv, 'bn_gamma': bn_gamma, 'bn_beta': bn_beta, 'w_dw': w_dw, 'w_pw': w_pw, 'w_res': w_res, 'b_res': b_res}
    _L0_mix_all = _L0_mix_setup()
    _L0_mix_in = {k: v for k, v in _L0_mix_all.items() if k in ('w_qkv', 'bn_gamma', 'bn_beta', 'w_dw', 'w_pw', 'w_res', 'b_res')}
    del _L0_mix_all

    def _L0_ffn_setup():
        import math
        import jax, jax.numpy as jnp
        import numpy as np
        CAPACITY_FACTOR = 1.25
        key = jax.random.key(seed)
        ks = jax.random.split(key, 5)
        B, L, D, F, E = (8, 256, 256, 1024, 8)
        h = jax.random.normal(ks[0], (B, L, D), dtype=jnp.float32)
        gate_w = jax.random.normal(ks[1], (D, E), dtype=jnp.float32) * 0.02
        gate_b = jnp.zeros((E,), dtype=jnp.float32)
        w1 = jax.random.normal(ks[2], (E, D, F), dtype=jnp.float32) * (1.0 / math.sqrt(D))
        b1 = jnp.zeros((E, F), dtype=jnp.float32)
        w2 = jax.random.normal(ks[3], (E, F, D), dtype=jnp.float32) * (1.0 / math.sqrt(F))
        b2 = jnp.zeros((E, D), dtype=jnp.float32)
        return {'h': h, 'gate_w': gate_w, 'gate_b': gate_b, 'w1': w1, 'b1': b1, 'w2': w2, 'b2': b2}
    _L0_ffn_all = _L0_ffn_setup()
    _L0_ffn_in = {k: v for k, v in _L0_ffn_all.items() if k in ('gate_w', 'gate_b', 'w1', 'b1', 'w2', 'b2')}
    del _L0_ffn_all

    def _L1_gnn_setup():
        import jax, jax.numpy as jnp
        import numpy as np
        N_NODES = 3125
        N_EDGES = 100000
        IN_F = 256
        OUT_F = 256
        key = jax.random.key(seed)
        k1, k2, k3, k4, k5, k6 = jax.random.split(key, 6)
        stdv = 1.0 / np.sqrt(IN_F)
        return {'x': jax.random.normal(k1, (N_NODES, IN_F), dtype=jnp.float32), 'edge_row': jax.random.randint(k2, (N_EDGES,), 0, N_NODES, dtype=jnp.int32), 'edge_col': jax.random.randint(k3, (N_EDGES,), 0, N_NODES, dtype=jnp.int32), 'adj_val': jax.random.uniform(k4, (N_EDGES,), dtype=jnp.float32), 'weight': jax.random.normal(k5, (IN_F, OUT_F), dtype=jnp.float32) * stdv, 'bias': jax.random.normal(k6, (OUT_F,), dtype=jnp.float32)}
    _L1_gnn_all = _L1_gnn_setup()
    _L1_gnn_in = {k: v for k, v in _L1_gnn_all.items() if k in ('weight', 'bias')}
    del _L1_gnn_all

    def _L1_mix_setup():
        import jax, jax.numpy as jnp
        import numpy as np
        D_MODEL = 256
        NHEAD = 8
        D_HEAD = D_MODEL // NHEAD
        DIM_FF = 1024
        B, L = (4, 512)
        LN_EPS = 1e-05

        def _layernorm(x, g, b):
            mu = jnp.mean(x, axis=-1, keepdims=True)
            var = jnp.mean((x - mu) ** 2, axis=-1, keepdims=True)
            return (x - mu) * jax.lax.rsqrt(var + LN_EPS) * g + b

        def _phi(x):
            return jnp.where(x > 0, x + 1.0, jnp.exp(x))
        key = jax.random.key(seed)
        ks = jax.random.split(key, 16)
        s_in = 1.0 / np.sqrt(D_MODEL)
        s_ff = 1.0 / np.sqrt(DIM_FF)
        inp = {'x': jax.random.normal(ks[0], (B, L, D_MODEL), dtype=jnp.float32), 'Wq': jax.random.normal(ks[1], (D_MODEL, D_MODEL), dtype=jnp.float32) * s_in, 'bq': jnp.zeros((D_MODEL,), jnp.float32), 'Wk': jax.random.normal(ks[2], (D_MODEL, D_MODEL), dtype=jnp.float32) * s_in, 'bk': jnp.zeros((D_MODEL,), jnp.float32), 'Wv': jax.random.normal(ks[3], (D_MODEL, D_MODEL), dtype=jnp.float32) * s_in, 'bv': jnp.zeros((D_MODEL,), jnp.float32), 'Wo': jax.random.normal(ks[4], (D_MODEL, D_MODEL), dtype=jnp.float32) * s_in, 'bo': jnp.zeros((D_MODEL,), jnp.float32), 'W1': jax.random.normal(ks[5], (D_MODEL, DIM_FF), dtype=jnp.float32) * s_in, 'b1': jnp.zeros((DIM_FF,), jnp.float32), 'W2': jax.random.normal(ks[6], (DIM_FF, D_MODEL), dtype=jnp.float32) * s_ff, 'b2': jnp.zeros((D_MODEL,), jnp.float32), 'ln1_g': jnp.ones((D_MODEL,), jnp.float32), 'ln1_b': jnp.zeros((D_MODEL,), jnp.float32), 'ln2_g': jnp.ones((D_MODEL,), jnp.float32), 'ln2_b': jnp.zeros((D_MODEL,), jnp.float32)}
        return inp
    _L1_mix_all = _L1_mix_setup()
    _L1_mix_in = {k: v for k, v in _L1_mix_all.items() if k in ('Wq', 'bq', 'Wk', 'bk', 'Wv', 'bv', 'Wo', 'bo', 'W1', 'b1', 'W2', 'b2', 'ln1_g', 'ln1_b', 'ln2_g', 'ln2_b')}
    del _L1_mix_all

    def _L1_ffn_setup():
        import jax, jax.numpy as jnp
        import numpy as np
        B, S, D = (8, 128, 256)
        H = 4 * D
        CAPACITY = 0.5
        key = jax.random.key(seed)
        ks = jax.random.split(key, 6)
        x = jax.random.normal(ks[0], (B, S, D), dtype=jnp.float32)
        attention_mask = jnp.zeros((B, 1, 1, S), dtype=jnp.float32)
        wr = jax.random.normal(ks[1], (D, 1), dtype=jnp.float32) * 0.02
        br = jnp.zeros((1,), dtype=jnp.float32)
        w1 = jax.random.normal(ks[2], (D, H), dtype=jnp.float32) * 0.02
        b1 = jnp.zeros((H,), dtype=jnp.float32)
        w2 = jax.random.normal(ks[3], (H, D), dtype=jnp.float32) * 0.02
        b2 = jnp.zeros((D,), dtype=jnp.float32)
        return {'x': x, 'attention_mask': attention_mask, 'wr': wr, 'br': br, 'w1': w1, 'b1': b1, 'w2': w2, 'b2': b2}
    _L1_ffn_all = _L1_ffn_setup()
    _L1_ffn_in = {k: v for k, v in _L1_ffn_all.items() if k in ('attention_mask', 'wr', 'br', 'w1', 'b1', 'w2', 'b2')}
    del _L1_ffn_all
    return {'x': x, 'src': src, 'dst': dst, 'edge_type_2': edge_type_2, 'edge_weight': edge_weight, 'L0_gnn_query': _L0_gnn_in['query'], 'L0_gnn_gate_w1': _L0_gnn_in['gate_w1'], 'L0_gnn_gate_b1': _L0_gnn_in['gate_b1'], 'L0_gnn_gate_w2': _L0_gnn_in['gate_w2'], 'L0_gnn_gate_b2': _L0_gnn_in['gate_b2'], 'L0_gnn_W1': _L0_gnn_in['W1'], 'L0_gnn_q1': _L0_gnn_in['q1'], 'L0_gnn_k1': _L0_gnn_in['k1'], 'L0_gnn_b1': _L0_gnn_in['b1'], 'L0_gnn_W2': _L0_gnn_in['W2'], 'L0_gnn_q2': _L0_gnn_in['q2'], 'L0_gnn_k2': _L0_gnn_in['k2'], 'L0_gnn_b2': _L0_gnn_in['b2'], 'L0_gnn_W3': _L0_gnn_in['W3'], 'L0_gnn_q3': _L0_gnn_in['q3'], 'L0_gnn_k3': _L0_gnn_in['k3'], 'L0_gnn_b3': _L0_gnn_in['b3'], 'L0_gnn_proj_w': _L0_gnn_in['proj_w'], 'L0_gnn_proj_b': _L0_gnn_in['proj_b'], 'L0_mix_w_qkv': _L0_mix_in['w_qkv'], 'L0_mix_bn_gamma': _L0_mix_in['bn_gamma'], 'L0_mix_bn_beta': _L0_mix_in['bn_beta'], 'L0_mix_w_dw': _L0_mix_in['w_dw'], 'L0_mix_w_pw': _L0_mix_in['w_pw'], 'L0_mix_w_res': _L0_mix_in['w_res'], 'L0_mix_b_res': _L0_mix_in['b_res'], 'L0_ffn_gate_w': _L0_ffn_in['gate_w'], 'L0_ffn_gate_b': _L0_ffn_in['gate_b'], 'L0_ffn_w1': _L0_ffn_in['w1'], 'L0_ffn_b1': _L0_ffn_in['b1'], 'L0_ffn_w2': _L0_ffn_in['w2'], 'L0_ffn_b2': _L0_ffn_in['b2'], 'L1_gnn_weight': _L1_gnn_in['weight'], 'L1_gnn_bias': _L1_gnn_in['bias'], 'L1_mix_Wq': _L1_mix_in['Wq'], 'L1_mix_bq': _L1_mix_in['bq'], 'L1_mix_Wk': _L1_mix_in['Wk'], 'L1_mix_bk': _L1_mix_in['bk'], 'L1_mix_Wv': _L1_mix_in['Wv'], 'L1_mix_bv': _L1_mix_in['bv'], 'L1_mix_Wo': _L1_mix_in['Wo'], 'L1_mix_bo': _L1_mix_in['bo'], 'L1_mix_W1': _L1_mix_in['W1'], 'L1_mix_b1': _L1_mix_in['b1'], 'L1_mix_W2': _L1_mix_in['W2'], 'L1_mix_b2': _L1_mix_in['b2'], 'L1_mix_ln1_g': _L1_mix_in['ln1_g'], 'L1_mix_ln1_b': _L1_mix_in['ln1_b'], 'L1_mix_ln2_g': _L1_mix_in['ln2_g'], 'L1_mix_ln2_b': _L1_mix_in['ln2_b'], 'L1_ffn_attention_mask': _L1_ffn_in['attention_mask'], 'L1_ffn_wr': _L1_ffn_in['wr'], 'L1_ffn_br': _L1_ffn_in['br'], 'L1_ffn_w1': _L1_ffn_in['w1'], 'L1_ffn_b1': _L1_ffn_in['b1'], 'L1_ffn_w2': _L1_ffn_in['w2'], 'L1_ffn_b2': _L1_ffn_in['b2']}

def reference(x, src, dst, edge_type_2, edge_weight, L0_gnn_query, L0_gnn_gate_w1, L0_gnn_gate_b1, L0_gnn_gate_w2, L0_gnn_gate_b2, L0_gnn_W1, L0_gnn_q1, L0_gnn_k1, L0_gnn_b1, L0_gnn_W2, L0_gnn_q2, L0_gnn_k2, L0_gnn_b2, L0_gnn_W3, L0_gnn_q3, L0_gnn_k3, L0_gnn_b3, L0_gnn_proj_w, L0_gnn_proj_b, L0_mix_w_qkv, L0_mix_bn_gamma, L0_mix_bn_beta, L0_mix_w_dw, L0_mix_w_pw, L0_mix_w_res, L0_mix_b_res, L0_ffn_gate_w, L0_ffn_gate_b, L0_ffn_w1, L0_ffn_b1, L0_ffn_w2, L0_ffn_b2, L1_gnn_weight, L1_gnn_bias, L1_mix_Wq, L1_mix_bq, L1_mix_Wk, L1_mix_bk, L1_mix_Wv, L1_mix_bv, L1_mix_Wo, L1_mix_bo, L1_mix_W1, L1_mix_b1, L1_mix_W2, L1_mix_b2, L1_mix_ln1_g, L1_mix_ln1_b, L1_mix_ln2_g, L1_mix_ln2_b, L1_ffn_attention_mask, L1_ffn_wr, L1_ffn_br, L1_ffn_w1, L1_ffn_b1, L1_ffn_w2, L1_ffn_b2):
    import jax
    import jax.numpy as jnp

    def _L0_gnn_ref(x, query, edge_index, edge_type, batch, gate_w1, gate_b1, gate_w2, gate_b2, W1, q1, k1, b1, W2, q2, k2, b2, W3, q3, k3, b3, proj_w, proj_b):
        import jax, jax.numpy as jnp
        import numpy as np
        N, E, B = (1250, 10000, 64)
        D = 256
        HID = 128
        H = 4
        SLOPE = 0.2

        def _segment_softmax(alpha, dst, n):
            amax = jax.lax.stop_gradient(jax.ops.segment_max(alpha, dst, num_segments=n))
            ex = jnp.exp(alpha - amax[dst])
            den = jax.ops.segment_sum(ex, dst, num_segments=n)
            return ex / (den[dst] + 1e-16)

        def _rgat(x, src, dst, etype, W, Q, K, b, heads, out_ch, n):
            xw = jnp.einsum('ni,rio->rno', x, W)
            out_i = xw[etype, dst]
            out_j = xw[etype, src]
            alpha = jax.nn.leaky_relu(out_i @ Q + out_j @ K, SLOPE)
            alpha = _segment_softmax(alpha, dst, n)
            msg = (out_j.reshape(-1, heads, out_ch) * alpha[..., None]).reshape(-1, heads * out_ch)
            return jax.ops.segment_sum(msg, dst, num_segments=n) + b
        n = x.shape[0]
        src, dst = (edge_index[0], edge_index[1])
        q_node = query[batch]
        interaction = x * q_node
        gh = jax.nn.relu(jnp.concatenate([x, q_node], axis=-1) @ gate_w1 + gate_b1)
        gate = jax.nn.sigmoid(gh @ gate_w2 + gate_b2)
        x0 = x * gate
        h = jnp.concatenate([x0, q_node, interaction], axis=-1)
        h = jax.nn.relu(_rgat(h, src, dst, edge_type, W1, q1, k1, b1, H, HID, n))
        h = h + jax.nn.relu(_rgat(h, src, dst, edge_type, W2, q2, k2, b2, H, HID, n))
        h = jax.nn.relu(_rgat(h, src, dst, edge_type, W3, q3, k3, b3, 1, HID, n))
        out = h @ proj_w + proj_b + x0
        nrm = jnp.linalg.norm(out, axis=-1, keepdims=True)
        return out / jnp.maximum(nrm, 1e-12)

    def _L0_mix_ref(x, w_qkv, bn_gamma, bn_beta, w_dw, w_pw, w_res, b_res):
        import jax, jax.numpy as jnp
        import numpy as np
        C_CURV = 1.0
        MIN_NORM = 1e-15
        BALL_EPS = 1e-05
        ATT_EPS = 1e-15
        DIM = 32

        def _norm(x):
            return jnp.clip(jnp.linalg.norm(x, axis=-1, keepdims=True), MIN_NORM)

        def proj(x, c):
            maxnorm = (1.0 - BALL_EPS) / jnp.sqrt(c)
            n = _norm(x)
            return jnp.where(n > maxnorm, x / n * maxnorm, x)

        def expmap0(u, c):
            sc = jnp.sqrt(c)
            n = _norm(u)
            return jnp.tanh(sc * n) * u / (sc * n)

        def logmap0(p, c):
            sc = jnp.sqrt(c)
            n = _norm(p)
            return jnp.arctanh(jnp.clip(sc * n, -1.0 + 1e-07, 1.0 - 1e-07)) * p / (sc * n)

        def mobius_add(x, y, c):
            x2 = jnp.sum(x * x, -1, keepdims=True)
            y2 = jnp.sum(y * y, -1, keepdims=True)
            xy = jnp.sum(x * y, -1, keepdims=True)
            num = (1 + 2 * c * xy + c * y2) * x + (1 - c * x2) * y
            den = 1 + 2 * c * xy + c * c * x2 * y2
            return num / jnp.clip(den, MIN_NORM)

        def conv1d(x, w, pad, groups=1):
            return jax.lax.conv_general_dilated(x, w, (1,), [(pad, pad)], dimension_numbers=('NCH', 'OIH', 'NCH'), feature_group_count=groups)

        def batchnorm(x, gamma, beta):
            mean = jnp.mean(x, axis=(0, 2), keepdims=True)
            var = jnp.var(x, axis=(0, 2), keepdims=True)
            xn = (x - mean) * jax.lax.rsqrt(var + 1e-05)
            return gamma[None, :, None] * xn + beta[None, :, None]

        def _reference_tuple_inner(x, w_qkv, bn_gamma, bn_beta, w_dw, w_pw, w_res, b_res):
            c = C_CURV
            h = logmap0(proj(x, c), c)
            h = jnp.transpose(h, (1, 2, 0))
            h = conv1d(h, w_qkv, pad=2)
            h = batchnorm(h, bn_gamma, bn_beta)
            h = jax.nn.relu(jnp.transpose(h, (2, 0, 1)))
            qkv = proj(expmap0(h, c), c)
            t = jnp.transpose(logmap0(proj(qkv, c), c), (1, 2, 0))
            s = conv1d(t, w_dw, pad=2, groups=t.shape[1])
            s = conv1d(s, w_pw, pad=0, groups=t.shape[1] // DIM)
            cat = jnp.concatenate([t, s], axis=1)
            ai = proj(expmap0(jnp.transpose(cat, (2, 0, 1)), c), c)
            t2 = logmap0(proj(ai, c), c)
            L, N, C2 = t2.shape
            g = C2 // (3 * DIM)
            qkv3 = jnp.transpose(t2, (1, 2, 0)).reshape(N, g, 3 * DIM, L)
            q, k, v = jnp.split(qkv3, 3, axis=2)
            q = jax.nn.relu(q)
            k = jax.nn.relu(k)
            vk = jnp.einsum('ngdl,ngel->ngde', v, k)
            out = jnp.einsum('ngde,ngdl->ngdl', vk, q)
            out = out / (jnp.sum(v, -1, keepdims=True) + ATT_EPS)
            out = jnp.transpose(out.reshape(N, g * DIM, L), (2, 0, 1))
            fx_h = proj(expmap0(out, c), c)
            ft = jnp.transpose(logmap0(proj(fx_h, c), c), (1, 2, 0))
            ft = conv1d(ft, w_res, pad=0) + b_res[None, :, None]
            fx = proj(expmap0(jnp.transpose(ft, (2, 0, 1)), c), c)
            residual = mobius_add(fx, x, c)
            return (fx, residual)
        return _reference_tuple_inner(x, w_qkv, bn_gamma, bn_beta, w_dw, w_pw, w_res, b_res)[0]

    def _L0_ffn_ref(h, gate_w, gate_b, w1, b1, w2, b2):
        import math
        import jax, jax.numpy as jnp
        import numpy as np
        CAPACITY_FACTOR = 1.25
        B, L, D = h.shape
        E = gate_w.shape[1]
        T = B * L
        C = max(1, math.ceil(CAPACITY_FACTOR * T / E))
        x = h.reshape(T, D)
        logits = x @ gate_w + gate_b
        probs = jax.nn.softmax(logits, axis=-1)
        idx = jnp.argmax(probs, axis=-1)
        prb = jnp.take_along_axis(probs, idx[:, None], axis=1)[:, 0]
        one_hot = jax.nn.one_hot(idx, E, dtype=jnp.float32)
        pos = (jnp.cumsum(one_hot, axis=0) * one_hot).sum(-1).astype(jnp.int32) - 1
        kept = pos < C
        pos_safe = jnp.where(kept, pos, C)
        buf = jnp.zeros((E, C, D), dtype=h.dtype).at[idx, pos_safe].set(x, mode='drop')
        hmid = jax.nn.relu(jnp.einsum('ecd,edf->ecf', buf, w1) + b1[:, None, :])
        ybuf = jnp.einsum('ecf,efd->ecd', hmid, w2) + b2[:, None, :]
        pos_g = jnp.minimum(pos, C - 1)
        y_tok = ybuf[idx, pos_g] * (prb * kept)[:, None]
        y = y_tok.reshape(B, L, D)
        y = jnp.nan_to_num(y, nan=0.0, posinf=10000.0, neginf=-10000.0)
        return y

    def _L1_gnn_ref(x, edge_row, edge_col, adj_val, weight, bias):
        import jax, jax.numpy as jnp
        import numpy as np
        N_NODES = 3125
        N_EDGES = 100000
        IN_F = 256
        OUT_F = 256
        support = x @ weight
        msgs = adj_val[:, None] * support[edge_col]
        output = jax.ops.segment_sum(msgs, edge_row, num_segments=x.shape[0])
        return output + bias

    def _L1_mix_ref(x, Wq, bq, Wk, bk, Wv, bv, Wo, bo, W1, b1, W2, b2, ln1_g, ln1_b, ln2_g, ln2_b):
        import jax, jax.numpy as jnp
        import numpy as np
        D_MODEL = 256
        NHEAD = 8
        D_HEAD = D_MODEL // NHEAD
        DIM_FF = 1024
        B, L = (4, 512)
        LN_EPS = 1e-05

        def _layernorm(x, g, b):
            mu = jnp.mean(x, axis=-1, keepdims=True)
            var = jnp.mean((x - mu) ** 2, axis=-1, keepdims=True)
            return (x - mu) * jax.lax.rsqrt(var + LN_EPS) * g + b

        def _phi(x):
            return jnp.where(x > 0, x + 1.0, jnp.exp(x))
        Bq, Lq, _ = x.shape
        q = (x @ Wq + bq).reshape(Bq, Lq, NHEAD, D_HEAD)
        k = (x @ Wk + bk).reshape(Bq, Lq, NHEAD, D_HEAD)
        v = (x @ Wv + bv).reshape(Bq, Lq, NHEAD, D_HEAD)
        q_phi = _phi(q)
        k_phi = _phi(k)
        kv = jnp.einsum('blhd,blhe->bhde', k_phi, v)
        k_sum = k_phi.sum(axis=1)
        z = 1.0 / (jnp.einsum('blhd,bhd->blh', q_phi, k_sum) + 1e-06)
        out = jnp.einsum('blhd,bhde,blh->blhe', q_phi, kv, z)
        out = out.reshape(Bq, Lq, D_MODEL) @ Wo + bo
        x = _layernorm(x + out, ln1_g, ln1_b)
        ff = jax.nn.relu(x @ W1 + b1) @ W2 + b2
        x = _layernorm(x + ff, ln2_g, ln2_b)
        return x

    def _L1_ffn_ref(x, attention_mask, wr, br, w1, b1, w2, b2):
        import jax, jax.numpy as jnp
        import numpy as np
        B, S, D = (8, 128, 256)
        H = 4 * D
        CAPACITY = 0.5
        b, s, d = x.shape
        weights = (jnp.einsum('bsd,do->bso', x, wr) + br)[..., 0]
        k = max(1, int(CAPACITY * s))
        kk = k - 1 if k > 1 else 1
        _, idx = jax.lax.top_k(weights, k)
        sel_idx = idx[:, :kk]
        sel = jnp.take_along_axis(x, sel_idx[:, :, None], axis=1)
        h = jax.nn.gelu(jnp.einsum('bkd,dh->bkh', sel, w1) + b1)
        y = jnp.einsum('bkh,hd->bkd', h, w2) + b2
        w_sel = jnp.take_along_axis(weights, sel_idx, axis=1)
        y = y * w_sel[..., None]
        batch_idx = jnp.arange(b)[:, None]
        processed = jnp.zeros_like(x).at[batch_idx, sel_idx].set(y)
        return processed + x
    edge_index = jnp.stack([src, dst])
    batch0 = jnp.zeros((3125,), jnp.int32)
    xn = _layernorm(x, axis=-1)
    x = x + _L0_gnn_ref(xn, L0_gnn_query, edge_index, edge_type_2, batch0, L0_gnn_gate_w1, L0_gnn_gate_b1, L0_gnn_gate_w2, L0_gnn_gate_b2, L0_gnn_W1, L0_gnn_q1, L0_gnn_k1, L0_gnn_b1, L0_gnn_W2, L0_gnn_q2, L0_gnn_k2, L0_gnn_b2, L0_gnn_W3, L0_gnn_q3, L0_gnn_k3, L0_gnn_b3, L0_gnn_proj_w, L0_gnn_proj_b) + _L0_mix_ref(xn[None], L0_mix_w_qkv, L0_mix_bn_gamma, L0_mix_bn_beta, L0_mix_w_dw, L0_mix_w_pw, L0_mix_w_res, L0_mix_b_res)[0]
    x = x + _L0_ffn_ref(_layernorm(x, axis=-1)[None], L0_ffn_gate_w, L0_ffn_gate_b, L0_ffn_w1, L0_ffn_b1, L0_ffn_w2, L0_ffn_b2)[0]
    xn = _layernorm(x, axis=-1)
    x = x + _L1_gnn_ref(xn, src, dst, edge_weight, L1_gnn_weight, L1_gnn_bias) + _L1_mix_ref(xn[None], L1_mix_Wq, L1_mix_bq, L1_mix_Wk, L1_mix_bk, L1_mix_Wv, L1_mix_bv, L1_mix_Wo, L1_mix_bo, L1_mix_W1, L1_mix_b1, L1_mix_W2, L1_mix_b2, L1_mix_ln1_g, L1_mix_ln1_b, L1_mix_ln2_g, L1_mix_ln2_b)[0]
    x = x + _L1_ffn_ref(_layernorm(x, axis=-1)[None], L1_ffn_attention_mask, L1_ffn_wr, L1_ffn_br, L1_ffn_w1, L1_ffn_b1, L1_ffn_w2, L1_ffn_b2)[0]
    return x

_drawn_inputs = setup_inputs


def setup_inputs(seed=0):
    import zlib

    import numpy as np

    out = dict(_drawn_inputs(seed))
    spreads = {'L0_gnn_gate_b1': (0.0, 0.8),
     'L0_gnn_gate_b2': (0.0, 0.8),
     'L0_gnn_b1': (0.0, 0.8),
     'L0_gnn_b2': (0.0, 0.795),
     'L0_gnn_b3': (0.0, 0.597),
     'L0_gnn_proj_b': (0.0, 0.1),
     'L0_mix_bn_gamma': (1.0, 0.6),
     'L0_mix_bn_beta': (0.0, 0.33),
     'L0_mix_b_res': (0.0, 0.1),
     'L0_ffn_gate_b': (0.0, 0.1),
     'L0_ffn_b1': (0.0, 0.539),
     'L0_ffn_b2': (0.0, 0.358),
     'L1_mix_bq': (0.0, 2.0),
     'L1_mix_bk': (0.0, 2.0),
     'L1_mix_bv': (0.0, 0.1),
     'L1_mix_bo': (0.0, 0.268),
     'L1_mix_b1': (0.0, 0.456),
     'L1_mix_b2': (0.0, 0.324),
     'L1_mix_ln1_g': (1.0, 0.2),
     'L1_mix_ln1_b': (0.0, 0.1),
     'L1_mix_ln2_g': (1.0, 0.2),
     'L1_mix_ln2_b': (0.0, 0.278),
     'L1_ffn_b1': (0.0, 0.8),
     'L1_ffn_b2': (0.0, 0.8)}
    factors = {'L0_gnn_gate_w1': 3.23,
     'L0_gnn_gate_w2': 2.775,
     'L0_gnn_q1': 5.743,
     'L0_gnn_k1': 4.647,
     'L0_gnn_W2': 2.683,
     'L0_gnn_q2': 8.0,
     'L0_gnn_k2': 8.0,
     'L0_gnn_q3': 24.215,
     'L0_gnn_k3': 8.0,
     'L0_mix_w_dw': 3.459,
     'L0_mix_w_pw': 3.431,
     'L1_mix_Wq': 8.0,
     'L1_mix_Wk': 8.0,
     'L1_mix_Wv': 4.402,
     'L1_ffn_wr': 7.294,
     'L1_ffn_w1': 8.0,
     'L1_ffn_w2': 8.0}
    for name, (base, spread) in spreads.items():
        noise = np.random.default_rng([zlib.crc32(name.encode()), seed]).standard_normal(out[name].shape)
        drawn = base * np.exp(spread * noise) if base else spread * noise
        out[name] = jnp.asarray(drawn.astype(out[name].dtype))
    for name, factor in factors.items():
        out[name] = (out[name] * factor).astype(out[name].dtype)
    return out
```

```python
from contextlib import ExitStack, contextmanager

import concourse.bass as bass
from concourse import mybir

F32 = mybir.dt.float32
I32 = mybir.dt.int32
ALU = mybir.AluOpType
ACT = mybir.ActivationFunctionType
AX = mybir.AxisListType

N = 3125
D = 256
E = 53125
P = 128
TP = 125
NT = N // TP
GROUP = 5
NG = NT // GROUP
CH = 416
CK = 104
KB = CH // CK
EP = CH * P
PAD_NODE = N
PART0 = N + 1
AGG_ROWS = PART0 + CH
SKIP = 1 << 17
HEADS = 4
HID = 128
BIG = 1.0e30
MAXNORM = 0.9999899864196777
ATANH_MAX = 6.102495471
MIN_NORM = 1e-15
SLOPE = 0.2


def ready(i, u):
    return GROUP * i + u + 1


def freed(i, u, depth):
    return GROUP * i + max(u + 1 - depth, 0)


class Shared:
    pass


def after(eng, ins, sem, value):
    ins.then_inc(sem, 1)
    eng.wait_ge(sem, value)


class Steps:

    def __init__(self, eng, sem, base=0):
        self.eng, self.sem, self.n, self.base = eng, sem, 0, base

    def __call__(self, ins):
        self.n += 1
        ins.then_inc(self.sem, 1)
        self.eng.wait_ge(self.sem, self.base + self.n)


class Alloc:
    def __init__(self, nc, ctx, tag=""):
        self.nc, self.ctx, self.tag, self.sems = nc, ctx, tag, []
        self.pool_dmas = False

    def sb(self, name, shape, dt=F32):
        return self.ctx.enter_context(self.nc.sbuf_tensor(self.tag + name, shape, dt))

    def ps(self, name, shape, dt=F32):
        return self.ctx.enter_context(self.nc.psum_tensor(self.tag + name, shape, dt))

    def sem(self, name):
        s = self.ctx.enter_context(self.nc.semaphore(self.tag + name))
        self.sems.append(s)
        return s

    def borrow(self, sems):
        self.sems.extend(s for s in sems if s not in self.sems)
        self.pool_dmas = True
        return sems


@contextmanager
def stage(nc, tag):
    with ExitStack() as ctx:
        a = Alloc(nc, ctx, tag)
        yield a
        with nc.Block() as block:
            @block.gpsimd
            def _(pool):
                if a.pool_dmas:
                    pool.dma_reset()
                for s in a.sems:
                    pool.sem_clear(s)


def row_of(ap):
    return ap.rearrange("(a b) -> a b", a=1)


def spread(ap, parts):
    return row_of(ap).broadcast_to([parts, ap.shape[0]])


def tiles_of(ap):
    return ap.rearrange("(t p) d -> p t d", p=TP)


def constants(nc, g, S):
    S.ident = g.sb("ident", [P, P])
    S.ones = g.sb("ones", [P, P])
    S.iota_row = g.sb("iota_row", [P, P])
    S.part_col = g.sb("part_col", [P, 1])
    S.zeros = g.sb("zeros", [P, 1024])
    S.pool_dma = [g.sem(f"pool_dma{n}") for n in range(6)]
    iota_i = g.sb("iota_i", [P, P], I32)
    part_i = g.sb("part_i", [P, 1], I32)
    made = g.sem("constants_made")
    with nc.Block() as block:
        @block.gpsimd
        def _(pool):
            pool.iota(iota_i[:], pattern=[[1, P]], base=0, channel_multiplier=0).then_inc(made, 1)
            pool.iota(part_i[:], pattern=[[1, 1]], base=0, channel_multiplier=1).then_inc(made, 1)

        @block.vector
        def _(dve):
            dve.memset(S.ones[:], 1.0)
            dve.memset(S.zeros[:], 0.0)
            dve.wait_ge(made, 2)
            dve.tensor_copy(S.iota_row[:], iota_i[:]).then_inc(made, 1)
            dve.tensor_copy(S.part_col[:], part_i[:]).then_inc(made, 1)
            dve.wait_ge(made, 4)
            dve.tensor_scalar(S.ident[:], S.iota_row[:], S.part_col[:, 0:1], None, ALU.is_equal)


def edges(nc, g, S, src, dst, etype, ew):
    S.dst_pad = nc.dram_tensor("dst_pad", [EP + 2], I32, kind="Internal").ap()
    S.src_pad = nc.dram_tensor("src_pad", [EP], I32, kind="Internal").ap()
    typ_pad = nc.dram_tensor("typ_pad", [EP], I32, kind="Internal").ap()
    ew_pad = nc.dram_tensor("ew_pad", [EP], F32, kind="Internal").ap()
    S.agg = nc.dram_tensor("agg_rows", [AGG_ROWS, HEADS * HID + HEADS], F32, kind="Internal").ap()
    S.agg3 = nc.dram_tensor("agg3_rows", [AGG_ROWS, HID + 1], F32, kind="Internal").ap()
    S.acc = [nc.dram_tensor(f"acc_rows{u}", [N + P, D], F32, kind="Internal").ap() for u in range(4)]

    S.dst_c, S.src_c, S.ew_c = (g.sb(name, [P, CH]) for name in ("dst_c", "src_c", "ew_c"))
    S.row_src, S.row_dst, S.row_out, S.node_dst = (
        g.sb(name, [P, CH], I32) for name in ("row_src", "row_dst", "row_out", "node_dst"))
    S.pen_start = g.sb("pen_start", [CK, KB, P])
    S.pen_end = g.sb("pen_end", [CK, KB, P])
    S.pen_first = g.sb("pen_first", [CK, KB, P])
    S.pen_last = g.sb("pen_last", [CK, KB, P])
    S.link = g.sb("link", [HEADS, CH])
    S.carry_f = g.sb("carry_f", [HEADS, CH])
    S.carry_b = g.sb("carry_b", [HEADS, CH])
    S.part_rel = g.sb("part_rel", [CK, NT, KB])

    with stage(nc, "ed_") as a:
        pad_i = a.sb("pad_i", [1, 128], I32)
        pad_n = a.sb("pad_n", [1, 128], I32)
        pad_m = a.sb("pad_m", [1, 1], I32)
        raw = {n: a.sb("raw_" + n, [CK, KB, P], F32 if n == "ew" else I32)
               for n in ("src", "dst", "prev", "next", "typ", "ew")}
        f = {n: a.sb("f_" + n, [CK, KB, P]) for n in ("src", "dst", "prev", "next", "typ")}
        w = {n: a.sb("w_" + n, [CK, KB, P]) for n in ("rs", "rd", "ro", "nd", "t0", "t1")}
        tmp_i = a.sb("tmp_i", [CK, KB], F32)
        chunk_no = a.sb("chunk_no", [CK, KB], F32)
        rows_i = a.sb("rows_i", [HEADS, 2, CH + 1], I32)
        rows_f = a.sb("rows_f", [HEADS, 2, CH + 1])
        eq = a.sb("eq", [HEADS, 2, CH])
        turn = a.ps("turn", [P, 7, 512])
        pads_set, filled = a.sem("pads_set"), a.sem("filled")
        copied, loaded = a.sem("copied"), a.sem("loaded")
        step_s, turned = a.sem("step"), a.sem("turned")
        PADE = EP - E

        with nc.Block() as block:
            @block.sync
            def _(sp):
                sp.dma_start(S.dst_pad[1:E + 1], dst).then_inc(copied, 16)
                sp.dma_start(S.src_pad[0:E], src).then_inc(copied, 16)
                sp.dma_start(typ_pad[0:E], etype).then_inc(copied, 16)
                sp.dma_start(ew_pad[0:E], ew).then_inc(copied, 16)
                sp.wait_ge(pads_set, 3)
                sp.dma_start(row_of(S.dst_pad[E + 1:EP + 1]), pad_n[0:1, 0:PADE]).then_inc(copied, 16)
                sp.dma_start(row_of(S.dst_pad[EP + 1:EP + 2]), pad_m[:]).then_inc(copied, 16)
                sp.dma_start(row_of(S.dst_pad[0:1]), pad_m[:]).then_inc(copied, 16)
                sp.dma_start(row_of(S.src_pad[E:EP]), pad_i[0:1, 0:PADE]).then_inc(copied, 16)
                sp.dma_start(row_of(typ_pad[E:EP]), pad_i[0:1, 0:PADE]).then_inc(copied, 16)
                sp.dma_start(row_of(ew_pad[E:EP]), S.zeros[0:1, 0:PADE]).then_inc(copied, 16)
                sp.wait_ge(copied, 160)
                rows = lambda x: x.rearrange("(k c j) -> c k j", k=KB, c=CK)
                sp.dma_start(raw["src"][:], rows(S.src_pad)).then_inc(loaded, 16)
                sp.dma_start(raw["dst"][:], rows(S.dst_pad[1:EP + 1])).then_inc(loaded, 16)
                sp.dma_start(raw["prev"][:], rows(S.dst_pad[0:EP])).then_inc(loaded, 16)
                sp.dma_start(raw["next"][:], rows(S.dst_pad[2:EP + 2])).then_inc(loaded, 16)
                sp.dma_start(raw["typ"][:], rows(typ_pad)).then_inc(loaded, 16)
                sp.dma_start(raw["ew"][:], rows(ew_pad)).then_inc(loaded, 16)
                for h in range(HEADS):
                    sp.dma_start(rows_i[h:h + 1, 0, 0:CH], S.dst_pad[1:EP + 1].rearrange(
                        "(a c j) -> a c j", a=1, j=P)[:, :, 0:1].rearrange("a c j -> a (c j)"),
                                 allow_slow_non_contiguous=True).then_inc(loaded, 16)
                    sp.dma_start(rows_i[h:h + 1, 1, 0:CH], S.dst_pad[1:EP + 1].rearrange(
                        "(a c j) -> a c j", a=1, j=P)[:, :, P - 1:P].rearrange("a c j -> a (c j)"),
                                 allow_slow_non_contiguous=True).then_inc(loaded, 16)
                for table, width in ((S.agg, HEADS * HID + HEADS), (S.agg3, HID + 1)):
                    for r in range(0, AGG_ROWS, P):
                        m = min(P, AGG_ROWS - r)
                        sp.dma_start(table[r:r + m, :], S.zeros[0:m, 0:width]).then_inc(filled, 16)
                for u in range(4):
                    for r in range(0, N + P, P):
                        m = min(P, N + P - r)
                        sp.dma_start(S.acc[u][r:r + m, :], S.zeros[0:m, 0:D]).then_inc(filled, 16)
                fills = 2 * len(range(0, AGG_ROWS, P)) + 4 * len(range(0, N + P, P))
                sp.wait_ge(filled, 16 * fills)

            @block.vector
            def _(dve):
                dve.memset(pad_i[:], 0).then_inc(pads_set, 1)
                dve.memset(pad_n[:], PAD_NODE).then_inc(pads_set, 1)
                dve.memset(pad_m[:], 2 * PAD_NODE).then_inc(pads_set, 1)
                st = Steps(dve, step_s)
                for k in range(KB):
                    st(dve.tensor_scalar(chunk_no[:, k:k + 1], S.part_col[0:CK, 0:1], float(k * CK), None, ALU.add))
                dve.wait_ge(loaded, 16 * (6 + 2 * HEADS))
                for n in f:
                    st(dve.tensor_copy(f[n][:], raw[n][:]))
                st(dve.tensor_copy(rows_f[:, :, 0:CH], rows_i[:, :, 0:CH]))
                st(dve.scalar_tensor_tensor(w["rs"][:], f["typ"][:], float(N), f["src"][:], ALU.mult, ALU.add))
                st(dve.tensor_scalar(w["nd"][:], f["dst"][:], float(N - 1), None, ALU.min))
                st(dve.scalar_tensor_tensor(w["rd"][:], f["typ"][:], float(N), w["nd"][:], ALU.mult, ALU.add))
                st(dve.tensor_tensor(w["t0"][:], f["dst"][:], f["next"][:], ALU.not_equal))
                st(dve.tensor_scalar(w["t1"][:], f["dst"][:], float(-SKIP), None, ALU.add))
                st(dve.tensor_tensor(w["ro"][:], w["t0"][:], w["t1"][:], ALU.mult))
                st(dve.tensor_scalar(w["ro"][:], w["ro"][:], float(SKIP), None, ALU.add))
                st(dve.tensor_scalar(w["ro"][:, :, P - 1:P], chunk_no[:, :].unsqueeze(2), float(PART0), None, ALU.add))
                st(dve.tensor_tensor(w["t1"][:], f["dst"][:], f["prev"][:], ALU.not_equal))
                st(dve.tensor_scalar(S.pen_start[:], w["t1"][:], -BIG, None, ALU.mult))
                st(dve.memset(S.pen_start[:, :, 0:1], -BIG))
                st(dve.tensor_scalar(S.pen_end[:], w["t0"][:], -BIG, None, ALU.mult))
                st(dve.memset(S.pen_end[:, :, P - 1:P], -BIG))
                first = f["dst"][:, :, 0:1].broadcast_to([CK, KB, P])
                last = f["dst"][:, :, P - 1:P].broadcast_to([CK, KB, P])
                st(dve.tensor_tensor(w["t1"][:], f["dst"][:], first, ALU.not_equal))
                st(dve.tensor_scalar(S.pen_first[:], w["t1"][:], -BIG, None, ALU.mult))
                st(dve.tensor_tensor(w["t1"][:], f["dst"][:], last, ALU.not_equal))
                st(dve.tensor_scalar(S.pen_last[:], w["t1"][:], -BIG, None, ALU.mult))
                for t in range(NT):
                    dve.tensor_scalar(S.part_rel[:, t, :], f["dst"][:, :, P - 1], float(-TP * t), None, ALU.add)
                st(dve.memset(eq[:], 0.0))
                st(dve.tensor_tensor(eq[:, 0, :], rows_f[:, 0, 0:CH], rows_f[:, 1, 0:CH], ALU.is_equal))
                st(dve.tensor_tensor(eq[:, 1, 1:CH], rows_f[:, 0, 1:CH], rows_f[:, 1, 0:CH - 1], ALU.is_equal))
                st(dve.tensor_scalar(S.link[:], eq[:, 1, :], -1.0, BIG, ALU.add, ALU.mult))
                st(dve.tensor_tensor(S.carry_f[:], eq[:, 0, :], eq[:, 1, :], ALU.mult))
                st(dve.tensor_scalar(S.carry_f[:], S.carry_f[:], -1.0, BIG, ALU.add, ALU.mult))
                st(dve.memset(S.carry_b[:], 0.0))
                st(dve.tensor_tensor(S.carry_b[:, 0:CH - 1], eq[:, 0, 0:CH - 1], eq[:, 1, 1:CH], ALU.mult))
                st(dve.tensor_scalar(S.carry_b[:], S.carry_b[:], -1.0, BIG, ALU.add, ALU.mult))
                dve.memset(tmp_i[:], 0.0).then_inc(turned, 1)
                dve.wait_ge(turned, 2)
                for n, to in enumerate((S.dst_c, S.src_c, S.ew_c, S.row_src, S.row_dst, S.row_out, S.node_dst)):
                    dve.tensor_copy(to[:], turn[:, n, 0:CH])

            @block.tensor
            def _(pe):
                pe.wait_ge(turned, 1)
                for n, x in enumerate((f["dst"], f["src"], raw["ew"], w["rs"], w["rd"], w["ro"], w["nd"])):
                    for k in range(KB):
                        last = pe.transpose(turn[:, n, k * CK:(k + 1) * CK], x[:, k, :], S.ident[0:CK, 0:CK])
                last.then_inc(turned, 1)


def edge_softmax(nc, S, tag, q_tab, k_tab, H):
    SET = 8
    LOOPS = CH // (2 * SET)
    with stage(nc, tag) as a:
        score = a.sb("score", [P, CH, H])
        qs = [a.sb(f"qs{s}", [P, SET, H]) for s in range(2)]
        ks = [a.sb(f"ks{s}", [P, SET, H]) for s in range(2)]
        qi = [a.sb(f"qi{s}", [P, SET], I32) for s in range(2)]
        ki = [a.sb(f"ki{s}", [P, SET], I32) for s in range(2)]
        rowed = a.sb("rowed", [CK, H, KB, P])
        fwd = a.sb("fwd", [CK, H, KB, P])
        bwd = a.sb("bwd", [CK, H, KB, P])
        edge_f, edge_b = a.sb("edge_f", [HEADS, CH]), a.sb("edge_b", [HEADS, CH])
        run_f, run_b = a.sb("run_f", [HEADS, CH]), a.sb("run_b", [HEADS, CH])
        in_f, in_b = a.sb("in_f", [HEADS, CH]), a.sb("in_b", [HEADS, CH])
        carried = a.sb("carried", [CK, 2, KB, H])
        rows_ps = a.ps("rows_ps", [P, H, KB, P])
        small_ps = a.ps("small_ps", [HEADS, 2, 512])
        back_ps = a.ps("back_ps", [CK, 2, KB, H])
        index_ready = [a.sem(f"index_ready{s}") for s in range(2)]
        landed = a.borrow(S.pool_dma[0:2])
        added = [a.sem(f"added{s}") for s in range(2)]
        pool_go = a.sem("pool_go")
        scored, turned, rows_done, scans_done = a.sem("scored"), a.sem("turned"), a.sem("rows_done"), a.sem("scans_done")
        ends_turned, carries_done, carries_back = a.sem("ends_turned"), a.sem("carries_done"), a.sem("carries_back")
        less_max, exp_done, exp_turned, dve_step = a.sem("less_max"), a.sem("exp_done"), a.sem("exp_turned"), a.sem("dve_step")

        with nc.Block() as block:
            @block.scalar
            def _(act):
                with act.Fori(0, LOOPS) as i:
                    for s in range(2):
                        cols = bass.ds(i * (2 * SET) + s * SET, SET)
                        act.wait_ge(added[s], i)
                        nc.scalar.copy(qi[s][:], S.row_dst[:, cols]).then_inc(index_ready[s], 1)
                        nc.scalar.copy(ki[s][:], S.row_src[:, cols]).then_inc(index_ready[s], 1)

            @block.gpsimd
            def _(pool):
                with pool.Fori(0, LOOPS) as i:
                    for s in range(2):
                        pool.wait_ge(index_ready[s], i * 2 + 2)
                        pool.sem_inc(pool_go, 1)
                        for u in range(SET):
                            pool.indirect_dma_start(
                                qs[s][:, u, :], None, q_tab,
                                bass.IndirectOffsetOnAxis(ap=qi[s][:, u:u + 1], axis=0)).then_inc(landed[s], 16)
                            pool.indirect_dma_start(
                                ks[s][:, u, :], None, k_tab,
                                bass.IndirectOffsetOnAxis(ap=ki[s][:, u:u + 1], axis=0)).then_inc(landed[s], 16)

            @block.vector
            def _(dve):
                with dve.Fori(0, LOOPS) as i:
                    for s in range(2):
                        dve.wait_ge(landed[s], i * (32 * SET) + 32 * SET)
                        dve.tensor_tensor(score[:, bass.ds(i * (2 * SET) + s * SET, SET), :], qs[s][:], ks[s][:],
                                          ALU.add).then_inc(added[s], 1)
                for s in range(2):
                    dve.wait_ge(added[s], LOOPS)
                dve.scalar_tensor_tensor(score[:], score[:], SLOPE, score[:], ALU.mult, ALU.max).then_inc(scored, 1)
                dve.wait_ge(rows_done, 1)
                for h in range(H):
                    x = rowed[:, h].rearrange("c k j -> c (k j)")
                    fw = fwd[:, h].rearrange("c k j -> c (k j)")
                    bw = bwd[:, h].rearrange("c k j -> c (k j)")
                    start = S.pen_start[:].rearrange("c k j -> c (k j)")
                    end = S.pen_end[:].rearrange("c k j -> c (k j)")
                    dve.tensor_tensor_scan(fw, start, x, -BIG, ALU.add, ALU.max).then_inc(scans_done, 1)
                    dve.tensor_tensor_scan(bw[:, ::-1], end[:, ::-1], x[:, ::-1], -BIG, ALU.add,
                                           ALU.max).then_inc(scans_done, 1)
                st = Steps(dve, dve_step)
                dve.wait_ge(ends_turned, 1)
                st(dve.tensor_copy(edge_f[0:H, :], small_ps[0:H, 0, 0:CH]))
                st(dve.tensor_copy(edge_b[0:H, :], small_ps[0:H, 1, 0:CH]))
                st(dve.tensor_tensor_scan(run_f[0:H, :], S.carry_f[0:H, :], edge_f[0:H, :], -BIG, ALU.add, ALU.max))
                st(dve.tensor_tensor_scan(run_b[0:H, ::-1], S.carry_b[0:H, ::-1], edge_b[0:H, ::-1], -BIG, ALU.add,
                                          ALU.max))
                st(dve.memset(in_f[0:H, :], -BIG))
                st(dve.memset(in_b[0:H, :], -BIG))
                dve.tensor_tensor(in_f[0:H, 1:CH], run_f[0:H, 0:CH - 1], S.link[0:H, 1:CH],
                                  ALU.add).then_inc(carries_done, 1)
                dve.tensor_tensor(in_b[0:H, 0:CH - 1], run_b[0:H, 1:CH], S.link[0:H, 1:CH],
                                  ALU.add).then_inc(carries_done, 1)
                dve.wait_ge(carries_back, 1)
                st(dve.tensor_copy(carried[:], back_ps[:]))
                st(dve.tensor_tensor(fwd[:], fwd[:], bwd[:], ALU.max))
                for n, pen in ((0, S.pen_first), (1, S.pen_last)):
                    for h in range(H):
                        dve.tensor_tensor(bwd[:, h], pen[:], carried[:, n, :, h].unsqueeze(2).broadcast_to([CK, KB, P]),
                                          ALU.add).then_inc(dve_step, 1)
                    st.n += H
                    dve.wait_ge(dve_step, st.n)
                    st(dve.tensor_tensor(fwd[:], fwd[:], bwd[:], ALU.max))
                dve.tensor_tensor(rowed[:], rowed[:], fwd[:], ALU.subtract).then_inc(less_max, 1)
                dve.wait_ge(exp_turned, 1)
                for k in range(KB):
                    dve.tensor_copy(S.ex[:, k * CK:(k + 1) * CK, 0:H],
                                    rows_ps[:, :, k, 0:CK].rearrange("p h c -> p c h"))

            @block.tensor
            def _(pe):
                pe.wait_ge(scored, 1)
                for h in range(H):
                    for k in range(KB):
                        last = pe.transpose(rows_ps[0:CK, h, k, :], score[:, k * CK:(k + 1) * CK, h], S.ident[:])
                last.then_inc(turned, 1)
                pe.wait_ge(scans_done, 2 * H)
                for n, (x, j) in enumerate(((fwd, P - 1), (bwd, 0))):
                    for k in range(KB):
                        last = pe.transpose(small_ps[0:H, n, k * CK:(k + 1) * CK], x[:, :, k, j], S.ident[0:CK, 0:CK])
                last.then_inc(ends_turned, 1)
                pe.wait_ge(carries_done, 2)
                for n, x in enumerate((in_f, in_b)):
                    for k in range(KB):
                        last = pe.transpose(back_ps[:, n, k, :], x[0:H, k * CK:(k + 1) * CK], S.ident[0:H, 0:H])
                last.then_inc(carries_back, 1)
                pe.wait_ge(exp_done, 1)
                for h in range(H):
                    for k in range(KB):
                        last = pe.transpose(rows_ps[:, h, k, 0:CK], rowed[:, h, k, :], S.ident[0:CK, 0:CK])
                last.then_inc(exp_turned, 1)

            @block.scalar
            def _(act):
                act.wait_ge(turned, 1)
                nc.scalar.copy(rowed[:], rows_ps[0:CK]).then_inc(rows_done, 1)
                act.wait_ge(less_max, 1)
                nc.scalar.activation(rowed[:], rowed[:], ACT.Exp).then_inc(exp_done, 1)


def edge_sums(nc, S, tag, table, width, weights, H, gather_rows, key_col, key_pad, scatter_rows, out_tab, accumulate):
    SET = 4
    LOOPS = CH // (2 * SET)
    HW = width // H
    HX = 0 if accumulate else H
    with stage(nc, tag) as a:
        x = [a.sb(f"x{s}", [P, SET, width]) for s in range(2)]
        wt = [a.sb(f"wt{s}", [P, SET, H]) for s in range(2)]
        keys = [a.sb(f"keys{s}", [P, SET, P], I32) for s in range(2)]
        mask = [a.sb(f"mask{s}", [P, SET, P]) for s in range(2)]
        out = [a.sb(f"out{s}", [P, SET, width + HX]) for s in range(2)]
        gi = [a.sb(f"gi{s}", [P, SET], I32) for s in range(2)]
        si = [a.sb(f"si{s}", [P, SET], I32) for s in range(2)]
        sums = a.ps("sums", [P, SET, 512])
        dens = a.ps("dens", [P, 2, SET, HEADS])
        names = ("index_ready", "keys_landed", "masked", "weighted", "summed", "copied")
        index_ready, keys_landed, masked, weighted, summed, copied = (
            [a.sem(f"{n}{s}") for s in range(2)] for n in names)
        landed = a.borrow(S.pool_dma[0:2])
        scatters = a.borrow(S.pool_dma[2:2 + SET])
        scattered = scatters[0:2]
        added = scatters
        pool_go = a.sem("pool_go")

        def cols(i, s):
            return bass.ds(i * (2 * SET) + s * SET, SET)

        with nc.Block() as block:
            @block.sync
            def _(sp):
                with sp.Fori(0, LOOPS) as i:
                    for s in range(2):
                        sp.wait_ge(masked[s], i)
                        first = i * (2 * SET * P) + s * SET * P
                        sp.dma_start(keys[s][:].rearrange("p u j -> p (u j)"),
                                     row_of(key_pad[bass.ds(first, SET * P)]).broadcast_to([P, SET * P])
                                     ).then_inc(keys_landed[s], 16)

            @block.gpsimd
            def _(pool):
                def gather(i, s):
                    pool.wait_ge(index_ready[s], i + 1)
                    pool.sem_inc(pool_go, 1)
                    for u in range(SET):
                        pool.indirect_dma_start(
                            x[s][:, u, :], None, table,
                            bass.IndirectOffsetOnAxis(ap=gi[s][:, u:u + 1], axis=0)).then_inc(landed[s], 16)

                def scatter(i, s):
                    pool.wait_ge(copied[s], i * 3 + 3)
                    pool.sem_inc(pool_go, 1)
                    for u in range(SET):
                        to = bass.IndirectOffsetOnAxis(ap=si[s][:, u:u + 1], axis=0)
                        if accumulate:
                            pool.wait_ge(added[u], i * 32 + 16 * s)
                            pool.sem_inc(pool_go, 1)
                            pool.indirect_dma_start(out_tab[u], to, out[s][:, u, :], None,
                                                    compute_op=ALU.add).then_inc(added[u], 16)
                        else:
                            pool.indirect_dma_start(out_tab, to, out[s][:, u, :], None, bounds_check=AGG_ROWS - 1,
                                                    oob_is_err=False).then_inc(scattered[s], 16)

                gather(0, 0)
                with pool.Fori(0, LOOPS - 1) as i:
                    gather(i, 1)
                    scatter(i, 0)
                    gather(i + 1, 0)
                    scatter(i, 1)
                gather(LOOPS - 1, 1)
                scatter(LOOPS - 1, 0)
                scatter(LOOPS - 1, 1)
                for s in range(2):
                    if not accumulate:
                        pool.wait_ge(scattered[s], 16 * SET * LOOPS)
                for u in range(SET):
                    if accumulate:
                        pool.wait_ge(added[u], 32 * LOOPS)

            @block.scalar
            def _(act):
                def indices(i, s):
                    act.wait_ge(summed[s], i)
                    nc.scalar.copy(gi[s][:], gather_rows[:, cols(i, s)]).then_inc(index_ready[s], 1)

                def results(i, s):
                    if accumulate:
                        for u in range(SET):
                            act.wait_ge(added[u], i * 32 + (0 if s == 0 else 0))
                    else:
                        act.wait_ge(scattered[s], i * (16 * SET))
                    nc.scalar.copy(si[s][:], scatter_rows[:, cols(i, s)]).then_inc(copied[s], 1)
                    act.wait_ge(summed[s], i + 1)
                    nc.scalar.copy(out[s][:, :, 0:width], sums[:, :, 0:width]).then_inc(copied[s], 1)
                    if HX:
                        nc.scalar.copy(out[s][:, :, width:width + HX], dens[:, s, :, 0:HX]).then_inc(copied[s], 1)
                    else:
                        act.sem_inc(copied[s], 1)

                with act.Fori(0, LOOPS) as i:
                    indices(i, 0)
                    indices(i, 1)
                    results(i, 0)
                    results(i, 1)

            @block.vector
            def _(dve):
                with dve.Fori(0, LOOPS) as i:
                    for s in range(2):
                        dve.wait_ge(keys_landed[s], i * 16 + 16)
                        dve.wait_ge(summed[s], i)
                        dve.tensor_tensor(mask[s][:], keys[s][:],
                                          key_col[:, cols(i, s)].unsqueeze(2).broadcast_to([P, SET, P]),
                                          ALU.is_equal).then_inc(masked[s], 1)
                        if HX:
                            dve.tensor_copy(wt[s][:], weights[:, cols(i, s), 0:H]).then_inc(weighted[s], 1)
                        dve.wait_ge(landed[s], i * (16 * SET) + 16 * SET)
                        by = weights[:, cols(i, s), 0:H].rearrange("p u h -> p (u h)")
                        v = x[s][:].rearrange("p u (h w) -> p (u h) w", h=H)
                        dve.tensor_tensor(v, v, by.unsqueeze(2).broadcast_to([P, SET * H, HW]),
                                          ALU.mult).then_inc(weighted[s], 1)

            @block.tensor
            def _(pe):
                with pe.Fori(0, LOOPS) as i:
                    for s in range(2):
                        pe.wait_ge(masked[s], i + 1)
                        pe.wait_ge(weighted[s], i * 2 + 2 if HX else i + 1)
                        pe.wait_ge(copied[1 - s], i * 3 + 3 * s)
                        for u in range(SET):
                            last = pe.matmul(sums[:, u, 0:width], mask[s][:, u, :], x[s][:, u, :], start=True, stop=True)
                            if HX:
                                last = pe.matmul(dens[:, s, u, 0:H], mask[s][:, u, :], wt[s][:, u, :],
                                                 start=True, stop=True)
                        last.then_inc(summed[s], 1)


def representatives(nc, g, S):
    SET = 8
    LOOPS = CH // SET
    S.row_rep = g.sb("row_rep", [P, CH], I32)
    with stage(nc, "rep_") as a:
        keys = [a.sb(f"keys{s}", [P, SET, P], I32) for s in range(2)]
        same = a.sb("same", [P, SET, P])
        later_mask = a.sb("later_mask", [P, P])
        later = a.sb("later", [P, CH])
        dummy = a.sb("dummy", [P, 1])
        row = a.sb("row", [P, CH])
        keys_landed = [a.sem(f"keys_landed{s}") for s in range(2)]
        counted = a.sem("counted")
        step_s = a.sem("step")
        loop_s = a.sem("loop")
        with nc.Block() as block:
            @block.sync
            def _(sp):
                with sp.Fori(0, LOOPS // 2) as i:
                    for s in range(2):
                        sp.wait_ge(counted, i * 2)
                        first = i * (2 * SET * P) + s * SET * P
                        sp.dma_start(keys[s][:].rearrange("p u j -> p (u j)"),
                                     row_of(S.src_pad[bass.ds(first, SET * P)]).broadcast_to([P, SET * P])
                                     ).then_inc(keys_landed[s], 16)

            @block.vector
            def _(dve):
                st = Steps(dve, step_s)
                st(dve.tensor_scalar(later_mask[:], S.iota_row[:], S.part_col[:, 0:1], None, ALU.is_gt))
                with dve.Fori(0, LOOPS // 2) as i:
                    for s in range(2):
                        cols = bass.ds(i * (2 * SET) + s * SET, SET)
                        dve.wait_ge(keys_landed[s], i * 16 + 16)
                        dve.tensor_tensor(same[:], keys[s][:], S.src_c[:, cols].unsqueeze(2).broadcast_to([P, SET, P]),
                                          ALU.is_equal).then_inc(loop_s, 1)
                        dve.wait_ge(loop_s, i * 4 + 2 * s + 1)
                        dve.tensor_tensor(same[:], same[:], later_mask[:].unsqueeze(1).broadcast_to([P, SET, P]),
                                          ALU.mult).then_inc(loop_s, 1)
                        dve.wait_ge(loop_s, i * 4 + 2 * s + 2)
                        dve.tensor_reduce(later[:, cols], same[:], AX.X, ALU.max).then_inc(counted, 1)
                        dve.wait_ge(counted, i * 2 + s + 1)
                st(dve.tensor_scalar(dummy[:], S.part_col[:], float(N), None, ALU.add))
                st(dve.tensor_scalar(row[:], S.src_c[:], dummy[:, 0:1], None, ALU.subtract))
                st(dve.tensor_tensor(later[:], row[:], later[:], ALU.mult))
                st(dve.tensor_tensor(row[:], S.src_c[:], later[:], ALU.subtract))
                dve.tensor_copy(S.row_rep[:], row[:])


def layernorm_stats(nc, S, tag, x, eps=1e-5):
    with stage(nc, tag) as a:
        stats = a.sb("stats", [TP, NT, 6])
        mv = a.sb("mv", [TP, NT, 2])
        counted, var_ready, root_ready, step_s = a.sem("counted"), a.sem("var_ready"), a.sem("root_ready"), a.sem("step")
        with nc.Block() as block:
            @block.vector
            def _(dve):
                with dve.Fori(0, NG) as i:
                    for u in range(GROUP):
                        t = i * GROUP + u
                        dve.bn_stats(stats[:, bass.ds(t, 1), :].rearrange("p a s -> p (a s)"),
                                     x[:, bass.ds(t, 1), :].rearrange("p a d -> p (a d)")).then_inc(counted, 1)
                dve.wait_ge(counted, NT)
                for t in range(NT):
                    last = dve.bn_aggr(mv[:, t, :], stats[:, t, :])
                    last.then_inc(counted, 1)
                dve.wait_ge(counted, 2 * NT)
                dve.tensor_scalar(S.ln_r[:], mv[:, :, 1], eps, None, ALU.add).then_inc(var_ready, 1)
                dve.wait_ge(root_ready, 1)
                st = Steps(dve, step_s)
                st(dve.reciprocal(S.ln_r[:], S.ln_r[:]))
                dve.scalar_tensor_tensor(S.ln_b[:], mv[:, :, 0], -1.0, S.ln_r[:], ALU.mult, ALU.mult)

            @block.scalar
            def _(act):
                act.wait_ge(var_ready, 1)
                nc.scalar.activation(S.ln_r[:], S.ln_r[:], ACT.Sqrt).then_inc(root_ready, 1)


def col(ap, t):
    return ap[:, bass.ds(t, 1)]


def tile(ap, t):
    return ap[:, bass.ds(t, 1), :].rearrange("p a d -> p (a d)")


def mix0(nc, g, S, w_conv, bn_gamma, bn_beta, w_dw, pw_blocks, w_res, b_res):
    C6 = 6
    with stage(nc, "m0_") as a:
        h = a.sb("h", [P, C6, N])
        affine = a.sb("affine", [P, C6, 2])
        pw = a.sb("pw", [P, C6, P])
        wres = a.sb("wres", [P, 4, D])
        bres = a.sb("bres", [TP, D])
        group_ones = a.sb("group_ones", [P, P])
        weights_in = a.sem("weights_in")

        with stage(nc, "m0a_") as b:
            wconv = b.sb("wconv", [P, 2, C6 * P])
            dw = b.sb("dw", [P, C6])
            gb = b.sb("gb", [P, 2, C6])
            sq_junk = b.sb("sq_junk", [TP, D])
            ss, m, lo, hi, pick, sc, sr, sb_ = (b.sb(n, [TP, NT]) for n in (
                "ss", "m", "lo", "hi", "pick", "sc", "sr", "sb"))
            xm = [b.sb(f"xm{s}", [TP, D]) for s in range(2)]
            xt = [b.sb(f"xt{s}", [P, 2, TP]) for s in range(2)]
            stats = b.sb("stats", [P, C6, 7, 6])
            mv = b.sb("mv", [P, C6, 2])
            turn_ps = b.ps("turn", [P, 2, 512])
            conv_ps = b.ps("conv", [P, 2, 2, 512])
            squared, step_s, roots, logs = b.sem("squared"), b.sem("step"), b.sem("roots"), b.sem("logs")
            scaled, turned, turn_copied = b.sem("scaled"), b.sem("turned"), b.sem("turn_copied")
            conv_done, conv_copied, bn_step, bn_root = (
                b.sem("conv_done"), b.sem("conv_copied"), b.sem("bn_step"), b.sem("bn_root"))
            affine_ready, zeroed, root_asked = b.sem("affine_ready"), b.sem("zeroed"), b.sem("root_asked")
            WIDTHS = [448] * 6 + [N - 6 * 448]
            with nc.Block() as block:
                @block.sync
                def _(sp):
                    sp.dma_start(wconv[:], w_conv.rearrange("(k p) c -> p k c", p=P)).then_inc(weights_in, 16)
                    for n, x in enumerate((bn_gamma, bn_beta)):
                        sp.dma_start(gb[:, n, :], x.rearrange("(c p) -> p c", p=P),
                                     allow_slow_non_contiguous=True).then_inc(weights_in, 16)
                    sp.dma_start(dw[:], w_dw.rearrange("(c p) -> p c", p=P),
                                 allow_slow_non_contiguous=True).then_inc(weights_in, 16)
                    sp.dma_start(wres[:], w_res.rearrange("(k p) c -> p k c", p=P)).then_inc(weights_in, 16)
                    sp.dma_start(bres[:], spread(b_res, TP)).then_inc(weights_in, 16)
                    sp.wait_ge(zeroed, 1)
                    for q in range(4):
                        sp.dma_start(pw[32 * q:32 * q + 32, :, 32 * q:32 * q + 32], pw_blocks[q]).then_inc(weights_in, 16)

                @block.scalar
                def _(act):
                    with act.Fori(0, NG) as i:
                        for u in range(GROUP):
                            t = i * GROUP + u
                            act.wait_ge(squared, i * GROUP + u)
                            nc.scalar.activation(sq_junk[:], tile(S.x, t), ACT.Square, scale=col(S.ln_r, t),
                                                 bias=col(S.ln_b, t), accum_out=col(ss, t)).then_inc(squared, 1)
                    act.wait_ge(root_asked, 1)
                    nc.scalar.activation(m[:], ss[:], ACT.Sqrt).then_inc(roots, 1)
                    act.wait_ge(root_asked, 2)
                    nc.scalar.activation(lo[:], lo[:], ACT.Ln).then_inc(logs, 1)
                    nc.scalar.activation(hi[:], hi[:], ACT.Ln).then_inc(logs, 1)
                    with act.Fori(0, NG) as i:
                        for u in range(GROUP):
                            act.wait_ge(turned, ready(i, u))
                            act.wait_ge(conv_done, freed(i, u, 2))
                            nc.scalar.copy(xt[u % 2][:], turn_ps[:, u % 2, 0:2 * TP].rearrange("p (k n) -> p k n", k=2)
                                           ).then_inc(turn_copied, 1)
                    act.wait_ge(bn_root, 1)
                    nc.scalar.activation(affine[:, :, 0], affine[:, :, 0], ACT.Sqrt).then_inc(bn_root, 1)
                    act.wait_ge(affine_ready, 1)
                    for c in range(C6):
                        nc.scalar.activation(h[:, c, :], h[:, c, :], ACT.Relu, scale=affine[:, c, 0:1],
                                             bias=affine[:, c, 1:2])

                @block.vector
                def _(dve):
                    st = Steps(dve, step_s)
                    dve.memset(pw[:], 0.0).then_inc(zeroed, 1)
                    st(dve.memset(group_ones[:], 0.0))
                    for q in range(4):
                        dve.memset(group_ones[32 * q:32 * q + 32, 32 * q:32 * q + 32], 1.0)
                    dve.wait_ge(squared, NT)
                    dve.tensor_scalar(ss[:], ss[:], MIN_NORM * MIN_NORM, None, ALU.max).then_inc(root_asked, 1)
                    dve.wait_ge(roots, 1)
                    st(dve.reciprocal(sc[:], m[:]))
                    st(dve.tensor_scalar(m[:], m[:], MAXNORM, None, ALU.min))
                    st(dve.tensor_scalar(lo[:], m[:], -1.0, 1.0, ALU.mult, ALU.add))
                    dve.tensor_scalar(hi[:], m[:], 1.0, None, ALU.add).then_inc(root_asked, 1)
                    st(dve.tensor_tensor(sr[:], m[:], m[:], ALU.mult))
                    st(dve.tensor_scalar(sb_[:], sr[:], 1.0 / 7, 1.0 / 5, ALU.mult, ALU.add))
                    st(dve.tensor_tensor(sb_[:], sb_[:], sr[:], ALU.mult))
                    st(dve.tensor_scalar(sb_[:], sb_[:], 1.0 / 3, None, ALU.add))
                    st(dve.tensor_tensor(sb_[:], sb_[:], sr[:], ALU.mult))
                    st(dve.scalar_tensor_tensor(sb_[:], sb_[:], 1.0, m[:], ALU.add, ALU.mult))
                    st(dve.tensor_scalar(pick[:], m[:], 0.0625, None, ALU.is_lt))
                    dve.wait_ge(logs, 2)
                    st(dve.tensor_tensor(hi[:], hi[:], lo[:], ALU.subtract))
                    st(dve.tensor_scalar(hi[:], hi[:], 0.5, None, ALU.mult))
                    st(dve.tensor_tensor(sb_[:], sb_[:], hi[:], ALU.subtract))
                    st(dve.tensor_tensor(sb_[:], sb_[:], pick[:], ALU.mult))
                    st(dve.tensor_tensor(hi[:], hi[:], sb_[:], ALU.add))
                    st(dve.tensor_tensor(sc[:], sc[:], hi[:], ALU.mult))
                    st(dve.tensor_tensor(sr[:], S.ln_r[:], sc[:], ALU.mult))
                    st(dve.tensor_tensor(sb_[:], S.ln_b[:], sc[:], ALU.mult))

                    def log_map(t, u, free):
                        dve.wait_ge(turned, free)
                        dve.tensor_scalar(xm[u % 2][:], tile(S.x, t), col(sr, t), col(sb_, t), ALU.mult,
                                          ALU.add).then_inc(scaled, 1)

                    with dve.Fori(0, NG) as i:
                        for u in range(GROUP):
                            t = i * GROUP + u
                            log_map(t, u, freed(i, u, 2))
                            dve.wait_ge(conv_done, ready(i, u))
                            dve.tensor_copy(h[:, :, bass.ds(t * TP, TP)].rearrange("p (b c) n -> p b c n", b=2),
                                            conv_ps[:, u % 2, :, 0:3 * TP].rearrange("p b (c n) -> p b c n", c=3)
                                            ).then_inc(conv_copied, 1)
                    dve.wait_ge(conv_copied, NT)
                    for c in range(C6):
                        for w, width in enumerate(WIDTHS):
                            last = dve.bn_stats(stats[:, c, w, :], h[:, c, 448 * w:448 * w + width])
                    bn = Steps(dve, bn_step)
                    bn(last)
                    for c in range(C6):
                        last = dve.bn_aggr(mv[:, c, :], stats[:, c].rearrange("p w s -> p (w s)"))
                    bn(last)
                    dve.tensor_scalar(affine[:, :, 0], mv[:, :, 1], 1e-5, None, ALU.add).then_inc(bn_root, 1)
                    dve.wait_ge(bn_root, 2)
                    dve.wait_ge(weights_in, 160)
                    bn(dve.reciprocal(affine[:, :, 0], affine[:, :, 0]))
                    bn(dve.tensor_tensor(affine[:, :, 0], affine[:, :, 0], gb[:, 0, :], ALU.mult))
                    bn(dve.tensor_tensor(affine[:, :, 1], mv[:, :, 0], affine[:, :, 0], ALU.mult))
                    dve.tensor_tensor(affine[:, :, 1], gb[:, 1, :], affine[:, :, 1],
                                      ALU.subtract).then_inc(affine_ready, 1)
                    for c in range(C6):
                        dve.tensor_scalar(pw[:, c, :], pw[:, c, :], dw[:, c:c + 1], None, ALU.mult)

                @block.tensor
                def _(pe):
                    pe.wait_ge(weights_in, 160)
                    with pe.Fori(0, NG) as i:
                        for u in range(GROUP):
                            pe.wait_ge(scaled, ready(i, u))
                            pe.wait_ge(turn_copied, freed(i, u, 2))
                            for k in range(2):
                                last = pe.transpose(turn_ps[:, u % 2, k * TP:(k + 1) * TP],
                                                    xm[u % 2][:, k * P:(k + 1) * P], S.ident[0:TP, 0:TP])
                            last.then_inc(turned, 1)
                            pe.wait_ge(turn_copied, ready(i, u))
                            pe.wait_ge(conv_copied, freed(i, u, 2))
                            for c in range(C6):
                                for k in range(2):
                                    last = pe.matmul(conv_ps[:, u % 2, c // 3, (c % 3) * TP:(c % 3 + 1) * TP],
                                                     wconv[:, k, c * P:(c + 1) * P], xt[u % 2][:, k, :],
                                                     start=(k == 0), stop=(k == 1))
                            last.then_inc(conv_done, 1)

        with stage(nc, "m0b_") as b:
            t_sq = b.sb("t_sq", [P, C6, TP])
            cat = [b.sb(f"cat{s}", [P, 3, 4, TP]) for s in range(2)]
            cat_sq = b.sb("cat_sq", [P, 3, 4, TP])
            n1, r1, n2, r2 = (b.sb(n, [P, TP]) for n in ("n1", "r1", "n2", "r2"))
            rq, rk, vv, rv, o, o_sq = (b.sb(n, [P, 4, TP]) for n in ("rq", "rk", "vv", "rv", "o", "o_sq"))
            ss3, f3, ss4, f4 = (b.sb(n, [TP, NT]) for n in ("ss3", "f3", "ss4", "f4"))
            junk = b.sb("junk", [TP, D])
            norm_ps = b.ps("norm", [P, 2, 512])
            point_ps = b.ps("point", [P, 2, 512])
            ksum_ps = b.ps("ksum", [P, 512])
            proj_ps = b.ps("proj", [TP, 512])
            n3_ps = b.ps("n3", [TP, 512])
            names = ("t_squared", "n1_mm", "n1_in", "n1_root", "t_made", "point_mm", "point_copied", "cat_squared",
                     "n2_mm", "n2_in", "n2_root", "rk_made", "k_summed", "o_made", "o_squared", "n3_mm", "n3_copied",
                     "proj_mm", "proj_copied", "dstep", "f3_in", "f3_root", "f3_done", "sq4", "biased", "f4_root", "f4_in", "f4_step")
            (t_squared, n1_mm, n1_in, n1_root, t_made, point_mm, point_copied, cat_squared, n2_mm, n2_in, n2_root,
             rk_made, k_summed, o_made, o_squared, n3_mm, n3_copied, proj_mm, proj_copied, dstep, f3_in, f3_root,
             f3_done, sq4, biased, f4_root, f4_in, f4_step) = (b.sem(n) for n in names)
            with nc.Block() as block:
                @block.scalar
                def _(act):
                    with act.Fori(0, NG) as i:
                        for u in range(GROUP):
                            t = i * GROUP + u
                            act.wait_ge(n1_mm, freed(i, u, 1))
                            nc.scalar.activation(t_sq[:], h[:, :, bass.ds(t * TP, TP)], ACT.Square).then_inc(t_squared, 1)
                            act.wait_ge(n1_in, ready(i, u))
                            nc.scalar.activation(n1[:], n1[:], ACT.Sqrt).then_inc(n1_root, 1)
                            act.wait_ge(point_mm, ready(i, u))
                            for half in range(2):
                                for c in range(3 * half, 3 * half + 3):
                                    nc.scalar.copy(cat[u % 2][:, c // 2, 2 + c % 2, :],
                                                   point_ps[:, half, (c % 3) * TP:(c % 3 + 1) * TP]
                                                   ).then_inc(point_copied, 1)
                            act.wait_ge(t_made, ready(i, u))
                            act.wait_ge(point_copied, i * (6 * GROUP) + 6 * (u + 1))
                            act.wait_ge(n2_mm, freed(i, u, 1))
                            nc.scalar.activation(cat_sq[:], cat[u % 2][:], ACT.Square).then_inc(cat_squared, 1)
                            act.wait_ge(n2_in, ready(i, u))
                            nc.scalar.activation(n2[:], n2[:], ACT.Sqrt).then_inc(n2_root, 1)
                            act.wait_ge(o_made, ready(i, u))
                            act.wait_ge(n3_mm, freed(i, u, 1))
                            nc.scalar.activation(o_sq[:], o[:], ACT.Square).then_inc(o_squared, 1)
                            act.wait_ge(n3_mm, ready(i, u))
                            nc.scalar.copy(col(ss3, t), n3_ps[:, 0:1]).then_inc(n3_copied, 1)
                            act.wait_ge(proj_mm, ready(i, u))
                            nc.scalar.copy(tile(S.fx, t), proj_ps[:, 0:D]).then_inc(proj_copied, 1)
                    act.wait_ge(f3_in, 1)
                    nc.scalar.activation(f3[:], ss3[:], ACT.Sqrt).then_inc(f3_root, 1)
                    with act.Fori(0, NG) as i:
                        for u in range(GROUP):
                            t = i * GROUP + u
                            act.wait_ge(biased, ready(i, u))
                            act.wait_ge(sq4, i * GROUP + u)
                            nc.scalar.activation(junk[:], tile(S.fx, t), ACT.Square, accum_out=col(ss4, t)).then_inc(sq4, 1)
                    act.wait_ge(f4_in, 1)
                    nc.scalar.activation(ss4[:], ss4[:], ACT.Sqrt).then_inc(f4_root, 1)
                    act.wait_ge(f4_root, 1)
                    nc.scalar.activation(f4[:], ss4[:], ACT.Tanh).then_inc(f4_root, 1)

                @block.vector
                def _(dve):
                    def over(x, m):
                        return x[:].unsqueeze(1).broadcast_to([P, m, TP])

                    with dve.Fori(0, NG) as i:
                        for u in range(GROUP):
                            t = i * GROUP + u
                            base = i * (8 * GROUP) + 8 * u
                            c = cat[u % 2]
                            dve.wait_ge(n1_mm, ready(i, u))
                            dve.tensor_scalar(n1[:], norm_ps[:, 0, 0:TP], MIN_NORM * MIN_NORM, None,
                                              ALU.max).then_inc(n1_in, 1)
                            dve.wait_ge(n1_root, ready(i, u))
                            after(dve, dve.reciprocal(r1[:], n1[:]), dstep, base + 1)
                            after(dve, dve.scalar_tensor_tensor(r1[:], n1[:], ATANH_MAX, r1[:], ALU.min, ALU.mult),
                                  dstep, base + 2)
                            dve.wait_ge(cat_squared, freed(i, u, 2))
                            hv = h[:, :, bass.ds(t * TP, TP)].rearrange("p (r c) n -> p r c n", r=3)
                            for r in range(3):
                                ins = dve.tensor_tensor(c[:, r, 0:2, :], hv[:, r], over(r1, 2), ALU.mult)
                            ins.then_inc(t_made, 1)
                            dve.wait_ge(n2_mm, ready(i, u))
                            dve.tensor_scalar(n2[:], norm_ps[:, 1, 0:TP], MIN_NORM * MIN_NORM, None,
                                              ALU.max).then_inc(n2_in, 1)
                            dve.wait_ge(n2_root, ready(i, u))
                            after(dve, dve.reciprocal(r2[:], n2[:]), dstep, base + 3)
                            after(dve, dve.scalar_tensor_tensor(r2[:], n2[:], ATANH_MAX, r2[:], ALU.min, ALU.mult),
                                  dstep, base + 4)
                            dve.wait_ge(k_summed, freed(i, u, 1))
                            dve.scalar_tensor_tensor(rk[:], c[:, 1], 0.0, over(r2, 4), ALU.max,
                                                     ALU.mult).then_inc(rk_made, 1)
                            dve.scalar_tensor_tensor(rq[:], c[:, 0], 0.0, over(r2, 4), ALU.max, ALU.mult)
                            after(dve, dve.tensor_tensor(vv[:], c[:, 2], over(r2, 4), ALU.mult), dstep, base + 5)
                            after(dve, dve.tensor_scalar(rv[:], vv[:], 1e-15, None, ALU.add), dstep, base + 6)
                            after(dve, dve.reciprocal(rv[:], rv[:]), dstep, base + 7)
                            dve.wait_ge(k_summed, ready(i, u))
                            dve.wait_ge(proj_mm, freed(i, u, 1))
                            dve.wait_ge(o_squared, freed(i, u, 1))
                            after(dve, dve.tensor_tensor(o[:].rearrange("p a n -> p (a n)"),
                                                         rq[:].rearrange("p a n -> p (a n)"),
                                                         ksum_ps[:, 0:4 * TP], ALU.mult), dstep, base + 8)
                            dve.tensor_tensor(vv[:], vv[:], rv[:], ALU.mult).then_inc(rk_made, 1)
                            dve.wait_ge(rk_made, i * (2 * GROUP) + 2 * u + 2)
                            dve.tensor_tensor(o[:], o[:], vv[:], ALU.mult).then_inc(o_made, 1)
                    st = Steps(dve, f4_step)
                    dve.wait_ge(n3_copied, NT)
                    dve.tensor_scalar(ss3[:], ss3[:], MIN_NORM * MIN_NORM, None, ALU.max).then_inc(f3_in, 1)
                    dve.wait_ge(f3_root, 1)
                    st(dve.reciprocal(ss3[:], f3[:]))
                    st(dve.scalar_tensor_tensor(f3[:], f3[:], ATANH_MAX, ss3[:], ALU.min, ALU.mult))
                    dve.wait_ge(proj_copied, NT)
                    with dve.Fori(0, NG) as i:
                        for u in range(GROUP):
                            t = i * GROUP + u
                            dve.scalar_tensor_tensor(tile(S.fx, t), tile(S.fx, t), col(f3, t), bres[:], ALU.mult,
                                                     ALU.add).then_inc(biased, 1)
                    dve.wait_ge(sq4, NT)
                    dve.tensor_scalar(ss4[:], ss4[:], MIN_NORM * MIN_NORM, None, ALU.max).then_inc(f4_in, 1)
                    dve.wait_ge(f4_root, 2)
                    st(dve.reciprocal(ss4[:], ss4[:]))
                    st(dve.scalar_tensor_tensor(f4[:], f4[:], MAXNORM, ss4[:], ALU.min, ALU.mult))
                    with dve.Fori(0, NG) as i:
                        for u in range(GROUP):
                            t = i * GROUP + u
                            dve.tensor_scalar(tile(S.fx, t), tile(S.fx, t), col(f4, t), None, ALU.mult)

                @block.tensor
                def _(pe):
                    with pe.Fori(0, NG) as i:
                        for u in range(GROUP):
                            c = cat[u % 2]
                            pe.wait_ge(t_squared, ready(i, u))
                            pe.wait_ge(n1_in, freed(i, u, 1))
                            for k in range(C6):
                                last = pe.matmul(norm_ps[:, 0, 0:TP], S.ones[:], t_sq[:, k, :],
                                                 start=(k == 0), stop=(k == C6 - 1))
                            last.then_inc(n1_mm, 1)
                            pe.wait_ge(t_made, ready(i, u))
                            pe.wait_ge(point_copied, i * (6 * GROUP) + 6 * u)
                            for k in range(C6):
                                last = pe.matmul(point_ps[:, k // 3, (k % 3) * TP:(k % 3 + 1) * TP], pw[:, k, :],
                                                 c[:, k // 2, k % 2, :], start=True, stop=True)
                            last.then_inc(point_mm, 1)
                            pe.wait_ge(cat_squared, ready(i, u))
                            pe.wait_ge(n2_in, freed(i, u, 1))
                            for k in range(12):
                                last = pe.matmul(norm_ps[:, 1, 0:TP], S.ones[:], cat_sq[:, k // 4, k % 4, :],
                                                 start=(k == 0), stop=(k == 11))
                            last.then_inc(n2_mm, 1)
                            pe.wait_ge(rk_made, i * (2 * GROUP) + 2 * u + 1)
                            pe.wait_ge(o_made, freed(i, u, 1))
                            pe.matmul(ksum_ps[:, 0:4 * TP], group_ones[:], rk[:].rearrange("p a n -> p (a n)"),
                                      start=True, stop=True).then_inc(k_summed, 1)
                            pe.wait_ge(o_made, ready(i, u))
                            pe.wait_ge(proj_copied, freed(i, u, 1))
                            for k in range(4):
                                last = pe.matmul(proj_ps[:, 0:D], o[:, k, :], wres[:, k, :], start=(k == 0), stop=(k == 3))
                            last.then_inc(proj_mm, 1)
                            pe.wait_ge(o_squared, ready(i, u))
                            pe.wait_ge(n3_copied, freed(i, u, 1))
                            for k in range(4):
                                last = pe.matmul(n3_ps[:, 0:1], o_sq[:, k, :], S.ones[:, 0:1], start=(k == 0), stop=(k == 3))
                            last.then_inc(n3_mm, 1)


def load_nodes(nc, g, S, x):
    S.x = g.sb("x", [TP, NT, D])
    S.fx = g.sb("fx", [TP, NT, D])
    S.ln_r, S.ln_b = g.sb("ln_r", [TP, NT]), g.sb("ln_b", [TP, NT])
    loaded = g.sem("x_loaded")
    with nc.Block() as block:
        @block.sync
        def _(sp):
            sp.dma_start(S.x[:], tiles_of(x)).then_inc(loaded, 16)
            sp.wait_ge(loaded, 16)


def slot_uses(i, u):
    return i * ((GROUP + 1) // 2 if u % 2 == 0 else GROUP // 2) + u // 2


def psum_cols(ap, n):
    return ap[:, 0:n]


def load_projection(nc, keep, a, W, W_T, q, k, H, width, chunks):
    OC = width // P
    w = keep.sb("w", [P, chunks, 2, width])
    wqk = keep.sb("wqk", [P, chunks, 2, 2, H])
    w_t = [a.sb(f"w_t{r}", [P, OC, chunks * P]) for r in range(2)]
    qk = a.sb("qk", [P, OC, 2, H])
    wqk_ps = a.ps("wqk_ps", [P, 512])
    loaded, multiplied = a.sem("w_loaded"), a.sem("wqk_multiplied")
    with nc.Block() as block:
        @block.sync
        def _(sp):
            sp.dma_start(qk[:, :, 0, :], q.rearrange("(c p) h -> p c h", p=P),
                         allow_slow_non_contiguous=True).then_inc(loaded, 16)
            sp.dma_start(qk[:, :, 1, :], k.rearrange("(c p) h -> p c h", p=P),
                         allow_slow_non_contiguous=True).then_inc(loaded, 16)
            for r in range(2):
                sp.dma_start(w_t[r][:], W_T[r].rearrange("(c p) i -> p c i", p=P)).then_inc(loaded, 16)
                sp.dma_start(w[:, :, r, :], W[r].rearrange("(c p) o -> p c o", p=P)).then_inc(loaded, 16)

        @block.tensor
        def _(pe):
            pe.wait_ge(loaded, 96)
            for c in range(chunks):
                for r in range(2):
                    at = (c * 2 + r) * 2 * H
                    for o in range(OC):
                        last = pe.matmul(wqk_ps[:, at:at + 2 * H], w_t[r][:, o, c * P:(c + 1) * P],
                                         qk[:, o].rearrange("p s h -> p (s h)"), start=(o == 0), stop=(o == OC - 1))
            last.then_inc(multiplied, 1)

        @block.vector
        def _(dve):
            dve.wait_ge(multiplied, 1)
            dve.tensor_copy(wqk[:].rearrange("p c r s h -> p (c r s h)"), wqk_ps[:, 0:chunks * 4 * H])
    return w, wqk


class Projector:

    def __init__(self, nc, a, w, wqk, width, H, table, q_tab, k_tab, const=None):
        self.nc, self.w, self.wqk, self.width, self.H, self.const = nc, w, wqk, width, H, const
        self.table, self.q_tab, self.k_tab = table, q_tab, k_tab
        self.out = [a.sb(f"proj_out{s}", [TP, 2, width]) for s in range(2)]
        self.qk = [a.sb(f"proj_qk{s}", [TP, 2, 2, H]) for s in range(2)]
        self.ps = a.ps("proj_ps", [TP, 2, 512])
        self.qk_ps = a.ps("proj_qk_ps", [TP, 512])
        self.done, self.copied = a.sem("proj_done"), a.sem("proj_copied")
        self.stored = [a.sem(f"proj_stored{s}") for s in range(2)]
        self.DMAS = 4

    def multiply(self, pe, i, u, chunks):
        pe.wait_ge(self.copied, i * (2 * GROUP) + 2 * u)
        n = len(chunks)
        for r in range(2):
            for c, x in enumerate(chunks):
                pe.matmul(self.ps[:, r, 0:self.width], x, self.w[:, c, r, :], start=(c == 0),
                          stop=(c == n - 1 and self.const is None))
            if self.const is not None:
                pe.matmul(self.ps[:, r, 0:self.width], self.const[2], self.const[0][0:1, r, :], start=False, stop=True)
        for c, x in enumerate(chunks):
            last = pe.matmul(self.qk_ps[:, 0:4 * self.H], x, self.wqk[:, c].rearrange("p r s h -> p (r s h)"),
                             start=(c == 0), stop=(c == n - 1 and self.const is None))
        if self.const is not None:
            last = pe.matmul(self.qk_ps[:, 0:4 * self.H], self.const[2], self.const[1][0:1, :], start=False, stop=True)
        last.then_inc(self.done, 1)

    def copy(self, act, i, u):
        s = u % 2
        act.wait_ge(self.done, ready(i, u))
        act.wait_ge(self.stored[s], slot_uses(i, u) * (16 * self.DMAS))
        self.nc.scalar.copy(self.out[s][:], self.ps[:, :, 0:self.width]).then_inc(self.copied, 1)
        self.nc.scalar.copy(self.qk[s][:].rearrange("p r s h -> p (r s h)"),
                            self.qk_ps[:, 0:4 * self.H]).then_inc(self.copied, 1)

    def store(self, sp, i, u):
        s = u % 2
        t = i * GROUP + u
        rows = bass.ds(t * TP, TP)
        sp.wait_ge(self.copied, i * (2 * GROUP) + 2 * u + 2)
        for r in range(2):
            sp.dma_start(self.table[r * N:(r + 1) * N, :][rows, :], self.out[s][:, r, :]).then_inc(self.stored[s], 16)
        for n, tab in enumerate((self.q_tab, self.k_tab)):
            sp.dma_start(tab.rearrange("(r n) h -> n r h", r=2)[rows], self.qk[s][:, :, n, :],
                         allow_slow_non_contiguous=True).then_inc(self.stored[s], 16)

    def finish(self, sp):
        for s in range(2):
            uses = NG * ((GROUP + 1) // 2 if s == 0 else GROUP // 2)
            sp.wait_ge(self.stored[s], uses * 16 * self.DMAS)


def gnn_first(nc, S, query, gate_w1, gate_b1, gate_w2, gate_b2, W, W_T, q, k):
    width = HEADS * HID
    with stage(nc, "g1_") as a:
        w = a.sb("w4", [P, 4, 2, width])
        wqk = a.sb("wqk4", [P, 4, 2, 2, HEADS])
        const_row = a.sb("const_row", [1, 2, width])
        const_qk = a.sb("const_qk", [1, 4 * HEADS])
        qcol = a.sb("qcol", [P, 2])
        gw1, gw2 = a.sb("gw1", [P, 4, D]), a.sb("gw2", [P, 2, D])
        gb = a.sb("gb", [P, 2, 2])
        gconst = a.sb("gconst", [P, 2])
        with stage(nc, "g1w_") as b:
            w6, wqk6 = load_projection(nc, b, b, W, W_T, q, k, HEADS, width, 6)
            row_ps, gate_ps = b.ps("row_ps", [1, 3, 512]), b.ps("gate_ps", [P, 512])
            loaded, multiplied = b.sem("loaded"), b.sem("multiplied")
            with nc.Block() as block:
                @block.sync
                def _(sp):
                    sp.dma_start(qcol[:], query[0].rearrange("(k p) -> p k", p=P),
                                 allow_slow_non_contiguous=True).then_inc(loaded, 16)
                    sp.dma_start(gw1[:], gate_w1.rearrange("(k p) c -> p k c", p=P)).then_inc(loaded, 16)
                    sp.dma_start(gw2[:], gate_w2.rearrange("(k p) c -> p k c", p=P)).then_inc(loaded, 16)
                    for n, x in enumerate((gate_b1, gate_b2)):
                        sp.dma_start(gb[:, n, :], x.rearrange("(k p) -> p k", p=P),
                                     allow_slow_non_contiguous=True).then_inc(loaded, 16)

                @block.tensor
                def _(pe):
                    pe.wait_ge(loaded, 80)
                    for r in range(2):
                        for c in range(2):
                            pe.matmul(row_ps[:, r, :], qcol[:, c:c + 1], w6[:, 2 + c, r, :], start=(c == 0), stop=(c == 1))
                    for c in range(2):
                        pe.matmul(row_ps[:, 2, 0:4 * HEADS], qcol[:, c:c + 1],
                                  wqk6[:, 2 + c].rearrange("p r s h -> p (r s h)"), start=(c == 0), stop=(c == 1))
                    for o in range(2):
                        for c in range(2):
                            last = pe.matmul(gate_ps[:, o:o + 1], gw1[:, 2 + c, o * P:(o + 1) * P], qcol[:, c:c + 1],
                                             start=(c == 0), stop=(c == 1))
                    last.then_inc(multiplied, 1)

                @block.vector
                def _(dve):
                    dve.wait_ge(loaded, 80)
                    dve.tensor_copy(w[:, 0:2], w6[:, 0:2])
                    dve.tensor_copy(wqk[:, 0:2], wqk6[:, 0:2])
                    for c in range(2):
                        dve.tensor_scalar(w[:, 2 + c], w6[:, 4 + c], qcol[:, c:c + 1], None, ALU.mult)
                        dve.tensor_scalar(wqk[:, 2 + c], wqk6[:, 4 + c], qcol[:, c:c + 1], None, ALU.mult)
                    dve.wait_ge(multiplied, 1)
                    dve.tensor_copy(const_row[:], row_ps[:, 0:2, :])
                    dve.tensor_copy(const_qk[:], row_ps[:, 2, 0:4 * HEADS])
                    dve.tensor_tensor(gconst[:], gate_ps[:, 0:2], gb[:, 0, :], ALU.add)

        with stage(nc, "g1t_") as b:
            proj = Projector(nc, b, w, wqk, width, HEADS, S.table, S.q_tab, S.k_tab,
                             const=(const_row, const_qk, S.ones[0:1, 0:TP]))
            xn = [b.sb(f"xn{s}", [TP, D]) for s in range(2)]
            xt = [b.sb(f"xt{s}", [P, 2, TP]) for s in range(2)]
            x0 = [b.sb(f"x0{s}", [P, 2, TP]) for s in range(2)]
            gh, gate = b.sb("gh", [P, 2, TP]), b.sb("gate", [P, 2, TP])
            turn_ps = b.ps("turn", [P, 512])
            gate_ps = b.ps("gate_ps", [P, 2, 512])
            normed, turned, turn_copied, hidden_mm, hidden, gate_mm, gated, x0_made = (
                b.sem(n) for n in ("normed", "turned", "turn_copied", "hidden_mm", "hidden", "gate_mm", "gated", "x0_made"))
            x0_stored = [b.sem(f"x0_stored{s}") for s in range(2)]
            with nc.Block() as block:
                @block.vector
                def _(dve):
                    with dve.Fori(0, NG) as i:
                        for u in range(GROUP):
                            t = i * GROUP + u
                            dve.wait_ge(turned, freed(i, u, 2))
                            dve.tensor_scalar(xn[u % 2][:], tile(S.x, t), col(S.ln_r, t), col(S.ln_b, t), ALU.mult,
                                              ALU.add).then_inc(normed, 1)
                            dve.wait_ge(gated, i * (2 * GROUP) + 2 * u + 2)
                            dve.wait_ge(proj.done, freed(i, u, 2))
                            dve.wait_ge(x0_stored[u % 2], slot_uses(i, u) * 16)
                            dve.tensor_tensor(x0[u % 2][:], gate[:], xt[u % 2][:], ALU.mult).then_inc(x0_made, 1)

                @block.scalar
                def _(act):
                    with act.Fori(0, NG) as i:
                        for u in range(GROUP):
                            act.wait_ge(turned, ready(i, u))
                            act.wait_ge(proj.done, freed(i, u, 2))
                            nc.scalar.copy(xt[u % 2][:], turn_ps[:, 0:2 * TP].rearrange("p (k n) -> p k n", k=2)
                                           ).then_inc(turn_copied, 1)
                            act.wait_ge(hidden_mm, ready(i, u))
                            for o in range(2):
                                nc.scalar.activation(gh[:, o, :], gate_ps[:, 0, o * TP:(o + 1) * TP], ACT.Relu,
                                                     bias=gconst[:, o:o + 1]).then_inc(hidden, 1)
                            act.wait_ge(gate_mm, ready(i, u))
                            act.wait_ge(x0_made, freed(i, u, 1))
                            for o in range(2):
                                nc.scalar.activation(gate[:, o, :], gate_ps[:, 1, o * TP:(o + 1) * TP], ACT.Sigmoid,
                                                     bias=gb[:, 1, o:o + 1]).then_inc(gated, 1)
                            proj.copy(act, i, u)

                @block.tensor
                def _(pe):
                    with pe.Fori(0, NG) as i:
                        for u in range(GROUP):
                            x = xt[u % 2]
                            pe.wait_ge(normed, ready(i, u))
                            pe.wait_ge(turn_copied, freed(i, u, 1))
                            for c in range(2):
                                last = pe.transpose(turn_ps[:, c * TP:(c + 1) * TP], xn[u % 2][:, c * P:(c + 1) * P],
                                                    S.ident[0:TP, 0:TP])
                            last.then_inc(turned, 1)
                            pe.wait_ge(turn_copied, ready(i, u))
                            pe.wait_ge(hidden, i * (2 * GROUP) + 2 * u)
                            for o in range(2):
                                for c in range(2):
                                    last = pe.matmul(gate_ps[:, 0, o * TP:(o + 1) * TP], gw1[:, c, o * P:(o + 1) * P],
                                                     x[:, c, :], start=(c == 0), stop=(c == 1))
                            last.then_inc(hidden_mm, 1)
                            pe.wait_ge(hidden, i * (2 * GROUP) + 2 * u + 2)
                            pe.wait_ge(gated, i * (2 * GROUP) + 2 * u)
                            for o in range(2):
                                for c in range(2):
                                    last = pe.matmul(gate_ps[:, 1, o * TP:(o + 1) * TP], gw2[:, c, o * P:(o + 1) * P],
                                                     gh[:, c, :], start=(c == 0), stop=(c == 1))
                            last.then_inc(gate_mm, 1)
                            pe.wait_ge(x0_made, ready(i, u))
                            proj.multiply(pe, i, u, [x0[u % 2][:, 0, :], x0[u % 2][:, 1, :], x[:, 0, :], x[:, 1, :]])

                @block.sync
                def _(sp):
                    with sp.Fori(0, NG) as i:
                        for u in range(GROUP):
                            t = i * GROUP + u
                            sp.wait_ge(x0_made, ready(i, u))
                            sp.dma_start(S.x0_t[bass.ds(t, 1)].rearrange("a p k n -> (a p) k n"),
                                         x0[u % 2][:]).then_inc(x0_stored[u % 2], 16)
                            proj.store(sp, i, u)
                    proj.finish(sp)
                    for s in range(2):
                        sp.wait_ge(x0_stored[s], 16 * NG * ((GROUP + 1) // 2 if s == 0 else GROUP // 2))


def gnn_nodes(nc, S, tag, agg, width, H, bias, residual, keep, W=None, W_T=None, q=None, k=None, next_H=None,
              next_width=None, table=None, out_w=None, out_b=None):
    CHUNKS = width // P
    last_layer = out_w is not None
    with stage(nc, tag) as a:
        if not last_layer:
            with stage(nc, tag + "w_") as b:
                w, wqk = load_projection(nc, a, b, W, W_T, q, k, next_H, next_width, CHUNKS)
            proj = Projector(nc, a, w, wqk, next_width, next_H, table, S.q_tab3 if next_H == 1 else S.q_tab,
                             S.k_tab3 if next_H == 1 else S.k_tab)
        else:
            ow, ob = a.sb("ow", [P, D]), a.sb("ob", [1, D])
            x0 = [a.sb(f"x0{s}", [P, 2, TP]) for s in range(2)]
            x0_landed = [a.sem(f"x0_landed{s}") for s in range(2)]
            out_ps = a.ps("out_ps", [TP, 512])
            junk = a.sb("junk", [TP, D])
            out_mm, out_copied = a.sem("out_mm"), a.sem("out_copied")
        part = a.sb("part", [CK, KB, width + H])
        bias_row = a.sb("bias_row", [TP, width])
        ag = [a.sb(f"ag{s}", [TP, width + H]) for s in range(2)]
        pm = [a.sb(f"pm{s}", [CK, KB, TP]) for s in range(2)]
        den = a.sb("den", [TP, H])
        h = [a.sb(f"h{s}", [TP, width]) for s in range(2)]
        ht = [a.sb(f"ht{s}", [P, CHUNKS, TP]) for s in range(2)]
        fix_ps = a.ps("fix", [TP, 512])
        den_ps = a.ps("den_ps", [TP, 512])
        turn_ps = a.ps("turn", [P, 512])
        preload = a.sem("preload")
        ag_landed = [a.sem(f"ag_landed{s}") for s in range(2)]
        pm_made, fixed, dstep, h_made, turned, turn_copied, h_kept, ht_used = (
            a.sem(n) for n in ("pm_made", "fixed", "dstep", "h_made", "turned", "turn_copied", "h_kept", "ht_used"))
        used = out_mm if last_layer else proj.done
        K6 = 6 if not residual else 7
        with nc.Block() as block:
            @block.sync
            def _(sp):
                sp.dma_start(part[:], agg[PART0:PART0 + CH, :].rearrange("(k c) w -> c k w", c=CK)).then_inc(preload, 16)
                sp.dma_start(bias_row[:], spread(bias, TP)).then_inc(preload, 16)
                if last_layer:
                    sp.dma_start(ow[:], out_w).then_inc(preload, 16)
                    sp.dma_start(ob[:], row_of(out_b)).then_inc(preload, 16)

                def load(i, u):
                    t = i * GROUP + u
                    sp.wait_ge(h_made, freed(i, u, 2))
                    sp.dma_start(ag[u % 2][:], agg[bass.ds(t * TP, TP), :]).then_inc(ag_landed[u % 2], 16)
                    if last_layer:
                        sp.wait_ge(out_mm, freed(i, u, 2))
                        sp.dma_start(x0[u % 2][:], S.x0_t[bass.ds(t, 1)].rearrange("a p k n -> (a p) k n")
                                     ).then_inc(x0_landed[u % 2], 16)

                with sp.Fori(0, NG) as i:
                    for u in range(GROUP):
                        load(i, u)
                        if not last_layer and u > 0:
                            proj.store(sp, i, u - 1)
                    if not last_layer:
                        proj.store(sp, i, GROUP - 1)
                if not last_layer:
                    proj.finish(sp)

            @block.vector
            def _(dve):
                dve.wait_ge(preload, 64 if last_layer else 32)
                with dve.Fori(0, NG) as i:
                    for u in range(GROUP):
                        t = i * GROUP + u
                        s = u % 2
                        base = (i * GROUP + u) * 5
                        dve.wait_ge(fixed, freed(i, u, 2))
                        dve.tensor_tensor(pm[s][:], S.iota_row[0:CK, 0:TP].unsqueeze(1).broadcast_to([CK, KB, TP]),
                                          tile(S.part_rel, t).unsqueeze(2).broadcast_to([CK, KB, TP]),
                                          ALU.is_equal).then_inc(pm_made, 1)
                        dve.wait_ge(ag_landed[s], (slot_uses(i, u) + 1) * 16)
                        dve.wait_ge(fixed, ready(i, u))
                        after(dve, dve.tensor_tensor(den[:], ag[s][:, width:width + H], den_ps[:, 0:H], ALU.add),
                              dstep, base + 1)
                        after(dve, dve.tensor_scalar(den[:], den[:], 1e-16, None, ALU.add), dstep, base + 2)
                        dve.reciprocal(den[:], den[:]).then_inc(dstep, 1)
                        dve.tensor_tensor(ag[s][:, 0:width], ag[s][:, 0:width], fix_ps[:, 0:width],
                                          ALU.add).then_inc(dstep, 1)
                        dve.wait_ge(dstep, base + 4)
                        v = ag[s][:, 0:width].rearrange("p (h w) -> p h w", h=H)
                        after(dve, dve.tensor_tensor(v, v, den[:].unsqueeze(2).broadcast_to([TP, H, width // H]),
                                                     ALU.mult), dstep, base + 5)
                        dve.wait_ge(turned, freed(i, u, 2))
                        if keep:
                            dve.wait_ge(h_kept, freed(i, u, 2))
                        after(dve, dve.tensor_tensor(h[s][:], ag[s][:, 0:width], bias_row[:], ALU.add),
                              ht_used, i * GROUP + u + 1)
                        if residual:
                            ins = dve.scalar_tensor_tensor(h[s][:], h[s][:], 0.0, tile(S.h, t), ALU.max, ALU.add)
                        else:
                            ins = dve.tensor_scalar(h[s][:], h[s][:], 0.0, None, ALU.max)
                        ins.then_inc(h_made, 1)

            @block.tensor
            def _(pe):
                pe.wait_ge(preload, 64 if last_layer else 32)
                with pe.Fori(0, NG) as i:
                    for u in range(GROUP):
                        s = u % 2
                        pe.wait_ge(pm_made, ready(i, u))
                        pe.wait_ge(h_made, freed(i, u, 1))
                        for kb in range(KB):
                            pe.matmul(fix_ps[:, 0:width], pm[s][:, kb, :], part[:, kb, 0:width],
                                      start=(kb == 0), stop=(kb == KB - 1))
                        for kb in range(KB):
                            last = pe.matmul(den_ps[:, 0:H], pm[s][:, kb, :], part[:, kb, width:width + H],
                                             start=(kb == 0), stop=(kb == KB - 1))
                        last.then_inc(fixed, 1)
                        pe.wait_ge(h_made, ready(i, u))
                        pe.wait_ge(turn_copied, freed(i, u, 1))
                        for c in range(CHUNKS):
                            last = pe.transpose(turn_ps[:, c * TP:(c + 1) * TP], h[s][:, c * P:(c + 1) * P],
                                                S.ident[0:TP, 0:TP])
                        last.then_inc(turned, 1)
                        pe.wait_ge(turn_copied, ready(i, u))
                        if not last_layer:
                            proj.multiply(pe, i, u, [ht[s][:, c, :] for c in range(CHUNKS)])
                        else:
                            pe.wait_ge(out_copied, i * (2 * GROUP) + 2 * u)
                            pe.wait_ge(x0_landed[s], (slot_uses(i, u) + 1) * 16)
                            pe.matmul(out_ps[:, 0:D], ht[s][:, 0, :], ow[:], start=True, stop=False)
                            pe.matmul(out_ps[:, 0:D], S.ones[0:1, 0:TP], ob[:], start=False, stop=False)
                            for c in range(2):
                                last = pe.matmul(out_ps[:, c * P:(c + 1) * P], x0[s][:, c, :], S.ident[:],
                                                 start=False, stop=(c == 1))
                            last.then_inc(out_mm, 1)

            @block.scalar
            def _(act):
                with act.Fori(0, NG) as i:
                    for u in range(GROUP):
                        t = i * GROUP + u
                        s = u % 2
                        act.wait_ge(turned, ready(i, u))
                        act.wait_ge(used, freed(i, u, 2))
                        nc.scalar.copy(ht[s][:], turn_ps[:, 0:CHUNKS * TP].rearrange("p (k n) -> p k n", k=CHUNKS)
                                       ).then_inc(turn_copied, 1)
                        if keep:
                            act.wait_ge(h_made, ready(i, u))
                            nc.scalar.copy(tile(S.h, t), h[s][:]).then_inc(h_kept, 1)
                        if not last_layer:
                            proj.copy(act, i, u)
                        else:
                            act.wait_ge(out_mm, ready(i, u))
                            act.wait_ge(out_copied, i * (2 * GROUP) + 2 * u)
                            nc.scalar.copy(tile(S.gout, t), out_ps[:, 0:D]).then_inc(out_copied, 1)
                            nc.scalar.activation(junk[:], out_ps[:, 0:D], ACT.Square,
                                                 accum_out=col(S.gss, t)).then_inc(out_copied, 1)


def gnn0(nc, g, S, A):
    dram = lambda name, shape: nc.dram_tensor(name, shape, F32, kind="Internal").ap()
    S.table = dram("table", [2 * N, HEADS * HID])
    S.table3 = dram("table3", [2 * N, HID])
    S.q_tab, S.k_tab = dram("q_tab", [2 * N, HEADS]), dram("k_tab", [2 * N, HEADS])
    S.q_tab3, S.k_tab3 = dram("q_tab3", [2 * N, 1]), dram("k_tab3", [2 * N, 1])
    S.x0_t = dram("x0_t", [NT, P, 2, TP])
    S.gss = g.sb("gss", [TP, NT])
    with stage(nc, "gn_") as a:
        S.ex = a.sb("ex", [P, CH, HEADS])
        keys = S.dst_pad[1:EP + 1]
        W512 = HEADS * HID
        gnn_first(nc, S, A["L0_gnn_query"], A["L0_gnn_gate_w1"], A["L0_gnn_gate_b1"], A["L0_gnn_gate_w2"],
                  A["L0_gnn_gate_b2"], A["W1"], A["W1_T"], A["L0_gnn_q1"], A["L0_gnn_k1"])
        S.h = a.sb("h", [TP, NT, W512])
        S.gout = S.h[:, :, 0:D]
        for layer in (1, 2):
            edge_softmax(nc, S, f"s{layer}_", S.q_tab, S.k_tab, HEADS)
            edge_sums(nc, S, f"a{layer}_", S.table, W512, S.ex, HEADS, S.row_src, S.dst_c, keys, S.row_out, S.agg, False)
            n = layer + 1
            gnn_nodes(nc, S, f"n{layer}_", S.agg, W512, HEADS, A[f"L0_gnn_b{layer}"], residual=(layer == 2),
                      keep=(layer == 1), W=A[f"W{n}"], W_T=A[f"W{n}_T"], q=A[f"L0_gnn_q{n}"], k=A[f"L0_gnn_k{n}"],
                      next_H=HEADS if layer == 1 else 1, next_width=W512 if layer == 1 else HID,
                      table=S.table if layer == 1 else S.table3)
        edge_softmax(nc, S, "s3_", S.q_tab3, S.k_tab3, 1)
        edge_sums(nc, S, "a3_", S.table3, HID, S.ex, 1, S.row_src, S.dst_c, keys, S.row_out, S.agg3, False)
        gnn_nodes(nc, S, "n3_", S.agg3, HID, 1, A["L0_gnn_b3"], residual=False, keep=False,
                  out_w=A["L0_gnn_proj_w"], out_b=A["L0_gnn_proj_b"])
        add_gnn0(nc, S)


def add_gnn0(nc, S):
    with stage(nc, "c0_") as a:
        root, asked, step_s, scaled = a.sem("root"), a.sem("asked"), a.sem("step"), a.sem("scaled")
        with nc.Block() as block:
            @block.scalar
            def _(act):
                act.wait_ge(asked, 1)
                nc.scalar.activation(S.gss[:], S.gss[:], ACT.Sqrt).then_inc(root, 1)

            @block.vector
            def _(dve):
                dve.tensor_scalar(S.gss[:], S.gss[:], 1e-24, None, ALU.max).then_inc(asked, 1)
                dve.wait_ge(root, 1)
                st = Steps(dve, step_s)
                st(dve.reciprocal(S.gss[:], S.gss[:]))
                with dve.Fori(0, NG) as i:
                    for u in range(GROUP):
                        t = i * GROUP + u
                        dve.scalar_tensor_tensor(tile(S.x, t), tile(S.gout, t), col(S.gss, t), tile(S.x, t), ALU.mult,
                                                 ALU.add).then_inc(scaled, 1)
                        dve.wait_ge(scaled, ready(i, u))
                        dve.tensor_tensor(tile(S.x, t), tile(S.x, t), tile(S.fx, t), ALU.add)


EXPERTS = 8
FF = 1024
CAP = -(-5 * N // (4 * EXPERTS))
SLOTS = 4 * P
FLT_MAX = 3.4028234663852886e38


def moe(nc, S, gate_w, gate_b, w1, b1, w2, b2):
    EX = EXPERTS
    buf = nc.dram_tensor("expert_in", [EX * SLOTS, D], F32, kind="Internal").ap()
    ybuf = nc.dram_tensor("expert_out", [EX * SLOTS, D], F32, kind="Internal").ap()
    with stage(nc, "mo_") as a:
        row_in, row_out = a.sb("row_in", [TP, NT], I32), a.sb("row_out", [TP, NT], I32)
        weight = a.sb("weight", [TP, NT])
        with stage(nc, "mor_") as b:
            gw, gb = b.sb("gw", [P, 2, EX]), b.sb("gb", [TP, EX])
            xl = [b.sb(f"xl{s}", [TP, D]) for s in range(2)]
            xt = [b.sb(f"xt{s}", [P, 2, TP]) for s in range(2)]
            logit = b.sb("logit", [TP, NT, EX])
            one_hot, cand, prefix, total, scan = (b.sb(n, [TP, NT, EX]) for n in
                                                  ("one_hot", "cand", "prefix", "total", "scan"))
            until = b.sb("until", [TP, TP])
            ones_t = b.sb("ones_t", [TP, NT])
            top, den, best, pos, kept, idx = (b.sb(n, [TP, NT]) for n in ("top", "den", "best", "pos", "kept", "idx"))
            turn_ps, logit_ps = b.ps("turn", [P, 2, 512]), b.ps("logit_ps", [TP, 512])
            pre_ps, tot_ps = b.ps("pre", [TP, 512]), b.ps("tot", [TP, 512])
            loaded, zeroed, normed, turned, turn_copied, logit_mm, logit_in, shifted, exped, hot, summed, step_s = (
                b.sem(n) for n in ("loaded", "zeroed", "normed", "turned", "turn_copied", "logit_mm", "logit_in",
                                   "shifted", "exped", "hot", "summed", "step"))
            with nc.Block() as block:
                @block.sync
                def _(sp):
                    sp.dma_start(gw[:], gate_w.rearrange("(k p) e -> p k e", p=P)).then_inc(loaded, 16)
                    sp.dma_start(gb[:], spread(gate_b, TP)).then_inc(loaded, 16)
                    rows = buf.rearrange("(p r) d -> p (r d)", p=P)
                    for c in range(0, EX * SLOTS * D // P, 1024):
                        sp.dma_start(rows[:, c:c + 1024], S.zeros[:]).then_inc(zeroed, 16)
                    sp.wait_ge(zeroed, 16 * (EX * SLOTS * D // P // 1024))

                @block.vector
                def _(dve):
                    dve.wait_ge(loaded, 32)
                    with dve.Fori(0, NG) as i:
                        for u in range(GROUP):
                            t = i * GROUP + u
                            dve.wait_ge(turned, freed(i, u, 2))
                            dve.tensor_scalar(xl[u % 2][:], tile(S.x, t), col(S.ln_r, t), col(S.ln_b, t), ALU.mult,
                                              ALU.add).then_inc(normed, 1)
                            dve.wait_ge(logit_mm, ready(i, u))
                            dve.tensor_tensor(tile(logit, t), logit_ps[:, 0:EX], gb[:], ALU.add).then_inc(logit_in, 1)
                    dve.wait_ge(logit_in, NT)
                    st = Steps(dve, step_s)

                    def wide(x):
                        return x[:].unsqueeze(2).broadcast_to([TP, NT, EX])

                    st(dve.tensor_reduce(top[:], logit[:], AX.X, ALU.max))
                    dve.tensor_tensor(logit[:], logit[:], wide(top), ALU.subtract).then_inc(shifted, 1)
                    dve.wait_ge(exped, 1)
                    st(dve.tensor_reduce(den[:], logit[:], AX.X, ALU.add))
                    st(dve.reciprocal(den[:], den[:]))
                    st(dve.tensor_tensor(logit[:], logit[:], wide(den), ALU.mult))
                    st(dve.tensor_reduce(best[:], logit[:], AX.X, ALU.max))
                    st(dve.tensor_tensor(one_hot[:], logit[:], wide(best), ALU.is_equal))
                    expert_no = S.iota_row[0:TP, 0:EX].unsqueeze(1).broadcast_to([TP, NT, EX])
                    st(dve.scalar_tensor_tensor(cand[:], expert_no, float(-EX), one_hot[:], ALU.add, ALU.mult))
                    st(dve.tensor_reduce(idx[:], cand[:], AX.X, ALU.min))
                    st(dve.tensor_scalar(idx[:], idx[:], float(EX), None, ALU.add))
                    st(dve.tensor_tensor(one_hot[:], expert_no, wide(idx), ALU.is_equal))
                    dve.tensor_scalar(until[:], S.iota_row[0:TP, 0:TP], S.part_col[0:TP, 0:1], None,
                                      ALU.is_ge).then_inc(hot, 1)
                    st(dve.memset(ones_t[:], 1.0))
                    dve.wait_ge(summed, 1)
                    st(dve.tensor_copy(prefix[:].rearrange("p t e -> p (t e)"), pre_ps[:, 0:NT * EX]))
                    st(dve.tensor_copy(total[:].rearrange("p t e -> p (t e)"), tot_ps[:, 0:NT * EX]))
                    for e in range(EX):
                        last = dve.tensor_tensor_scan(scan[:, :, e], ones_t[:], total[:, :, e], 0.0, ALU.mult, ALU.add)
                    st(last)
                    st(dve.tensor_tensor(scan[:], scan[:], total[:], ALU.subtract))
                    st(dve.tensor_tensor(scan[:], scan[:], prefix[:], ALU.add))
                    st(dve.tensor_tensor(scan[:], scan[:], one_hot[:], ALU.mult))
                    st(dve.tensor_reduce(pos[:], scan[:], AX.X, ALU.add))
                    st(dve.tensor_scalar(pos[:], pos[:], -1.0, None, ALU.add))
                    st(dve.tensor_scalar(kept[:], pos[:], float(CAP), None, ALU.is_lt))
                    st(dve.tensor_tensor(weight[:], best[:], kept[:], ALU.mult))
                    st(dve.tensor_scalar(pos[:], pos[:], float(CAP - 1), None, ALU.min))
                    st(dve.scalar_tensor_tensor(pos[:], idx[:], float(SLOTS), pos[:], ALU.mult, ALU.add))
                    st(dve.tensor_copy(row_out[:], pos[:]))
                    st(dve.scalar_tensor_tensor(pos[:], pos[:], float(-SKIP), kept[:], ALU.add, ALU.mult))
                    st(dve.tensor_scalar(pos[:], pos[:], float(SKIP), None, ALU.add))
                    dve.tensor_copy(row_in[:], pos[:])

                @block.scalar
                def _(act):
                    with act.Fori(0, NG) as i:
                        for u in range(GROUP):
                            act.wait_ge(turned, ready(i, u))
                            act.wait_ge(logit_mm, freed(i, u, 2))
                            nc.scalar.copy(xt[u % 2][:], turn_ps[:, u % 2, 0:2 * TP].rearrange("p (k n) -> p k n", k=2)
                                           ).then_inc(turn_copied, 1)
                    act.wait_ge(shifted, 1)
                    nc.scalar.activation(logit[:], logit[:], ACT.Exp).then_inc(exped, 1)

                @block.tensor
                def _(pe):
                    pe.wait_ge(loaded, 32)
                    with pe.Fori(0, NG) as i:
                        for u in range(GROUP):
                            pe.wait_ge(normed, ready(i, u))
                            pe.wait_ge(turn_copied, freed(i, u, 2))
                            for c in range(2):
                                last = pe.transpose(turn_ps[:, u % 2, c * TP:(c + 1) * TP], xl[u % 2][:, c * P:(c + 1) * P],
                                                    S.ident[0:TP, 0:TP])
                            last.then_inc(turned, 1)
                            pe.wait_ge(turn_copied, ready(i, u))
                            pe.wait_ge(logit_in, freed(i, u, 1))
                            for c in range(2):
                                last = pe.matmul(logit_ps[:, 0:EX], xt[u % 2][:, c, :], gw[:, c, :], start=(c == 0),
                                                 stop=(c == 1))
                            last.then_inc(logit_mm, 1)
                    pe.wait_ge(hot, 1)
                    hots = one_hot[:].rearrange("p t e -> p (t e)")
                    pe.matmul(pre_ps[:, 0:NT * EX], until[:], hots, start=True, stop=True)
                    pe.matmul(tot_ps[:, 0:NT * EX], S.ones[0:TP, 0:TP], hots, start=True, stop=True).then_inc(summed, 1)

        with stage(nc, "mod_") as b:
            xl = [b.sb(f"xl{s}", [TP, D]) for s in range(2)]
            at = [b.sb(f"at{s}", [TP, 1], I32) for s in range(2)]
            normed, pool_go = b.sem("normed"), b.sem("pool_go")
            scattered = b.borrow(S.pool_dma[0:2])
            with nc.Block() as block:
                @block.vector
                def _(dve):
                    with dve.Fori(0, NG) as i:
                        for u in range(GROUP):
                            t, s = i * GROUP + u, u % 2
                            dve.wait_ge(scattered[s], slot_uses(i, u) * 16)
                            dve.tensor_copy(at[s][:], col(row_in, t)).then_inc(normed, 1)
                            dve.tensor_scalar(xl[s][:], tile(S.x, t), col(S.ln_r, t), col(S.ln_b, t), ALU.mult,
                                              ALU.add).then_inc(normed, 1)

                @block.gpsimd
                def _(pool):
                    with pool.Fori(0, NG) as i:
                        for u in range(GROUP):
                            s = u % 2
                            pool.wait_ge(normed, i * (2 * GROUP) + 2 * u + 2)
                            pool.sem_inc(pool_go, 1)
                            pool.indirect_dma_start(buf, bass.IndirectOffsetOnAxis(ap=at[s][:, 0:1], axis=0), xl[s][:],
                                                    None, bounds_check=EX * SLOTS - 1, oob_is_err=False
                                                    ).then_inc(scattered[s], 16)
                    for s in range(2):
                        pool.wait_ge(scattered[s], 16 * NG * (3 - s))

        with stage(nc, "moe_") as b:
            FC = FF // P
            w1s = [b.sb(f"w1{s}", [P, 2, FF]) for s in range(2)]
            w2s = [b.sb(f"w2{s}", [P, FC, D]) for s in range(2)]
            b1s = [b.sb(f"b1{s}", [P, FC]) for s in range(2)]
            b2s = [b.sb(f"b2{s}", [1, D]) for s in range(2)]
            xs = [b.sb(f"xs{s}", [P, 4, D]) for s in range(2)]
            xt = b.sb("xt", [P, 2, SLOTS])
            hid = b.sb("hid", [P, FC, SLOTS])
            out = [b.sb(f"out{s}", [P, 4, D]) for s in range(2)]
            turn_ps = b.ps("turn", [P, 2, 512])
            hid_ps = b.ps("hid_ps", [P, 2, 512])
            out_ps = b.ps("out_ps", [P, 4, 512])
            w_landed = [b.sem(f"w_landed{s}") for s in range(2)]
            out_mm = [b.sem(f"out_mm{s}") for s in range(2)]
            stored = b.borrow(S.pool_dma[0:2])
            turned, turn_copied, hid_mm, hid_done, out_copied, pool_go = (
                b.sem(n) for n in ("turned", "turn_copied", "hid_mm", "hid_done", "out_copied", "pool_go"))
            with nc.Block() as block:
                @block.sync
                def _(sp):
                    with sp.Fori(0, EX // 2) as i:
                        for s in range(2):
                            e = i * 2 + s
                            one = bass.ds(e, 1)
                            sp.wait_ge(out_mm[s], i * 4)
                            sp.dma_start(xs[s][:], buf[bass.ds(e * SLOTS, SLOTS), :].rearrange("(r p) d -> p r d", p=P)
                                         ).then_inc(w_landed[s], 16)
                            sp.dma_start(w1s[s][:], w1[one].rearrange("a (k p) f -> (a p) k f", p=P)).then_inc(w_landed[s], 16)
                            sp.dma_start(b1s[s][:], b1[one].rearrange("a (k p) -> (a p) k", p=P),
                                         allow_slow_non_contiguous=True).then_inc(w_landed[s], 16)
                            sp.dma_start(b2s[s][:], b2[one]).then_inc(w_landed[s], 16)
                            sp.dma_start(w2s[s][:], w2[one].rearrange("a (k p) f -> (a p) k f", p=P)).then_inc(w_landed[s], 16)

                @block.tensor
                def _(pe):
                    with pe.Fori(0, EX // 2) as i:
                        for s in range(2):
                            pe.wait_ge(w_landed[s], i * 80 + 80)
                            pe.wait_ge(turn_copied, i * 2 + s)
                            for r in range(4):
                                for c in range(2):
                                    last = pe.transpose(turn_ps[:, c, r * P:(r + 1) * P], xs[s][:, r, c * P:(c + 1) * P],
                                                        S.ident[:])
                            last.then_inc(turned, 1)
                            pe.wait_ge(turn_copied, i * 2 + s + 1)
                            for o in range(FC):
                                if o >= 2:
                                    pe.wait_ge(hid_done, i * (2 * FC) + s * FC + o - 1)
                                else:
                                    pe.wait_ge(hid_done, i * (2 * FC) + s * FC)
                                for c in range(2):
                                    last = pe.matmul(hid_ps[:, o % 2, :], w1s[s][:, c, o * P:(o + 1) * P], xt[:, c, :],
                                                     start=(c == 0), stop=(c == 1))
                                last.then_inc(hid_mm, 1)
                            pe.wait_ge(hid_done, i * (2 * FC) + (s + 1) * FC)
                            pe.wait_ge(out_copied, i * 2 + s)
                            for r in range(4):
                                for o in range(FC):
                                    pe.matmul(out_ps[:, r, 0:D], hid[:, o, r * P:(r + 1) * P], w2s[s][:, o, :],
                                              start=(o == 0), stop=False)
                                pe.matmul(out_ps[:, r, 0:D], S.ones[0:1, :], b2s[s][:], start=False, stop=True
                                          ).then_inc(out_mm[s], 1)

                @block.scalar
                def _(act):
                    with act.Fori(0, EX // 2) as i:
                        for s in range(2):
                            for o in range(FC):
                                act.wait_ge(hid_mm, i * (2 * FC) + s * FC + o + 1)
                                act.wait_ge(out_mm[1 - s], (i + s) * 4)
                                nc.scalar.activation(hid[:, o, :], hid_ps[:, o % 2, :], ACT.Relu,
                                                     bias=b1s[s][:, o:o + 1]).then_inc(hid_done, 1)

                @block.vector
                def _(dve):
                    with dve.Fori(0, EX // 2) as i:
                        for s in range(2):
                            dve.wait_ge(turned, i * 2 + s + 1)
                            dve.wait_ge(hid_mm, i * (2 * FC) + s * FC)
                            dve.tensor_copy(xt[:], turn_ps[:]).then_inc(turn_copied, 1)
                            dve.wait_ge(out_mm[s], i * 4 + 4)
                            dve.wait_ge(stored[s], i * 16)
                            dve.tensor_copy(out[s][:], out_ps[:, :, 0:D]).then_inc(out_copied, 1)

                @block.gpsimd
                def _(pool):
                    with pool.Fori(0, EX // 2) as i:
                        for s in range(2):
                            pool.wait_ge(out_copied, i * 2 + s + 1)
                            pool.sem_inc(pool_go, 1)
                            pool.dma_start(ybuf[bass.ds((i * 2 + s) * SLOTS, SLOTS), :].rearrange(
                                "(r p) d -> p r d", p=P), out[s][:]).then_inc(stored[s], 16)
                    for s in range(2):
                        pool.wait_ge(stored[s], 16 * (EX // 2))

        with stage(nc, "mog_") as b:
            y = [b.sb(f"y{s}", [TP, D]) for s in range(2)]
            at = [b.sb(f"at{s}", [TP, 1], I32) for s in range(2)]
            z, mask = b.sb("z", [TP, D]), b.sb("mask", [TP, 3, D], I32)
            limit = b.sb("limit", [TP, 2, D])
            limits, indexed, weighted, masked, replaced, y_used, pool_go, dve_go = (
                b.sem(n) for n in ("limits", "indexed", "weighted", "masked", "replaced", "y_used", "pool_go", "dve_go"))
            landed = b.borrow(S.pool_dma[0:2])
            with nc.Block() as block:
                @block.scalar
                def _(act):
                    with act.Fori(0, NG) as i:
                        for u in range(GROUP):
                            act.wait_ge(y_used, freed(i, u, 2))
                            nc.scalar.copy(at[u % 2][:], col(row_out, i * GROUP + u)).then_inc(indexed, 1)

                @block.gpsimd
                def _(pool):
                    with pool.Fori(0, NG) as i:
                        for u in range(GROUP):
                            s = u % 2
                            pool.wait_ge(indexed, ready(i, u))
                            pool.sem_inc(pool_go, 1)
                            pool.indirect_dma_start(y[s][:], None, ybuf, bass.IndirectOffsetOnAxis(ap=at[s][:, 0:1], axis=0)
                                                    ).then_inc(landed[s], 16)

                @block.vector
                def _(dve):
                    dve.memset(limit[:, 0], 1e4).then_inc(limits, 1)
                    dve.memset(limit[:, 1], -1e4).then_inc(limits, 1)
                    dve.wait_ge(limits, 2)
                    with dve.Fori(0, NG) as i:
                        for u in range(GROUP):
                            t, s = i * GROUP + u, u % 2
                            dve.memset(z[:], 0.0).then_inc(replaced, 1)
                            dve.wait_ge(landed[s], (slot_uses(i, u) + 1) * 16)
                            after(dve, dve.tensor_scalar(y[s][:], y[s][:], col(weight, t), None, ALU.mult),
                                  weighted, i * GROUP + u + 1)
                            dve.tensor_tensor(mask[:, 0], y[s][:], y[s][:], ALU.is_equal).then_inc(masked, 1)
                            dve.tensor_scalar(mask[:, 1], y[s][:], FLT_MAX, None, ALU.is_gt).then_inc(masked, 1)
                            dve.tensor_scalar(mask[:, 2], y[s][:], -FLT_MAX, None, ALU.is_lt).then_inc(masked, 1)
                            dve.wait_ge(masked, i * (3 * GROUP) + 3 * u + 3)
                            base = i * (4 * GROUP) + 4 * u
                            for n, value in enumerate((y[s][:], limit[:, 0], limit[:, 1])):
                                dve.wait_ge(replaced, base + n + 1)
                                dve.sem_inc(dve_go, 1)
                                dve.copy_predicated(z[:], mask[:, n], value).then_inc(replaced, 1)
                            dve.wait_ge(replaced, base + 4)
                            after(dve, dve.tensor_tensor(tile(S.x, t), tile(S.x, t), z[:], ALU.add),
                                  y_used, i * GROUP + u + 1)


def linear_attention(nc, S, Wg, Wq, bq, Wk, bk, Wv, bv, Wo, bo):
    S.support = nc.dram_tensor("support", [N, D], F32, kind="Internal").ap()
    with stage(nc, "la_") as a:
        wg, wq, wo = (a.sb(n, [P, 2, D]) for n in ("wg", "wq", "wo"))
        wkv, bkv = a.sb("wkv", [P, 2, 2, D]), a.sb("bkv", [1, 2 * D])
        bqc, bor = a.sb("bqc", [P, 2]), a.sb("bor", [1, D])
        group_ones = a.sb("group_ones", [P, P])
        kv_block, k_block = a.sb("kv_block", [P, 2, P]), a.sb("k_block", [P, 2, P])
        loaded = a.sem("loaded")

        with stage(nc, "lak_") as b:
            xn = [b.sb(f"xn{s}", [TP, D]) for s in range(2)]
            xt = [b.sb(f"xt{s}", [P, 2, TP]) for s in range(2)]
            low = b.sb("low", [TP, D])
            kp = [b.sb(f"kp{s}", [TP, D]) for s in range(2)]
            v = [b.sb(f"v{s}", [TP, 2, P + 1]) for s in range(2)]
            sup = [b.sb(f"sup{s}", [TP, D]) for s in range(2)]
            ksum = b.sb("ksum", [P, 2])
            turn_ps, kv_ps, sup_ps = b.ps("turn", [P, 512]), b.ps("kv", [TP, 2, 512]), b.ps("sup_ps", [TP, 512])
            sum_ps = b.ps("sum", [P, 2, 512])
            (normed, turned, turn_copied, kv_mm, low_made, exped, k_made, v_made, sup_mm, sup_copied, summed, init,
             step_s) = (b.sem(n) for n in ("normed", "turned", "turn_copied", "kv_mm", "low_made", "exped", "k_made",
                                           "v_made", "sup_mm", "sup_copied", "summed", "init", "step"))
            stored = [b.sem(f"stored{s}") for s in range(2)]
            with nc.Block() as block:
                @block.sync
                def _(sp):
                    for to, of in ((wg, Wg), (wq, Wq), (wo, Wo)):
                        sp.dma_start(to[:], of.rearrange("(k p) c -> p k c", p=P)).then_inc(loaded, 16)
                    for n, (w, bias) in enumerate(((Wk, bk), (Wv, bv))):
                        sp.dma_start(wkv[:, :, n, :], w.rearrange("(k p) c -> p k c", p=P)).then_inc(loaded, 16)
                        sp.dma_start(bkv[0:1, n * D:(n + 1) * D], row_of(bias)).then_inc(loaded, 16)
                    sp.dma_start(bqc[:], bq.rearrange("(k p) -> p k", p=P),
                                 allow_slow_non_contiguous=True).then_inc(loaded, 16)
                    sp.dma_start(bor[:], row_of(bo)).then_inc(loaded, 16)
                    with sp.Fori(0, NG) as i:
                        for u in range(GROUP):
                            sp.wait_ge(sup_copied, ready(i, u))
                            sp.dma_start(S.support[bass.ds((i * GROUP + u) * TP, TP), :], sup[u % 2][:]
                                         ).then_inc(stored[u % 2], 16)
                    for s in range(2):
                        sp.wait_ge(stored[s], 16 * NG * (3 - s))

                @block.vector
                def _(dve):
                    st = Steps(dve, step_s)
                    st(dve.memset(group_ones[:], 0.0))
                    for q in range(4):
                        dve.memset(group_ones[32 * q:32 * q + 32, 32 * q:32 * q + 32], 1.0)
                    for s in range(2):
                        dve.memset(v[s][:, :, P:P + 1], 1.0).then_inc(init, 1)
                    dve.wait_ge(init, 2)
                    with dve.Fori(0, NG) as i:
                        for u in range(GROUP):
                            t, s = i * GROUP + u, u % 2
                            dve.wait_ge(turned, freed(i, u, 2))
                            dve.tensor_scalar(xn[s][:], tile(S.x, t), col(S.ln_r, t), col(S.ln_b, t), ALU.mult,
                                              ALU.add).then_inc(normed, 1)
                            dve.wait_ge(kv_mm, ready(i, u))
                            dve.wait_ge(exped, freed(i, u, 1))
                            dve.tensor_scalar(low[:], kv_ps[:, 0, 0:D], 0.0, None, ALU.min).then_inc(low_made, 1)
                            dve.wait_ge(summed, freed(i, u, 2))
                            dve.tensor_copy(v[s][:, :, 0:P], kv_ps[:, 1, 0:D].rearrange("p (c e) -> p c e", c=2)
                                            ).then_inc(v_made, 1)
                            dve.wait_ge(exped, ready(i, u))
                            dve.scalar_tensor_tensor(kp[s][:], kv_ps[:, 0, 0:D], 0.0, low[:], ALU.max,
                                                     ALU.add).then_inc(k_made, 1)
                    dve.wait_ge(summed, NT + 1)
                    for c in range(2):
                        dve.tensor_tensor(kv_block[:, c, :], sum_ps[:, c, 0:P], group_ones[:], ALU.mult)
                        st(dve.tensor_copy(ksum[:, c:c + 1], sum_ps[:, c, P:P + 1]))
                        dve.tensor_scalar(k_block[:, c, :], group_ones[:], ksum[:, c:c + 1], None, ALU.mult)

                @block.scalar
                def _(act):
                    with act.Fori(0, NG) as i:
                        for u in range(GROUP):
                            s = u % 2
                            act.wait_ge(turned, ready(i, u))
                            act.wait_ge(sup_mm, freed(i, u, 2))
                            nc.scalar.copy(xt[s][:], turn_ps[:, 0:2 * TP].rearrange("p (k n) -> p k n", k=2)
                                           ).then_inc(turn_copied, 1)
                            act.wait_ge(low_made, ready(i, u))
                            act.wait_ge(k_made, freed(i, u, 1))
                            nc.scalar.activation(low[:], low[:], ACT.Exp).then_inc(exped, 1)
                            act.wait_ge(sup_mm, ready(i, u))
                            act.wait_ge(stored[s], slot_uses(i, u) * 16)
                            nc.scalar.copy(sup[s][:], sup_ps[:, 0:D]).then_inc(sup_copied, 1)

                @block.tensor
                def _(pe):
                    pe.wait_ge(loaded, 16 * 9)
                    for c in range(2):
                        pe.matmul(sum_ps[:, c, 0:P + 1], S.zeros[:, 0:P], S.zeros[:, 0:P + 1], start=True, stop=False)
                    with pe.Fori(0, NG) as i:
                        for u in range(GROUP):
                            s = u % 2
                            pe.wait_ge(normed, ready(i, u))
                            pe.wait_ge(turn_copied, freed(i, u, 1))
                            for c in range(2):
                                last = pe.transpose(turn_ps[:, c * TP:(c + 1) * TP], xn[s][:, c * P:(c + 1) * P],
                                                    S.ident[0:TP, 0:TP])
                            last.then_inc(turned, 1)
                            pe.wait_ge(turn_copied, ready(i, u))
                            pe.wait_ge(k_made, freed(i, u, 1))
                            pe.wait_ge(v_made, freed(i, u, 1))
                            for n in range(2):
                                for c in range(2):
                                    pe.matmul(kv_ps[:, n, 0:D], xt[s][:, c, :], wkv[:, c, n, :], start=(c == 0), stop=False)
                                last = pe.matmul(kv_ps[:, n, 0:D], S.ones[0:1, 0:TP], bkv[:, n * D:(n + 1) * D],
                                                 start=False, stop=True)
                            last.then_inc(kv_mm, 1)
                            pe.wait_ge(sup_copied, freed(i, u, 1))
                            for c in range(2):
                                last = pe.matmul(sup_ps[:, 0:D], xt[s][:, c, :], wg[:, c, :], start=(c == 0), stop=(c == 1))
                            last.then_inc(sup_mm, 1)
                            pe.wait_ge(k_made, ready(i, u))
                            pe.wait_ge(v_made, ready(i, u))
                            for c in range(2):
                                last = pe.matmul(sum_ps[:, c, 0:P + 1], kp[s][:, c * P:(c + 1) * P], v[s][:, c, :],
                                                 start=False, stop=False)
                            last.then_inc(summed, 1)
                    for c in range(2):
                        last = pe.matmul(sum_ps[:, c, 0:P + 1], S.zeros[:, 0:P], S.zeros[:, 0:P + 1], start=False, stop=True)
                    last.then_inc(summed, 1)

        with stage(nc, "laq_") as b:
            xn = [b.sb(f"xn{s}", [TP, D]) for s in range(2)]
            xt = [b.sb(f"xt{s}", [P, 2, TP]) for s in range(2)]
            low, high, qp, rz, o = (b.sb(n, [P, 2, TP]) for n in ("low", "high", "qp", "rz", "o"))
            turn_ps, q_ps, o_ps, att_ps = (b.ps("turn", [P, 512]), b.ps("q_ps", [P, 512]), b.ps("o_ps", [P, 512]),
                                           b.ps("att", [TP, 512]))
            normed, turned, turn_copied, q_mm, low_made, exped, q_made, o_mm, dstep, o_made, att_mm, att_added = (
                b.sem(n) for n in ("normed", "turned", "turn_copied", "q_mm", "low_made", "exped", "q_made", "o_mm",
                                   "dstep", "o_made", "att_mm", "att_added"))
            with nc.Block() as block:
                @block.vector
                def _(dve):
                    with dve.Fori(0, NG) as i:
                        for u in range(GROUP):
                            t, s = i * GROUP + u, u % 2
                            base = i * (2 * GROUP) + 2 * u
                            dve.wait_ge(turned, freed(i, u, 2))
                            dve.wait_ge(att_added, freed(i, u, 2))
                            dve.tensor_scalar(xn[s][:], tile(S.x, t), col(S.ln_r, t), col(S.ln_b, t), ALU.mult,
                                              ALU.add).then_inc(normed, 1)
                            dve.wait_ge(q_mm, ready(i, u))
                            dve.wait_ge(exped, freed(i, u, 1))
                            for c in range(2):
                                dve.tensor_scalar(low[:, c], q_ps[:, c * TP:(c + 1) * TP], bqc[:, c:c + 1], 0.0, ALU.add,
                                                  ALU.min).then_inc(low_made, 1)
                                dve.tensor_scalar(high[:, c], q_ps[:, c * TP:(c + 1) * TP], bqc[:, c:c + 1], 0.0, ALU.add,
                                                  ALU.max).then_inc(low_made, 1)
                            dve.wait_ge(exped, ready(i, u))
                            dve.wait_ge(low_made, i * (4 * GROUP) + 4 * u + 4)
                            dve.wait_ge(o_mm, freed(i, u, 1))
                            dve.tensor_tensor(qp[:], high[:], low[:], ALU.add).then_inc(q_made, 1)
                            dve.wait_ge(o_mm, ready(i, u))
                            after(dve, dve.tensor_scalar(rz[:].rearrange("p c n -> p (c n)"), o_ps[:, 2 * TP:4 * TP], 1e-6,
                                                         None, ALU.add), dstep, base + 1)
                            after(dve, dve.reciprocal(rz[:], rz[:]), dstep, base + 2)
                            dve.wait_ge(att_mm, freed(i, u, 1))
                            dve.tensor_tensor(o[:].rearrange("p c n -> p (c n)"), o_ps[:, 0:2 * TP],
                                              rz[:].rearrange("p c n -> p (c n)"), ALU.mult).then_inc(o_made, 1)
                            dve.wait_ge(att_mm, ready(i, u))
                            dve.tensor_tensor(tile(S.y, t), att_ps[:, 0:D], xn[s][:], ALU.add).then_inc(att_added, 1)

                @block.scalar
                def _(act):
                    with act.Fori(0, NG) as i:
                        for u in range(GROUP):
                            s = u % 2
                            act.wait_ge(turned, ready(i, u))
                            act.wait_ge(q_mm, freed(i, u, 2))
                            nc.scalar.copy(xt[s][:], turn_ps[:, 0:2 * TP].rearrange("p (k n) -> p k n", k=2)
                                           ).then_inc(turn_copied, 1)
                            act.wait_ge(low_made, i * (4 * GROUP) + 4 * u + 4)
                            nc.scalar.activation(low[:], low[:], ACT.Exp).then_inc(exped, 1)

                @block.tensor
                def _(pe):
                    with pe.Fori(0, NG) as i:
                        for u in range(GROUP):
                            s = u % 2
                            pe.wait_ge(normed, ready(i, u))
                            pe.wait_ge(turn_copied, freed(i, u, 1))
                            for c in range(2):
                                last = pe.transpose(turn_ps[:, c * TP:(c + 1) * TP], xn[s][:, c * P:(c + 1) * P],
                                                    S.ident[0:TP, 0:TP])
                            last.then_inc(turned, 1)
                            pe.wait_ge(turn_copied, ready(i, u))
                            pe.wait_ge(low_made, i * (4 * GROUP) + 4 * u)
                            for o_ in range(2):
                                for c in range(2):
                                    last = pe.matmul(q_ps[:, o_ * TP:(o_ + 1) * TP], wq[:, c, o_ * P:(o_ + 1) * P],
                                                     xt[s][:, c, :], start=(c == 0), stop=(c == 1))
                            last.then_inc(q_mm, 1)
                            pe.wait_ge(q_made, ready(i, u))
                            pe.wait_ge(o_made, freed(i, u, 1))
                            for n, w in enumerate((kv_block, k_block)):
                                for c in range(2):
                                    at = (2 * n + c) * TP
                                    last = pe.matmul(o_ps[:, at:at + TP], w[:, c, :], qp[:, c, :], start=True, stop=True)
                            last.then_inc(o_mm, 1)
                            pe.wait_ge(o_made, ready(i, u))
                            pe.wait_ge(att_added, freed(i, u, 1))
                            for c in range(2):
                                pe.matmul(att_ps[:, 0:D], o[:, c, :], wo[:, c, :], start=(c == 0), stop=False)
                            pe.matmul(att_ps[:, 0:D], S.ones[0:1, 0:TP], bor[:], start=False, stop=True).then_inc(att_mm, 1)


def feed_forward(nc, S, tag, src, gamma, beta, w1, b1, w2, b2, func, out=None, coef=None):
    FC = FF // P
    with stage(nc, tag) as a:
        w1s, w2s = a.sb("w1", [P, 2, FF]), a.sb("w2", [P, FC, D])
        b1s, b2s = a.sb("b1", [P, FC]), a.sb("b2", [1, D])
        xa = [a.sb(f"xa{s}", [TP, D]) for s in range(2)]
        xt = [a.sb(f"xt{s}", [P, 2, TP]) for s in range(2)]
        hid = [a.sb(f"hid{s}", [P, FC, TP]) for s in range(2)]
        res = [a.sb(f"res{s}", [TP, D]) for s in range(2)]
        turn_ps, hid_ps, f_ps = a.ps("turn", [P, 512]), a.ps("hid_ps", [P, 2, 2, 512]), a.ps("f_ps", [TP, 2, 512])
        loaded, normed, dstep, turned, turn_copied, hid_mm, hid_done, f_mm, f_used, base_made = (
            a.sem(n) for n in ("loaded", "normed", "dstep", "turned", "turn_copied", "hid_mm", "hid_done", "f_mm",
                               "f_used", "base_made"))
        stored = [a.sem(f"stored{s}") for s in range(2)]
        affine = gamma is not None
        if affine:
            ga, be = a.sb("ga", [TP, D]), a.sb("be", [TP, D])
        LOADS = 16 * (6 if affine else 4)
        with nc.Block() as block:
            @block.sync
            def _(sp):
                sp.dma_start(w1s[:], w1.rearrange("(k p) f -> p k f", p=P)).then_inc(loaded, 16)
                sp.dma_start(w2s[:], w2.rearrange("(k p) f -> p k f", p=P)).then_inc(loaded, 16)
                sp.dma_start(b1s[:], b1.rearrange("(k p) -> p k", p=P), allow_slow_non_contiguous=True).then_inc(loaded, 16)
                sp.dma_start(b2s[:], row_of(b2)).then_inc(loaded, 16)
                if affine:
                    sp.dma_start(ga[:], spread(gamma, TP)).then_inc(loaded, 16)
                    sp.dma_start(be[:], spread(beta, TP)).then_inc(loaded, 16)
                if out is not None:
                    with sp.Fori(0, NG) as i:
                        for u in range(GROUP):
                            sp.wait_ge(f_used, ready(i, u))
                            sp.dma_start(out[bass.ds((i * GROUP + u) * TP, TP), :], res[u % 2][:]).then_inc(stored[u % 2], 16)
                    for s in range(2):
                        sp.wait_ge(stored[s], 16 * NG * (3 - s))

            @block.vector
            def _(dve):
                dve.wait_ge(loaded, LOADS)

                def norm(i, u, t, s):
                    dve.wait_ge(turned, freed(i, u, 2))
                    dve.wait_ge(f_used, freed(i, u, 2))
                    ins = dve.tensor_scalar(xa[s][:], tile(src, t), col(S.ln_r, t), col(S.ln_b, t), ALU.mult, ALU.add)
                    if affine:
                        base = i * (2 * GROUP) + 2 * u
                        after(dve, ins, dstep, base + 1)
                        after(dve, dve.tensor_tensor(xa[s][:], xa[s][:], ga[:], ALU.mult), dstep, base + 2)
                        ins = dve.tensor_tensor(xa[s][:], xa[s][:], be[:], ALU.add)
                    ins.then_inc(normed, 1)
                    if out is not None:
                        dve.wait_ge(normed, ready(i, u))
                        dve.wait_ge(stored[s], slot_uses(i, u) * 16)
                        dve.tensor_tensor(res[s][:], xa[s][:], tile(src, t), ALU.add).then_inc(base_made, 1)

                with dve.Fori(0, NG) as i:
                    for u in range(GROUP):
                        t, s = i * GROUP + u, u % 2
                        norm(i, u, t, s)
                        dve.wait_ge(f_mm, ready(i, u))
                        if out is None:
                            dve.wait_ge(normed, ready(i, u))
                            dve.tensor_tensor(tile(S.y, t), f_ps[:, s, 0:D], xa[s][:], ALU.add).then_inc(f_used, 1)
                        else:
                            dve.wait_ge(base_made, ready(i, u))
                            dve.scalar_tensor_tensor(res[s][:], f_ps[:, s, 0:D], col(coef, t), res[s][:], ALU.mult,
                                                     ALU.add).then_inc(f_used, 1)

            @block.scalar
            def _(act):
                with act.Fori(0, NG) as i:
                    for u in range(GROUP):
                        s = u % 2
                        act.wait_ge(turned, ready(i, u))
                        act.wait_ge(hid_mm, freed(i, u, 2))
                        nc.scalar.copy(xt[s][:], turn_ps[:, 0:2 * TP].rearrange("p (k n) -> p k n", k=2)
                                       ).then_inc(turn_copied, 1)
                        act.wait_ge(hid_mm, ready(i, u))
                        act.wait_ge(f_mm, freed(i, u, 2))
                        for o in range(FC):
                            nc.scalar.activation(hid[s][:, o, :], hid_ps[:, s, o // 4, (o % 4) * TP:(o % 4 + 1) * TP], func,
                                                 bias=b1s[:, o:o + 1]).then_inc(hid_done, 1)

            @block.tensor
            def _(pe):
                pe.wait_ge(loaded, LOADS)
                with pe.Fori(0, NG) as i:
                    for u in range(GROUP):
                        s = u % 2
                        pe.wait_ge(normed, ready(i, u))
                        pe.wait_ge(turn_copied, freed(i, u, 1))
                        for c in range(2):
                            last = pe.transpose(turn_ps[:, c * TP:(c + 1) * TP], xa[s][:, c * P:(c + 1) * P],
                                                S.ident[0:TP, 0:TP])
                        last.then_inc(turned, 1)
                        pe.wait_ge(turn_copied, ready(i, u))
                        pe.wait_ge(hid_done, i * (FC * GROUP) + FC * max(u - 1, 0))
                        for o in range(FC):
                            for c in range(2):
                                last = pe.matmul(hid_ps[:, s, o // 4, (o % 4) * TP:(o % 4 + 1) * TP],
                                                 w1s[:, c, o * P:(o + 1) * P], xt[s][:, c, :], start=(c == 0), stop=(c == 1))
                        last.then_inc(hid_mm, 1)
                        pe.wait_ge(hid_done, i * (FC * GROUP) + FC * (u + 1))
                        pe.wait_ge(f_used, freed(i, u, 2))
                        for o in range(FC):
                            pe.matmul(f_ps[:, s, 0:D], hid[s][:, o, :], w2s[:, o, :], start=(o == 0), stop=False)
                        pe.matmul(f_ps[:, s, 0:D], S.ones[0:1, 0:TP], b2s[:], start=False, stop=True).then_inc(f_mm, 1)


def add_l1(nc, S, gamma, beta, bias):
    with stage(nc, "c1_") as a:
        ga, be, bi = (a.sb(n, [TP, D]) for n in ("ga", "be", "bi"))
        rows = [a.sb(f"rows{s}", [TP, 4, D]) for s in range(2)]
        t0 = a.sb("t0", [TP, D])
        loaded, step_s, used = a.sem("loaded"), a.sem("step"), a.sem("used")
        landed = [a.sem(f"landed{s}") for s in range(2)]
        with nc.Block() as block:
            @block.sync
            def _(sp):
                for to, of in ((ga, gamma), (be, beta), (bi, bias)):
                    sp.dma_start(to[:], spread(of, TP)).then_inc(loaded, 16)
                with sp.Fori(0, NG) as i:
                    for u in range(GROUP):
                        sp.wait_ge(used, freed(i, u, 2))
                        for n in range(4):
                            sp.dma_start(rows[u % 2][:, n, :], S.acc[n][bass.ds((i * GROUP + u) * TP, TP), :]
                                         ).then_inc(landed[u % 2], 16)

            @block.vector
            def _(dve):
                dve.wait_ge(loaded, 48)
                after(dve, dve.tensor_tensor(be[:], be[:], bi[:], ALU.add), step_s, 1)
                with dve.Fori(0, NG) as i:
                    for u in range(GROUP):
                        t, s = i * GROUP + u, u % 2
                        base = i * (6 * GROUP) + 6 * u + 1
                        dve.tensor_scalar(t0[:], tile(S.y, t), col(S.ln_r, t), col(S.ln_b, t), ALU.mult,
                                          ALU.add).then_inc(step_s, 1)
                        dve.wait_ge(landed[s], (slot_uses(i, u) + 1) * 64)
                        dve.tensor_tensor(rows[s][:, 0:2], rows[s][:, 0:2], rows[s][:, 2:4], ALU.add).then_inc(step_s, 1)
                        dve.wait_ge(step_s, base + 2)
                        dve.tensor_tensor(t0[:], t0[:], ga[:], ALU.mult).then_inc(step_s, 1)
                        dve.tensor_tensor(rows[s][:, 0], rows[s][:, 0], rows[s][:, 1], ALU.add).then_inc(step_s, 1)
                        dve.wait_ge(step_s, base + 4)
                        dve.tensor_tensor(t0[:], t0[:], be[:], ALU.add).then_inc(step_s, 1)
                        dve.tensor_tensor(tile(S.x, t), tile(S.x, t), rows[s][:, 0], ALU.add).then_inc(step_s, 1)
                        dve.wait_ge(step_s, base + 6)
                        dve.tensor_tensor(tile(S.x, t), tile(S.x, t), t0[:], ALU.add).then_inc(used, 1)
                        dve.wait_ge(used, ready(i, u))


KEEP = int(0.5 * N) - 1


def depth_weights(nc, S, wr, br):
    w_dram = nc.dram_tensor("depth_weights", [N], F32, kind="Internal").ap()
    with stage(nc, "dw_") as a:
        wrr, brr = a.sb("wrr", [TP, D]), a.sb("brr", [TP, 1])
        xl, junk = a.sb("xl", [TP, D]), a.sb("junk", [TP, D])
        w, rank = a.sb("weight", [TP, NT]), a.sb("rank", [TP, 4, NT])
        w_rows, big = a.sb("w_rows", [TP, N]), a.sb("big", [TP, N])
        earlier, w_group = a.sb("earlier", [TP, TP]), a.sb("w_group", [TP, GROUP])
        grouped = a.sem("grouped")
        loaded, normed, multiplied, step_s, done, spread_in = (
            a.sem(n) for n in ("loaded", "normed", "multiplied", "step", "done", "spread_in"))
        with nc.Block() as block:
            @block.sync
            def _(sp):
                sp.dma_start(wrr[:], spread(wr.rearrange("d o -> (d o)"), TP)).then_inc(loaded, 16)
                sp.dma_start(brr[:], spread(br, TP)).then_inc(loaded, 16)
                sp.wait_ge(done, 1)
                sp.dma_start(w_dram.rearrange("(t p) -> p t", p=TP), w[:],
                             allow_slow_non_contiguous=True).then_inc(spread_in, 16)
                sp.wait_ge(spread_in, 16)
                sp.dma_start(w_rows[:], spread(w_dram, TP)).then_inc(spread_in, 16)

            @block.vector
            def _(dve):
                dve.wait_ge(loaded, 32)
                with dve.Fori(0, NG) as i:
                    for u in range(GROUP):
                        t = i * GROUP + u
                        after(dve, dve.tensor_scalar(xl[:], tile(S.x, t), col(S.ln_r, t), col(S.ln_b, t), ALU.mult,
                                                     ALU.add), normed, ready(i, u))
                        after(dve, dve.tensor_tensor_reduce(junk[:], xl[:], wrr[:], 1.0, 0.0, ALU.mult, ALU.add,
                                                            w_group[:, u:u + 1]), multiplied, ready(i, u))
                    after(dve, dve.tensor_copy(w[:, bass.ds(i * GROUP, GROUP)], w_group[:]), grouped, i + 1)
                st = Steps(dve, step_s)
                dve.tensor_scalar(w[:], w[:], brr[:, 0:1], None, ALU.add).then_inc(done, 1)
                st(dve.tensor_scalar(earlier[:], S.iota_row[0:TP, 0:TP], S.part_col[0:TP, 0:1], None, ALU.is_lt))
                st(dve.memset(rank[:], 0.0))
                dve.wait_ge(done, 1)
                dve.wait_ge(spread_in, 32)
                for t in range(NT):
                    lo, hi = t * TP, (t + 1) * TP
                    me = w[:, t:t + 1]
                    if lo:
                        st(dve.tensor_scalar(big[:, 0:lo], w_rows[:, 0:lo], me, None, ALU.is_ge, ALU.add,
                                             accum_out=rank[:, 0, t:t + 1]))
                    st(dve.tensor_scalar(big[:, lo:N], w_rows[:, lo:N], me, None, ALU.is_gt, ALU.add,
                                         accum_out=rank[:, 1, t:t + 1]))
                    st(dve.scalar_tensor_tensor(big[:, lo:hi], w_rows[:, lo:hi], me, earlier[:], ALU.is_equal, ALU.mult,
                                                accum_out=rank[:, 2, t:t + 1]))
                st(dve.tensor_tensor(rank[:, 0], rank[:, 0], rank[:, 1], ALU.add))
                st(dve.tensor_tensor(rank[:, 0], rank[:, 0], rank[:, 2], ALU.add))
                st(dve.tensor_scalar(rank[:, 0], rank[:, 0], float(KEEP), None, ALU.is_lt))
                dve.tensor_tensor(S.coef[:], rank[:, 0], w[:], ALU.mult)


def network(nc, A, out):
    with ExitStack() as ctx:
        g = Alloc(nc, ctx)
        S = Shared()
        constants(nc, g, S)
        load_nodes(nc, g, S, A["x"])
        layernorm_stats(nc, S, "l0_", S.x)
        mix0(nc, g, S, A["conv_w"], A["bn_gamma"], A["bn_beta"], A["dw_w"], A["pw_w"], A["res_w"], A["L0_mix_b_res"])
        edges(nc, g, S, A["src"], A["dst"], A["edge_type_2"], A["edge_weight"])
        gnn0(nc, g, S, A)
        layernorm_stats(nc, S, "l1_", S.x)
        moe(nc, S, A["L0_ffn_gate_w"], A["L0_ffn_gate_b"], A["L0_ffn_w1"], A["L0_ffn_b1"], A["L0_ffn_w2"], A["L0_ffn_b2"])
        layer1(nc, g, S, A, out)


def layer1(nc, g, S, A, out):
    S.y = g.sb("y", [TP, NT, D])
    S.coef = g.sb("coef", [TP, NT])
    layernorm_stats(nc, S, "l2_", S.x)
    M = {k[len("L1_mix_"):]: v for k, v in A.items() if k.startswith("L1_mix_")}
    linear_attention(nc, S, A["L1_gnn_weight"], M["Wq"], M["bq"], M["Wk"], M["bk"], M["Wv"], M["bv"], M["Wo"], M["bo"])
    representatives(nc, g, S)
    edge_sums(nc, S, "a4_", S.support, D, S.ew_c[:].unsqueeze(2), 1, S.node_dst, S.src_c, S.src_pad, S.row_rep, S.acc, True)
    layernorm_stats(nc, S, "l3_", S.y)
    feed_forward(nc, S, "f1_", S.y, M["ln1_g"], M["ln1_b"], M["W1"], M["b1"], M["W2"], M["b2"], ACT.Relu)
    layernorm_stats(nc, S, "l4_", S.y)
    add_l1(nc, S, M["ln2_g"], M["ln2_b"], A["L1_gnn_bias"])
    layernorm_stats(nc, S, "l5_", S.x)
    depth_weights(nc, S, A["L1_ffn_wr"], A["L1_ffn_br"])
    feed_forward(nc, S, "f2_", S.x, None, None, A["L1_ffn_w1"], A["L1_ffn_b1"], A["L1_ffn_w2"], A["L1_ffn_b2"],
                 ACT.Gelu_apprx_tanh, out=out, coef=S.coef)


def lay_out(inputs):
    import numpy as np

    a = {k: np.ascontiguousarray(v) for k, v in inputs.items()}
    perm = np.arange(768).reshape(8, 3, 32).transpose(1, 0, 2).reshape(-1)
    a["conv_w"] = np.ascontiguousarray(a["L0_mix_w_qkv"][perm, :, 2].T)
    a["bn_gamma"] = np.ascontiguousarray(a["L0_mix_bn_gamma"][perm])
    a["bn_beta"] = np.ascontiguousarray(a["L0_mix_bn_beta"][perm])
    a["dw_w"] = np.ascontiguousarray(a["L0_mix_w_dw"][perm, 0, 2])
    a["pw_w"] = np.ascontiguousarray(a["L0_mix_w_pw"][perm, :, 0].reshape(6, 4, 32, 32).transpose(1, 3, 0, 2))
    a["res_w"] = np.ascontiguousarray(a["L0_mix_w_res"][:, :, 0].T)
    for layer in (1, 2, 3):
        a[f"W{layer}"] = a[f"L0_gnn_W{layer}"]
        a[f"W{layer}_T"] = np.ascontiguousarray(a[f"L0_gnn_W{layer}"].transpose(0, 2, 1))
    for name in ("L0_mix_w_qkv", "L0_mix_bn_gamma", "L0_mix_bn_beta", "L0_mix_w_dw", "L0_mix_w_pw", "L0_mix_w_res",
                 "L0_gnn_W1", "L0_gnn_W2", "L0_gnn_W3", "L1_ffn_attention_mask"):
        del a[name]
    return a


def kernel(**inputs):
    import concourse.bacc as bacc
    from concourse.bass_utils import run_bass_kernel_spmd

    nc = bacc.Bacc("TRN2", target_bir_lowering=False, num_devices=1)
    arrays = lay_out(inputs)
    A = {k: nc.dram_tensor(f"in_{k}", v.shape, mybir.dt.from_np(v.dtype), kind="ExternalInput").ap()
         for k, v in arrays.items()}
    out = nc.dram_tensor("out_0", (N, D), F32, kind="ExternalOutput").ap()
    network(nc, A, out)
    r = run_bass_kernel_spmd(nc, [{f"in_{k}": v for k, v in arrays.items()}], core_ids=[0])
    return r.results[0]["out_0"]
```

```python
from contextlib import ExitStack, contextmanager

import concourse.bass as bass
from concourse import mybir

F32 = mybir.dt.float32
I32 = mybir.dt.int32
ALU = mybir.AluOpType
ACT = mybir.ActivationFunctionType
AX = mybir.AxisListType

N = 3125
D = 256
E = 53125
P = 128
TP = 125
NT = N // TP
GROUP = 5
NG = NT // GROUP
CH = 416
CK = 104
KB = CH // CK
EP = CH * P
PAD_NODE = N
QUAD = 4
QUADS = CH // QUAD
VISITS = QUADS + NT - 1
SKIP = 1 << 17
HEADS = 4
HID = 128
BIG = 1.0e30
MAXNORM = 0.9999899864196777
ATANH_MAX = 6.102495471
MIN_NORM = 1e-15
SLOPE = 0.2


def ready(i, u):
    return GROUP * i + u + 1


def freed(i, u, depth):
    return GROUP * i + max(u + 1 - depth, 0)


def stagger(i, *phases, oldest_first=False):
    for step in range(GROUP + len(phases) - 1):
        for k, phase in sorted(enumerate(phases), key=lambda x: x[0], reverse=oldest_first):
            if 0 <= step - k < GROUP:
                phase(i, step - k)


def nothing(i, u):
    pass


def nothing_more(engine, i, part):
    pass


class Shared:
    pass


def after(eng, ins, sem, value):
    ins.then_inc(sem, 1)
    eng.wait_ge(sem, value)


class Steps:

    def __init__(self, eng, sem, base=0):
        self.eng, self.sem, self.n, self.base = eng, sem, 0, base

    def __call__(self, ins):
        self.n += 1
        ins.then_inc(self.sem, 1)
        self.eng.wait_ge(self.sem, self.base + self.n)


class Alloc:
    def __init__(self, nc, ctx, tag=""):
        self.nc, self.ctx, self.tag, self.sems = nc, ctx, tag, []
        self.pool_dmas = False

    def sb(self, name, shape, dt=F32):
        return self.ctx.enter_context(self.nc.sbuf_tensor(self.tag + name, shape, dt))

    def ps(self, name, shape, dt=F32):
        return self.ctx.enter_context(self.nc.psum_tensor(self.tag + name, shape, dt))

    def sem(self, name):
        s = self.ctx.enter_context(self.nc.semaphore(self.tag + name))
        self.sems.append(s)
        return s

    def borrow(self, sems):
        self.sems.extend(s for s in sems if s not in self.sems)
        self.pool_dmas = True
        return sems


@contextmanager
def stage(nc, tag):
    with ExitStack() as ctx:
        a = Alloc(nc, ctx, tag)
        yield a
        with nc.Block() as block:
            @block.gpsimd
            def _(pool):
                if a.pool_dmas:
                    pool.dma_reset()
                for s in a.sems:
                    pool.sem_clear(s)


def row_of(ap):
    return ap.rearrange("(a b) -> a b", a=1)


def spread(ap, parts):
    return row_of(ap).broadcast_to([parts, ap.shape[0]])


def tiles_of(ap):
    return ap.rearrange("(t p) d -> p t d", p=TP)


def constants(nc, g, S):
    S.ident = g.sb("ident", [P, P])
    S.ones = g.sb("ones", [P, P])
    S.iota_row = g.sb("iota_row", [P, P])
    S.part_col = g.sb("part_col", [P, 1])
    S.zeros = g.sb("zeros", [P, P + 1])
    S.pool_dma = [g.sem(f"pool_dma{n}") for n in range(8)]
    with stage(nc, "co_") as a, nc.Block() as block:
        iota_i = a.sb("iota_i", [P, P], I32)
        part_i = a.sb("part_i", [P, 1], I32)
        made = a.sem("constants_made")

        @block.gpsimd
        def _(pool):
            pool.iota(iota_i[:], pattern=[[1, P]], base=0, channel_multiplier=0).then_inc(made, 1)
            pool.iota(part_i[:], pattern=[[1, 1]], base=0, channel_multiplier=1).then_inc(made, 1)

        @block.vector
        def _(dve):
            dve.memset(S.ones[:], 1.0)
            dve.memset(S.zeros[:], 0.0)
            dve.wait_ge(made, 2)
            dve.tensor_copy(S.iota_row[:], iota_i[:]).then_inc(made, 1)
            dve.tensor_copy(S.part_col[:], part_i[:]).then_inc(made, 1)
            dve.wait_ge(made, 4)
            dve.tensor_scalar(S.ident[:], S.iota_row[:], S.part_col[:, 0:1], None, ALU.is_equal)


def edges(nc, g, S, src, dst, etype, ew):
    S.dst_pad = nc.dram_tensor("dst_pad", [EP + 2], I32, kind="Internal").ap()
    S.src_pad = nc.dram_tensor("src_pad", [EP], I32, kind="Internal").ap()
    S.typ_pad = nc.dram_tensor("typ_pad", [EP], I32, kind="Internal").ap()
    ew_pad = nc.dram_tensor("ew_pad", [EP], F32, kind="Internal").ap()
    S.q_at = nc.dram_tensor("q_at", [EP, 2 * HEADS], F32, kind="Internal").ap()
    S.q_at3 = nc.dram_tensor("q_at3", [EP, 2], F32, kind="Internal").ap()
    S.acc = [nc.dram_tensor(f"acc_rows{u}", [N + P, D], F32, kind="Internal").ap() for u in range(4)]

    S.dst_c, S.src_c, S.ew_c = (g.sb(name, [P, CH]) for name in ("dst_c", "src_c", "ew_c"))
    S.row_src, S.node_dst = (g.sb(name, [P, CH], I32) for name in ("row_src", "node_dst"))
    S.row_rep = S.dst_c
    S.pen_start = g.sb("pen_start", [CK, KB, P])
    S.pen_end = g.sb("pen_end", [CK, KB, P])
    S.pen_first = g.sb("pen_first", [CK, KB, P])
    S.pen_last = g.sb("pen_last", [CK, KB, P])
    S.inside = g.sb("inside", [CK, KB, P])
    S.first_run = g.sb("first_run", [CK, KB, P])
    S.type1 = g.sb("type1", [CK, KB, P])
    S.passes = g.sb("passes", [2 * HEADS, CH])
    S.linked = g.sb("linked", [2 * HEADS, CH])
    S.link = g.sb("link", [HEADS, CH])
    S.carry_f = g.sb("carry_f", [HEADS, CH])
    S.carry_b = g.sb("carry_b", [HEADS, CH])

    with stage(nc, "ed_") as a:
        pad_i = a.sb("pad_i", [1, 128], I32)
        pad_n = a.sb("pad_n", [1, 128], I32)
        pad_m = a.sb("pad_m", [1, 1], I32)
        zeros = a.sb("zeros_wide", [P, HEADS * HID + HEADS])
        raw = {n: a.sb("raw_" + n, [CK, KB, P], F32 if n == "ew" else I32)
               for n in ("src", "dst", "prev", "next", "typ", "ew")}
        f = {n: a.sb("f_" + n, [CK, KB, P]) for n in ("src", "dst", "prev", "next", "typ")}
        w = {n: a.sb("w_" + n, [CK, KB, P]) for n in ("rs", "nd", "t0", "t1")}
        tmp_i = a.sb("tmp_i", [CK, KB], F32)
        chunk_no = a.sb("chunk_no", [CK, KB], F32)
        rows_i = a.sb("rows_i", [2 * HEADS, 2, CH + 1], I32)
        rows_f = a.sb("rows_f", [2 * HEADS, 2, CH + 1])
        eq = a.sb("eq", [2 * HEADS, 2, CH])
        turn = a.ps("turn", [P, 5, 512])
        pads_set, filled = a.sem("pads_set"), a.sem("filled")
        copied, loaded = a.sem("copied"), a.sem("loaded")
        step_s, turned = a.sem("step"), a.sem("turned")
        PADE = EP - E
        ZW = zeros.shape[1]

        with nc.Block() as block:
            @block.sync
            def _(sp):
                sp.dma_start(S.dst_pad[1:E + 1], dst).then_inc(copied, 16)
                sp.dma_start(S.src_pad[0:E], src).then_inc(copied, 16)
                sp.dma_start(S.typ_pad[0:E], etype).then_inc(copied, 16)
                sp.dma_start(ew_pad[0:E], ew).then_inc(copied, 16)
                sp.wait_ge(pads_set, 4)
                sp.dma_start(row_of(S.dst_pad[E + 1:EP + 1]), pad_n[0:1, 0:PADE]).then_inc(copied, 16)
                sp.dma_start(row_of(S.dst_pad[EP + 1:EP + 2]), pad_m[:]).then_inc(copied, 16)
                sp.dma_start(row_of(S.dst_pad[0:1]), pad_m[:]).then_inc(copied, 16)
                sp.dma_start(row_of(S.src_pad[E:EP]), pad_i[0:1, 0:PADE]).then_inc(copied, 16)
                sp.dma_start(row_of(S.typ_pad[E:EP]), pad_i[0:1, 0:PADE]).then_inc(copied, 16)
                sp.dma_start(row_of(ew_pad[E:EP]), S.zeros[0:1, 0:PADE]).then_inc(copied, 16)
                sp.wait_ge(copied, 160)
                rows = lambda x: x.rearrange("(k c j) -> c k j", k=KB, c=CK)
                sp.dma_start(raw["src"][:], rows(S.src_pad)).then_inc(loaded, 16)
                sp.dma_start(raw["dst"][:], rows(S.dst_pad[1:EP + 1])).then_inc(loaded, 16)
                sp.dma_start(raw["prev"][:], rows(S.dst_pad[0:EP])).then_inc(loaded, 16)
                sp.dma_start(raw["next"][:], rows(S.dst_pad[2:EP + 2])).then_inc(loaded, 16)
                sp.dma_start(raw["typ"][:], rows(S.typ_pad)).then_inc(loaded, 16)
                sp.dma_start(raw["ew"][:], rows(ew_pad)).then_inc(loaded, 16)
                for h in range(2 * HEADS):
                    sp.dma_start(rows_i[h:h + 1, 0, 0:CH], S.dst_pad[1:EP + 1].rearrange(
                        "(a c j) -> a c j", a=1, j=P)[:, :, 0:1].rearrange("a c j -> a (c j)"),
                                 allow_slow_non_contiguous=True).then_inc(loaded, 16)
                    sp.dma_start(rows_i[h:h + 1, 1, 0:CH], S.dst_pad[1:EP + 1].rearrange(
                        "(a c j) -> a c j", a=1, j=P)[:, :, P - 1:P].rearrange("a c j -> a (c j)"),
                                 allow_slow_non_contiguous=True).then_inc(loaded, 16)
                for u in range(4):
                    for r in range(0, N + P, P):
                        m = min(P, N + P - r)
                        sp.dma_start(S.acc[u][r:r + m, :], zeros[0:m, 0:D]).then_inc(filled, 16)
                for table in (S.q_at, S.q_at3):
                    flat = table.rearrange("(p r) h -> p (r h)", p=P)
                    for r in range(0, flat.shape[1], ZW):
                        m = min(ZW, flat.shape[1] - r)
                        sp.dma_start(flat[:, r:r + m], zeros[:, 0:m]).then_inc(filled, 16)
                fills = sum(len(range(0, EP * w // P, ZW)) for w in (2 * HEADS, 2))
                fills += 4 * len(range(0, N + P, P))
                sp.wait_ge(filled, 16 * fills)

            @block.vector
            def _(dve):
                dve.memset(zeros[:], 0.0).then_inc(pads_set, 1)
                dve.memset(pad_i[:], 0).then_inc(pads_set, 1)
                dve.memset(pad_n[:], PAD_NODE).then_inc(pads_set, 1)
                dve.memset(pad_m[:], 2 * PAD_NODE).then_inc(pads_set, 1)
                st = Steps(dve, step_s)
                for k in range(KB):
                    st(dve.tensor_scalar(chunk_no[:, k:k + 1], S.part_col[0:CK, 0:1], float(k * CK), None, ALU.add))
                dve.wait_ge(loaded, 16 * (6 + 4 * HEADS))
                for n in f:
                    st(dve.tensor_copy(f[n][:], raw[n][:]))
                st(dve.tensor_copy(rows_f[:, :, 0:CH], rows_i[:, :, 0:CH]))
                st(dve.scalar_tensor_tensor(w["rs"][:], f["typ"][:], float(N), f["src"][:], ALU.mult, ALU.add))
                st(dve.tensor_scalar(w["nd"][:], f["dst"][:], float(N - 1), None, ALU.min))
                st(dve.tensor_tensor(w["t0"][:], f["dst"][:], f["next"][:], ALU.not_equal))
                st(dve.tensor_tensor(w["t1"][:], f["dst"][:], f["prev"][:], ALU.not_equal))
                st(dve.tensor_scalar(S.pen_start[:], w["t1"][:], -BIG, None, ALU.mult))
                st(dve.memset(S.pen_start[:, :, 0:1], -BIG))
                st(dve.tensor_scalar(S.inside[:], w["t1"][:], -1.0, 1.0, ALU.mult, ALU.add))
                st(dve.memset(S.inside[:, :, 0:1], 0.0))
                st(dve.tensor_copy(S.type1[:], f["typ"][:]))
                st(dve.tensor_scalar(S.pen_end[:], w["t0"][:], -BIG, None, ALU.mult))
                st(dve.memset(S.pen_end[:, :, P - 1:P], -BIG))
                first = f["dst"][:, :, 0:1].broadcast_to([CK, KB, P])
                last = f["dst"][:, :, P - 1:P].broadcast_to([CK, KB, P])
                st(dve.tensor_tensor(w["t1"][:], f["dst"][:], first, ALU.not_equal))
                st(dve.tensor_scalar(S.pen_first[:], w["t1"][:], -BIG, None, ALU.mult))
                st(dve.tensor_scalar(S.first_run[:], w["t1"][:], -1.0, 1.0, ALU.mult, ALU.add))
                st(dve.tensor_tensor(w["t1"][:], f["dst"][:], last, ALU.not_equal))
                st(dve.tensor_scalar(S.pen_last[:], w["t1"][:], -BIG, None, ALU.mult))
                st(dve.memset(eq[:], 0.0))
                st(dve.tensor_tensor(eq[:, 0, :], rows_f[:, 0, 0:CH], rows_f[:, 1, 0:CH], ALU.is_equal))
                st(dve.tensor_tensor(eq[:, 1, 1:CH], rows_f[:, 0, 1:CH], rows_f[:, 1, 0:CH - 1], ALU.is_equal))
                H4 = slice(0, HEADS)
                st(dve.tensor_copy(S.linked[:], eq[:, 1, :]))
                st(dve.tensor_scalar(S.link[:], eq[H4, 1, :], -1.0, BIG, ALU.add, ALU.mult))
                st(dve.tensor_tensor(S.passes[:], eq[:, 0, :], eq[:, 1, :], ALU.mult))
                st(dve.tensor_scalar(S.carry_f[:], S.passes[H4], -1.0, BIG, ALU.add, ALU.mult))
                st(dve.memset(S.carry_b[:], 0.0))
                st(dve.tensor_tensor(S.carry_b[:, 0:CH - 1], eq[H4, 0, 0:CH - 1], eq[H4, 1, 1:CH], ALU.mult))
                st(dve.tensor_scalar(S.carry_b[:], S.carry_b[:], -1.0, BIG, ALU.add, ALU.mult))
                dve.memset(tmp_i[:], 0.0).then_inc(turned, 1)
                dve.wait_ge(turned, 2)
                for n, to in enumerate((S.dst_c, S.src_c, S.ew_c, S.row_src, S.node_dst)):
                    dve.tensor_copy(to[:], turn[:, n, 0:CH])

            @block.tensor
            def _(pe):
                pe.wait_ge(turned, 1)
                for n, x in enumerate((f["dst"], f["src"], raw["ew"], w["rs"], w["nd"])):
                    for k in range(KB):
                        last = pe.transpose(turn[:, n, k * CK:(k + 1) * CK], x[:, k, :], S.ident[0:CK, 0:CK])
                last.then_inc(turned, 1)


def row_starts(nc, g, S):
    BL = 32
    BF16 = mybir.dt.bfloat16
    S.start_row = g.sb("start_row", [TP, NT], I32)
    with stage(nc, "rs_") as a:
        bound_row = a.sb("bound_row", [P, NT])
        ge = a.sb("ge", [P, BL, NT])
        hi, lo = a.sb("hi", [P, CH]), a.sb("lo", [P, CH])
        one_hi = a.sb("one_hi", [P, CH, NT], BF16)
        one_lo = [a.sb(f"one_lo{s}", [P, BL, TP], BF16) for s in range(2)]
        zero_b = a.sb("zero_b", [P, P], BF16)
        before = a.sb("before", [TP, TP])
        deg, tot, scan, none, pos, ones_t = (a.sb(n, [TP, NT]) for n in ("deg", "tot", "scan", "none", "pos", "ones_t"))
        deg_ps, pre_ps, tot_ps = a.ps("deg_ps", [TP, 512]), a.ps("pre", [TP, 512]), a.ps("tot_ps", [TP, 512])
        step_s, made, counted, deg_in, summed = (a.sem(n) for n in ("step", "made", "counted", "deg_in", "summed"))
        with nc.Block() as block:
            @block.vector
            def _(dve):
                st = Steps(dve, step_s)
                st(dve.memset(zero_b[:], 0.0))
                st(dve.memset(ones_t[:], 1.0))
                st(dve.tensor_scalar(bound_row[:], S.iota_row[:, 0:NT], 1.0, float(TP), ALU.add, ALU.mult))
                st(dve.tensor_scalar(before[:], S.iota_row[0:TP, 0:TP], S.part_col[0:TP, 0:1], None, ALU.is_gt))
                for c in range(0, CH, BL):
                    dst = S.dst_c[:, c:c + BL].unsqueeze(2).broadcast_to([P, BL, NT])
                    st(dve.tensor_tensor(ge[:], dst, bound_row[:].unsqueeze(1).broadcast_to([P, BL, NT]), ALU.is_ge))
                    st(dve.tensor_reduce(hi[:, c:c + BL], ge[:], AX.X, ALU.add))
                st(dve.scalar_tensor_tensor(lo[:], hi[:], float(-TP), S.dst_c[:], ALU.mult, ALU.add))
                for c in range(0, CH, BL):
                    last = dve.tensor_tensor(one_hi[:, c:c + BL, :], hi[:, c:c + BL].unsqueeze(2).broadcast_to([P, BL, NT]),
                                             S.iota_row[:, 0:NT].unsqueeze(1).broadcast_to([P, BL, NT]), ALU.is_equal)
                last.then_inc(made, 1)
                for n, c in enumerate(range(0, CH, BL)):
                    if n >= 2:
                        dve.wait_ge(counted, n - 1)
                    dve.tensor_tensor(one_lo[n % 2][:], lo[:, c:c + BL].unsqueeze(2).broadcast_to([P, BL, TP]),
                                      S.iota_row[:, 0:TP].unsqueeze(1).broadcast_to([P, BL, TP]),
                                      ALU.is_equal).then_inc(made, 1)
                dve.wait_ge(counted, CH // BL)
                dve.tensor_copy(deg[:], deg_ps[:, 0:NT]).then_inc(deg_in, 1)
                dve.wait_ge(summed, 1)
                st(dve.tensor_copy(tot[:], tot_ps[:, 0:NT]))
                st(dve.tensor_tensor_scan(scan[:], ones_t[:], tot[:], 0.0, ALU.mult, ALU.add))
                st(dve.tensor_tensor(scan[:], scan[:], tot[:], ALU.subtract))
                st(dve.tensor_tensor(pos[:], scan[:], pre_ps[:, 0:NT], ALU.add))
                st(dve.tensor_scalar(none[:], deg[:], 0.0, float(SKIP), ALU.is_equal, ALU.mult))
                st(dve.tensor_tensor(pos[:], pos[:], none[:], ALU.add))
                dve.tensor_copy(S.start_row[:], pos[:])

            @block.tensor
            def _(pe):
                pe.wait_ge(made, 1)
                for n, c in enumerate(range(0, CH, BL)):
                    pe.wait_ge(made, n + 2)
                    for b in range(BL):
                        last = pe.matmul(deg_ps[:, 0:NT], one_lo[n % 2][:, b, :], one_hi[:, c + b, :],
                                         start=(c + b == 0), stop=(c + b == CH - 1))
                    last.then_inc(counted, 1)
                pe.wait_ge(deg_in, 1)
                pe.matmul(pre_ps[:, 0:NT], before[:], deg[:], start=True, stop=True)
                pe.matmul(tot_ps[:, 0:NT], S.ones[0:TP, 0:TP], deg[:], start=True, stop=True).then_inc(summed, 1)


def visits(nc, a, S):
    VC = VISITS * QUAD
    S.visit_quad = a.sb("visit_quad", [P, VISITS])
    S.visit_tile = a.sb("visit_tile", [1, VISITS], I32)
    S.visit_row = a.sb("visit_row", [P, VC], I32)
    S.visit_rel = a.sb("visit_rel", [P, VC])
    with stage(nc, "vi_") as b:
        last_i, last = b.sb("last_i", [QUADS, 1], I32), b.sb("last", [QUADS, 1])
        ge, bound = b.sb("ge", [QUADS, NT - 1]), b.sb("bound", [QUADS, NT - 1])
        end, before = b.sb("end", [QUADS, 1]), b.sb("before", [QUADS, VISITS])
        tile_at = b.sb("tile_at", [P, VISITS])
        pick = b.sb("pick", [CK, KB, VC])
        raw = [b.sb(f"raw{n}", [CK, KB, P], I32) for n in range(3)]
        dst, row = b.sb("dst", [CK, KB, P]), b.sb("row", [CK, KB, P])
        quad_ps, dst_ps, row_ps = b.ps("quad", [P, 512]), b.ps("dst_ps", [P, 512]), b.ps("row_ps", [P, 512])
        loaded, step_s, compared, counted, picked, expanded = (
            b.sem(n) for n in ("loaded", "step", "compared", "counted", "picked", "expanded"))
        with nc.Block() as block:
            @block.sync
            def _(sp):
                rows = lambda x: x.rearrange("(k c j) -> c k j", k=KB, c=CK)
                sp.dma_start(last_i[:], S.dst_pad[1:EP + 1].rearrange("(q j) -> q j", q=QUADS)[:, QUAD * P - 1:QUAD * P],
                             allow_slow_non_contiguous=True).then_inc(loaded, 16)
                for n, x in enumerate((S.dst_pad[1:EP + 1], S.src_pad, S.typ_pad)):
                    sp.dma_start(raw[n][:], rows(x)).then_inc(loaded, 16)

            @block.vector
            def _(dve):
                st = Steps(dve, step_s)
                st(dve.tensor_scalar(bound[:], S.iota_row[0:QUADS, 0:NT - 1], 1.0, float(TP), ALU.add, ALU.mult))
                dve.wait_ge(loaded, 64)
                st(dve.tensor_copy(last[:], last_i[:]))
                st(dve.tensor_scalar(ge[:], bound[:], last[:, 0:1], None, ALU.is_le))
                st(dve.tensor_reduce(end[:], ge[:], AX.X, ALU.add))
                st(dve.tensor_tensor(end[:], end[:], S.part_col[0:QUADS], ALU.add))
                dve.tensor_scalar(before[:], S.iota_row[0:QUADS, 0:VISITS], end[:, 0:1], None,
                                  ALU.is_gt).then_inc(compared, 1)
                st(dve.tensor_copy(dst[:], raw[0][:]))
                st(dve.tensor_copy(row[:], raw[1][:]))
                st(dve.scalar_tensor_tensor(row[:], raw[2][:], float(N), row[:], ALU.mult, ALU.add))
                dve.wait_ge(counted, 1)
                st(dve.tensor_copy(S.visit_quad[:], quad_ps[:, 0:VISITS]))
                st(dve.tensor_tensor(tile_at[:], S.iota_row[:, 0:VISITS], S.visit_quad[:], ALU.subtract))
                st(dve.tensor_copy(S.visit_tile[:], tile_at[0:1, :]))
                pick_chunks(dve, st, S, pick)
                dve.sem_inc(picked, 1)
                dve.wait_ge(expanded, 1)
                dve.tensor_copy(S.visit_row[:], row_ps[:, 0:VC])
                at = tile_at[:].unsqueeze(2).broadcast_to([P, VISITS, QUAD])
                dve.scalar_tensor_tensor(S.visit_rel[:].rearrange("p (v u) -> p v u", u=QUAD), at, float(-TP),
                                         dst_ps[:, 0:VC].rearrange("p (v u) -> p v u", u=QUAD), ALU.mult, ALU.add)

            @block.tensor
            def _(pe):
                pe.wait_ge(compared, 1)
                pe.matmul(quad_ps[:, 0:VISITS], S.ones[0:QUADS, :], before[:], start=True, stop=True).then_inc(counted, 1)
                pe.wait_ge(picked, 1)
                for x, ps in ((dst, dst_ps), (row, row_ps)):
                    for k in range(KB):
                        last_mm = pe.matmul(ps[:, 0:VC], x[:, k, :], pick[:, k, :], start=(k == 0), stop=(k == KB - 1))
                last_mm.then_inc(expanded, 1)


def pick_chunks(dve, st, S, pick):
    for u in range(QUAD):
        for k in range(KB):
            st(dve.tensor_scalar(pick[:, k, u::QUAD], S.visit_quad[0:CK, :], float(QUAD), float(u - k * CK),
                                 ALU.mult, ALU.add))
    st(dve.tensor_scalar(pick[:], pick[:], S.part_col[0:CK, 0:1], None, ALU.is_equal))


class KeyGather:

    SET = 8

    def __init__(self, nc, S, a, H, k_tab, q_at):
        self.S, self.H, self.k_tab, self.q_at = S, H, k_tab, q_at
        self.slot = [a.sb(f"kg_slot{s}", [P, self.SET, H]) for s in range(2)]
        self.index = [a.sb(f"kg_index{s}", [P, self.SET], I32) for s in range(2)]
        self.landed = a.borrow(S.pool_dma[0:2])
        self.q_placed = a.borrow(S.pool_dma[2:3])[0]
        self.indexed, self.go, self.kept = a.sem("kg_indexed"), a.sem("kg_go"), a.sem("kg_kept")

    def __call__(self, pool):
        S, SET = self.S, self.SET
        LOOPS = CH // (2 * SET)

        def gather(i, s):
            cols = bass.ds(i * (2 * SET) + s * SET, SET)
            pool.tensor_copy(self.index[s][:], S.row_src[:, cols]).then_inc(self.indexed, 1)
            pool.wait_ge(self.indexed, i * 2 + s + 1)
            pool.sem_inc(self.go, 1)
            for u in range(SET):
                pool.indirect_dma_start(self.slot[s][:, u, :], None, self.k_tab,
                                        bass.IndirectOffsetOnAxis(ap=self.index[s][:, u:u + 1], axis=0)
                                        ).then_inc(self.landed[s], 16)

        def keep(i, s):
            pool.wait_ge(self.landed[s], i * (16 * SET) + 16 * SET)
            pool.sem_inc(self.go, 1)
            pool.tensor_copy(S.k_edge[:, bass.ds(i * (2 * SET) + s * SET, SET), 0:self.H], self.slot[s][:]
                             ).then_inc(self.kept, 1)
            pool.wait_ge(self.kept, i * 2 + s + 1)
            pool.sem_inc(self.go, 1)

        for t in range(NT):
            pool.indirect_dma_start(self.q_at, bass.IndirectOffsetOnAxis(ap=S.start_row[:, t:t + 1], axis=0),
                                    S.q_node[:, t, 0:2 * self.H], None, bounds_check=EP - 1, oob_is_err=False
                                    ).then_inc(self.q_placed, 16)
        gather(0, 0)
        with pool.Fori(0, LOOPS - 1) as i:
            gather(i, 1)
            keep(i, 0)
            gather(i + 1, 0)
            keep(i, 1)
        gather(LOOPS - 1, 1)
        keep(LOOPS - 1, 0)
        keep(LOOPS - 1, 1)
        pool.wait_ge(self.q_placed, 16 * NT)


def edge_softmax(nc, S, tag, q_at, H):
    H2 = 2 * H
    with stage(nc, tag) as a:
        q_rows = a.sb("q_rows", [CK, KB, P, H2])
        q_all = a.sb("q_all", [CK, H2, KB, P])
        rowed = a.sb("rowed", [CK, H, KB, P])
        fwd = q_all[:, 0:H]
        bwd = q_all[:, H:H2]
        end_q, run_q, in_q = (a.sb(n, [2 * HEADS, CH]) for n in ("end_q", "run_q", "in_q"))
        edge_f, edge_b = a.sb("edge_f", [HEADS, CH]), a.sb("edge_b", [HEADS, CH])
        run_f, run_b = a.sb("run_f", [HEADS, CH]), a.sb("run_b", [HEADS, CH])
        in_f, in_b = a.sb("in_f", [HEADS, CH]), a.sb("in_b", [HEADS, CH])
        carried = a.sb("carried", [CK, 2, KB, H])
        carried_q = a.sb("carried_q", [CK, KB, H2])
        pick = a.sb("pick", [CK, KB, VISITS * QUAD])
        rows_ps = a.ps("rows_ps", [P, H, KB, P])
        small_ps = a.ps("small_ps", [2 * HEADS, 2, 512])
        back_ps = a.ps("back_ps", [CK, 2, KB, H])
        back_q_ps = a.ps("back_q_ps", [CK, KB, H2])
        (q_landed, q_filled, q_turned, q_carried, q_back, turned, rows_done, scans_done, ends_turned, carries_done,
         carries_back, less_max, exp_done, exp_turned, dve_step) = (a.sem(n) for n in (
             "q_landed", "q_filled", "q_turned", "q_carried", "q_back", "turned", "rows_done", "scans_done",
             "ends_turned", "carries_done", "carries_back", "less_max", "exp_done", "exp_turned", "dve_step"))
        flat = lambda x: x.rearrange("c k j -> c (k j)")

        with nc.Block() as block:
            @block.sync
            def _(sp):
                sp.dma_start(q_rows[:], q_at.rearrange("(k c j) h -> c k j h", k=KB, c=CK)).then_inc(q_landed, 16)

            @block.vector
            def _(dve):
                st = Steps(dve, dve_step)
                pick_chunks(dve, st, S, pick)
                dve.wait_ge(q_landed, 16)
                for x in range(H2):
                    dve.tensor_tensor_scan(flat(q_all[:, x]), flat(S.inside[:]),
                                           q_rows[:, :, :, x].rearrange("c k j -> c (k j)"), 0.0, ALU.mult,
                                           ALU.add).then_inc(q_filled, 1)
                dve.wait_ge(q_turned, 1)
                st(dve.tensor_copy(end_q[0:H2, :], small_ps[0:H2, 0, 0:CH]))
                st(dve.tensor_tensor_scan(run_q[0:H2, :], S.passes[0:H2, :], end_q[0:H2, :], 0.0, ALU.mult, ALU.add))
                st(dve.memset(in_q[0:H2, :], 0.0))
                dve.tensor_tensor(in_q[0:H2, 1:CH], run_q[0:H2, 0:CH - 1], S.linked[0:H2, 1:CH],
                                  ALU.mult).then_inc(q_carried, 1)
                dve.wait_ge(q_back, 1)
                st(dve.tensor_copy(carried_q[:], back_q_ps[:]))
                qr = q_rows[:].rearrange("c k j h -> c (k j h)").rearrange("c (h k j) -> c h k j", h=H2, k=KB)
                for x in range(H2):
                    last = dve.tensor_tensor(qr[:, x], S.first_run[:],
                                             carried_q[:, :, x].unsqueeze(2).broadcast_to([CK, KB, P]), ALU.mult)
                st(last)
                st(dve.tensor_tensor(q_all[:], q_all[:], qr, ALU.add))
                st(dve.tensor_scalar(qr[:, 0], S.type1[:], -1.0, 1.0, ALU.mult, ALU.add))
                over = lambda m: m.rearrange("c k j -> c (k j)").unsqueeze(1).broadcast_to([CK, H, KB * P])
                fl4 = lambda m: m.rearrange("c h k j -> c h (k j)")
                dve.tensor_tensor(fl4(q_all[:, 0:H]), fl4(q_all[:, 0:H]), over(qr[:, 0]), ALU.mult)
                st(dve.tensor_tensor(fl4(q_all[:, H:H2]), fl4(q_all[:, H:H2]), over(S.type1[:]), ALU.mult))
                st(dve.tensor_tensor(q_all[:, 0:H], q_all[:, 0:H], q_all[:, H:H2], ALU.add))
                dve.wait_ge(turned, 1)
                st(dve.tensor_tensor(rowed[:], rows_ps[0:CK], q_all[:, 0:H], ALU.add))
                st(dve.scalar_tensor_tensor(rowed[:], rowed[:], SLOPE, rowed[:], ALU.mult, ALU.max))
                for h in range(H):
                    x, fw, bw = flat(rowed[:, h]), flat(fwd[:, h]), flat(bwd[:, h])
                    start, end = flat(S.pen_start[:]), flat(S.pen_end[:])
                    dve.tensor_tensor_scan(fw, start, x, -BIG, ALU.add, ALU.max).then_inc(scans_done, 1)
                    dve.tensor_tensor_scan(bw[:, ::-1], end[:, ::-1], x[:, ::-1], -BIG, ALU.add,
                                           ALU.max).then_inc(scans_done, 1)
                dve.wait_ge(ends_turned, 1)
                st(dve.tensor_copy(edge_f[0:H, :], small_ps[0:H, 0, 0:CH]))
                st(dve.tensor_copy(edge_b[0:H, :], small_ps[0:H, 1, 0:CH]))
                st(dve.tensor_tensor_scan(run_f[0:H, :], S.carry_f[0:H, :], edge_f[0:H, :], -BIG, ALU.add, ALU.max))
                st(dve.tensor_tensor_scan(run_b[0:H, ::-1], S.carry_b[0:H, ::-1], edge_b[0:H, ::-1], -BIG, ALU.add,
                                          ALU.max))
                st(dve.memset(in_f[0:H, :], -BIG))
                st(dve.memset(in_b[0:H, :], -BIG))
                dve.tensor_tensor(in_f[0:H, 1:CH], run_f[0:H, 0:CH - 1], S.link[0:H, 1:CH],
                                  ALU.add).then_inc(carries_done, 1)
                dve.tensor_tensor(in_b[0:H, 0:CH - 1], run_b[0:H, 1:CH], S.link[0:H, 1:CH],
                                  ALU.add).then_inc(carries_done, 1)
                dve.wait_ge(carries_back, 1)
                st(dve.tensor_copy(carried[:], back_ps[:]))
                st(dve.tensor_tensor(fwd[:], fwd[:], bwd[:], ALU.max))
                for n, pen in ((0, S.pen_first), (1, S.pen_last)):
                    for h in range(H):
                        dve.tensor_tensor(bwd[:, h], pen[:], carried[:, n, :, h].unsqueeze(2).broadcast_to([CK, KB, P]),
                                          ALU.add).then_inc(dve_step, 1)
                    st.n += H
                    dve.wait_ge(dve_step, st.n)
                    st(dve.tensor_tensor(fwd[:], fwd[:], bwd[:], ALU.max))
                dve.tensor_tensor(rowed[:], rowed[:], fwd[:], ALU.subtract).then_inc(less_max, 1)
                dve.wait_ge(exp_turned, 1)
                dve.tensor_copy(S.ex[:, :, 0:H], rows_ps[:].rearrange("p h k c -> p (k c) h"))

            @block.tensor
            def _(pe):
                for h in range(H):
                    for k in range(KB):
                        last = pe.transpose(rows_ps[0:CK, h, k, :], S.k_edge[:, k * CK:(k + 1) * CK, h], S.ident[:])
                last.then_inc(turned, 1)
                pe.wait_ge(q_filled, H2)
                for k in range(KB):
                    last = pe.transpose(small_ps[0:H2, 0, k * CK:(k + 1) * CK], q_all[:, :, k, P - 1], S.ident[0:CK, 0:CK])
                last.then_inc(q_turned, 1)
                pe.wait_ge(q_carried, 1)
                for k in range(KB):
                    last = pe.transpose(back_q_ps[:, k, :], in_q[0:H2, k * CK:(k + 1) * CK], S.ident[0:H2, 0:H2])
                last.then_inc(q_back, 1)
                pe.wait_ge(scans_done, 2 * H)
                for n, (x, j) in enumerate(((fwd, P - 1), (bwd, 0))):
                    for k in range(KB):
                        last = pe.transpose(small_ps[0:H, n, k * CK:(k + 1) * CK], x[:, :, k, j], S.ident[0:CK, 0:CK])
                last.then_inc(ends_turned, 1)
                pe.wait_ge(carries_done, 2)
                for n, x in enumerate((in_f, in_b)):
                    for k in range(KB):
                        last = pe.transpose(back_ps[:, n, k, :], x[0:H, k * CK:(k + 1) * CK], S.ident[0:H, 0:H])
                last.then_inc(carries_back, 1)
                pe.wait_ge(exp_done, 1)
                for h in range(H):
                    for k in range(KB):
                        last = pe.matmul(rows_ps[:, h].rearrange("p k c -> p (k c)"), rowed[:, h, k, :], pick[:, k, :],
                                         start=(k == 0), stop=(k == KB - 1))
                last.then_inc(exp_turned, 1)

            @block.scalar
            def _(act):
                act.wait_ge(less_max, 1)
                nc.scalar.activation(rowed[:], rowed[:], ACT.Exp).then_inc(exp_done, 1)


def edge_sums(nc, S, tag, table, width, weights, H, gather_rows, key_col, key_pad, scatter_rows, out_tab, accumulate,
              guest=None):
    SET = 4
    BODY = 4
    LEAD = 3
    LOOPS = CH // (BODY * SET)
    HW = width // H
    HX = 0 if accumulate else H
    with stage(nc, tag) as a:
        x = [a.sb(f"x{s}", [P, SET, width]) for s in range(BODY)]
        gi = [a.sb(f"gi{s}", [P, SET], I32) for s in range(BODY)]
        wt = [a.sb(f"wt{s}", [P, SET, H]) for s in range(2)]
        keys = [a.sb(f"keys{s}", [P, SET, P], I32) for s in range(2)]
        mask = [a.sb(f"mask{s}", [P, SET, P]) for s in range(2)]
        out = [a.sb(f"out{s}", [P, SET, width + HX]) for s in range(2)]
        si = [a.sb(f"si{s}", [P, SET], I32) for s in range(2)]
        sums = a.ps("sums", [P, SET, 512])
        if HX:
            dens = a.ps("dens", [P, 2, 512])
        guest_scalar, guest_vector, guest_tensor = (nothing_more,) * 3 if guest is None else guest(a)
        index_ready, masked, weighted, place_ready, out_free = (
            a.sem(n) for n in ("index_ready", "masked", "weighted", "place_ready", "out_free"))
        summed = [a.sem(f"summed{h}") for h in range(2)]
        copied = [a.sem(f"copied{h}") for h in range(2)]
        keys_landed = [a.sem(f"keys_landed{s}") for s in range(2)]
        dens_copied = [a.sem(f"dens_copied{s}") for s in range(2)]
        landed = a.borrow(S.pool_dma[0:BODY])
        scatters = a.borrow(S.pool_dma[BODY:BODY + SET])
        scattered = scatters[0:2]
        added = scatters
        pool_go = a.sem("pool_go")

        def cols(i, s):
            return bass.ds(i * (BODY * SET) + s * SET, SET)

        def before(i, s):
            return i * BODY + s

        def slot_before(i, s):
            return i * (BODY // 2) + s // 2

        with nc.Block() as block:
            @block.sync
            def _(sp):
                with sp.Fori(0, LOOPS) as i:
                    for s in range(BODY):
                        sp.wait_ge(masked, before(i, max(s - 1, 0)))
                        first = i * (BODY * SET * P) + s * SET * P
                        sp.dma_start(keys[s % 2][:].rearrange("p u j -> p (u j)"),
                                     row_of(key_pad[bass.ds(first, SET * P)]).broadcast_to([P, SET * P])
                                     ).then_inc(keys_landed[s % 2], 16)

            @block.gpsimd
            def _(pool):
                def gather(i, s):
                    pool.wait_ge(index_ready, before(i, s + 1))
                    pool.sem_inc(pool_go, 1)
                    for u in range(SET):
                        pool.indirect_dma_start(
                            x[s][:, u, :], None, table,
                            bass.IndirectOffsetOnAxis(ap=gi[s][:, u:u + 1], axis=0)).then_inc(landed[s], 16)

                def scatter(i, s):
                    pool.wait_ge(place_ready, before(i, s + 1))
                    if HX:
                        pool.wait_ge(dens_copied[s % 2], slot_before(i, s + 2))
                    pool.wait_ge(copied[0], before(i, s + 1))
                    pool.wait_ge(copied[1], before(i, s + 1))
                    pool.sem_inc(pool_go, 1)
                    for u in range(SET):
                        to = bass.IndirectOffsetOnAxis(ap=si[s % 2][:, u:u + 1], axis=0)
                        if accumulate:
                            pool.wait_ge(added[u], before(i, s) * 16)
                            pool.sem_inc(out_free if u == SET - 1 else pool_go, 1)
                            pool.indirect_dma_start(out_tab[u], to, out[s % 2][:, u, :], None,
                                                    compute_op=ALU.add).then_inc(added[u], 16)
                        else:
                            pool.indirect_dma_start(out_tab, to, out[s % 2][:, u, :], None, bounds_check=SKIP,
                                                    oob_is_err=False).then_inc(scattered[s % 2], 16)

                for s in range(LEAD):
                    gather(0, s)
                with pool.Fori(0, LOOPS - 1) as i:
                    for s in range(BODY):
                        gather(i + (s + LEAD) // BODY, (s + LEAD) % BODY)
                        scatter(i, s)
                for s in range(BODY):
                    if s + LEAD < BODY:
                        gather(LOOPS - 1, s + LEAD)
                    scatter(LOOPS - 1, s)
                if accumulate:
                    for u in range(SET):
                        pool.wait_ge(added[u], 16 * BODY * LOOPS)
                else:
                    for s in range(2):
                        pool.wait_ge(scattered[s], 16 * SET * (BODY // 2) * LOOPS)

            @block.scalar
            def _(act):
                def indices(i, s):
                    for h in range(2):
                        act.wait_ge(summed[h], before(i, s - LEAD) if s >= LEAD else before(i - 1, s - LEAD + BODY))
                    nc.scalar.copy(gi[s][:], gather_rows[:, cols(i, s)]).then_inc(index_ready, 1)

                def results(i, s):
                    if accumulate:
                        act.wait_ge(out_free, before(i, s))
                    else:
                        act.wait_ge(scattered[s % 2], slot_before(i, s) * (16 * SET))
                    nc.scalar.copy(si[s % 2][:], scatter_rows[:, cols(i, s)]).then_inc(place_ready, 1)
                    for h in range(2):
                        act.wait_ge(summed[h], before(i, s + 1))
                        nc.scalar.copy(out[s % 2][:, 2 * h:2 * h + 2, 0:width],
                                       sums[:, 2 * h:2 * h + 2, 0:width]).then_inc(copied[h], 1)
                    if HX:
                        nc.scalar.copy(out[s % 2][:, :, width:width + HX],
                                       dens[:, s % 2, 0:SET * HX].rearrange("p (u h) -> p u h", h=HX)
                                       ).then_inc(dens_copied[s % 2], 1)

                for s in range(LEAD):
                    nc.scalar.copy(gi[s][:], gather_rows[:, s * SET:(s + 1) * SET]).then_inc(index_ready, 1)
                with act.Fori(0, LOOPS - 1) as i:
                    for s in range(BODY):
                        indices(i + (s + LEAD) // BODY, (s + LEAD) % BODY)
                        results(i, s)
                        guest_scalar(act, i, s)
                indices(LOOPS - 1, BODY - 1)
                for s in range(BODY):
                    results(LOOPS - 1, s)

            @block.vector
            def _(dve):
                def weigh(i, s):
                    dve.wait_ge(keys_landed[s % 2], slot_before(i, s + 2) * 16)
                    dve.wait_ge(summed[1], before(i, max(s - 1, 0)))
                    dve.tensor_tensor(mask[s % 2][:], keys[s % 2][:],
                                      key_col[:, cols(i, s)].unsqueeze(2).broadcast_to([P, SET, P]),
                                      ALU.is_equal).then_inc(masked, 1)
                    if HX:
                        dve.tensor_copy(wt[s % 2][:], weights[:, cols(i, s), 0:H]).then_inc(weighted, 1)
                    dve.wait_ge(landed[s], i * (16 * SET) + 16 * SET)
                    by = weights[:, cols(i, s), 0:H].rearrange("p u h -> p (u h)")
                    v = x[s][:].rearrange("p u (h w) -> p (u h) w", h=H)
                    dve.tensor_tensor(v, v, by.unsqueeze(2).broadcast_to([P, SET * H, HW]), ALU.mult).then_inc(weighted, 1)

                with dve.Fori(0, LOOPS - 1) as i:
                    for s in range(BODY):
                        weigh(i, s)
                        guest_vector(dve, i, s)
                for s in range(BODY):
                    weigh(LOOPS - 1, s)

            @block.tensor
            def _(pe):
                def add_up(i, s):
                    pe.wait_ge(masked, before(i, s + 1))
                    pe.wait_ge(weighted, before(i, s + 1) * (2 if HX else 1))
                    if HX:
                        pe.wait_ge(dens_copied[s % 2], slot_before(i, s))
                    for h in range(2):
                        pe.wait_ge(copied[h], before(i, s))
                        for u in (2 * h, 2 * h + 1):
                            last = pe.matmul(sums[:, u, 0:width], mask[s % 2][:, u, :], x[s][:, u, :],
                                             start=True, stop=True)
                            if HX:
                                last = pe.matmul(dens[:, s % 2, u * H:(u + 1) * H], mask[s % 2][:, u, :],
                                                 wt[s % 2][:, u, :], start=True, stop=True)
                        last.then_inc(summed[h], 1)

                with pe.Fori(0, LOOPS - 1) as i:
                    for s in range(BODY):
                        add_up(i, s)
                        guest_tensor(pe, i, s)
                for s in range(BODY):
                    add_up(LOOPS - 1, s)


def edge_tiles(nc, S, tag, table, width, H):
    BODY = 4
    LEAD = 3
    LOOPS = VISITS // BODY
    HW = width // H
    with stage(nc, tag) as a:
        x = [a.sb(f"x{s}", [P, QUAD, width]) for s in range(BODY)]
        gi = [a.sb(f"gi{s}", [P, QUAD], I32) for s in range(BODY)]
        mask = [a.sb(f"mask{s}", [P, QUAD, TP]) for s in range(2)]
        sums = a.ps("sums", [TP, BODY, 512])
        dens = a.ps("dens", [TP, BODY, 512])
        index_ready, masked, weighted, summed, cleared = (
            a.sem(n) for n in ("index_ready", "masked", "weighted", "summed", "cleared"))
        added = [a.sem(f"added{s}") for s in range(BODY)]
        landed = a.borrow(S.pool_dma[0:BODY])
        pool_go, dve_go = a.sem("pool_go"), a.sem("dve_go")

        def cols(i, s):
            return bass.ds(i * (BODY * QUAD) + s * QUAD, QUAD)

        def before(i, s):
            return i * BODY + s

        with nc.Block() as block:
            @block.gpsimd
            def _(pool):
                def gather(i, s):
                    pool.wait_ge(index_ready, before(i, s + 1))
                    pool.sem_inc(pool_go, 1)
                    for u in range(QUAD):
                        pool.indirect_dma_start(
                            x[s][:, u, :], None, table,
                            bass.IndirectOffsetOnAxis(ap=gi[s][:, u:u + 1], axis=0)).then_inc(landed[s], 16)

                with pool.Fori(0, LOOPS) as i:
                    for s in range(BODY):
                        gather(i, s)
                for s in range(BODY):
                    pool.wait_ge(landed[s], 16 * QUAD * LOOPS)

            @block.scalar
            def _(act):
                for s in range(LEAD):
                    nc.scalar.copy(gi[s][:], S.visit_row[:, s * QUAD:(s + 1) * QUAD]).then_inc(index_ready, 1)
                with act.Fori(0, LOOPS - 1) as i:
                    for s in range(BODY):
                        act.wait_ge(summed, before(i, s))
                        j, to = i + (s + LEAD) // BODY, (s + LEAD) % BODY
                        nc.scalar.copy(gi[to][:], S.visit_row[:, cols(j, to)]).then_inc(index_ready, 1)
                act.wait_ge(summed, before(LOOPS - 1, 0))
                nc.scalar.copy(gi[BODY - 1][:], S.visit_row[:, cols(LOOPS - 1, BODY - 1)]).then_inc(index_ready, 1)

            @block.vector
            def _(dve):
                def weigh(i, s, done=None):
                    if done is not None:
                        dve.wait_ge(summed, done)
                    dve.tensor_tensor(mask[s % 2][:], S.iota_row[:, 0:TP].unsqueeze(1).broadcast_to([P, QUAD, TP]),
                                      S.visit_rel[:, cols(i, s)].unsqueeze(2).broadcast_to([P, QUAD, TP]),
                                      ALU.is_equal).then_inc(masked, 1)
                    dve.wait_ge(landed[s], i * (16 * QUAD) + 16 * QUAD)
                    by = S.ex[:, cols(i, s), 0:H].rearrange("p u h -> p (u h)")
                    v = x[s][:].rearrange("p u (h w) -> p (u h) w", h=H)
                    dve.tensor_tensor(v, v, by.unsqueeze(2).broadcast_to([P, QUAD * H, HW]), ALU.mult).then_inc(weighted, 1)

                def tile_number(i, s):
                    return dve.value_load(S.visit_tile[0:1, bass.ds(before(i, s), 1)], min_val=0, max_val=NT - 1)

                def add(i, s, t):
                    dve.wait_ge(summed, before(i, s + 1))
                    dve.wait_ge(added[(s - 1) % BODY], i * 2 + (2 if s else 0))
                    dve.sem_inc(dve_go, 1)
                    at = S.agg[:, bass.ds(t, 1), 0:width].rearrange("p a w -> p (a w)")
                    dve.tensor_tensor(at, at, sums[:, s, 0:width], ALU.add).then_inc(added[s], 1)
                    at = S.agg[:, bass.ds(t, 1), width:width + H].rearrange("p a w -> p (a w)")
                    dve.tensor_tensor(at, at, dens[:, s, 0:H], ALU.add).then_inc(added[s], 1)

                after(dve, dve.memset(S.agg[:, :, 0:width + H], 0.0), cleared, 1)
                weigh(0, 0)
                weigh(0, 1)
                with dve.Fori(0, LOOPS - 1) as i:
                    for s in range(BODY):
                        t = tile_number(i, s)
                        weigh(i + (s + 2) // BODY, (s + 2) % BODY, before(i, s + 1))
                        add(i, s, t)
                for s in range(BODY):
                    if s + 2 < BODY:
                        weigh(LOOPS - 1, s + 2, before(LOOPS - 1, s + 1))
                    add(LOOPS - 1, s, tile_number(LOOPS - 1, s))

            @block.tensor
            def _(pe):
                with pe.Fori(0, LOOPS) as i:
                    for s in range(BODY):
                        pe.wait_ge(masked, before(i, s + 1))
                        pe.wait_ge(weighted, before(i, s + 1))
                        pe.wait_ge(added[s], i * 2)
                        for u in range(QUAD):
                            pe.matmul(sums[:, s, 0:width], mask[s % 2][:, u, :], x[s][:, u, :],
                                      start=(u == 0), stop=(u == QUAD - 1))
                        for u in range(QUAD):
                            w = S.ex[:, bass.ds(i * (BODY * QUAD) + s * QUAD + u, 1), 0:H].rearrange("p a h -> p (a h)")
                            last = pe.matmul(dens[:, s, 0:H], mask[s % 2][:, u, :], w, start=(u == 0),
                                             stop=(u == QUAD - 1))
                        last.then_inc(summed, 1)


class Representatives:

    SET = 8

    def __init__(self, nc, S, a):
        self.S = S
        self.keys = [a.sb(f"rep_keys{s}", [P, self.SET, P], I32) for s in range(2)]
        self.same = [a.sb(f"rep_same{s}", [P, self.SET, P]) for s in range(2)]
        self.later_mask = a.sb("rep_later_mask", [P, P])
        self.later = a.sb("rep_later", [P, CH])
        self.dummy = a.sb("rep_dummy", [P, 1])
        self.row = a.sb("rep_row", [P, CH])
        self.keys_landed = [a.sem(f"rep_keys_landed{s}") for s in range(2)]
        self.compared, self.counted, self.step = a.sem("rep_compared"), a.sem("rep_counted"), a.sem("rep_step")
        self.masked = a.sem("rep_masked")

    def load(self, sp):
        SET = self.SET
        with sp.Fori(0, CH // (2 * SET)) as i:
            for s in range(2):
                sp.wait_ge(self.compared, i * 2)
                first = i * (2 * SET * P) + s * SET * P
                sp.dma_start(self.keys[s][:].rearrange("p u j -> p (u j)"),
                             row_of(self.S.src_pad[bass.ds(first, SET * P)]).broadcast_to([P, SET * P])
                             ).then_inc(self.keys_landed[s], 16)

    def find(self, dve):
        S, SET, later, row = self.S, self.SET, self.later, self.row
        st = Steps(dve, self.step)
        st(dve.tensor_scalar(self.later_mask[:], S.iota_row[:], S.part_col[:, 0:1], None, ALU.is_gt))
        with dve.Fori(0, CH // (2 * SET)) as i:
            cols = [bass.ds(i * (2 * SET) + s * SET, SET) for s in range(2)]
            for s in range(2):
                dve.wait_ge(self.keys_landed[s], i * 16 + 16)
                dve.wait_ge(self.counted, i * 2)
                dve.tensor_tensor(self.same[s][:], self.keys[s][:],
                                  S.src_c[:, cols[s]].unsqueeze(2).broadcast_to([P, SET, P]),
                                  ALU.is_equal).then_inc(self.compared, 1)
            for s in range(2):
                dve.wait_ge(self.compared, i * 2 + s + 1)
                dve.tensor_tensor(self.same[s][:], self.same[s][:],
                                  self.later_mask[:].unsqueeze(1).broadcast_to([P, SET, P]),
                                  ALU.mult).then_inc(self.masked, 1)
            for s in range(2):
                dve.wait_ge(self.masked, i * 2 + s + 1)
                dve.tensor_reduce(later[:, cols[s]], self.same[s][:], AX.X, ALU.max).then_inc(self.counted, 1)
        dve.wait_ge(self.counted, CH // SET)
        st(dve.tensor_scalar(self.dummy[:], S.part_col[:], float(N), None, ALU.add))
        st(dve.tensor_scalar(row[:], S.src_c[:], self.dummy[:, 0:1], None, ALU.subtract))
        st(dve.tensor_tensor(later[:], row[:], later[:], ALU.mult))
        st(dve.tensor_tensor(row[:], S.src_c[:], later[:], ALU.subtract))
        dve.tensor_copy(S.row_rep[:], row[:])


def layernorm_stats(nc, S, tag, x, eps=1e-5):
    with stage(nc, tag) as a:
        stats = a.sb("stats", [TP, NT, 6])
        mv = a.sb("mv", [TP, NT, 2])
        counted, var_ready, root_ready, step_s = a.sem("counted"), a.sem("var_ready"), a.sem("root_ready"), a.sem("step")
        with nc.Block() as block:
            @block.vector
            def _(dve):
                with dve.Fori(0, NG) as i:
                    for u in range(GROUP):
                        t = i * GROUP + u
                        dve.bn_stats(stats[:, bass.ds(t, 1), :].rearrange("p a s -> p (a s)"),
                                     x[:, bass.ds(t, 1), :].rearrange("p a d -> p (a d)")).then_inc(counted, 1)
                dve.wait_ge(counted, NT)
                for t in range(NT):
                    last = dve.bn_aggr(mv[:, t, :], stats[:, t, :])
                    last.then_inc(counted, 1)
                dve.wait_ge(counted, 2 * NT)
                dve.tensor_scalar(S.ln_r[:], mv[:, :, 1], eps, None, ALU.add).then_inc(var_ready, 1)
                dve.wait_ge(root_ready, 1)
                st = Steps(dve, step_s)
                st(dve.reciprocal(S.ln_r[:], S.ln_r[:]))
                dve.scalar_tensor_tensor(S.ln_b[:], mv[:, :, 0], -1.0, S.ln_r[:], ALU.mult, ALU.mult)

            @block.scalar
            def _(act):
                act.wait_ge(var_ready, 1)
                nc.scalar.activation(S.ln_r[:], S.ln_r[:], ACT.Sqrt).then_inc(root_ready, 1)


def col(ap, t):
    return ap[:, bass.ds(t, 1)]


def tile(ap, t):
    return ap[:, bass.ds(t, 1), :].rearrange("p a d -> p (a d)")


def mix0(nc, g, S, w_conv, bn_gamma, bn_beta, w_dw, pw_blocks, w_res, b_res, pool_work):
    C6 = 6
    with stage(nc, "m0_") as a:
        h = a.sb("h", [P, C6, N])
        affine = a.sb("affine", [P, C6, 2])
        pw = a.sb("pw", [P, C6, P])
        wres = a.sb("wres", [P, 4, D])
        bres = a.sb("bres", [TP, D])
        group_ones = a.sb("group_ones", [P, P])
        weights_in = a.sem("weights_in")

        with stage(nc, "m0a_") as b:
            wconv = b.sb("wconv", [P, 2, C6 * P])
            dw = b.sb("dw", [P, C6])
            gb = b.sb("gb", [P, 2, C6])
            sq_junk = b.sb("sq_junk", [TP, D])
            ss, m, lo, hi, pick, sc, sr, sb_ = (b.sb(n, [TP, NT]) for n in (
                "ss", "m", "lo", "hi", "pick", "sc", "sr", "sb"))
            xm = [b.sb(f"xm{s}", [TP, D]) for s in range(2)]
            xt = [b.sb(f"xt{s}", [P, 2, TP]) for s in range(2)]
            stats = b.sb("stats", [P, C6, 7, 6])
            mv = b.sb("mv", [P, C6, 2])
            turn_ps = b.ps("turn", [P, 2, 512])
            conv_ps = b.ps("conv", [P, 2, 2, 512])
            squared, step_s, roots, logs = b.sem("squared"), b.sem("step"), b.sem("roots"), b.sem("logs")
            scaled, turned, turn_copied = b.sem("scaled"), b.sem("turned"), b.sem("turn_copied")
            conv_done, conv_copied, bn_step, bn_root = (
                b.sem("conv_done"), b.sem("conv_copied"), b.sem("bn_step"), b.sem("bn_root"))
            affine_ready, zeroed, root_asked = b.sem("affine_ready"), b.sem("zeroed"), b.sem("root_asked")
            WIDTHS = [448] * 6 + [N - 6 * 448]
            with nc.Block() as block:
                @block.sync
                def _(sp):
                    sp.dma_start(wconv[:], w_conv.rearrange("(k p) c -> p k c", p=P)).then_inc(weights_in, 16)
                    for n, x in enumerate((bn_gamma, bn_beta)):
                        sp.dma_start(gb[:, n, :], x.rearrange("(c p) -> p c", p=P),
                                     allow_slow_non_contiguous=True).then_inc(weights_in, 16)
                    sp.dma_start(dw[:], w_dw.rearrange("(c p) -> p c", p=P),
                                 allow_slow_non_contiguous=True).then_inc(weights_in, 16)
                    sp.dma_start(wres[:], w_res.rearrange("(k p) c -> p k c", p=P)).then_inc(weights_in, 16)
                    sp.dma_start(bres[:], spread(b_res, TP)).then_inc(weights_in, 16)
                    sp.wait_ge(zeroed, 1)
                    for q in range(4):
                        sp.dma_start(pw[32 * q:32 * q + 32, :, 32 * q:32 * q + 32], pw_blocks[q]).then_inc(weights_in, 16)

                @block.scalar
                def _(act):
                    with act.Fori(0, NG) as i:
                        for u in range(GROUP):
                            t = i * GROUP + u
                            act.wait_ge(squared, i * GROUP + u)
                            nc.scalar.activation(sq_junk[:], tile(S.x, t), ACT.Square, scale=col(S.ln_r, t),
                                                 bias=col(S.ln_b, t), accum_out=col(ss, t)).then_inc(squared, 1)
                    act.wait_ge(root_asked, 1)
                    nc.scalar.activation(m[:], ss[:], ACT.Sqrt).then_inc(roots, 1)
                    act.wait_ge(root_asked, 2)
                    nc.scalar.activation(lo[:], lo[:], ACT.Ln).then_inc(logs, 1)
                    nc.scalar.activation(hi[:], hi[:], ACT.Ln).then_inc(logs, 1)
                    with act.Fori(0, NG) as i:
                        for u in range(GROUP):
                            act.wait_ge(turned, ready(i, u))
                            act.wait_ge(conv_done, freed(i, u, 2))
                            nc.scalar.copy(xt[u % 2][:], turn_ps[:, u % 2, 0:2 * TP].rearrange("p (k n) -> p k n", k=2)
                                           ).then_inc(turn_copied, 1)
                    act.wait_ge(bn_root, 1)
                    nc.scalar.activation(affine[:, :, 0], affine[:, :, 0], ACT.Sqrt).then_inc(bn_root, 1)
                    act.wait_ge(affine_ready, 1)
                    for c in range(C6):
                        nc.scalar.activation(h[:, c, :], h[:, c, :], ACT.Relu, scale=affine[:, c, 0:1],
                                             bias=affine[:, c, 1:2])

                @block.vector
                def _(dve):
                    st = Steps(dve, step_s)
                    dve.memset(pw[:], 0.0).then_inc(zeroed, 1)
                    st(dve.memset(group_ones[:], 0.0))
                    for q in range(4):
                        dve.memset(group_ones[32 * q:32 * q + 32, 32 * q:32 * q + 32], 1.0)
                    dve.wait_ge(squared, NT)
                    dve.tensor_scalar(ss[:], ss[:], MIN_NORM * MIN_NORM, None, ALU.max).then_inc(root_asked, 1)
                    dve.wait_ge(roots, 1)
                    st(dve.reciprocal(sc[:], m[:]))
                    st(dve.tensor_scalar(m[:], m[:], MAXNORM, None, ALU.min))
                    st(dve.tensor_scalar(lo[:], m[:], -1.0, 1.0, ALU.mult, ALU.add))
                    dve.tensor_scalar(hi[:], m[:], 1.0, None, ALU.add).then_inc(root_asked, 1)
                    st(dve.tensor_tensor(sr[:], m[:], m[:], ALU.mult))
                    st(dve.tensor_scalar(sb_[:], sr[:], 1.0 / 7, 1.0 / 5, ALU.mult, ALU.add))
                    st(dve.tensor_tensor(sb_[:], sb_[:], sr[:], ALU.mult))
                    st(dve.tensor_scalar(sb_[:], sb_[:], 1.0 / 3, None, ALU.add))
                    st(dve.tensor_tensor(sb_[:], sb_[:], sr[:], ALU.mult))
                    st(dve.scalar_tensor_tensor(sb_[:], sb_[:], 1.0, m[:], ALU.add, ALU.mult))
                    st(dve.tensor_scalar(pick[:], m[:], 0.0625, None, ALU.is_lt))
                    dve.wait_ge(logs, 2)
                    st(dve.tensor_tensor(hi[:], hi[:], lo[:], ALU.subtract))
                    st(dve.tensor_scalar(hi[:], hi[:], 0.5, None, ALU.mult))
                    st(dve.tensor_tensor(sb_[:], sb_[:], hi[:], ALU.subtract))
                    st(dve.tensor_tensor(sb_[:], sb_[:], pick[:], ALU.mult))
                    st(dve.tensor_tensor(hi[:], hi[:], sb_[:], ALU.add))
                    st(dve.tensor_tensor(sc[:], sc[:], hi[:], ALU.mult))
                    st(dve.tensor_tensor(sr[:], S.ln_r[:], sc[:], ALU.mult))
                    st(dve.tensor_tensor(sb_[:], S.ln_b[:], sc[:], ALU.mult))

                    def log_map(t, u, free):
                        dve.wait_ge(turned, free)
                        dve.tensor_scalar(xm[u % 2][:], tile(S.x, t), col(sr, t), col(sb_, t), ALU.mult,
                                          ALU.add).then_inc(scaled, 1)

                    with dve.Fori(0, NG) as i:
                        for u in range(GROUP):
                            t = i * GROUP + u
                            log_map(t, u, freed(i, u, 2))
                            dve.wait_ge(conv_done, ready(i, u))
                            dve.tensor_copy(h[:, :, bass.ds(t * TP, TP)].rearrange("p (b c) n -> p b c n", b=2),
                                            conv_ps[:, u % 2, :, 0:3 * TP].rearrange("p b (c n) -> p b c n", c=3)
                                            ).then_inc(conv_copied, 1)
                    dve.wait_ge(conv_copied, NT)
                    for c in range(C6):
                        for w, width in enumerate(WIDTHS):
                            last = dve.bn_stats(stats[:, c, w, :], h[:, c, 448 * w:448 * w + width])
                    bn = Steps(dve, bn_step)
                    bn(last)
                    for c in range(C6):
                        last = dve.bn_aggr(mv[:, c, :], stats[:, c].rearrange("p w s -> p (w s)"))
                    bn(last)
                    dve.tensor_scalar(affine[:, :, 0], mv[:, :, 1], 1e-5, None, ALU.add).then_inc(bn_root, 1)
                    dve.wait_ge(bn_root, 2)
                    dve.wait_ge(weights_in, 160)
                    bn(dve.reciprocal(affine[:, :, 0], affine[:, :, 0]))
                    bn(dve.tensor_tensor(affine[:, :, 0], affine[:, :, 0], gb[:, 0, :], ALU.mult))
                    bn(dve.tensor_tensor(affine[:, :, 1], mv[:, :, 0], affine[:, :, 0], ALU.mult))
                    dve.tensor_tensor(affine[:, :, 1], gb[:, 1, :], affine[:, :, 1],
                                      ALU.subtract).then_inc(affine_ready, 1)
                    for c in range(C6):
                        dve.tensor_scalar(pw[:, c, :], pw[:, c, :], dw[:, c:c + 1], None, ALU.mult)

                @block.tensor
                def _(pe):
                    pe.wait_ge(weights_in, 160)
                    with pe.Fori(0, NG) as i:
                        for u in range(GROUP):
                            pe.wait_ge(scaled, ready(i, u))
                            pe.wait_ge(turn_copied, freed(i, u, 2))
                            for k in range(2):
                                last = pe.transpose(turn_ps[:, u % 2, k * TP:(k + 1) * TP],
                                                    xm[u % 2][:, k * P:(k + 1) * P], S.ident[0:TP, 0:TP])
                            last.then_inc(turned, 1)
                            pe.wait_ge(turn_copied, ready(i, u))
                            pe.wait_ge(conv_copied, freed(i, u, 2))
                            for c in range(C6):
                                for k in range(2):
                                    last = pe.matmul(conv_ps[:, u % 2, c // 3, (c % 3) * TP:(c % 3 + 1) * TP],
                                                     wconv[:, k, c * P:(c + 1) * P], xt[u % 2][:, k, :],
                                                     start=(k == 0), stop=(k == 1))
                            last.then_inc(conv_done, 1)

        with stage(nc, "m0b_") as b:
            t_sq = b.sb("t_sq", [P, C6, TP])
            cat = [b.sb(f"cat{s}", [P, 3, 4, TP]) for s in range(2)]
            cat_sq = b.sb("cat_sq", [P, 3, 4, TP])
            n1, r1, n2, r2 = (b.sb(n, [P, TP]) for n in ("n1", "r1", "n2", "r2"))
            rq, rk, vv, o = (b.sb(n, [P, 4, TP]) for n in ("rq", "rk", "vv", "o"))
            o_sq = t_sq[:, 0:4, :]
            rv = cat_sq[:, 0]
            ss3, f3, ss4, f4 = (b.sb(n, [TP, NT]) for n in ("ss3", "f3", "ss4", "f4"))
            junk = t_sq[0:TP].rearrange("p c n -> p (c n)")[:, 0:D]
            norm_ps = b.ps("norm", [P, 2, 512])
            point_ps = b.ps("point", [P, 2, 512])
            ksum_ps = b.ps("ksum", [P, 512])
            proj_ps = b.ps("proj", [TP, 512])
            n3_ps = b.ps("n3", [TP, 512])
            names = ("t_squared", "n1_mm", "n1_in", "n1_root", "t_made", "point_mm", "point_copied", "cat_squared",
                     "n2_mm", "n2_in", "n2_root", "rk_made", "cat_used", "k_summed", "o_made", "o_squared", "n3_mm", "n3_copied",
                     "proj_mm", "proj_copied", "step1", "step2", "step3", "f3_in", "f3_root", "f3_done", "sq4", "biased", "f4_root", "f4_in", "f4_step")
            (t_squared, n1_mm, n1_in, n1_root, t_made, point_mm, point_copied, cat_squared, n2_mm, n2_in, n2_root,
             rk_made, cat_used, k_summed, o_made, o_squared, n3_mm, n3_copied, proj_mm, proj_copied, step1, step2, step3, f3_in, f3_root,
             f3_done, sq4, biased, f4_root, f4_in, f4_step) = (b.sem(n) for n in names)
            with nc.Block() as block:
                @block.gpsimd
                def _(pool):
                    pool_work(pool)

                @block.scalar
                def _(act):
                    def tap(i, u):
                        act.wait_ge(n1_mm, freed(i, u, 1))
                        act.wait_ge(n3_mm, i * GROUP + max(u - 2, 0))
                        nc.scalar.activation(t_sq[:], h[:, :, bass.ds((i * GROUP + u) * TP, TP)],
                                             ACT.Square).then_inc(t_squared, 1)
                        act.wait_ge(n1_in, ready(i, u))
                        nc.scalar.activation(n1[:], n1[:], ACT.Sqrt).then_inc(n1_root, 1)

                    def point(i, u):
                        act.wait_ge(point_mm, ready(i, u))
                        for c, n in ((0, 2), (2, 1), (3, 1), (4, 2)):
                            nc.scalar.copy(cat[u % 2][:, c // 2, 2 + c % 2:2 + c % 2 + n, :].rearrange("p c n -> p (c n)"),
                                           point_ps[:, c // 3, (c % 3) * TP:(c % 3 + n) * TP]).then_inc(point_copied, 1)
                        act.wait_ge(t_made, ready(i, u))
                        act.wait_ge(point_copied, i * (4 * GROUP) + 4 * (u + 1))
                        act.wait_ge(n2_mm, freed(i, u, 1))
                        act.wait_ge(step2, (i * GROUP + u) * 6)
                        nc.scalar.activation(cat_sq[:], cat[u % 2][:], ACT.Square).then_inc(cat_squared, 1)
                        act.wait_ge(n2_in, ready(i, u))
                        nc.scalar.activation(n2[:], n2[:], ACT.Sqrt).then_inc(n2_root, 1)

                    def attend(i, u):
                        t = i * GROUP + u
                        act.wait_ge(o_made, ready(i, u))
                        act.wait_ge(n3_mm, freed(i, u, 1))
                        act.wait_ge(n1_mm, i * GROUP + min(u + 2, GROUP))
                        nc.scalar.activation(o_sq, o[:], ACT.Square).then_inc(o_squared, 1)
                        act.wait_ge(proj_mm, ready(i, u))
                        nc.scalar.copy(tile(S.fx, t), proj_ps[:, 0:D]).then_inc(proj_copied, 1)
                        act.wait_ge(n3_mm, ready(i, u))
                        nc.scalar.copy(col(ss3, t), n3_ps[:, 0:1]).then_inc(n3_copied, 1)

                    with act.Fori(0, NG) as i:
                        stagger(i, tap, point, attend, oldest_first=True)
                    act.wait_ge(f3_in, 1)
                    nc.scalar.activation(f3[:], ss3[:], ACT.Sqrt).then_inc(f3_root, 1)
                    with act.Fori(0, NG) as i:
                        for u in range(GROUP):
                            t = i * GROUP + u
                            act.wait_ge(biased, ready(i, u))
                            act.wait_ge(sq4, i * GROUP + u)
                            nc.scalar.activation(junk, tile(S.fx, t), ACT.Square, accum_out=col(ss4, t)).then_inc(sq4, 1)
                    act.wait_ge(f4_in, 1)
                    nc.scalar.activation(ss4[:], ss4[:], ACT.Sqrt).then_inc(f4_root, 1)
                    act.wait_ge(f4_root, 1)
                    nc.scalar.activation(f4[:], ss4[:], ACT.Tanh).then_inc(f4_root, 1)

                @block.vector
                def _(dve):
                    def over(x, m):
                        return x[:].unsqueeze(1).broadcast_to([P, m, TP])

                    def tap(i, u):
                        dve.wait_ge(n1_mm, ready(i, u))
                        dve.tensor_scalar(n1[:], norm_ps[:, 0, 0:TP], MIN_NORM * MIN_NORM, None, ALU.max).then_inc(n1_in, 1)
                        dve.wait_ge(n1_root, ready(i, u))
                        after(dve, dve.reciprocal(r1[:], n1[:]), step1, (i * GROUP + u) * 2 + 1)
                        after(dve, dve.scalar_tensor_tensor(r1[:], n1[:], ATANH_MAX, r1[:], ALU.min, ALU.mult),
                              step1, (i * GROUP + u) * 2 + 2)
                        dve.wait_ge(cat_squared, freed(i, u, 2))
                        hv = h[:, :, bass.ds((i * GROUP + u) * TP, TP)].rearrange("p (r c) n -> p r c n", r=3)
                        for r in range(3):
                            ins = dve.tensor_tensor(cat[u % 2][:, r, 0:2, :], hv[:, r], over(r1, 2), ALU.mult)
                        ins.then_inc(t_made, 1)

                    def point(i, u):
                        c = cat[u % 2]
                        base = (i * GROUP + u) * 6
                        dve.wait_ge(n2_mm, ready(i, u))
                        dve.tensor_scalar(n2[:], norm_ps[:, 1, 0:TP], MIN_NORM * MIN_NORM, None, ALU.max).then_inc(n2_in, 1)
                        dve.wait_ge(n2_root, ready(i, u))
                        after(dve, dve.reciprocal(r2[:], n2[:]), step2, base + 1)
                        after(dve, dve.scalar_tensor_tensor(r2[:], n2[:], ATANH_MAX, r2[:], ALU.min, ALU.mult),
                              step2, base + 2)
                        dve.wait_ge(k_summed, freed(i, u, 1))
                        dve.scalar_tensor_tensor(rk[:], c[:, 1], 0.0, over(r2, 4), ALU.max, ALU.mult).then_inc(rk_made, 1)
                        dve.tensor_tensor(vv[:], c[:, 2], over(r2, 4), ALU.mult).then_inc(step2, 1)
                        dve.scalar_tensor_tensor(rq[:], c[:, 0], 0.0, over(r2, 4), ALU.max, ALU.mult).then_inc(cat_used, 1)
                        dve.wait_ge(step2, base + 3)
                        after(dve, dve.tensor_scalar(rv, vv[:], 1e-15, None, ALU.add), step2, base + 4)
                        after(dve, dve.reciprocal(rv, rv), step2, base + 5)
                        dve.tensor_tensor(vv[:], vv[:], rv, ALU.mult).then_inc(step2, 1)

                    def attend(i, u):
                        dve.wait_ge(cat_used, ready(i, u))
                        dve.wait_ge(step2, (i * GROUP + u) * 6 + 6)
                        dve.wait_ge(k_summed, ready(i, u))
                        dve.wait_ge(proj_mm, freed(i, u, 1))
                        dve.wait_ge(o_squared, freed(i, u, 1))
                        after(dve, dve.tensor_tensor(o[:].rearrange("p a n -> p (a n)"), rq[:].rearrange("p a n -> p (a n)"),
                                                     ksum_ps[:, 0:4 * TP], ALU.mult), step3, i * GROUP + u + 1)
                        dve.tensor_tensor(o[:], o[:], vv[:], ALU.mult).then_inc(o_made, 1)

                    with dve.Fori(0, NG) as i:
                        stagger(i, tap, point, attend, oldest_first=True)
                    st = Steps(dve, f4_step)
                    dve.wait_ge(n3_copied, NT)
                    dve.tensor_scalar(ss3[:], ss3[:], MIN_NORM * MIN_NORM, None, ALU.max).then_inc(f3_in, 1)
                    dve.wait_ge(f3_root, 1)
                    st(dve.reciprocal(ss3[:], f3[:]))
                    st(dve.scalar_tensor_tensor(f3[:], f3[:], ATANH_MAX, ss3[:], ALU.min, ALU.mult))
                    dve.wait_ge(proj_copied, NT)
                    with dve.Fori(0, NG) as i:
                        for u in range(GROUP):
                            t = i * GROUP + u
                            dve.scalar_tensor_tensor(tile(S.fx, t), tile(S.fx, t), col(f3, t), bres[:], ALU.mult,
                                                     ALU.add).then_inc(biased, 1)
                    dve.wait_ge(sq4, NT)
                    dve.tensor_scalar(ss4[:], ss4[:], MIN_NORM * MIN_NORM, None, ALU.max).then_inc(f4_in, 1)
                    dve.wait_ge(f4_root, 2)
                    st(dve.reciprocal(ss4[:], ss4[:]))
                    st(dve.scalar_tensor_tensor(f4[:], f4[:], MAXNORM, ss4[:], ALU.min, ALU.mult))
                    with dve.Fori(0, NG) as i:
                        for u in range(GROUP):
                            t = i * GROUP + u
                            dve.tensor_scalar(tile(S.fx, t), tile(S.fx, t), col(f4, t), None, ALU.mult)

                @block.tensor
                def _(pe):
                    def tap(i, u):
                        pe.wait_ge(t_squared, ready(i, u))
                        pe.wait_ge(n1_in, freed(i, u, 1))
                        for k in range(C6):
                            last = pe.matmul(norm_ps[:, 0, 0:TP], S.ones[:], t_sq[:, k, :],
                                             start=(k == 0), stop=(k == C6 - 1))
                        last.then_inc(n1_mm, 1)

                    def point(i, u):
                        c = cat[u % 2]
                        pe.wait_ge(t_made, ready(i, u))
                        pe.wait_ge(point_copied, i * (4 * GROUP) + 4 * u)
                        for k in range(C6):
                            last = pe.matmul(point_ps[:, k // 3, (k % 3) * TP:(k % 3 + 1) * TP], pw[:, k, :],
                                             c[:, k // 2, k % 2, :], start=True, stop=True)
                        last.then_inc(point_mm, 1)
                        pe.wait_ge(cat_squared, ready(i, u))
                        pe.wait_ge(n2_in, freed(i, u, 1))
                        for k in range(12):
                            last = pe.matmul(norm_ps[:, 1, 0:TP], S.ones[:], cat_sq[:, k // 4, k % 4, :],
                                             start=(k == 0), stop=(k == 11))
                        last.then_inc(n2_mm, 1)

                    def attend(i, u):
                        pe.wait_ge(rk_made, ready(i, u))
                        pe.wait_ge(o_made, freed(i, u, 1))
                        pe.matmul(ksum_ps[:, 0:4 * TP], group_ones[:], rk[:].rearrange("p a n -> p (a n)"),
                                  start=True, stop=True).then_inc(k_summed, 1)
                        pe.wait_ge(o_made, ready(i, u))
                        pe.wait_ge(proj_copied, freed(i, u, 1))
                        for k in range(4):
                            last = pe.matmul(proj_ps[:, 0:D], o[:, k, :], wres[:, k, :], start=(k == 0), stop=(k == 3))
                        last.then_inc(proj_mm, 1)
                        pe.wait_ge(o_squared, ready(i, u))
                        pe.wait_ge(n3_copied, freed(i, u, 1))
                        for k in range(4):
                            last = pe.matmul(n3_ps[:, 0:1], o_sq[:, k, :], S.ones[:, 0:1], start=(k == 0), stop=(k == 3))
                        last.then_inc(n3_mm, 1)

                    with pe.Fori(0, NG) as i:
                        stagger(i, tap, point, attend, oldest_first=True)


def load_nodes(nc, g, S, x):
    S.x = g.sb("x", [TP, NT, D])
    S.fx_rows = nc.dram_tensor("fx_rows", [N, D], F32, kind="Internal").ap()
    S.ln_r, S.ln_b = g.sb("ln_r", [TP, NT]), g.sb("ln_b", [TP, NT])
    loaded = g.sem("x_loaded")
    with nc.Block() as block:
        @block.sync
        def _(sp):
            sp.dma_start(S.x[:], tiles_of(x)).then_inc(loaded, 16)
            sp.wait_ge(loaded, 16)


def slot_uses(i, u):
    return i * ((GROUP + 1) // 2 if u % 2 == 0 else GROUP // 2) + u // 2


def psum_cols(ap, n):
    return ap[:, 0:n]


def load_projection(nc, keep, a, W, W_T, q, k, H, width, chunks):
    OC = width // P
    w = keep.sb("w", [P, chunks, 2, width])
    wqk = keep.sb("wqk", [P, chunks, 2, 2, H])
    w_t = [a.sb(f"w_t{r}", [P, OC, chunks * P]) for r in range(2)]
    qk = a.sb("qk", [P, OC, 2, H])
    wqk_ps = a.ps("wqk_ps", [P, 512])
    loaded, multiplied = a.sem("w_loaded"), a.sem("wqk_multiplied")
    with nc.Block() as block:
        @block.sync
        def _(sp):
            sp.dma_start(qk[:, :, 0, :], q.rearrange("(c p) h -> p c h", p=P),
                         allow_slow_non_contiguous=True).then_inc(loaded, 16)
            sp.dma_start(qk[:, :, 1, :], k.rearrange("(c p) h -> p c h", p=P),
                         allow_slow_non_contiguous=True).then_inc(loaded, 16)
            for r in range(2):
                sp.dma_start(w_t[r][:], W_T[r].rearrange("(c p) i -> p c i", p=P)).then_inc(loaded, 16)
                sp.dma_start(w[:, :, r, :], W[r].rearrange("(c p) o -> p c o", p=P)).then_inc(loaded, 16)

        @block.tensor
        def _(pe):
            pe.wait_ge(loaded, 96)
            for c in range(chunks):
                for r in range(2):
                    at = (c * 2 + r) * 2 * H
                    for o in range(OC):
                        last = pe.matmul(wqk_ps[:, at:at + 2 * H], w_t[r][:, o, c * P:(c + 1) * P],
                                         qk[:, o].rearrange("p s h -> p (s h)"), start=(o == 0), stop=(o == OC - 1))
            last.then_inc(multiplied, 1)

        @block.vector
        def _(dve):
            dve.wait_ge(multiplied, 1)
            dve.tensor_copy(wqk[:].rearrange("p c r s h -> p (c r s h)"), wqk_ps[:, 0:chunks * 4 * H])
    return w, wqk


class Projector:

    def __init__(self, nc, S, a, w, wqk, width, H, table, k_tab, const=None):
        self.nc, self.w, self.wqk, self.width, self.H, self.const = nc, w, wqk, width, H, const
        self.S, self.table, self.k_tab = S, table, k_tab
        self.out = [a.sb(f"proj_out{s}", [TP, 2, width]) for s in range(2)]
        self.k = [a.sb(f"proj_k{s}", [TP, 2, H]) for s in range(2)]
        self.ps = a.ps("proj_ps", [TP, 2, 512])
        self.qk_ps = a.ps("proj_qk_ps", [TP, 512])
        self.done, self.copied = a.sem("proj_done"), a.sem("proj_copied")
        self.stored = [a.sem(f"proj_stored{s}") for s in range(2)]
        self.DMAS = 3

    def multiply(self, pe, i, u, chunks):
        pe.wait_ge(self.copied, i * (3 * GROUP) + 3 * u)
        n = len(chunks)
        for r in range(2):
            for c, x in enumerate(chunks):
                pe.matmul(self.ps[:, r, 0:self.width], x, self.w[:, c, r, :], start=(c == 0),
                          stop=(c == n - 1 and self.const is None))
            if self.const is not None:
                pe.matmul(self.ps[:, r, 0:self.width], self.const[2], self.const[0][0:1, r, :], start=False, stop=True)
        for c, x in enumerate(chunks):
            last = pe.matmul(self.qk_ps[:, 0:4 * self.H], x, self.wqk[:, c].rearrange("p r s h -> p (r s h)"),
                             start=(c == 0), stop=(c == n - 1 and self.const is None))
        if self.const is not None:
            last = pe.matmul(self.qk_ps[:, 0:4 * self.H], self.const[2], self.const[1][0:1, :], start=False, stop=True)
        last.then_inc(self.done, 1)

    def copy(self, act, i, u):
        s = u % 2
        act.wait_ge(self.done, ready(i, u))
        act.wait_ge(self.stored[s], slot_uses(i, u) * (16 * self.DMAS))
        self.nc.scalar.copy(self.out[s][:], self.ps[:, :, 0:self.width]).then_inc(self.copied, 1)
        both = self.qk_ps[:, 0:4 * self.H].rearrange("p (r s h) -> p r s h", r=2, s=2)
        at = self.S.q_node[:, bass.ds(i * GROUP + u, 1), 0:2 * self.H].rearrange("p a (r h) -> p (a r) h", r=2)
        self.nc.scalar.copy(at, both[:, :, 0]).then_inc(self.copied, 1)
        self.nc.scalar.copy(self.k[s][:], both[:, :, 1]).then_inc(self.copied, 1)

    def store(self, sp, i, u):
        s = u % 2
        t = i * GROUP + u
        rows = bass.ds(t * TP, TP)
        sp.wait_ge(self.copied, i * (3 * GROUP) + 3 * u + 3)
        for r in range(2):
            sp.dma_start(self.table[r * N:(r + 1) * N, :][rows, :], self.out[s][:, r, :]).then_inc(self.stored[s], 16)
        sp.dma_start(self.k_tab.rearrange("(r n) h -> n r h", r=2)[rows], self.k[s][:],
                     allow_slow_non_contiguous=True).then_inc(self.stored[s], 16)

    def finish(self, sp):
        for s in range(2):
            uses = NG * ((GROUP + 1) // 2 if s == 0 else GROUP // 2)
            sp.wait_ge(self.stored[s], uses * 16 * self.DMAS)


def gnn_first(nc, S, query, gate_w1, gate_b1, gate_w2, gate_b2, W, W_T, q, k):
    width = HEADS * HID
    with stage(nc, "g1_") as a:
        w = a.sb("w4", [P, 4, 2, width])
        wqk = a.sb("wqk4", [P, 4, 2, 2, HEADS])
        const_row = a.sb("const_row", [1, 2, width])
        const_qk = a.sb("const_qk", [1, 4 * HEADS])
        qcol = a.sb("qcol", [P, 2])
        gw1, gw2 = a.sb("gw1", [P, 4, D]), a.sb("gw2", [P, 2, D])
        gb = a.sb("gb", [P, 2, 2])
        gconst = a.sb("gconst", [P, 2])
        with stage(nc, "g1w_") as b:
            w6, wqk6 = load_projection(nc, b, b, W, W_T, q, k, HEADS, width, 6)
            row_ps, gate_ps = b.ps("row_ps", [1, 3, 512]), b.ps("gate_ps", [P, 512])
            loaded, multiplied = b.sem("loaded"), b.sem("multiplied")
            with nc.Block() as block:
                @block.sync
                def _(sp):
                    sp.dma_start(qcol[:], query[0].rearrange("(k p) -> p k", p=P),
                                 allow_slow_non_contiguous=True).then_inc(loaded, 16)
                    sp.dma_start(gw1[:], gate_w1.rearrange("(k p) c -> p k c", p=P)).then_inc(loaded, 16)
                    sp.dma_start(gw2[:], gate_w2.rearrange("(k p) c -> p k c", p=P)).then_inc(loaded, 16)
                    for n, x in enumerate((gate_b1, gate_b2)):
                        sp.dma_start(gb[:, n, :], x.rearrange("(k p) -> p k", p=P),
                                     allow_slow_non_contiguous=True).then_inc(loaded, 16)

                @block.tensor
                def _(pe):
                    pe.wait_ge(loaded, 80)
                    for r in range(2):
                        for c in range(2):
                            pe.matmul(row_ps[:, r, :], qcol[:, c:c + 1], w6[:, 2 + c, r, :], start=(c == 0), stop=(c == 1))
                    for c in range(2):
                        pe.matmul(row_ps[:, 2, 0:4 * HEADS], qcol[:, c:c + 1],
                                  wqk6[:, 2 + c].rearrange("p r s h -> p (r s h)"), start=(c == 0), stop=(c == 1))
                    for o in range(2):
                        for c in range(2):
                            last = pe.matmul(gate_ps[:, o:o + 1], gw1[:, 2 + c, o * P:(o + 1) * P], qcol[:, c:c + 1],
                                             start=(c == 0), stop=(c == 1))
                    last.then_inc(multiplied, 1)

                @block.vector
                def _(dve):
                    dve.wait_ge(loaded, 80)
                    dve.tensor_copy(w[:, 0:2], w6[:, 0:2])
                    dve.tensor_copy(wqk[:, 0:2], wqk6[:, 0:2])
                    for c in range(2):
                        dve.tensor_scalar(w[:, 2 + c], w6[:, 4 + c], qcol[:, c:c + 1], None, ALU.mult)
                        dve.tensor_scalar(wqk[:, 2 + c], wqk6[:, 4 + c], qcol[:, c:c + 1], None, ALU.mult)
                    dve.wait_ge(multiplied, 1)
                    dve.tensor_copy(const_row[:], row_ps[:, 0:2, :])
                    dve.tensor_copy(const_qk[:], row_ps[:, 2, 0:4 * HEADS])
                    dve.tensor_tensor(gconst[:], gate_ps[:, 0:2], gb[:, 0, :], ALU.add)

        with stage(nc, "g1t_") as b:
            proj = Projector(nc, S, b, w, wqk, width, HEADS, S.table, S.k_tab,
                             const=(const_row, const_qk, S.ones[0:1, 0:TP]))
            xn = [b.sb(f"xn{s}", [TP, D]) for s in range(2)]
            xt = [b.sb(f"xt{s}", [P, 2, TP]) for s in range(GROUP)]
            x0 = [b.sb(f"x0{s}", [P, 2, TP]) for s in range(GROUP)]
            gh, gate = b.sb("gh", [P, 2, TP]), b.sb("gate", [P, 2, TP])
            turn_ps = b.ps("turn", [P, 512])
            gate_ps = b.ps("gate_ps", [P, 2, 512])
            normed, turned, turn_copied, hidden_mm, hidden, gate_mm, gated, x0_made = (
                b.sem(n) for n in ("normed", "turned", "turn_copied", "hidden_mm", "hidden", "gate_mm", "gated", "x0_made"))
            x0_stored = [b.sem(f"x0_stored{s}") for s in range(GROUP)]
            with nc.Block() as block:
                @block.vector
                def _(dve):
                    def norm(i, u):
                        t = i * GROUP + u
                        dve.wait_ge(turned, freed(i, u, 2))
                        dve.tensor_scalar(xn[u % 2][:], tile(S.x, t), col(S.ln_r, t), col(S.ln_b, t), ALU.mult,
                                          ALU.add).then_inc(normed, 1)

                    def gate_it(i, u):
                        dve.wait_ge(gated, i * (2 * GROUP) + 2 * u + 2)
                        dve.wait_ge(proj.done, freed(i, u, GROUP))
                        dve.wait_ge(x0_stored[u], i * 16)
                        dve.tensor_tensor(x0[u][:], gate[:], xt[u][:], ALU.mult).then_inc(x0_made, 1)

                    with dve.Fori(0, NG) as i:
                        stagger(i, norm, gate_it)

                @block.scalar
                def _(act):
                    def turn(i, u):
                        act.wait_ge(turned, ready(i, u))
                        act.wait_ge(proj.done, freed(i, u, GROUP))
                        nc.scalar.copy(xt[u][:], turn_ps[:, 0:2 * TP].rearrange("p (k n) -> p k n", k=2)
                                       ).then_inc(turn_copied, 1)

                    def gate_it(i, u):
                        act.wait_ge(hidden_mm, ready(i, u))
                        for o in range(2):
                            nc.scalar.activation(gh[:, o, :], gate_ps[:, 0, o * TP:(o + 1) * TP], ACT.Relu,
                                                 bias=gconst[:, o:o + 1]).then_inc(hidden, 1)
                        act.wait_ge(gate_mm, ready(i, u))
                        act.wait_ge(x0_made, freed(i, u, 1))
                        for o in range(2):
                            nc.scalar.activation(gate[:, o, :], gate_ps[:, 1, o * TP:(o + 1) * TP], ACT.Sigmoid,
                                                 bias=gb[:, 1, o:o + 1]).then_inc(gated, 1)

                    def turn_and_gate(i, u):
                        turn(i, u)
                        gate_it(i, u)

                    with act.Fori(0, NG) as i:
                        stagger(i, turn_and_gate, lambda i, u: proj.copy(act, i, u))

                @block.tensor
                def _(pe):
                    def turn(i, u):
                        pe.wait_ge(normed, ready(i, u))
                        pe.wait_ge(turn_copied, freed(i, u, 1))
                        for c in range(2):
                            last = pe.transpose(turn_ps[:, c * TP:(c + 1) * TP], xn[u % 2][:, c * P:(c + 1) * P],
                                                S.ident[0:TP, 0:TP])
                        last.then_inc(turned, 1)

                    def hide(i, u):
                        pe.wait_ge(turn_copied, ready(i, u))
                        pe.wait_ge(hidden, i * (2 * GROUP) + 2 * u)
                        for o in range(2):
                            for c in range(2):
                                last = pe.matmul(gate_ps[:, 0, o * TP:(o + 1) * TP], gw1[:, c, o * P:(o + 1) * P],
                                                 xt[u][:, c, :], start=(c == 0), stop=(c == 1))
                        last.then_inc(hidden_mm, 1)

                    def gate_it(i, u):
                        pe.wait_ge(hidden, i * (2 * GROUP) + 2 * u + 2)
                        pe.wait_ge(gated, i * (2 * GROUP) + 2 * u)
                        for o in range(2):
                            for c in range(2):
                                last = pe.matmul(gate_ps[:, 1, o * TP:(o + 1) * TP], gw2[:, c, o * P:(o + 1) * P],
                                                 gh[:, c, :], start=(c == 0), stop=(c == 1))
                        last.then_inc(gate_mm, 1)

                    def project(i, u):
                        pe.wait_ge(x0_made, ready(i, u))
                        proj.multiply(pe, i, u, [x0[u][:, 0, :], x0[u][:, 1, :], xt[u][:, 0, :], xt[u][:, 1, :]])

                    with pe.Fori(0, NG) as i:
                        for step in range(GROUP + 1):
                            if step < GROUP:
                                turn(i, step)
                                hide(i, step)
                            if step:
                                project(i, step - 1)
                            if step < GROUP:
                                gate_it(i, step)

                @block.sync
                def _(sp):
                    with sp.Fori(0, NG) as i:
                        for u in range(GROUP):
                            t = i * GROUP + u
                            sp.wait_ge(x0_made, ready(i, u))
                            sp.dma_start(S.x0_t[bass.ds(t, 1)].rearrange("a p k n -> (a p) k n"),
                                         x0[u][:]).then_inc(x0_stored[u], 16)
                            proj.store(sp, i, u)
                    proj.finish(sp)
                    for s in range(GROUP):
                        sp.wait_ge(x0_stored[s], 16 * NG)


def gnn_nodes(nc, S, tag, width, H, bias, residual=False, wqk=None, next_H=None, k_tab=None, out_w=None,
              out_b=None):
    CHUNKS = width // P
    last_layer = out_w is not None
    with stage(nc, tag) as a:
        if last_layer:
            ow, ob = a.sb("ow", [P, D]), a.sb("ob", [1, D])
            x0 = [a.sb(f"x0{s}", [P, 2, TP]) for s in range(2)]
            x0_landed = [a.sem(f"x0_landed{s}") for s in range(2)]
            junk = a.sb("junk", [TP, D])
        else:
            k_out = [a.sb(f"k_out{s}", [TP, 2, next_H]) for s in range(2)]
            stored = [a.sem(f"stored{s}") for s in range(2)]
        bias_row = a.sb("bias_row", [TP, width])
        den = [a.sb(f"den{s}", [TP, H]) for s in range(2)]
        h = [a.sb(f"h{s}", [TP, width]) for s in range(2)]
        ht = [a.sb(f"ht{s}", [P, CHUNKS, TP]) for s in range(2)]
        turn_ps = a.ps("turn", [P, 2, 512])
        out_ps = a.ps("out_ps", [TP, 2, 512])
        preload = a.sem("preload")
        dstep, h_made, turned, turn_copied, kept, out_mm, out_copied, biased = (
            a.sem(n) for n in ("dstep", "h_made", "turned", "turn_copied", "kept", "out_mm",
                               "out_copied", "biased"))
        sp_go = a.sem("sp_go")

        def turned_rows(t):
            return S.h_t[:, :, bass.ds(t * TP, TP)]

        with nc.Block() as block:
            @block.sync
            def _(sp):
                sp.dma_start(bias_row[:], spread(bias, TP)).then_inc(preload, 16)
                if last_layer:
                    sp.dma_start(ow[:], out_w).then_inc(preload, 16)
                    sp.dma_start(ob[:], row_of(out_b)).then_inc(preload, 16)

                def load(i, u):
                    t = i * GROUP + u
                    if last_layer:
                        sp.wait_ge(out_mm, freed(i, u, 2))
                        sp.dma_start(x0[u % 2][:], S.x0_t[bass.ds(t, 1)].rearrange("a p k n -> (a p) k n")
                                     ).then_inc(x0_landed[u % 2], 16)

                def store(i, u):
                    if not last_layer:
                        sp.wait_ge(out_copied, i * (2 * GROUP) + 2 * u + 2)
                        sp.sem_inc(sp_go, 1)
                        sp.dma_start(k_tab.rearrange("(r n) h -> n r h", r=2)[bass.ds((i * GROUP + u) * TP, TP)],
                                     k_out[u % 2][:], allow_slow_non_contiguous=True).then_inc(stored[u % 2], 16)

                with sp.Fori(0, NG) as i:
                    stagger(i, load, nothing, nothing, store)
                if not last_layer:
                    for s in range(2):
                        sp.wait_ge(stored[s], 16 * NG * ((GROUP + 1 - s) // 2))

            @block.vector
            def _(dve):
                def finish(i, u):
                    s, t = u % 2, i * GROUP + u
                    base = (i * GROUP + u) * 3
                    rows = tile(S.agg, t)
                    after(dve, dve.tensor_scalar(den[s][:], rows[:, width:width + H], 1e-16, None, ALU.add), dstep, base + 1)
                    after(dve, dve.reciprocal(den[s][:], den[s][:]), dstep, base + 2)
                    dve.wait_ge(turned, freed(i, u, 2))
                    after(dve, dve.tensor_tensor(h[s][:].rearrange("p (h w) -> p h w", h=H),
                                                 rows[:, 0:width].rearrange("p (h w) -> p h w", h=H),
                                                 den[s][:].unsqueeze(2).broadcast_to([TP, H, width // H]), ALU.mult),
                          dstep, base + 3)
                    after(dve, dve.tensor_tensor(h[s][:], h[s][:], bias_row[:], ALU.add), biased, i * GROUP + u + 1)
                    dve.tensor_scalar(h[s][:], h[s][:], 0.0, None, ALU.max).then_inc(h_made, 1)

                def add(i, u):
                    if residual:
                        dve.wait_ge(turned, ready(i, u))
                        dve.wait_ge(kept, freed(i, u, 2))
                        dve.wait_ge(out_mm, freed(i, u, 2))
                        dve.tensor_tensor(ht[u % 2][:], turn_ps[:, u % 2, 0:CHUNKS * TP].rearrange(
                            "p (k n) -> p k n", k=CHUNKS), turned_rows(i * GROUP + u), ALU.add).then_inc(turn_copied, 1)

                dve.wait_ge(preload, 48 if last_layer else 16)
                with dve.Fori(0, NG) as i:
                    stagger(i, finish, nothing, add)

            @block.tensor
            def _(pe):
                def turn(i, u):
                    s = u % 2
                    pe.wait_ge(h_made, ready(i, u))
                    pe.wait_ge(turn_copied, freed(i, u, 2))
                    for c in range(CHUNKS):
                        last = pe.transpose(turn_ps[:, s, c * TP:(c + 1) * TP], h[s][:, c * P:(c + 1) * P],
                                            S.ident[0:TP, 0:TP])
                    last.then_inc(turned, 1)

                def project(i, u):
                    s = u % 2
                    pe.wait_ge(turn_copied, ready(i, u))
                    pe.wait_ge(out_copied, i * (2 * GROUP) + 2 * max(u - 1, 0))
                    if last_layer:
                        pe.wait_ge(x0_landed[s], (slot_uses(i, u) + 1) * 16)
                        pe.matmul(out_ps[:, s, 0:D], ht[s][:, 0, :], ow[:], start=True, stop=False)
                        pe.matmul(out_ps[:, s, 0:D], S.ones[0:1, 0:TP], ob[:], start=False, stop=False)
                        for c in range(2):
                            last = pe.matmul(out_ps[:, s, c * P:(c + 1) * P], x0[s][:, c, :], S.ident[:],
                                             start=False, stop=(c == 1))
                    else:
                        for c in range(CHUNKS):
                            last = pe.matmul(out_ps[:, s, 0:4 * next_H], ht[s][:, c, :],
                                             wqk[:, c].rearrange("p r s h -> p (r s h)"), start=(c == 0),
                                             stop=(c == CHUNKS - 1))
                    last.then_inc(out_mm, 1)

                pe.wait_ge(preload, 48 if last_layer else 16)
                with pe.Fori(0, NG) as i:
                    stagger(i, nothing, turn, project)

            @block.scalar
            def _(act):
                def copy(i, u):
                    s = u % 2
                    if not residual:
                        act.wait_ge(turned, ready(i, u))
                        act.wait_ge(out_mm, freed(i, u, 2))
                        act.wait_ge(kept, freed(i, u, 2))
                        nc.scalar.copy(ht[s][:], turn_ps[:, s, 0:CHUNKS * TP].rearrange("p (k n) -> p k n", k=CHUNKS)
                                       ).then_inc(turn_copied, 1)
                    act.wait_ge(turn_copied, ready(i, u))
                    if last_layer:
                        act.sem_inc(kept, 1)
                    else:
                        nc.scalar.copy(turned_rows(i * GROUP + u), ht[s][:]).then_inc(kept, 1)

                def results(i, u):
                    s, t = u % 2, i * GROUP + u
                    act.wait_ge(out_mm, ready(i, u))
                    if last_layer:
                        act.wait_ge(out_copied, i * (2 * GROUP) + 2 * u)
                        nc.scalar.copy(tile(S.gout, t), out_ps[:, s, 0:D]).then_inc(out_copied, 1)
                        nc.scalar.activation(junk[:], out_ps[:, s, 0:D], ACT.Square,
                                             accum_out=col(S.gss, t)).then_inc(out_copied, 1)
                    else:
                        both = out_ps[:, s, 0:4 * next_H].rearrange("p (r s h) -> p r s h", r=2, s=2)
                        at = S.q_node[:, bass.ds(t, 1), 0:2 * next_H].rearrange("p a (r h) -> p (a r) h", r=2)
                        nc.scalar.copy(at, both[:, :, 0]).then_inc(out_copied, 1)
                        act.wait_ge(stored[s], slot_uses(i, u) * 16)
                        nc.scalar.copy(k_out[s][:], both[:, :, 1]).then_inc(out_copied, 1)

                with act.Fori(0, NG) as i:
                    stagger(i, copy, results)


def project_rows(nc, S, tag, w, width, table, H, k_tab, q_at, with_representatives=False):
    CHUNKS = 4
    with stage(nc, tag) as a:
        keys = KeyGather(nc, S, a, H, k_tab, q_at)
        rep = Representatives(nc, S, a) if with_representatives else None
        ht = [a.sb(f"ht{s}", [P, CHUNKS, TP]) for s in range(2)]
        out = [a.sb(f"out{s}", [TP, 2, width]) for s in range(2)]
        ps = [a.ps(f"rows{s}", [TP, 2, 512]) for s in range(2)]
        picked, multiplied, copied = a.sem("picked"), a.sem("multiplied"), a.sem("copied")
        stored = [a.sem(f"stored{s}") for s in range(2)]
        with nc.Block() as block:
            @block.gpsimd
            def _(pool):
                keys(pool)

            if rep is not None:
                @block.sync
                def _(sp):
                    rep.load(sp)

                @block.vector
                def _(dve):
                    rep.find(dve)

            @block.scalar
            def _(act):
                def pick(i, u):
                    act.wait_ge(multiplied, freed(i, u, 2))
                    nc.scalar.copy(ht[u % 2][:], S.h_t[:, :, bass.ds((i * GROUP + u) * TP, TP)]).then_inc(picked, 1)

                def copy(i, u):
                    s = u % 2
                    act.wait_ge(multiplied, ready(i, u))
                    act.wait_ge(stored[s], slot_uses(i, u) * 32)
                    nc.scalar.copy(out[s][:], ps[s][:, :, 0:width]).then_inc(copied, 1)

                def store(i, u):
                    act.wait_ge(copied, ready(i, u))
                    for r in range(2):
                        act.dma_start(table[r * N:(r + 1) * N, :][bass.ds((i * GROUP + u) * TP, TP), :],
                                      out[u % 2][:, r, :]).then_inc(stored[u % 2], 16)

                with act.Fori(0, NG) as i:
                    stagger(i, pick, copy, store)
                for s in range(2):
                    act.wait_ge(stored[s], 32 * NG * ((GROUP + 1 - s) // 2))

            @block.tensor
            def _(pe):
                with pe.Fori(0, NG) as i:
                    for u in range(GROUP):
                        s = u % 2
                        pe.wait_ge(picked, ready(i, u))
                        pe.wait_ge(copied, freed(i, u, 2))
                        for r in range(2):
                            for c in range(CHUNKS):
                                last = pe.matmul(ps[s][:, r, 0:width], ht[s][:, c, :], w[:, c, r, :], start=(c == 0),
                                                 stop=(c == CHUNKS - 1))
                        last.then_inc(multiplied, 1)


def gnn0(nc, g, S, A):
    dram = lambda name, shape: nc.dram_tensor(name, shape, F32, kind="Internal").ap()
    S.table = dram("table", [2 * N, HEADS * HID])
    S.table3 = dram("table3", [2 * N, HID])
    S.k_tab, S.k_tab3 = dram("k_tab", [2 * N, HEADS]), dram("k_tab3", [2 * N, 1])
    S.x0_t = dram("x0_t", [NT, P, 2, TP])
    S.gss = g.sb("gss", [TP, NT])
    with stage(nc, "gn_") as a:
        S.ex = a.sb("ex", [P, VISITS * QUAD, HEADS])
        S.k_edge = S.ex[:, 0:CH, :]
        S.q_node = a.sb("q_node", [TP, NT, 2 * HEADS])
        W512 = HEADS * HID
        gnn_first(nc, S, A["L0_gnn_query"], A["L0_gnn_gate_w1"], A["L0_gnn_gate_b1"], A["L0_gnn_gate_w2"],
                  A["L0_gnn_gate_b2"], A["W1"], A["W1_T"], A["L0_gnn_q1"], A["L0_gnn_k1"])
        with stage(nc, "kg1_") as b:
            S.fx = b.sb("fx", [TP, NT, D])
            mix0(nc, g, S, A["conv_w"], A["bn_gamma"], A["bn_beta"], A["dw_w"], A["pw_w"], A["res_w"],
                 A["L0_mix_b_res"], KeyGather(nc, S, b, HEADS, S.k_tab, S.q_at))
            fx_stored = b.sem("fx_stored")
            with nc.Block() as block:
                @block.sync
                def _(sp):
                    sp.dma_start(tiles_of(S.fx_rows), S.fx[:]).then_inc(fx_stored, 16)
                    sp.wait_ge(fx_stored, 16)
        visits(nc, a, S)
        S.h_t = a.sb("h_t", [P, W512 // P, N])
        S.gout = S.h_t[0:TP].rearrange("p c n -> p (c n)")[:, 0:NT * D].rearrange("p (t d) -> p t d", d=D)
        for layer in (1, 2):
            edge_softmax(nc, S, f"s{layer}_", S.q_at, HEADS)
            n = layer + 1
            next_H, next_width = (HEADS, W512) if layer == 1 else (1, HID)
            table, k_tab, q_at = (S.table, S.k_tab, S.q_at) if layer == 1 else (S.table3, S.k_tab3, S.q_at3)
            with stage(nc, f"w{n}_") as b:
                S.agg = b.sb("agg", [TP, NT, W512 + HEADS])
                edge_tiles(nc, S, f"a{layer}_", S.table, W512, HEADS)
                with stage(nc, f"w{n}t_") as c:
                    w, wqk = load_projection(nc, b, c, A[f"W{n}"], A[f"W{n}_T"], A[f"L0_gnn_q{n}"], A[f"L0_gnn_k{n}"],
                                             next_H, next_width, W512 // P)
                gnn_nodes(nc, S, f"n{layer}_", W512, HEADS, A[f"L0_gnn_b{layer}"], residual=(layer == 2),
                          wqk=wqk, next_H=next_H, k_tab=k_tab)
                project_rows(nc, S, f"p{n}_", w, next_width, table, next_H, k_tab, q_at,
                             with_representatives=(layer == 2))
        edge_softmax(nc, S, "s3_", S.q_at3, 1)
        with stage(nc, "w4_") as b:
            S.agg = b.sb("agg", [TP, NT, HID + 1])
            edge_tiles(nc, S, "a3_", S.table3, HID, 1)
            gnn_nodes(nc, S, "n3_", HID, 1, A["L0_gnn_b3"], out_w=A["L0_gnn_proj_w"], out_b=A["L0_gnn_proj_b"])
        add_gnn0(nc, S)


def add_gnn0(nc, S):
    with stage(nc, "c0_") as a:
        fx, fx_landed = a.sb("fx", [TP, NT, D]), a.sem("fx_landed")
        root, asked, step_s, scaled = a.sem("root"), a.sem("asked"), a.sem("step"), a.sem("scaled")
        with nc.Block() as block:
            @block.sync
            def _(sp):
                sp.dma_start(fx[:], tiles_of(S.fx_rows)).then_inc(fx_landed, 16)

            @block.scalar
            def _(act):
                act.wait_ge(asked, 1)
                nc.scalar.activation(S.gss[:], S.gss[:], ACT.Sqrt).then_inc(root, 1)

            @block.vector
            def _(dve):
                dve.tensor_scalar(S.gss[:], S.gss[:], 1e-24, None, ALU.max).then_inc(asked, 1)
                dve.wait_ge(root, 1)
                st = Steps(dve, step_s)
                st(dve.reciprocal(S.gss[:], S.gss[:]))
                dve.wait_ge(fx_landed, 16)
                with dve.Fori(0, NG) as i:
                    for u in range(GROUP):
                        t = i * GROUP + u
                        dve.scalar_tensor_tensor(tile(S.x, t), tile(S.gout, t), col(S.gss, t), tile(S.x, t), ALU.mult,
                                                 ALU.add).then_inc(scaled, 1)
                        dve.wait_ge(scaled, ready(i, u))
                        dve.tensor_tensor(tile(S.x, t), tile(S.x, t), tile(fx, t), ALU.add)


EXPERTS = 8
FF = 1024
CAP = -(-5 * N // (4 * EXPERTS))
SLOTS = 4 * P
FLT_MAX = 3.4028234663852886e38


def moe(nc, S, gate_w, gate_b, w1, b1, w2, b2):
    EX = EXPERTS
    buf = nc.dram_tensor("expert_in", [EX * SLOTS, D], F32, kind="Internal").ap()
    ybuf = nc.dram_tensor("expert_out", [EX * SLOTS, D], F32, kind="Internal").ap()
    with stage(nc, "mo_") as a:
        row_in, row_out = a.sb("row_in", [TP, NT], I32), a.sb("row_out", [TP, NT], I32)
        weight = a.sb("weight", [TP, NT])
        with stage(nc, "mor_") as b:
            gw, gb = b.sb("gw", [P, 2, EX]), b.sb("gb", [TP, EX])
            xl = [b.sb(f"xl{s}", [TP, D]) for s in range(2)]
            xt = [b.sb(f"xt{s}", [P, 2, TP]) for s in range(2)]
            logit = b.sb("logit", [TP, NT, EX])
            one_hot, cand, prefix, total, scan = (b.sb(n, [TP, NT, EX]) for n in
                                                  ("one_hot", "cand", "prefix", "total", "scan"))
            until = b.sb("until", [TP, TP])
            ones_t = b.sb("ones_t", [TP, NT])
            top, den, best, pos, kept, idx = (b.sb(n, [TP, NT]) for n in ("top", "den", "best", "pos", "kept", "idx"))
            turn_ps, logit_ps = b.ps("turn", [P, 2, 512]), b.ps("logit_ps", [TP, 512])
            pre_ps, tot_ps = b.ps("pre", [TP, 512]), b.ps("tot", [TP, 512])
            zeros, zeros_set = b.sb("zeros_wide", [P, 512]), b.sem("zeros_set")
            loaded, zeroed, normed, turned, turn_copied, logit_mm, logit_in, shifted, exped, hot, summed, step_s = (
                b.sem(n) for n in ("loaded", "zeroed", "normed", "turned", "turn_copied", "logit_mm", "logit_in",
                                   "shifted", "exped", "hot", "summed", "step"))
            with nc.Block() as block:
                @block.sync
                def _(sp):
                    sp.dma_start(gw[:], gate_w.rearrange("(k p) e -> p k e", p=P)).then_inc(loaded, 16)
                    sp.dma_start(gb[:], spread(gate_b, TP)).then_inc(loaded, 16)
                    rows = buf.rearrange("(p r) d -> p (r d)", p=P)
                    sp.wait_ge(zeros_set, 1)
                    for c in range(0, EX * SLOTS * D // P, 512):
                        sp.dma_start(rows[:, c:c + 512], zeros[:]).then_inc(zeroed, 16)
                    sp.wait_ge(zeroed, 16 * (EX * SLOTS * D // P // 512))

                @block.vector
                def _(dve):
                    dve.memset(zeros[:], 0.0).then_inc(zeros_set, 1)
                    dve.wait_ge(loaded, 32)
                    with dve.Fori(0, NG) as i:
                        for u in range(GROUP):
                            t = i * GROUP + u
                            dve.wait_ge(turned, freed(i, u, 2))
                            dve.tensor_scalar(xl[u % 2][:], tile(S.x, t), col(S.ln_r, t), col(S.ln_b, t), ALU.mult,
                                              ALU.add).then_inc(normed, 1)
                            dve.wait_ge(logit_mm, ready(i, u))
                            dve.tensor_tensor(tile(logit, t), logit_ps[:, 0:EX], gb[:], ALU.add).then_inc(logit_in, 1)
                    dve.wait_ge(logit_in, NT)
                    st = Steps(dve, step_s)

                    def wide(x):
                        return x[:].unsqueeze(2).broadcast_to([TP, NT, EX])

                    st(dve.tensor_reduce(top[:], logit[:], AX.X, ALU.max))
                    dve.tensor_tensor(logit[:], logit[:], wide(top), ALU.subtract).then_inc(shifted, 1)
                    dve.wait_ge(exped, 1)
                    st(dve.tensor_reduce(den[:], logit[:], AX.X, ALU.add))
                    st(dve.reciprocal(den[:], den[:]))
                    st(dve.tensor_tensor(logit[:], logit[:], wide(den), ALU.mult))
                    st(dve.tensor_reduce(best[:], logit[:], AX.X, ALU.max))
                    st(dve.tensor_tensor(one_hot[:], logit[:], wide(best), ALU.is_equal))
                    expert_no = S.iota_row[0:TP, 0:EX].unsqueeze(1).broadcast_to([TP, NT, EX])
                    st(dve.scalar_tensor_tensor(cand[:], expert_no, float(-EX), one_hot[:], ALU.add, ALU.mult))
                    st(dve.tensor_reduce(idx[:], cand[:], AX.X, ALU.min))
                    st(dve.tensor_scalar(idx[:], idx[:], float(EX), None, ALU.add))
                    st(dve.tensor_tensor(one_hot[:], expert_no, wide(idx), ALU.is_equal))
                    dve.tensor_scalar(until[:], S.iota_row[0:TP, 0:TP], S.part_col[0:TP, 0:1], None,
                                      ALU.is_ge).then_inc(hot, 1)
                    st(dve.memset(ones_t[:], 1.0))
                    dve.wait_ge(summed, 1)
                    st(dve.tensor_copy(prefix[:].rearrange("p t e -> p (t e)"), pre_ps[:, 0:NT * EX]))
                    st(dve.tensor_copy(total[:].rearrange("p t e -> p (t e)"), tot_ps[:, 0:NT * EX]))
                    for e in range(EX):
                        last = dve.tensor_tensor_scan(scan[:, :, e], ones_t[:], total[:, :, e], 0.0, ALU.mult, ALU.add)
                    st(last)
                    st(dve.tensor_tensor(scan[:], scan[:], total[:], ALU.subtract))
                    st(dve.tensor_tensor(scan[:], scan[:], prefix[:], ALU.add))
                    st(dve.tensor_tensor(scan[:], scan[:], one_hot[:], ALU.mult))
                    st(dve.tensor_reduce(pos[:], scan[:], AX.X, ALU.add))
                    st(dve.tensor_scalar(pos[:], pos[:], -1.0, None, ALU.add))
                    st(dve.tensor_scalar(kept[:], pos[:], float(CAP), None, ALU.is_lt))
                    st(dve.tensor_tensor(weight[:], best[:], kept[:], ALU.mult))
                    st(dve.tensor_scalar(pos[:], pos[:], float(CAP - 1), None, ALU.min))
                    st(dve.scalar_tensor_tensor(pos[:], idx[:], float(SLOTS), pos[:], ALU.mult, ALU.add))
                    st(dve.tensor_copy(row_out[:], pos[:]))
                    st(dve.scalar_tensor_tensor(pos[:], pos[:], float(-SKIP), kept[:], ALU.add, ALU.mult))
                    st(dve.tensor_scalar(pos[:], pos[:], float(SKIP), None, ALU.add))
                    dve.tensor_copy(row_in[:], pos[:])

                @block.scalar
                def _(act):
                    with act.Fori(0, NG) as i:
                        for u in range(GROUP):
                            act.wait_ge(turned, ready(i, u))
                            act.wait_ge(logit_mm, freed(i, u, 2))
                            nc.scalar.copy(xt[u % 2][:], turn_ps[:, u % 2, 0:2 * TP].rearrange("p (k n) -> p k n", k=2)
                                           ).then_inc(turn_copied, 1)
                    act.wait_ge(shifted, 1)
                    nc.scalar.activation(logit[:], logit[:], ACT.Exp).then_inc(exped, 1)

                @block.tensor
                def _(pe):
                    pe.wait_ge(loaded, 32)
                    with pe.Fori(0, NG) as i:
                        for u in range(GROUP):
                            pe.wait_ge(normed, ready(i, u))
                            pe.wait_ge(turn_copied, freed(i, u, 2))
                            for c in range(2):
                                last = pe.transpose(turn_ps[:, u % 2, c * TP:(c + 1) * TP], xl[u % 2][:, c * P:(c + 1) * P],
                                                    S.ident[0:TP, 0:TP])
                            last.then_inc(turned, 1)
                            pe.wait_ge(turn_copied, ready(i, u))
                            pe.wait_ge(logit_in, freed(i, u, 1))
                            for c in range(2):
                                last = pe.matmul(logit_ps[:, 0:EX], xt[u % 2][:, c, :], gw[:, c, :], start=(c == 0),
                                                 stop=(c == 1))
                            last.then_inc(logit_mm, 1)
                    pe.wait_ge(hot, 1)
                    hots = one_hot[:].rearrange("p t e -> p (t e)")
                    pe.matmul(pre_ps[:, 0:NT * EX], until[:], hots, start=True, stop=True)
                    pe.matmul(tot_ps[:, 0:NT * EX], S.ones[0:TP, 0:TP], hots, start=True, stop=True).then_inc(summed, 1)

        with stage(nc, "mod_") as b:
            xl = [b.sb(f"xl{s}", [TP, D]) for s in range(2)]
            at = [b.sb(f"at{s}", [TP, 1], I32) for s in range(2)]
            normed, pool_go = b.sem("normed"), b.sem("pool_go")
            scattered = b.borrow(S.pool_dma[0:2])
            with nc.Block() as block:
                @block.vector
                def _(dve):
                    with dve.Fori(0, NG) as i:
                        for u in range(GROUP):
                            t, s = i * GROUP + u, u % 2
                            dve.wait_ge(scattered[s], slot_uses(i, u) * 16)
                            dve.tensor_copy(at[s][:], col(row_in, t)).then_inc(normed, 1)
                            dve.tensor_scalar(xl[s][:], tile(S.x, t), col(S.ln_r, t), col(S.ln_b, t), ALU.mult,
                                              ALU.add).then_inc(normed, 1)

                @block.gpsimd
                def _(pool):
                    with pool.Fori(0, NG) as i:
                        for u in range(GROUP):
                            s = u % 2
                            pool.wait_ge(normed, i * (2 * GROUP) + 2 * u + 2)
                            pool.sem_inc(pool_go, 1)
                            pool.indirect_dma_start(buf, bass.IndirectOffsetOnAxis(ap=at[s][:, 0:1], axis=0), xl[s][:],
                                                    None, bounds_check=EX * SLOTS - 1, oob_is_err=False
                                                    ).then_inc(scattered[s], 16)
                    for s in range(2):
                        pool.wait_ge(scattered[s], 16 * NG * (3 - s))

        with stage(nc, "moe_") as b:
            FC = FF // P
            w1s = [b.sb(f"w1{s}", [P, 2, FF]) for s in range(2)]
            w2s = [b.sb(f"w2{s}", [P, FC, D]) for s in range(2)]
            b1s = [b.sb(f"b1{s}", [P, FC]) for s in range(2)]
            b2s = [b.sb(f"b2{s}", [1, D]) for s in range(2)]
            xs = [b.sb(f"xs{s}", [P, 4, D]) for s in range(2)]
            xt = b.sb("xt", [P, 2, SLOTS])
            hid = b.sb("hid", [P, FC, SLOTS])
            out = [b.sb(f"out{s}", [P, 4, D]) for s in range(2)]
            turn_ps = b.ps("turn", [P, 2, 512])
            hid_ps = b.ps("hid_ps", [P, 2, 512])
            out_ps = b.ps("out_ps", [P, 4, 512])
            w_landed = [b.sem(f"w_landed{s}") for s in range(2)]
            out_mm = [b.sem(f"out_mm{s}") for s in range(2)]
            stored = b.borrow(S.pool_dma[0:2])
            turned, turn_copied, hid_mm, hid_done, out_copied, pool_go = (
                b.sem(n) for n in ("turned", "turn_copied", "hid_mm", "hid_done", "out_copied", "pool_go"))
            with nc.Block() as block:
                @block.sync
                def _(sp):
                    with sp.Fori(0, EX // 2) as i:
                        for s in range(2):
                            e = i * 2 + s
                            one = bass.ds(e, 1)
                            sp.wait_ge(out_mm[s], i * 4)
                            sp.dma_start(xs[s][:], buf[bass.ds(e * SLOTS, SLOTS), :].rearrange("(r p) d -> p r d", p=P)
                                         ).then_inc(w_landed[s], 16)
                            sp.dma_start(w1s[s][:], w1[one].rearrange("a (k p) f -> (a p) k f", p=P)).then_inc(w_landed[s], 16)
                            sp.dma_start(b1s[s][:], b1[one].rearrange("a (k p) -> (a p) k", p=P),
                                         allow_slow_non_contiguous=True).then_inc(w_landed[s], 16)
                            sp.dma_start(b2s[s][:], b2[one]).then_inc(w_landed[s], 16)
                            sp.dma_start(w2s[s][:], w2[one].rearrange("a (k p) f -> (a p) k f", p=P)).then_inc(w_landed[s], 16)

                @block.tensor
                def _(pe):
                    with pe.Fori(0, EX // 2) as i:
                        for s in range(2):
                            pe.wait_ge(w_landed[s], i * 80 + 80)
                            pe.wait_ge(turn_copied, i * 2 + s)
                            for r in range(4):
                                for c in range(2):
                                    last = pe.transpose(turn_ps[:, c, r * P:(r + 1) * P], xs[s][:, r, c * P:(c + 1) * P],
                                                        S.ident[:])
                            last.then_inc(turned, 1)
                            pe.wait_ge(turn_copied, i * 2 + s + 1)
                            for o in range(FC):
                                if o >= 2:
                                    pe.wait_ge(hid_done, i * (2 * FC) + s * FC + o - 1)
                                else:
                                    pe.wait_ge(hid_done, i * (2 * FC) + s * FC)
                                for c in range(2):
                                    last = pe.matmul(hid_ps[:, o % 2, :], w1s[s][:, c, o * P:(o + 1) * P], xt[:, c, :],
                                                     start=(c == 0), stop=(c == 1))
                                last.then_inc(hid_mm, 1)
                            pe.wait_ge(hid_done, i * (2 * FC) + (s + 1) * FC)
                            pe.wait_ge(out_copied, i * 2 + s)
                            for r in range(4):
                                for o in range(FC):
                                    pe.matmul(out_ps[:, r, 0:D], hid[:, o, r * P:(r + 1) * P], w2s[s][:, o, :],
                                              start=(o == 0), stop=False)
                                pe.matmul(out_ps[:, r, 0:D], S.ones[0:1, :], b2s[s][:], start=False, stop=True
                                          ).then_inc(out_mm[s], 1)

                @block.scalar
                def _(act):
                    with act.Fori(0, EX // 2) as i:
                        for s in range(2):
                            for o in range(FC):
                                act.wait_ge(hid_mm, i * (2 * FC) + s * FC + o + 1)
                                act.wait_ge(out_mm[1 - s], (i + s) * 4)
                                nc.scalar.activation(hid[:, o, :], hid_ps[:, o % 2, :], ACT.Relu,
                                                     bias=b1s[s][:, o:o + 1]).then_inc(hid_done, 1)

                @block.vector
                def _(dve):
                    with dve.Fori(0, EX // 2) as i:
                        for s in range(2):
                            dve.wait_ge(turned, i * 2 + s + 1)
                            dve.wait_ge(hid_mm, i * (2 * FC) + s * FC)
                            dve.tensor_copy(xt[:], turn_ps[:]).then_inc(turn_copied, 1)
                            dve.wait_ge(out_mm[s], i * 4 + 4)
                            dve.wait_ge(stored[s], i * 16)
                            dve.tensor_copy(out[s][:], out_ps[:, :, 0:D]).then_inc(out_copied, 1)

                @block.gpsimd
                def _(pool):
                    with pool.Fori(0, EX // 2) as i:
                        for s in range(2):
                            pool.wait_ge(out_copied, i * 2 + s + 1)
                            pool.sem_inc(pool_go, 1)
                            pool.dma_start(ybuf[bass.ds((i * 2 + s) * SLOTS, SLOTS), :].rearrange(
                                "(r p) d -> p r d", p=P), out[s][:]).then_inc(stored[s], 16)
                    for s in range(2):
                        pool.wait_ge(stored[s], 16 * (EX // 2))

        with stage(nc, "mog_") as b:
            y = [b.sb(f"y{s}", [TP, D]) for s in range(2)]
            at = [b.sb(f"at{s}", [TP, 1], I32) for s in range(2)]
            z, mask = b.sb("z", [TP, D]), b.sb("mask", [TP, 3, D], I32)
            limit = b.sb("limit", [TP, 2, D])
            limits, indexed, weighted, masked, replaced, y_used, pool_go, dve_go = (
                b.sem(n) for n in ("limits", "indexed", "weighted", "masked", "replaced", "y_used", "pool_go", "dve_go"))
            landed = b.borrow(S.pool_dma[0:2])
            with nc.Block() as block:
                @block.scalar
                def _(act):
                    with act.Fori(0, NG) as i:
                        for u in range(GROUP):
                            act.wait_ge(y_used, freed(i, u, 2))
                            nc.scalar.copy(at[u % 2][:], col(row_out, i * GROUP + u)).then_inc(indexed, 1)

                @block.gpsimd
                def _(pool):
                    with pool.Fori(0, NG) as i:
                        for u in range(GROUP):
                            s = u % 2
                            pool.wait_ge(indexed, ready(i, u))
                            pool.sem_inc(pool_go, 1)
                            pool.indirect_dma_start(y[s][:], None, ybuf, bass.IndirectOffsetOnAxis(ap=at[s][:, 0:1], axis=0)
                                                    ).then_inc(landed[s], 16)

                @block.vector
                def _(dve):
                    dve.memset(limit[:, 0], 1e4).then_inc(limits, 1)
                    dve.memset(limit[:, 1], -1e4).then_inc(limits, 1)
                    dve.wait_ge(limits, 2)
                    with dve.Fori(0, NG) as i:
                        for u in range(GROUP):
                            t, s = i * GROUP + u, u % 2
                            dve.memset(z[:], 0.0).then_inc(replaced, 1)
                            dve.wait_ge(landed[s], (slot_uses(i, u) + 1) * 16)
                            after(dve, dve.tensor_scalar(y[s][:], y[s][:], col(weight, t), None, ALU.mult),
                                  weighted, i * GROUP + u + 1)
                            dve.tensor_tensor(mask[:, 0], y[s][:], y[s][:], ALU.is_equal).then_inc(masked, 1)
                            dve.tensor_scalar(mask[:, 1], y[s][:], FLT_MAX, None, ALU.is_gt).then_inc(masked, 1)
                            dve.tensor_scalar(mask[:, 2], y[s][:], -FLT_MAX, None, ALU.is_lt).then_inc(masked, 1)
                            dve.wait_ge(masked, i * (3 * GROUP) + 3 * u + 3)
                            base = i * (4 * GROUP) + 4 * u
                            for n, value in enumerate((y[s][:], limit[:, 0], limit[:, 1])):
                                dve.wait_ge(replaced, base + n + 1)
                                dve.sem_inc(dve_go, 1)
                                dve.copy_predicated(z[:], mask[:, n], value).then_inc(replaced, 1)
                            dve.wait_ge(replaced, base + 4)
                            after(dve, dve.tensor_tensor(tile(S.x, t), tile(S.x, t), z[:], ALU.add),
                                  y_used, i * GROUP + u + 1)


class AttentionWeights:
    pass


def attention_sums(nc, S, a, Wg, Wq, bq, Wk, bk, Wv, bv, Wo, bo):
    S.support = nc.dram_tensor("support", [N, D], F32, kind="Internal").ap()
    wg, wq, wo = (a.sb(n, [P, 2, D]) for n in ("wg", "wq", "wo"))
    wkv, bkv = a.sb("wkv", [P, 2, 2, D]), a.sb("bkv", [1, 2 * D])
    bqc, bor = a.sb("bqc", [P, 2]), a.sb("bor", [1, D])
    group_ones = a.sb("group_ones", [P, P])
    kv_block, k_block = a.sb("kv_block", [P, 2, P]), a.sb("k_block", [P, 2, P])
    loaded = a.sem("loaded")

    with stage(nc, "lak_") as b:
        xn = [b.sb(f"xn{s}", [TP, D]) for s in range(2)]
        xt = [b.sb(f"xt{s}", [P, 2, TP]) for s in range(2)]
        low = b.sb("low", [TP, D])
        kp = [b.sb(f"kp{s}", [TP, D]) for s in range(2)]
        v = [b.sb(f"v{s}", [TP, 2, P + 1]) for s in range(2)]
        sup = [b.sb(f"sup{s}", [TP, D]) for s in range(2)]
        ksum = b.sb("ksum", [P, 2])
        turn_ps, kv_ps, sup_ps = b.ps("turn", [P, 512]), b.ps("kv", [TP, 2, 512]), b.ps("sup_ps", [TP, 512])
        sum_ps = b.ps("sum", [P, 2, 512])
        (normed, turned, turn_copied, kv_mm, low_made, exped, k_made, v_made, sup_mm, sup_copied, summed, init,
         step_s) = (b.sem(n) for n in ("normed", "turned", "turn_copied", "kv_mm", "low_made", "exped", "k_made",
                                       "v_made", "sup_mm", "sup_copied", "summed", "init", "step"))
        stored = [b.sem(f"stored{s}") for s in range(2)]
        with nc.Block() as block:
            @block.sync
            def _(sp):
                for to, of in ((wg, Wg), (wq, Wq), (wo, Wo)):
                    sp.dma_start(to[:], of.rearrange("(k p) c -> p k c", p=P)).then_inc(loaded, 16)
                for n, (w, bias) in enumerate(((Wk, bk), (Wv, bv))):
                    sp.dma_start(wkv[:, :, n, :], w.rearrange("(k p) c -> p k c", p=P)).then_inc(loaded, 16)
                    sp.dma_start(bkv[0:1, n * D:(n + 1) * D], row_of(bias)).then_inc(loaded, 16)
                sp.dma_start(bqc[:], bq.rearrange("(k p) -> p k", p=P),
                             allow_slow_non_contiguous=True).then_inc(loaded, 16)
                sp.dma_start(bor[:], row_of(bo)).then_inc(loaded, 16)
                with sp.Fori(0, NG) as i:
                    for u in range(GROUP):
                        sp.wait_ge(sup_copied, ready(i, u))
                        sp.dma_start(S.support[bass.ds((i * GROUP + u) * TP, TP), :], sup[u % 2][:]
                                     ).then_inc(stored[u % 2], 16)
                for s in range(2):
                    sp.wait_ge(stored[s], 16 * NG * (3 - s))

            @block.vector
            def _(dve):
                st = Steps(dve, step_s)
                st(dve.memset(group_ones[:], 0.0))
                for q in range(4):
                    dve.memset(group_ones[32 * q:32 * q + 32, 32 * q:32 * q + 32], 1.0)
                for s in range(2):
                    dve.memset(v[s][:, :, P:P + 1], 1.0).then_inc(init, 1)
                dve.wait_ge(init, 2)
                with dve.Fori(0, NG) as i:
                    for u in range(GROUP):
                        t, s = i * GROUP + u, u % 2
                        dve.wait_ge(turned, freed(i, u, 2))
                        dve.tensor_scalar(xn[s][:], tile(S.x, t), col(S.ln_r, t), col(S.ln_b, t), ALU.mult,
                                          ALU.add).then_inc(normed, 1)
                        dve.wait_ge(kv_mm, ready(i, u))
                        dve.wait_ge(exped, freed(i, u, 1))
                        dve.tensor_scalar(low[:], kv_ps[:, 0, 0:D], 0.0, None, ALU.min).then_inc(low_made, 1)
                        dve.wait_ge(summed, freed(i, u, 2))
                        dve.tensor_copy(v[s][:, :, 0:P], kv_ps[:, 1, 0:D].rearrange("p (c e) -> p c e", c=2)
                                        ).then_inc(v_made, 1)
                        dve.wait_ge(exped, ready(i, u))
                        dve.scalar_tensor_tensor(kp[s][:], kv_ps[:, 0, 0:D], 0.0, low[:], ALU.max,
                                                 ALU.add).then_inc(k_made, 1)
                dve.wait_ge(summed, NT + 1)
                for c in range(2):
                    dve.tensor_tensor(kv_block[:, c, :], sum_ps[:, c, 0:P], group_ones[:], ALU.mult)
                    st(dve.tensor_copy(ksum[:, c:c + 1], sum_ps[:, c, P:P + 1]))
                    dve.tensor_scalar(k_block[:, c, :], group_ones[:], ksum[:, c:c + 1], None, ALU.mult)

            @block.scalar
            def _(act):
                with act.Fori(0, NG) as i:
                    for u in range(GROUP):
                        s = u % 2
                        act.wait_ge(turned, ready(i, u))
                        act.wait_ge(sup_mm, freed(i, u, 2))
                        nc.scalar.copy(xt[s][:], turn_ps[:, 0:2 * TP].rearrange("p (k n) -> p k n", k=2)
                                       ).then_inc(turn_copied, 1)
                        act.wait_ge(low_made, ready(i, u))
                        act.wait_ge(k_made, freed(i, u, 1))
                        nc.scalar.activation(low[:], low[:], ACT.Exp).then_inc(exped, 1)
                        act.wait_ge(sup_mm, ready(i, u))
                        act.wait_ge(stored[s], slot_uses(i, u) * 16)
                        nc.scalar.copy(sup[s][:], sup_ps[:, 0:D]).then_inc(sup_copied, 1)

            @block.tensor
            def _(pe):
                pe.wait_ge(loaded, 16 * 9)
                for c in range(2):
                    pe.matmul(sum_ps[:, c, 0:P + 1], S.zeros[:, 0:P], S.zeros[:, 0:P + 1], start=True, stop=False)
                with pe.Fori(0, NG) as i:
                    for u in range(GROUP):
                        s = u % 2
                        pe.wait_ge(normed, ready(i, u))
                        pe.wait_ge(turn_copied, freed(i, u, 1))
                        for c in range(2):
                            last = pe.transpose(turn_ps[:, c * TP:(c + 1) * TP], xn[s][:, c * P:(c + 1) * P],
                                                S.ident[0:TP, 0:TP])
                        last.then_inc(turned, 1)
                        pe.wait_ge(turn_copied, ready(i, u))
                        pe.wait_ge(k_made, freed(i, u, 1))
                        pe.wait_ge(v_made, freed(i, u, 1))
                        for n in range(2):
                            for c in range(2):
                                pe.matmul(kv_ps[:, n, 0:D], xt[s][:, c, :], wkv[:, c, n, :], start=(c == 0), stop=False)
                            last = pe.matmul(kv_ps[:, n, 0:D], S.ones[0:1, 0:TP], bkv[:, n * D:(n + 1) * D],
                                             start=False, stop=True)
                        last.then_inc(kv_mm, 1)
                        pe.wait_ge(sup_copied, freed(i, u, 1))
                        for c in range(2):
                            last = pe.matmul(sup_ps[:, 0:D], xt[s][:, c, :], wg[:, c, :], start=(c == 0), stop=(c == 1))
                        last.then_inc(sup_mm, 1)
                        pe.wait_ge(k_made, ready(i, u))
                        pe.wait_ge(v_made, ready(i, u))
                        for c in range(2):
                            last = pe.matmul(sum_ps[:, c, 0:P + 1], kp[s][:, c * P:(c + 1) * P], v[s][:, c, :],
                                             start=False, stop=False)
                        last.then_inc(summed, 1)
                for c in range(2):
                    last = pe.matmul(sum_ps[:, c, 0:P + 1], S.zeros[:, 0:P], S.zeros[:, 0:P + 1], start=False, stop=True)
                last.then_inc(summed, 1)

    L = AttentionWeights()
    L.wq, L.wo, L.bqc, L.bor, L.kv_block, L.k_block = wq, wo, bqc, bor, kv_block, k_block
    return L


def attention_queries(nc, S, L):
    def make(a):
        xn, xt = a.sb("la_xn", [TP, D]), a.sb("la_xt", [P, 2, TP])
        low, high, qp, rz, o = (a.sb("la_" + n, [P, 2, TP]) for n in ("low", "high", "qp", "rz", "o"))
        turn_ps, q_ps, o_ps, att_ps = (a.ps("la_turn", [P, 512]), a.ps("la_q", [P, 512]), a.ps("la_o_ps", [P, 512]),
                                       a.ps("la_att", [TP, 512]))
        normed, turned, turn_copied, q_mm, low_made, exped, q_made, o_mm, dstep, o_made, att_mm, att_added = (
            a.sem("la_" + n) for n in ("normed", "turned", "turn_copied", "q_mm", "low_made", "exped", "q_made", "o_mm",
                                       "dstep", "o_made", "att_mm", "att_added"))

        def vector(dve, i, part):
            if part == 0:
                dve.wait_ge(att_added, i)
                dve.tensor_scalar(xn[:], tile(S.x, i), col(S.ln_r, i), col(S.ln_b, i), ALU.mult,
                                  ALU.add).then_inc(normed, 1)
            if part == 1:
                dve.wait_ge(q_mm, i + 1)
                for c in range(2):
                    dve.tensor_scalar(low[:, c], q_ps[:, c * TP:(c + 1) * TP], L.bqc[:, c:c + 1], 0.0, ALU.add,
                                      ALU.min).then_inc(low_made, 1)
                    dve.tensor_scalar(high[:, c], q_ps[:, c * TP:(c + 1) * TP], L.bqc[:, c:c + 1], 0.0, ALU.add,
                                      ALU.max).then_inc(low_made, 1)
            if part == 2:
                dve.wait_ge(exped, i + 1)
                dve.tensor_tensor(qp[:], high[:], low[:], ALU.add).then_inc(q_made, 1)
                dve.wait_ge(o_mm, i + 1)
                after(dve, dve.tensor_scalar(rz[:].rearrange("p c n -> p (c n)"), o_ps[:, 2 * TP:4 * TP], 1e-6,
                                             None, ALU.add), dstep, i * 2 + 1)
                after(dve, dve.reciprocal(rz[:], rz[:]), dstep, i * 2 + 2)
                dve.tensor_tensor(o[:].rearrange("p c n -> p (c n)"), o_ps[:, 0:2 * TP],
                                  rz[:].rearrange("p c n -> p (c n)"), ALU.mult).then_inc(o_made, 1)
            if part == 3:
                dve.wait_ge(att_mm, i + 1)
                dve.tensor_tensor(tile(S.y, i), att_ps[:, 0:D], xn[:], ALU.add).then_inc(att_added, 1)

        def scalar(act, i, part):
            if part == 0:
                act.wait_ge(turned, i + 1)
                nc.scalar.copy(xt[:], turn_ps[:, 0:2 * TP].rearrange("p (k n) -> p k n", k=2)).then_inc(turn_copied, 1)
            if part == 1:
                act.wait_ge(low_made, i * 4 + 4)
                nc.scalar.activation(low[:], low[:], ACT.Exp).then_inc(exped, 1)

        def tensor(pe, i, part):
            if part == 0:
                pe.wait_ge(normed, i + 1)
                for c in range(2):
                    last = pe.transpose(turn_ps[:, c * TP:(c + 1) * TP], xn[:, c * P:(c + 1) * P],
                                        S.ident[0:TP, 0:TP])
                last.then_inc(turned, 1)
                pe.wait_ge(turn_copied, i + 1)
                for o_ in range(2):
                    for c in range(2):
                        last = pe.matmul(q_ps[:, o_ * TP:(o_ + 1) * TP], L.wq[:, c, o_ * P:(o_ + 1) * P],
                                         xt[:, c, :], start=(c == 0), stop=(c == 1))
                last.then_inc(q_mm, 1)
            if part == 2:
                pe.wait_ge(q_made, i + 1)
                for n, w in enumerate((L.kv_block, L.k_block)):
                    for c in range(2):
                        at = (2 * n + c) * TP
                        last = pe.matmul(o_ps[:, at:at + TP], w[:, c, :], qp[:, c, :], start=True, stop=True)
                last.then_inc(o_mm, 1)
            if part == 3:
                pe.wait_ge(o_made, i + 1)
                for c in range(2):
                    pe.matmul(att_ps[:, 0:D], o[:, c, :], L.wo[:, c, :], start=(c == 0), stop=False)
                pe.matmul(att_ps[:, 0:D], S.ones[0:1, 0:TP], L.bor[:], start=False, stop=True).then_inc(att_mm, 1)

        return scalar, vector, tensor
    return make


def feed_forward(nc, S, tag, src, gamma, beta, w1, b1, w2, b2, func, out=None, coef=None):
    FC = FF // P
    with stage(nc, tag) as a:
        w1s, w2s = a.sb("w1", [P, 2, FF]), a.sb("w2", [P, FC, D])
        b1s, b2s = a.sb("b1", [P, FC]), a.sb("b2", [1, D])
        xa = [a.sb(f"xa{s}", [TP, D]) for s in range(GROUP)]
        xt = [a.sb(f"xt{s}", [P, 2, TP]) for s in range(2)]
        hid = [a.sb(f"hid{s}", [P, FC, TP]) for s in range(2)]
        res = [a.sb(f"res{s}", [TP, D]) for s in range(2)]
        turn_ps, hid_ps, f_ps = a.ps("turn", [P, 512]), a.ps("hid_ps", [P, 2, 2, 512]), a.ps("f_ps", [TP, 2, 512])
        loaded, normed, dstep, turned, turn_copied, hid_mm, hid_done, f_mm, f_used, base_made = (
            a.sem(n) for n in ("loaded", "normed", "dstep", "turned", "turn_copied", "hid_mm", "hid_done", "f_mm",
                               "f_used", "base_made"))
        stored = [a.sem(f"stored{s}") for s in range(2)]
        affine = gamma is not None
        if affine:
            ga, be = a.sb("ga", [TP, D]), a.sb("be", [TP, D])
        LOADS = 16 * (6 if affine else 4)
        with nc.Block() as block:
            @block.sync
            def _(sp):
                sp.dma_start(w1s[:], w1.rearrange("(k p) f -> p k f", p=P)).then_inc(loaded, 16)
                sp.dma_start(w2s[:], w2.rearrange("(k p) f -> p k f", p=P)).then_inc(loaded, 16)
                sp.dma_start(b1s[:], b1.rearrange("(k p) -> p k", p=P), allow_slow_non_contiguous=True).then_inc(loaded, 16)
                sp.dma_start(b2s[:], row_of(b2)).then_inc(loaded, 16)
                if affine:
                    sp.dma_start(ga[:], spread(gamma, TP)).then_inc(loaded, 16)
                    sp.dma_start(be[:], spread(beta, TP)).then_inc(loaded, 16)
                if out is not None:
                    with sp.Fori(0, NG) as i:
                        for u in range(GROUP):
                            sp.wait_ge(f_used, ready(i, u))
                            sp.dma_start(out[bass.ds((i * GROUP + u) * TP, TP), :], res[u % 2][:]).then_inc(stored[u % 2], 16)
                    for s in range(2):
                        sp.wait_ge(stored[s], 16 * NG * (3 - s))

            @block.vector
            def _(dve):
                dve.wait_ge(loaded, LOADS)

                def norm(i, u):
                    t, x = i * GROUP + u, xa[u]
                    dve.wait_ge(turned, freed(i, u, GROUP))
                    dve.wait_ge(f_used, freed(i, u, GROUP))
                    ins = dve.tensor_scalar(x[:], tile(src, t), col(S.ln_r, t), col(S.ln_b, t), ALU.mult, ALU.add)
                    if affine:
                        base = i * (2 * GROUP) + 2 * u
                        after(dve, ins, dstep, base + 1)
                        after(dve, dve.tensor_tensor(x[:], x[:], ga[:], ALU.mult), dstep, base + 2)
                        ins = dve.tensor_tensor(x[:], x[:], be[:], ALU.add)
                    ins.then_inc(normed, 1)

                def add(i, u):
                    t, s = i * GROUP + u, u % 2
                    dve.wait_ge(normed, ready(i, u))
                    if out is None:
                        dve.wait_ge(f_mm, ready(i, u))
                        dve.tensor_tensor(tile(S.y, t), f_ps[:, s, 0:D], xa[u][:], ALU.add).then_inc(f_used, 1)
                    else:
                        dve.wait_ge(stored[s], slot_uses(i, u) * 16)
                        dve.tensor_tensor(res[s][:], xa[u][:], tile(src, t), ALU.add).then_inc(base_made, 1)
                        dve.wait_ge(f_mm, ready(i, u))
                        dve.wait_ge(base_made, ready(i, u))
                        dve.scalar_tensor_tensor(res[s][:], f_ps[:, s, 0:D], col(coef, t), res[s][:], ALU.mult,
                                                 ALU.add).then_inc(f_used, 1)

                with dve.Fori(0, NG) as i:
                    stagger(i, norm, nothing, add)

            @block.scalar
            def _(act):
                def copy(i, u):
                    act.wait_ge(turned, ready(i, u))
                    act.wait_ge(hid_mm, freed(i, u, 2))
                    nc.scalar.copy(xt[u % 2][:], turn_ps[:, 0:2 * TP].rearrange("p (k n) -> p k n", k=2)
                                   ).then_inc(turn_copied, 1)

                def hide(i, u):
                    s = u % 2
                    act.wait_ge(hid_mm, ready(i, u))
                    act.wait_ge(f_mm, freed(i, u, 2))
                    for o in range(FC):
                        nc.scalar.activation(hid[s][:, o, :], hid_ps[:, s, o // 4, (o % 4) * TP:(o % 4 + 1) * TP], func,
                                             bias=b1s[:, o:o + 1]).then_inc(hid_done, 1)

                with act.Fori(0, NG) as i:
                    stagger(i, copy, hide)

            @block.tensor
            def _(pe):
                def turn(i, u):
                    pe.wait_ge(normed, ready(i, u))
                    pe.wait_ge(turn_copied, freed(i, u, 1))
                    for c in range(2):
                        last = pe.transpose(turn_ps[:, c * TP:(c + 1) * TP], xa[u][:, c * P:(c + 1) * P],
                                            S.ident[0:TP, 0:TP])
                    last.then_inc(turned, 1)

                def hide(i, u):
                    s = u % 2
                    pe.wait_ge(turn_copied, ready(i, u))
                    pe.wait_ge(hid_done, i * (FC * GROUP) + FC * max(u - 1, 0))
                    for o in range(FC):
                        for c in range(2):
                            last = pe.matmul(hid_ps[:, s, o // 4, (o % 4) * TP:(o % 4 + 1) * TP],
                                             w1s[:, c, o * P:(o + 1) * P], xt[s][:, c, :], start=(c == 0), stop=(c == 1))
                    last.then_inc(hid_mm, 1)

                def project(i, u):
                    s = u % 2
                    pe.wait_ge(hid_done, i * (FC * GROUP) + FC * (u + 1))
                    pe.wait_ge(f_used, freed(i, u, 2))
                    for o in range(FC):
                        pe.matmul(f_ps[:, s, 0:D], hid[s][:, o, :], w2s[:, o, :], start=(o == 0), stop=False)
                    pe.matmul(f_ps[:, s, 0:D], S.ones[0:1, 0:TP], b2s[:], start=False, stop=True).then_inc(f_mm, 1)

                pe.wait_ge(loaded, LOADS)
                with pe.Fori(0, NG) as i:
                    stagger(i, turn, hide, project)


def add_l1(nc, S, gamma, beta, bias):
    with stage(nc, "c1_") as a:
        ga, be, bi = (a.sb(n, [TP, D]) for n in ("ga", "be", "bi"))
        rows = [a.sb(f"rows{s}", [TP, 4, D]) for s in range(2)]
        t0 = a.sb("t0", [TP, D])
        loaded, step_s, used = a.sem("loaded"), a.sem("step"), a.sem("used")
        landed = [a.sem(f"landed{s}") for s in range(2)]
        with nc.Block() as block:
            @block.sync
            def _(sp):
                for to, of in ((ga, gamma), (be, beta), (bi, bias)):
                    sp.dma_start(to[:], spread(of, TP)).then_inc(loaded, 16)
                with sp.Fori(0, NG) as i:
                    for u in range(GROUP):
                        sp.wait_ge(used, freed(i, u, 2))
                        for n in range(4):
                            sp.dma_start(rows[u % 2][:, n, :], S.acc[n][bass.ds((i * GROUP + u) * TP, TP), :]
                                         ).then_inc(landed[u % 2], 16)

            @block.vector
            def _(dve):
                dve.wait_ge(loaded, 48)
                after(dve, dve.tensor_tensor(be[:], be[:], bi[:], ALU.add), step_s, 1)
                with dve.Fori(0, NG) as i:
                    for u in range(GROUP):
                        t, s = i * GROUP + u, u % 2
                        base = i * (6 * GROUP) + 6 * u + 1
                        dve.tensor_scalar(t0[:], tile(S.y, t), col(S.ln_r, t), col(S.ln_b, t), ALU.mult,
                                          ALU.add).then_inc(step_s, 1)
                        dve.wait_ge(landed[s], (slot_uses(i, u) + 1) * 64)
                        dve.tensor_tensor(rows[s][:, 0:2], rows[s][:, 0:2], rows[s][:, 2:4], ALU.add).then_inc(step_s, 1)
                        dve.wait_ge(step_s, base + 2)
                        dve.tensor_tensor(t0[:], t0[:], ga[:], ALU.mult).then_inc(step_s, 1)
                        dve.tensor_tensor(rows[s][:, 0], rows[s][:, 0], rows[s][:, 1], ALU.add).then_inc(step_s, 1)
                        dve.wait_ge(step_s, base + 4)
                        dve.tensor_tensor(t0[:], t0[:], be[:], ALU.add).then_inc(step_s, 1)
                        dve.tensor_tensor(tile(S.x, t), tile(S.x, t), rows[s][:, 0], ALU.add).then_inc(step_s, 1)
                        dve.wait_ge(step_s, base + 6)
                        dve.tensor_tensor(tile(S.x, t), tile(S.x, t), t0[:], ALU.add).then_inc(used, 1)
                        dve.wait_ge(used, ready(i, u))


KEEP = int(0.5 * N) - 1


def depth_weights(nc, S, wr, br):
    w_dram = nc.dram_tensor("depth_weights", [N], F32, kind="Internal").ap()
    with stage(nc, "dw_") as a:
        wrr, brr = a.sb("wrr", [TP, D]), a.sb("brr", [TP, 1])
        xl, junk = a.sb("xl", [TP, D]), a.sb("junk", [TP, D])
        w, rank = a.sb("weight", [TP, NT]), a.sb("rank", [TP, 4, NT])
        w_rows, big = a.sb("w_rows", [TP, N]), a.sb("big", [TP, N])
        earlier, w_group = a.sb("earlier", [TP, TP]), a.sb("w_group", [TP, GROUP])
        grouped = a.sem("grouped")
        loaded, normed, multiplied, step_s, done, spread_in = (
            a.sem(n) for n in ("loaded", "normed", "multiplied", "step", "done", "spread_in"))
        with nc.Block() as block:
            @block.sync
            def _(sp):
                sp.dma_start(wrr[:], spread(wr.rearrange("d o -> (d o)"), TP)).then_inc(loaded, 16)
                sp.dma_start(brr[:], spread(br, TP)).then_inc(loaded, 16)
                sp.wait_ge(done, 1)
                sp.dma_start(w_dram.rearrange("(t p) -> p t", p=TP), w[:],
                             allow_slow_non_contiguous=True).then_inc(spread_in, 16)
                sp.wait_ge(spread_in, 16)
                sp.dma_start(w_rows[:], spread(w_dram, TP)).then_inc(spread_in, 16)

            @block.vector
            def _(dve):
                dve.wait_ge(loaded, 32)
                with dve.Fori(0, NG) as i:
                    for u in range(GROUP):
                        t = i * GROUP + u
                        after(dve, dve.tensor_scalar(xl[:], tile(S.x, t), col(S.ln_r, t), col(S.ln_b, t), ALU.mult,
                                                     ALU.add), normed, ready(i, u))
                        after(dve, dve.tensor_tensor_reduce(junk[:], xl[:], wrr[:], 1.0, 0.0, ALU.mult, ALU.add,
                                                            w_group[:, u:u + 1]), multiplied, ready(i, u))
                    after(dve, dve.tensor_copy(w[:, bass.ds(i * GROUP, GROUP)], w_group[:]), grouped, i + 1)
                st = Steps(dve, step_s)
                dve.tensor_scalar(w[:], w[:], brr[:, 0:1], None, ALU.add).then_inc(done, 1)
                st(dve.tensor_scalar(earlier[:], S.iota_row[0:TP, 0:TP], S.part_col[0:TP, 0:1], None, ALU.is_lt))
                st(dve.memset(rank[:], 0.0))
                dve.wait_ge(done, 1)
                dve.wait_ge(spread_in, 32)
                for t in range(NT):
                    lo, hi = t * TP, (t + 1) * TP
                    me = w[:, t:t + 1]
                    if lo:
                        st(dve.tensor_scalar(big[:, 0:lo], w_rows[:, 0:lo], me, None, ALU.is_ge, ALU.add,
                                             accum_out=rank[:, 0, t:t + 1]))
                    st(dve.tensor_scalar(big[:, lo:N], w_rows[:, lo:N], me, None, ALU.is_gt, ALU.add,
                                         accum_out=rank[:, 1, t:t + 1]))
                    st(dve.scalar_tensor_tensor(big[:, lo:hi], w_rows[:, lo:hi], me, earlier[:], ALU.is_equal, ALU.mult,
                                                accum_out=rank[:, 2, t:t + 1]))
                st(dve.tensor_tensor(rank[:, 0], rank[:, 0], rank[:, 1], ALU.add))
                st(dve.tensor_tensor(rank[:, 0], rank[:, 0], rank[:, 2], ALU.add))
                st(dve.tensor_scalar(rank[:, 0], rank[:, 0], float(KEEP), None, ALU.is_lt))
                dve.tensor_tensor(S.coef[:], rank[:, 0], w[:], ALU.mult)


def network(nc, A, out):
    with ExitStack() as ctx:
        g = Alloc(nc, ctx)
        S = Shared()
        constants(nc, g, S)
        load_nodes(nc, g, S, A["x"])
        layernorm_stats(nc, S, "l0_", S.x)
        edges(nc, g, S, A["src"], A["dst"], A["edge_type_2"], A["edge_weight"])
        row_starts(nc, g, S)
        gnn0(nc, g, S, A)
        layernorm_stats(nc, S, "l1_", S.x)
        moe(nc, S, A["L0_ffn_gate_w"], A["L0_ffn_gate_b"], A["L0_ffn_w1"], A["L0_ffn_b1"], A["L0_ffn_w2"], A["L0_ffn_b2"])
        layer1(nc, g, S, A, out)


def layer1(nc, g, S, A, out):
    S.y = g.sb("y", [TP, NT, D])
    S.coef = g.sb("coef", [TP, NT])
    layernorm_stats(nc, S, "l2_", S.x)
    M = {k[len("L1_mix_"):]: v for k, v in A.items() if k.startswith("L1_mix_")}
    with stage(nc, "la_") as a:
        L = attention_sums(nc, S, a, A["L1_gnn_weight"], M["Wq"], M["bq"], M["Wk"], M["bk"], M["Wv"], M["bv"], M["Wo"],
                           M["bo"])
        edge_sums(nc, S, "a4_", S.support, D, S.ew_c[:].unsqueeze(2), 1, S.node_dst, S.src_c, S.src_pad, S.row_rep,
                  S.acc, True, guest=attention_queries(nc, S, L))
    layernorm_stats(nc, S, "l3_", S.y)
    feed_forward(nc, S, "f1_", S.y, M["ln1_g"], M["ln1_b"], M["W1"], M["b1"], M["W2"], M["b2"], ACT.Relu)
    layernorm_stats(nc, S, "l4_", S.y)
    add_l1(nc, S, M["ln2_g"], M["ln2_b"], A["L1_gnn_bias"])
    layernorm_stats(nc, S, "l5_", S.x)
    depth_weights(nc, S, A["L1_ffn_wr"], A["L1_ffn_br"])
    feed_forward(nc, S, "f2_", S.x, None, None, A["L1_ffn_w1"], A["L1_ffn_b1"], A["L1_ffn_w2"], A["L1_ffn_b2"],
                 ACT.Gelu_apprx_tanh, out=out, coef=S.coef)


def lay_out(inputs):
    import numpy as np

    a = {k: np.ascontiguousarray(v) for k, v in inputs.items()}
    perm = np.arange(768).reshape(8, 3, 32).transpose(1, 0, 2).reshape(-1)
    a["conv_w"] = np.ascontiguousarray(a["L0_mix_w_qkv"][perm, :, 2].T)
    a["bn_gamma"] = np.ascontiguousarray(a["L0_mix_bn_gamma"][perm])
    a["bn_beta"] = np.ascontiguousarray(a["L0_mix_bn_beta"][perm])
    a["dw_w"] = np.ascontiguousarray(a["L0_mix_w_dw"][perm, 0, 2])
    a["pw_w"] = np.ascontiguousarray(a["L0_mix_w_pw"][perm, :, 0].reshape(6, 4, 32, 32).transpose(1, 3, 0, 2))
    a["res_w"] = np.ascontiguousarray(a["L0_mix_w_res"][:, :, 0].T)
    for layer in (1, 2, 3):
        a[f"W{layer}"] = a[f"L0_gnn_W{layer}"]
        a[f"W{layer}_T"] = np.ascontiguousarray(a[f"L0_gnn_W{layer}"].transpose(0, 2, 1))
    for name in ("L0_mix_w_qkv", "L0_mix_bn_gamma", "L0_mix_bn_beta", "L0_mix_w_dw", "L0_mix_w_pw", "L0_mix_w_res",
                 "L0_gnn_W1", "L0_gnn_W2", "L0_gnn_W3", "L1_ffn_attention_mask"):
        del a[name]
    return a


def kernel(**inputs):
    import concourse.bacc as bacc
    from concourse.bass_utils import run_bass_kernel_spmd

    nc = bacc.Bacc("TRN2", target_bir_lowering=False, num_devices=1)
    arrays = lay_out(inputs)
    A = {k: nc.dram_tensor(f"in_{k}", v.shape, mybir.dt.from_np(v.dtype), kind="ExternalInput").ap()
         for k, v in arrays.items()}
    out = nc.dram_tensor("out_0", (N, D), F32, kind="ExternalOutput").ap()
    network(nc, A, out)
    r = run_bass_kernel_spmd(nc, [{f"in_{k}": v for k, v in arrays.items()}], core_ids=[0])
    return r.results[0]["out_0"]
```

```python
from contextlib import ExitStack, contextmanager

import concourse.bass as bass
from concourse import mybir

F32 = mybir.dt.float32
I32 = mybir.dt.int32
ALU = mybir.AluOpType
ACT = mybir.ActivationFunctionType
AX = mybir.AxisListType

N = 3125
D = 256
E = 53125
P = 128
TP = 125
NT = N // TP
GROUP = 5
NG = NT // GROUP
PIPE = 4
CH = 416
CK = 104
KB = CH // CK
EP = CH * P
PAD_NODE = N
QUAD = 4
QUADS = CH // QUAD
VISITS = QUADS + NT - 1
SKIP = 1 << 17
HEADS = 4
HID = 128
BIG = 1.0e30
MAXNORM = 0.9999899864196777
ATANH_MAX = 6.102495471
MIN_NORM = 1e-15
SLOPE = 0.2


def ready(i, u, group=GROUP):
    return group * i + u + 1


def freed(i, u, depth, group=GROUP):
    return group * i + max(u + 1 - depth, 0)


def pipeline(engine, *phases, lag=0):
    lag = max(lag, *(behind for behind, _ in phases))
    loops = (NT - lag) // PIPE

    def step(i, u):
        for behind, phase in phases:
            if not isinstance(i, int) or 0 <= i * PIPE + u - behind < NT:
                phase(i, u - behind)

    for u in range(lag):
        step(0, u)
    with engine.Fori(0, loops) as i:
        for u in range(PIPE):
            step(i, lag + u)
    for u in range(NT - loops * PIPE):
        step(loops, lag + u)


def capped(count):
    return min(count, NT) if isinstance(count, int) else count


def stagger(i, *phases, oldest_first=False):
    for step in range(GROUP + len(phases) - 1):
        for k, phase in sorted(enumerate(phases), key=lambda x: x[0], reverse=oldest_first):
            if 0 <= step - k < GROUP:
                phase(i, step - k)


def nothing(i, u):
    pass


class Shared:
    pass


def after(eng, ins, sem, value):
    ins.then_inc(sem, 1)
    eng.wait_ge(sem, value)


class Steps:

    def __init__(self, eng, sem, base=0):
        self.eng, self.sem, self.n, self.base = eng, sem, 0, base

    def __call__(self, ins):
        self.n += 1
        ins.then_inc(self.sem, 1)
        self.eng.wait_ge(self.sem, self.base + self.n)


class Alloc:
    def __init__(self, nc, ctx, tag=""):
        self.nc, self.ctx, self.tag, self.sems = nc, ctx, tag, []
        self.pool_dmas = False

    def sb(self, name, shape, dt=F32):
        return self.ctx.enter_context(self.nc.sbuf_tensor(self.tag + name, shape, dt))

    def ps(self, name, shape, dt=F32):
        return self.ctx.enter_context(self.nc.psum_tensor(self.tag + name, shape, dt))

    def sem(self, name):
        s = self.ctx.enter_context(self.nc.semaphore(self.tag + name))
        self.sems.append(s)
        return s

    def borrow(self, sems):
        self.sems.extend(s for s in sems if s not in self.sems)
        self.pool_dmas = True
        return sems


@contextmanager
def stage(nc, tag):
    with ExitStack() as ctx:
        a = Alloc(nc, ctx, tag)
        yield a
        with nc.Block() as block:
            @block.gpsimd
            def _(pool):
                if a.pool_dmas:
                    pool.dma_reset()
                for s in a.sems:
                    pool.sem_clear(s)


def row_of(ap):
    return ap.rearrange("(a b) -> a b", a=1)


def spread(ap, parts):
    return row_of(ap).broadcast_to([parts, ap.shape[0]])


def tiles_of(ap):
    return ap.rearrange("(t p) d -> p t d", p=TP)


def constants(nc, g, S):
    S.ident = g.sb("ident", [P, P])
    S.ones = g.sb("ones", [P, P])
    S.iota_row = g.sb("iota_row", [P, P])
    S.part_col = g.sb("part_col", [P, 1])
    S.zeros = g.sb("zeros", [P, P + 1])
    S.pool_dma = [g.sem(f"pool_dma{n}") for n in range(8)]
    with stage(nc, "co_") as a, nc.Block() as block:
        iota_i = a.sb("iota_i", [P, P], I32)
        part_i = a.sb("part_i", [P, 1], I32)
        made = a.sem("constants_made")

        @block.gpsimd
        def _(pool):
            pool.iota(iota_i[:], pattern=[[1, P]], base=0, channel_multiplier=0).then_inc(made, 1)
            pool.iota(part_i[:], pattern=[[1, 1]], base=0, channel_multiplier=1).then_inc(made, 1)

        @block.vector
        def _(dve):
            dve.memset(S.ones[:], 1.0)
            dve.memset(S.zeros[:], 0.0)
            dve.wait_ge(made, 2)
            dve.tensor_copy(S.iota_row[:], iota_i[:]).then_inc(made, 1)
            dve.tensor_copy(S.part_col[:], part_i[:]).then_inc(made, 1)
            dve.wait_ge(made, 4)
            dve.tensor_scalar(S.ident[:], S.iota_row[:], S.part_col[:, 0:1], None, ALU.is_equal)


def edges(nc, g, S, src, dst, etype, ew):
    S.dst_pad = nc.dram_tensor("dst_pad", [EP + 2], I32, kind="Internal").ap()
    S.src_pad = nc.dram_tensor("src_pad", [EP], I32, kind="Internal").ap()
    S.typ_pad = nc.dram_tensor("typ_pad", [EP], I32, kind="Internal").ap()
    ew_pad = nc.dram_tensor("ew_pad", [EP], F32, kind="Internal").ap()
    S.q_at = nc.dram_tensor("q_at", [EP, 2 * HEADS], F32, kind="Internal").ap()
    S.q_at3 = nc.dram_tensor("q_at3", [EP, 2], F32, kind="Internal").ap()
    S.acc = [nc.dram_tensor(f"acc_rows{u}", [N + P, D], F32, kind="Internal").ap() for u in range(4)]

    S.dst_c, S.src_c, S.ew_c = (g.sb(name, [P, CH]) for name in ("dst_c", "src_c", "ew_c"))
    S.row_src, S.node_dst = (g.sb(name, [P, CH], I32) for name in ("row_src", "node_dst"))
    S.row_rep = S.dst_c
    S.pen_start = g.sb("pen_start", [CK, KB, P])
    S.pen_end = g.sb("pen_end", [CK, KB, P])
    S.pen_first = g.sb("pen_first", [CK, KB, P])
    S.pen_last = g.sb("pen_last", [CK, KB, P])
    S.inside = g.sb("inside", [CK, KB, P])
    S.first_run = g.sb("first_run", [CK, KB, P])
    S.type1 = g.sb("type1", [CK, KB, P])
    S.passes = g.sb("passes", [2 * HEADS, CH])
    S.linked = g.sb("linked", [2 * HEADS, CH])
    S.link = g.sb("link", [HEADS, CH])
    S.carry_f = g.sb("carry_f", [HEADS, CH])
    S.carry_b = g.sb("carry_b", [HEADS, CH])

    with stage(nc, "ed_") as a:
        pad_i = a.sb("pad_i", [1, 128], I32)
        pad_n = a.sb("pad_n", [1, 128], I32)
        pad_m = a.sb("pad_m", [1, 1], I32)
        zeros = a.sb("zeros_wide", [P, HEADS * HID + HEADS])
        raw = {n: a.sb("raw_" + n, [CK, KB, P], F32 if n == "ew" else I32)
               for n in ("src", "dst", "prev", "next", "typ", "ew")}
        f = {n: a.sb("f_" + n, [CK, KB, P]) for n in ("src", "dst", "prev", "next", "typ")}
        w = {n: a.sb("w_" + n, [CK, KB, P]) for n in ("rs", "nd", "t0", "t1")}
        tmp = a.sb("tmp", [CK, KB])
        rows_i = a.sb("rows_i", [2 * HEADS, 2, CH + 1], I32)
        rows_f = a.sb("rows_f", [2 * HEADS, 2, CH + 1])
        eq = a.sb("eq", [2 * HEADS, 2, CH])
        turn = a.ps("turn", [P, 5, 512])
        pads_set, filled = a.sem("pads_set"), a.sem("filled")
        copied, loaded = a.sem("copied"), a.sem("loaded")
        step_s, turned = a.sem("step"), a.sem("turned")
        PADE = EP - E
        ZW = zeros.shape[1]

        with nc.Block() as block:
            @block.sync
            def _(sp):
                sp.dma_start(S.dst_pad[1:E + 1], dst).then_inc(copied, 16)
                sp.dma_start(S.src_pad[0:E], src).then_inc(copied, 16)
                sp.dma_start(S.typ_pad[0:E], etype).then_inc(copied, 16)
                sp.dma_start(ew_pad[0:E], ew).then_inc(copied, 16)
                sp.wait_ge(pads_set, 4)
                sp.dma_start(row_of(S.dst_pad[E + 1:EP + 1]), pad_n[0:1, 0:PADE]).then_inc(copied, 16)
                sp.dma_start(row_of(S.dst_pad[EP + 1:EP + 2]), pad_m[:]).then_inc(copied, 16)
                sp.dma_start(row_of(S.dst_pad[0:1]), pad_m[:]).then_inc(copied, 16)
                sp.dma_start(row_of(S.src_pad[E:EP]), pad_i[0:1, 0:PADE]).then_inc(copied, 16)
                sp.dma_start(row_of(S.typ_pad[E:EP]), pad_i[0:1, 0:PADE]).then_inc(copied, 16)
                sp.dma_start(row_of(ew_pad[E:EP]), S.zeros[0:1, 0:PADE]).then_inc(copied, 16)
                sp.wait_ge(copied, 160)
                rows = lambda x: x.rearrange("(k c j) -> c k j", k=KB, c=CK)
                sp.dma_start(raw["src"][:], rows(S.src_pad)).then_inc(loaded, 16)
                sp.dma_start(raw["dst"][:], rows(S.dst_pad[1:EP + 1])).then_inc(loaded, 16)
                sp.dma_start(raw["prev"][:], rows(S.dst_pad[0:EP])).then_inc(loaded, 16)
                sp.dma_start(raw["next"][:], rows(S.dst_pad[2:EP + 2])).then_inc(loaded, 16)
                sp.dma_start(raw["typ"][:], rows(S.typ_pad)).then_inc(loaded, 16)
                sp.dma_start(raw["ew"][:], rows(ew_pad)).then_inc(loaded, 16)
                for h in range(2 * HEADS):
                    sp.dma_start(rows_i[h:h + 1, 0, 0:CH], S.dst_pad[1:EP + 1].rearrange(
                        "(a c j) -> a c j", a=1, j=P)[:, :, 0:1].rearrange("a c j -> a (c j)"),
                                 allow_slow_non_contiguous=True).then_inc(loaded, 16)
                    sp.dma_start(rows_i[h:h + 1, 1, 0:CH], S.dst_pad[1:EP + 1].rearrange(
                        "(a c j) -> a c j", a=1, j=P)[:, :, P - 1:P].rearrange("a c j -> a (c j)"),
                                 allow_slow_non_contiguous=True).then_inc(loaded, 16)
                for u in range(4):
                    for r in range(0, N + P, P):
                        m = min(P, N + P - r)
                        sp.dma_start(S.acc[u][r:r + m, :], zeros[0:m, 0:D]).then_inc(filled, 16)
                for table in (S.q_at, S.q_at3):
                    flat = table.rearrange("(p r) h -> p (r h)", p=P)
                    for r in range(0, flat.shape[1], ZW):
                        m = min(ZW, flat.shape[1] - r)
                        sp.dma_start(flat[:, r:r + m], zeros[:, 0:m]).then_inc(filled, 16)
                fills = sum(len(range(0, EP * w // P, ZW)) for w in (2 * HEADS, 2))
                fills += 4 * len(range(0, N + P, P))
                sp.wait_ge(filled, 16 * fills)

            @block.vector
            def _(dve):
                dve.memset(zeros[:], 0.0).then_inc(pads_set, 1)
                dve.memset(pad_i[:], 0).then_inc(pads_set, 1)
                dve.memset(pad_n[:], PAD_NODE).then_inc(pads_set, 1)
                dve.memset(pad_m[:], 2 * PAD_NODE).then_inc(pads_set, 1)
                st = Steps(dve, step_s)
                dve.wait_ge(loaded, 16 * (6 + 4 * HEADS))
                for n in f:
                    st(dve.tensor_copy(f[n][:], raw[n][:]))
                st(dve.tensor_copy(rows_f[:, :, 0:CH], rows_i[:, :, 0:CH]))
                st(dve.scalar_tensor_tensor(w["rs"][:], f["typ"][:], float(N), f["src"][:], ALU.mult, ALU.add))
                st(dve.tensor_scalar(w["nd"][:], f["dst"][:], float(N - 1), None, ALU.min))
                st(dve.tensor_tensor(w["t0"][:], f["dst"][:], f["next"][:], ALU.not_equal))
                st(dve.tensor_tensor(w["t1"][:], f["dst"][:], f["prev"][:], ALU.not_equal))
                st(dve.tensor_scalar(S.pen_start[:], w["t1"][:], -BIG, None, ALU.mult))
                st(dve.memset(S.pen_start[:, :, 0:1], -BIG))
                st(dve.tensor_scalar(S.inside[:], w["t1"][:], -1.0, 1.0, ALU.mult, ALU.add))
                st(dve.memset(S.inside[:, :, 0:1], 0.0))
                st(dve.tensor_copy(S.type1[:], f["typ"][:]))
                st(dve.tensor_scalar(S.pen_end[:], w["t0"][:], -BIG, None, ALU.mult))
                st(dve.memset(S.pen_end[:, :, P - 1:P], -BIG))
                first = f["dst"][:, :, 0:1].broadcast_to([CK, KB, P])
                last = f["dst"][:, :, P - 1:P].broadcast_to([CK, KB, P])
                st(dve.tensor_tensor(w["t1"][:], f["dst"][:], first, ALU.not_equal))
                st(dve.tensor_scalar(S.pen_first[:], w["t1"][:], -BIG, None, ALU.mult))
                st(dve.tensor_scalar(S.first_run[:], w["t1"][:], -1.0, 1.0, ALU.mult, ALU.add))
                st(dve.tensor_tensor(w["t1"][:], f["dst"][:], last, ALU.not_equal))
                st(dve.tensor_scalar(S.pen_last[:], w["t1"][:], -BIG, None, ALU.mult))
                st(dve.memset(eq[:], 0.0))
                st(dve.tensor_tensor(eq[:, 0, :], rows_f[:, 0, 0:CH], rows_f[:, 1, 0:CH], ALU.is_equal))
                st(dve.tensor_tensor(eq[:, 1, 1:CH], rows_f[:, 0, 1:CH], rows_f[:, 1, 0:CH - 1], ALU.is_equal))
                H4 = slice(0, HEADS)
                st(dve.tensor_copy(S.linked[:], eq[:, 1, :]))
                st(dve.tensor_scalar(S.link[:], eq[H4, 1, :], -1.0, BIG, ALU.add, ALU.mult))
                st(dve.tensor_tensor(S.passes[:], eq[:, 0, :], eq[:, 1, :], ALU.mult))
                st(dve.tensor_scalar(S.carry_f[:], S.passes[H4], -1.0, BIG, ALU.add, ALU.mult))
                st(dve.memset(S.carry_b[:], 0.0))
                st(dve.tensor_tensor(S.carry_b[:, 0:CH - 1], eq[H4, 0, 0:CH - 1], eq[H4, 1, 1:CH], ALU.mult))
                st(dve.tensor_scalar(S.carry_b[:], S.carry_b[:], -1.0, BIG, ALU.add, ALU.mult))
                dve.memset(tmp[:], 0.0).then_inc(turned, 1)
                dve.wait_ge(turned, 2)
                for n, to in enumerate((S.dst_c, S.src_c, S.ew_c, S.row_src, S.node_dst)):
                    dve.tensor_copy(to[:], turn[:, n, 0:CH])

            @block.tensor
            def _(pe):
                pe.wait_ge(turned, 1)
                for n, x in enumerate((f["dst"], f["src"], raw["ew"], w["rs"], w["nd"])):
                    for k in range(KB):
                        last = pe.transpose(turn[:, n, k * CK:(k + 1) * CK], x[:, k, :], S.ident[0:CK, 0:CK])
                last.then_inc(turned, 1)


def row_starts(nc, g, S):
    BL = 32
    BF16 = mybir.dt.bfloat16
    S.start_row = g.sb("start_row", [TP, NT], I32)
    with stage(nc, "rs_") as a:
        bound_row = a.sb("bound_row", [P, NT])
        ge = a.sb("ge", [P, BL, NT])
        hi, lo = a.sb("hi", [P, CH]), a.sb("lo", [P, CH])
        one_hi = a.sb("one_hi", [P, CH, NT], BF16)
        one_lo = [a.sb(f"one_lo{s}", [P, BL, TP], BF16) for s in range(2)]
        zero_b = a.sb("zero_b", [P, P], BF16)
        before = a.sb("before", [TP, TP])
        deg, tot, scan, none, pos, ones_t = (a.sb(n, [TP, NT]) for n in ("deg", "tot", "scan", "none", "pos", "ones_t"))
        deg_ps, pre_ps, tot_ps = a.ps("deg_ps", [TP, 512]), a.ps("pre", [TP, 512]), a.ps("tot_ps", [TP, 512])
        step_s, made, counted, deg_in, summed = (a.sem(n) for n in ("step", "made", "counted", "deg_in", "summed"))
        with nc.Block() as block:
            @block.vector
            def _(dve):
                st = Steps(dve, step_s)
                st(dve.memset(zero_b[:], 0.0))
                st(dve.memset(ones_t[:], 1.0))
                st(dve.tensor_scalar(bound_row[:], S.iota_row[:, 0:NT], 1.0, float(TP), ALU.add, ALU.mult))
                st(dve.tensor_scalar(before[:], S.iota_row[0:TP, 0:TP], S.part_col[0:TP, 0:1], None, ALU.is_gt))
                for c in range(0, CH, BL):
                    dst = S.dst_c[:, c:c + BL].unsqueeze(2).broadcast_to([P, BL, NT])
                    st(dve.tensor_tensor(ge[:], dst, bound_row[:].unsqueeze(1).broadcast_to([P, BL, NT]), ALU.is_ge))
                    st(dve.tensor_reduce(hi[:, c:c + BL], ge[:], AX.X, ALU.add))
                st(dve.scalar_tensor_tensor(lo[:], hi[:], float(-TP), S.dst_c[:], ALU.mult, ALU.add))
                for c in range(0, CH, BL):
                    last = dve.tensor_tensor(one_hi[:, c:c + BL, :], hi[:, c:c + BL].unsqueeze(2).broadcast_to([P, BL, NT]),
                                             S.iota_row[:, 0:NT].unsqueeze(1).broadcast_to([P, BL, NT]), ALU.is_equal)
                last.then_inc(made, 1)
                for n, c in enumerate(range(0, CH, BL)):
                    if n >= 2:
                        dve.wait_ge(counted, n - 1)
                    dve.tensor_tensor(one_lo[n % 2][:], lo[:, c:c + BL].unsqueeze(2).broadcast_to([P, BL, TP]),
                                      S.iota_row[:, 0:TP].unsqueeze(1).broadcast_to([P, BL, TP]),
                                      ALU.is_equal).then_inc(made, 1)
                dve.wait_ge(counted, CH // BL)
                dve.tensor_copy(deg[:], deg_ps[:, 0:NT]).then_inc(deg_in, 1)
                dve.wait_ge(summed, 1)
                st(dve.tensor_copy(tot[:], tot_ps[:, 0:NT]))
                st(dve.tensor_tensor_scan(scan[:], ones_t[:], tot[:], 0.0, ALU.mult, ALU.add))
                st(dve.tensor_tensor(scan[:], scan[:], tot[:], ALU.subtract))
                st(dve.tensor_tensor(pos[:], scan[:], pre_ps[:, 0:NT], ALU.add))
                st(dve.tensor_scalar(none[:], deg[:], 0.0, float(SKIP), ALU.is_equal, ALU.mult))
                st(dve.tensor_tensor(pos[:], pos[:], none[:], ALU.add))
                dve.tensor_copy(S.start_row[:], pos[:])

            @block.tensor
            def _(pe):
                pe.wait_ge(made, 1)
                for n, c in enumerate(range(0, CH, BL)):
                    pe.wait_ge(made, n + 2)
                    for b in range(BL):
                        last = pe.matmul(deg_ps[:, 0:NT], one_lo[n % 2][:, b, :], one_hi[:, c + b, :],
                                         start=(c + b == 0), stop=(c + b == CH - 1))
                    last.then_inc(counted, 1)
                pe.wait_ge(deg_in, 1)
                pe.matmul(pre_ps[:, 0:NT], before[:], deg[:], start=True, stop=True)
                pe.matmul(tot_ps[:, 0:NT], S.ones[0:TP, 0:TP], deg[:], start=True, stop=True).then_inc(summed, 1)


def visits(nc, a, S):
    VC = VISITS * QUAD
    S.visit_quad = a.sb("visit_quad", [P, VISITS])
    S.visit_tile = a.sb("visit_tile", [1, VISITS], I32)
    S.visit_row = a.sb("visit_row", [P, VC], I32)
    S.visit_rel = a.sb("visit_rel", [P, VC])
    with stage(nc, "vi_") as b:
        last_i, last = b.sb("last_i", [QUADS, 1], I32), b.sb("last", [QUADS, 1])
        ge, bound = b.sb("ge", [QUADS, NT - 1]), b.sb("bound", [QUADS, NT - 1])
        end, before = b.sb("end", [QUADS, 1]), b.sb("before", [QUADS, VISITS])
        tile_at = b.sb("tile_at", [P, VISITS])
        pick = b.sb("pick", [CK, KB, VC])
        raw = [b.sb(f"raw{n}", [CK, KB, P], I32) for n in range(3)]
        dst, row = b.sb("dst", [CK, KB, P]), b.sb("row", [CK, KB, P])
        quad_ps, dst_ps, row_ps = b.ps("quad", [P, 512]), b.ps("dst_ps", [P, 512]), b.ps("row_ps", [P, 512])
        loaded, step_s, compared, counted, picked, expanded = (
            b.sem(n) for n in ("loaded", "step", "compared", "counted", "picked", "expanded"))
        with nc.Block() as block:
            @block.sync
            def _(sp):
                rows = lambda x: x.rearrange("(k c j) -> c k j", k=KB, c=CK)
                sp.dma_start(last_i[:], S.dst_pad[1:EP + 1].rearrange("(q j) -> q j", q=QUADS)[:, QUAD * P - 1:QUAD * P],
                             allow_slow_non_contiguous=True).then_inc(loaded, 16)
                for n, x in enumerate((S.dst_pad[1:EP + 1], S.src_pad, S.typ_pad)):
                    sp.dma_start(raw[n][:], rows(x)).then_inc(loaded, 16)

            @block.vector
            def _(dve):
                st = Steps(dve, step_s)
                st(dve.tensor_scalar(bound[:], S.iota_row[0:QUADS, 0:NT - 1], 1.0, float(TP), ALU.add, ALU.mult))
                dve.wait_ge(loaded, 64)
                st(dve.tensor_copy(last[:], last_i[:]))
                st(dve.tensor_scalar(ge[:], bound[:], last[:, 0:1], None, ALU.is_le))
                st(dve.tensor_reduce(end[:], ge[:], AX.X, ALU.add))
                st(dve.tensor_tensor(end[:], end[:], S.part_col[0:QUADS], ALU.add))
                dve.tensor_scalar(before[:], S.iota_row[0:QUADS, 0:VISITS], end[:, 0:1], None,
                                  ALU.is_gt).then_inc(compared, 1)
                st(dve.tensor_copy(dst[:], raw[0][:]))
                st(dve.tensor_copy(row[:], raw[1][:]))
                st(dve.scalar_tensor_tensor(row[:], raw[2][:], float(N), row[:], ALU.mult, ALU.add))
                dve.wait_ge(counted, 1)
                st(dve.tensor_copy(S.visit_quad[:], quad_ps[:, 0:VISITS]))
                st(dve.tensor_tensor(tile_at[:], S.iota_row[:, 0:VISITS], S.visit_quad[:], ALU.subtract))
                st(dve.tensor_copy(S.visit_tile[:], tile_at[0:1, :]))
                pick_chunks(dve, st, S, pick)
                dve.sem_inc(picked, 1)
                dve.wait_ge(expanded, 1)
                dve.tensor_copy(S.visit_row[:], row_ps[:, 0:VC])
                at = tile_at[:].unsqueeze(2).broadcast_to([P, VISITS, QUAD])
                dve.scalar_tensor_tensor(S.visit_rel[:].rearrange("p (v u) -> p v u", u=QUAD), at, float(-TP),
                                         dst_ps[:, 0:VC].rearrange("p (v u) -> p v u", u=QUAD), ALU.mult, ALU.add)

            @block.tensor
            def _(pe):
                pe.wait_ge(compared, 1)
                pe.matmul(quad_ps[:, 0:VISITS], S.ones[0:QUADS, :], before[:], start=True, stop=True).then_inc(counted, 1)
                pe.wait_ge(picked, 1)
                for x, ps in ((dst, dst_ps), (row, row_ps)):
                    for k in range(KB):
                        last_mm = pe.matmul(ps[:, 0:VC], x[:, k, :], pick[:, k, :], start=(k == 0), stop=(k == KB - 1))
                last_mm.then_inc(expanded, 1)


def pick_chunks(dve, st, S, pick):
    for u in range(QUAD):
        for k in range(KB):
            st(dve.tensor_scalar(pick[:, k, u::QUAD], S.visit_quad[0:CK, :], float(QUAD), float(u - k * CK),
                                 ALU.mult, ALU.add))
    st(dve.tensor_scalar(pick[:], pick[:], S.part_col[0:CK, 0:1], None, ALU.is_equal))


class KeyGather:

    SET = 8

    def __init__(self, nc, S, a, H, k_tab, q_at):
        self.S, self.H, self.k_tab, self.q_at = S, H, k_tab, q_at
        self.slot = [a.sb(f"kg_slot{s}", [P, self.SET, H]) for s in range(2)]
        self.index = [a.sb(f"kg_index{s}", [P, self.SET], I32) for s in range(2)]
        self.landed = a.borrow(S.pool_dma[0:2])
        self.q_placed = a.borrow(S.pool_dma[2:3])[0]
        self.indexed, self.go, self.kept = a.sem("kg_indexed"), a.sem("kg_go"), a.sem("kg_kept")

    def __call__(self, pool):
        S, SET = self.S, self.SET
        LOOPS = CH // (2 * SET)

        def gather(i, s):
            cols = bass.ds(i * (2 * SET) + s * SET, SET)
            pool.tensor_copy(self.index[s][:], S.row_src[:, cols]).then_inc(self.indexed, 1)
            pool.wait_ge(self.indexed, i * 2 + s + 1)
            pool.sem_inc(self.go, 1)
            for u in range(SET):
                pool.indirect_dma_start(self.slot[s][:, u, :], None, self.k_tab,
                                        bass.IndirectOffsetOnAxis(ap=self.index[s][:, u:u + 1], axis=0)
                                        ).then_inc(self.landed[s], 16)

        def keep(i, s):
            pool.wait_ge(self.landed[s], i * (16 * SET) + 16 * SET)
            pool.sem_inc(self.go, 1)
            pool.tensor_copy(S.k_edge[:, bass.ds(i * (2 * SET) + s * SET, SET), 0:self.H], self.slot[s][:]
                             ).then_inc(self.kept, 1)
            pool.wait_ge(self.kept, i * 2 + s + 1)
            pool.sem_inc(self.go, 1)

        for t in range(NT):
            pool.indirect_dma_start(self.q_at, bass.IndirectOffsetOnAxis(ap=S.start_row[:, t:t + 1], axis=0),
                                    S.q_node[:, t, 0:2 * self.H], None, bounds_check=EP - 1, oob_is_err=False
                                    ).then_inc(self.q_placed, 16)
        gather(0, 0)
        with pool.Fori(0, LOOPS - 1) as i:
            gather(i, 1)
            keep(i, 0)
            gather(i + 1, 0)
            keep(i, 1)
        gather(LOOPS - 1, 1)
        keep(LOOPS - 1, 0)
        keep(LOOPS - 1, 1)
        pool.wait_ge(self.q_placed, 16 * NT)


def edge_softmax(nc, S, tag, q_at, H):
    H2 = 2 * H
    with stage(nc, tag) as a:
        q_rows = a.sb("q_rows", [CK, KB, P, H2])
        q_all = a.sb("q_all", [CK, H2, KB, P])
        rowed = a.sb("rowed", [CK, H, KB, P])
        fwd = q_all[:, 0:H]
        bwd = q_all[:, H:H2]
        end_q, run_q, in_q = (a.sb(n, [2 * HEADS, CH]) for n in ("end_q", "run_q", "in_q"))
        edge_f, edge_b = a.sb("edge_f", [HEADS, CH]), a.sb("edge_b", [HEADS, CH])
        run_f, run_b = a.sb("run_f", [HEADS, CH]), a.sb("run_b", [HEADS, CH])
        in_f, in_b = a.sb("in_f", [HEADS, CH]), a.sb("in_b", [HEADS, CH])
        carried = a.sb("carried", [CK, 2, KB, H])
        carried_q = a.sb("carried_q", [CK, KB, H2])
        pick = a.sb("pick", [CK, KB, VISITS * QUAD])
        rows_ps = a.ps("rows_ps", [P, H, KB, P])
        small_ps = a.ps("small_ps", [2 * HEADS, 2, 512])
        back_ps = a.ps("back_ps", [CK, 2, KB, H])
        back_q_ps = a.ps("back_q_ps", [CK, KB, H2])
        (q_landed, q_filled, q_turned, q_carried, q_back, turned, rows_done, scans_done, ends_turned, carries_done,
         carries_back, less_max, exp_done, exp_turned, dve_step) = (a.sem(n) for n in (
             "q_landed", "q_filled", "q_turned", "q_carried", "q_back", "turned", "rows_done", "scans_done",
             "ends_turned", "carries_done", "carries_back", "less_max", "exp_done", "exp_turned", "dve_step"))
        flat = lambda x: x.rearrange("c k j -> c (k j)")

        with nc.Block() as block:
            @block.sync
            def _(sp):
                sp.dma_start(q_rows[:], q_at.rearrange("(k c j) h -> c k j h", k=KB, c=CK)).then_inc(q_landed, 16)

            @block.vector
            def _(dve):
                st = Steps(dve, dve_step)
                pick_chunks(dve, st, S, pick)
                dve.wait_ge(q_landed, 16)
                for x in range(H2):
                    dve.tensor_tensor_scan(flat(q_all[:, x]), flat(S.inside[:]),
                                           q_rows[:, :, :, x].rearrange("c k j -> c (k j)"), 0.0, ALU.mult,
                                           ALU.add).then_inc(q_filled, 1)
                dve.wait_ge(q_turned, 1)
                st(dve.tensor_copy(end_q[0:H2, :], small_ps[0:H2, 0, 0:CH]))
                st(dve.tensor_tensor_scan(run_q[0:H2, :], S.passes[0:H2, :], end_q[0:H2, :], 0.0, ALU.mult, ALU.add))
                st(dve.memset(in_q[0:H2, :], 0.0))
                dve.tensor_tensor(in_q[0:H2, 1:CH], run_q[0:H2, 0:CH - 1], S.linked[0:H2, 1:CH],
                                  ALU.mult).then_inc(q_carried, 1)
                dve.wait_ge(q_back, 1)
                st(dve.tensor_copy(carried_q[:], back_q_ps[:]))
                qr = q_rows[:].rearrange("c k j h -> c (k j h)").rearrange("c (h k j) -> c h k j", h=H2, k=KB)
                for x in range(H2):
                    last = dve.tensor_tensor(qr[:, x], S.first_run[:],
                                             carried_q[:, :, x].unsqueeze(2).broadcast_to([CK, KB, P]), ALU.mult)
                st(last)
                st(dve.tensor_tensor(q_all[:], q_all[:], qr, ALU.add))
                st(dve.tensor_scalar(qr[:, 0], S.type1[:], -1.0, 1.0, ALU.mult, ALU.add))
                over = lambda m: m.rearrange("c k j -> c (k j)").unsqueeze(1).broadcast_to([CK, H, KB * P])
                fl4 = lambda m: m.rearrange("c h k j -> c h (k j)")
                dve.tensor_tensor(fl4(q_all[:, 0:H]), fl4(q_all[:, 0:H]), over(qr[:, 0]), ALU.mult)
                st(dve.tensor_tensor(fl4(q_all[:, H:H2]), fl4(q_all[:, H:H2]), over(S.type1[:]), ALU.mult))
                st(dve.tensor_tensor(q_all[:, 0:H], q_all[:, 0:H], q_all[:, H:H2], ALU.add))
                dve.wait_ge(turned, 1)
                st(dve.tensor_tensor(rowed[:], rows_ps[0:CK], q_all[:, 0:H], ALU.add))
                st(dve.scalar_tensor_tensor(rowed[:], rowed[:], SLOPE, rowed[:], ALU.mult, ALU.max))
                for h in range(H):
                    x, fw, bw = flat(rowed[:, h]), flat(fwd[:, h]), flat(bwd[:, h])
                    start, end = flat(S.pen_start[:]), flat(S.pen_end[:])
                    dve.tensor_tensor_scan(fw, start, x, -BIG, ALU.add, ALU.max).then_inc(scans_done, 1)
                    dve.tensor_tensor_scan(bw[:, ::-1], end[:, ::-1], x[:, ::-1], -BIG, ALU.add,
                                           ALU.max).then_inc(scans_done, 1)
                dve.wait_ge(ends_turned, 1)
                st(dve.tensor_copy(edge_f[0:H, :], small_ps[0:H, 0, 0:CH]))
                st(dve.tensor_copy(edge_b[0:H, :], small_ps[0:H, 1, 0:CH]))
                st(dve.tensor_tensor_scan(run_f[0:H, :], S.carry_f[0:H, :], edge_f[0:H, :], -BIG, ALU.add, ALU.max))
                st(dve.tensor_tensor_scan(run_b[0:H, ::-1], S.carry_b[0:H, ::-1], edge_b[0:H, ::-1], -BIG, ALU.add,
                                          ALU.max))
                st(dve.memset(in_f[0:H, :], -BIG))
                st(dve.memset(in_b[0:H, :], -BIG))
                dve.tensor_tensor(in_f[0:H, 1:CH], run_f[0:H, 0:CH - 1], S.link[0:H, 1:CH],
                                  ALU.add).then_inc(carries_done, 1)
                dve.tensor_tensor(in_b[0:H, 0:CH - 1], run_b[0:H, 1:CH], S.link[0:H, 1:CH],
                                  ALU.add).then_inc(carries_done, 1)
                dve.wait_ge(carries_back, 1)
                st(dve.tensor_copy(carried[:], back_ps[:]))
                st(dve.tensor_tensor(fwd[:], fwd[:], bwd[:], ALU.max))
                for n, pen in ((0, S.pen_first), (1, S.pen_last)):
                    for h in range(H):
                        dve.tensor_tensor(bwd[:, h], pen[:], carried[:, n, :, h].unsqueeze(2).broadcast_to([CK, KB, P]),
                                          ALU.add).then_inc(dve_step, 1)
                    st.n += H
                    dve.wait_ge(dve_step, st.n)
                    st(dve.tensor_tensor(fwd[:], fwd[:], bwd[:], ALU.max))
                dve.tensor_tensor(rowed[:], rowed[:], fwd[:], ALU.subtract).then_inc(less_max, 1)
                dve.wait_ge(exp_turned, 1)
                dve.tensor_copy(S.ex[:, :, 0:H], rows_ps[:].rearrange("p h k c -> p (k c) h"))

            @block.tensor
            def _(pe):
                for h in range(H):
                    for k in range(KB):
                        last = pe.transpose(rows_ps[0:CK, h, k, :], S.k_edge[:, k * CK:(k + 1) * CK, h], S.ident[:])
                last.then_inc(turned, 1)
                pe.wait_ge(q_filled, H2)
                for k in range(KB):
                    last = pe.transpose(small_ps[0:H2, 0, k * CK:(k + 1) * CK], q_all[:, :, k, P - 1], S.ident[0:CK, 0:CK])
                last.then_inc(q_turned, 1)
                pe.wait_ge(q_carried, 1)
                for k in range(KB):
                    last = pe.transpose(back_q_ps[:, k, :], in_q[0:H2, k * CK:(k + 1) * CK], S.ident[0:H2, 0:H2])
                last.then_inc(q_back, 1)
                pe.wait_ge(scans_done, 2 * H)
                for n, (x, j) in enumerate(((fwd, P - 1), (bwd, 0))):
                    for k in range(KB):
                        last = pe.transpose(small_ps[0:H, n, k * CK:(k + 1) * CK], x[:, :, k, j], S.ident[0:CK, 0:CK])
                last.then_inc(ends_turned, 1)
                pe.wait_ge(carries_done, 2)
                for n, x in enumerate((in_f, in_b)):
                    for k in range(KB):
                        last = pe.transpose(back_ps[:, n, k, :], x[0:H, k * CK:(k + 1) * CK], S.ident[0:H, 0:H])
                last.then_inc(carries_back, 1)
                pe.wait_ge(exp_done, 1)
                for h in range(H):
                    for k in range(KB):
                        last = pe.matmul(rows_ps[:, h].rearrange("p k c -> p (k c)"), rowed[:, h, k, :], pick[:, k, :],
                                         start=(k == 0), stop=(k == KB - 1))
                last.then_inc(exp_turned, 1)

            @block.scalar
            def _(act):
                act.wait_ge(less_max, 1)
                nc.scalar.activation(rowed[:], rowed[:], ACT.Exp).then_inc(exp_done, 1)


def source_sums(nc, S, tag, table, width, weights, gather_rows, key_col, key_pad, scatter_rows, out_tab, guest):
    SET = 4
    BODY = 4
    LEAD = 3
    LOOPS = CH // (BODY * SET)
    with stage(nc, tag) as a:
        x = [a.sb(f"x{s}", [P, SET, width]) for s in range(BODY)]
        gi = [a.sb(f"gi{s}", [P, SET], I32) for s in range(BODY)]
        keys = [a.sb(f"keys{s}", [P, SET, P], I32) for s in range(2)]
        mask = [a.sb(f"mask{s}", [P, SET, P]) for s in range(2)]
        out = [a.sb(f"out{s}", [P, SET, width]) for s in range(2)]
        si = [a.sb(f"si{s}", [P, SET], I32) for s in range(2)]
        sums = a.ps("sums", [P, SET, 512])
        guest_scalar, guest_vector, guest_tensor = guest(a)
        index_ready, masked, weighted, place_ready, out_free = (
            a.sem(n) for n in ("index_ready", "masked", "weighted", "place_ready", "out_free"))
        summed = [a.sem(f"summed{h}") for h in range(2)]
        copied = [a.sem(f"copied{h}") for h in range(2)]
        keys_landed = [a.sem(f"keys_landed{s}") for s in range(2)]
        landed = a.borrow(S.pool_dma[0:BODY])
        added = a.borrow(S.pool_dma[BODY:BODY + SET])
        pool_go = a.sem("pool_go")

        def cols(i, s):
            return bass.ds(i * (BODY * SET) + s * SET, SET)

        def before(i, s):
            return i * BODY + s

        def slot_before(i, s):
            return i * (BODY // 2) + s // 2

        with nc.Block() as block:
            @block.sync
            def _(sp):
                with sp.Fori(0, LOOPS) as i:
                    for s in range(BODY):
                        sp.wait_ge(masked, before(i, max(s - 1, 0)))
                        first = i * (BODY * SET * P) + s * SET * P
                        sp.dma_start(keys[s % 2][:].rearrange("p u j -> p (u j)"),
                                     row_of(key_pad[bass.ds(first, SET * P)]).broadcast_to([P, SET * P])
                                     ).then_inc(keys_landed[s % 2], 16)

            @block.gpsimd
            def _(pool):
                def gather(i, s):
                    pool.wait_ge(index_ready, before(i, s + 1))
                    pool.sem_inc(pool_go, 1)
                    for u in range(SET):
                        pool.indirect_dma_start(
                            x[s][:, u, :], None, table,
                            bass.IndirectOffsetOnAxis(ap=gi[s][:, u:u + 1], axis=0)).then_inc(landed[s], 16)

                def scatter(i, s):
                    pool.wait_ge(place_ready, before(i, s + 1))
                    pool.wait_ge(copied[0], before(i, s + 1))
                    pool.wait_ge(copied[1], before(i, s + 1))
                    pool.sem_inc(pool_go, 1)
                    for u in range(SET):
                        to = bass.IndirectOffsetOnAxis(ap=si[s % 2][:, u:u + 1], axis=0)
                        pool.wait_ge(added[u], before(i, s) * 16)
                        pool.sem_inc(out_free if u == SET - 1 else pool_go, 1)
                        pool.indirect_dma_start(out_tab[u], to, out[s % 2][:, u, :], None,
                                                compute_op=ALU.add).then_inc(added[u], 16)

                for s in range(LEAD):
                    gather(0, s)
                with pool.Fori(0, LOOPS - 1) as i:
                    for s in range(BODY):
                        gather(i + (s + LEAD) // BODY, (s + LEAD) % BODY)
                        scatter(i, s)
                for s in range(BODY):
                    if s + LEAD < BODY:
                        gather(LOOPS - 1, s + LEAD)
                    scatter(LOOPS - 1, s)
                for u in range(SET):
                    pool.wait_ge(added[u], 16 * BODY * LOOPS)

            @block.scalar
            def _(act):
                def indices(i, s):
                    for h in range(2):
                        act.wait_ge(summed[h], before(i, s - LEAD) if s >= LEAD else before(i - 1, s - LEAD + BODY))
                    nc.scalar.copy(gi[s][:], gather_rows[:, cols(i, s)]).then_inc(index_ready, 1)

                def results(i, s):
                    act.wait_ge(out_free, before(i, s))
                    nc.scalar.copy(si[s % 2][:], scatter_rows[:, cols(i, s)]).then_inc(place_ready, 1)
                    for h in range(2):
                        act.wait_ge(summed[h], before(i, s + 1))
                        nc.scalar.copy(out[s % 2][:, 2 * h:2 * h + 2, 0:width],
                                       sums[:, 2 * h:2 * h + 2, 0:width]).then_inc(copied[h], 1)

                for s in range(LEAD):
                    nc.scalar.copy(gi[s][:], gather_rows[:, s * SET:(s + 1) * SET]).then_inc(index_ready, 1)
                with act.Fori(0, LOOPS - 1) as i:
                    for s in range(BODY):
                        indices(i + (s + LEAD) // BODY, (s + LEAD) % BODY)
                        results(i, s)
                        guest_scalar(act, i, s)
                indices(LOOPS - 1, BODY - 1)
                for s in range(BODY):
                    results(LOOPS - 1, s)

            @block.vector
            def _(dve):
                def weigh(i, s):
                    dve.wait_ge(keys_landed[s % 2], slot_before(i, s + 2) * 16)
                    dve.wait_ge(summed[1], before(i, max(s - 1, 0)))
                    dve.tensor_tensor(mask[s % 2][:], keys[s % 2][:],
                                      key_col[:, cols(i, s)].unsqueeze(2).broadcast_to([P, SET, P]),
                                      ALU.is_equal).then_inc(masked, 1)
                    dve.wait_ge(landed[s], i * (16 * SET) + 16 * SET)
                    dve.tensor_tensor(x[s][:], x[s][:], weights[:, cols(i, s)].unsqueeze(2).broadcast_to([P, SET, width]),
                                      ALU.mult).then_inc(weighted, 1)

                with dve.Fori(0, LOOPS - 1) as i:
                    for s in range(BODY):
                        weigh(i, s)
                        guest_vector(dve, i, s)
                for s in range(BODY):
                    weigh(LOOPS - 1, s)

            @block.tensor
            def _(pe):
                def add_up(i, s):
                    pe.wait_ge(masked, before(i, s + 1))
                    pe.wait_ge(weighted, before(i, s + 1))
                    for h in range(2):
                        pe.wait_ge(copied[h], before(i, s))
                        for u in (2 * h, 2 * h + 1):
                            last = pe.matmul(sums[:, u, 0:width], mask[s % 2][:, u, :], x[s][:, u, :],
                                             start=True, stop=True)
                        last.then_inc(summed[h], 1)

                with pe.Fori(0, LOOPS - 1) as i:
                    for s in range(BODY):
                        add_up(i, s)
                        guest_tensor(pe, i, s)
                for s in range(BODY):
                    add_up(LOOPS - 1, s)


def edge_tiles(nc, S, tag, table, width, H):
    BODY = 4
    LEAD = 3
    LOOPS = VISITS // BODY
    HW = width // H
    with stage(nc, tag) as a:
        x = [a.sb(f"x{s}", [P, QUAD, width]) for s in range(BODY)]
        gi = [a.sb(f"gi{s}", [P, QUAD], I32) for s in range(BODY)]
        mask = [a.sb(f"mask{s}", [P, QUAD, TP]) for s in range(2)]
        sums = a.ps("sums", [TP, BODY, 512])
        dens = a.ps("dens", [TP, BODY, 512])
        index_ready, masked, weighted, summed, cleared = (
            a.sem(n) for n in ("index_ready", "masked", "weighted", "summed", "cleared"))
        added = [a.sem(f"added{s}") for s in range(BODY)]
        landed = a.borrow(S.pool_dma[0:BODY])
        pool_go, dve_go = a.sem("pool_go"), a.sem("dve_go")

        def cols(i, s):
            return bass.ds(i * (BODY * QUAD) + s * QUAD, QUAD)

        def before(i, s):
            return i * BODY + s

        with nc.Block() as block:
            @block.gpsimd
            def _(pool):
                def gather(i, s):
                    pool.wait_ge(index_ready, before(i, s + 1))
                    pool.sem_inc(pool_go, 1)
                    for u in range(QUAD):
                        pool.indirect_dma_start(
                            x[s][:, u, :], None, table,
                            bass.IndirectOffsetOnAxis(ap=gi[s][:, u:u + 1], axis=0)).then_inc(landed[s], 16)

                with pool.Fori(0, LOOPS) as i:
                    for s in range(BODY):
                        gather(i, s)
                for s in range(BODY):
                    pool.wait_ge(landed[s], 16 * QUAD * LOOPS)

            @block.scalar
            def _(act):
                for s in range(LEAD):
                    nc.scalar.copy(gi[s][:], S.visit_row[:, s * QUAD:(s + 1) * QUAD]).then_inc(index_ready, 1)
                with act.Fori(0, LOOPS - 1) as i:
                    for s in range(BODY):
                        act.wait_ge(summed, before(i, s))
                        j, to = i + (s + LEAD) // BODY, (s + LEAD) % BODY
                        nc.scalar.copy(gi[to][:], S.visit_row[:, cols(j, to)]).then_inc(index_ready, 1)
                act.wait_ge(summed, before(LOOPS - 1, 0))
                nc.scalar.copy(gi[BODY - 1][:], S.visit_row[:, cols(LOOPS - 1, BODY - 1)]).then_inc(index_ready, 1)

            @block.vector
            def _(dve):
                def weigh(i, s, done=None):
                    if done is not None:
                        dve.wait_ge(summed, done)
                    dve.tensor_tensor(mask[s % 2][:], S.iota_row[:, 0:TP].unsqueeze(1).broadcast_to([P, QUAD, TP]),
                                      S.visit_rel[:, cols(i, s)].unsqueeze(2).broadcast_to([P, QUAD, TP]),
                                      ALU.is_equal).then_inc(masked, 1)
                    dve.wait_ge(landed[s], i * (16 * QUAD) + 16 * QUAD)
                    by = S.ex[:, cols(i, s), 0:H].rearrange("p u h -> p (u h)")
                    v = x[s][:].rearrange("p u (h w) -> p (u h) w", h=H)
                    dve.tensor_tensor(v, v, by.unsqueeze(2).broadcast_to([P, QUAD * H, HW]), ALU.mult).then_inc(weighted, 1)

                def tile_number(i, s):
                    return dve.value_load(S.visit_tile[0:1, bass.ds(before(i, s), 1)], min_val=0, max_val=NT - 1)

                def add(i, s, t):
                    dve.wait_ge(summed, before(i, s + 1))
                    dve.wait_ge(added[(s - 1) % BODY], i * 2 + (2 if s else 0))
                    dve.sem_inc(dve_go, 1)
                    at = S.agg[:, bass.ds(t, 1), 0:width].rearrange("p a w -> p (a w)")
                    dve.tensor_tensor(at, at, sums[:, s, 0:width], ALU.add).then_inc(added[s], 1)
                    at = S.agg[:, bass.ds(t, 1), width:width + H].rearrange("p a w -> p (a w)")
                    dve.tensor_tensor(at, at, dens[:, s, 0:H], ALU.add).then_inc(added[s], 1)

                after(dve, dve.memset(S.agg[:, :, 0:width + H], 0.0), cleared, 1)
                weigh(0, 0)
                weigh(0, 1)
                with dve.Fori(0, LOOPS - 1) as i:
                    for s in range(BODY):
                        t = tile_number(i, s)
                        weigh(i + (s + 2) // BODY, (s + 2) % BODY, before(i, s + 1))
                        add(i, s, t)
                for s in range(BODY):
                    if s + 2 < BODY:
                        weigh(LOOPS - 1, s + 2, before(LOOPS - 1, s + 1))
                    add(LOOPS - 1, s, tile_number(LOOPS - 1, s))

            @block.tensor
            def _(pe):
                with pe.Fori(0, LOOPS) as i:
                    for s in range(BODY):
                        pe.wait_ge(masked, before(i, s + 1))
                        pe.wait_ge(weighted, before(i, s + 1))
                        pe.wait_ge(added[s], i * 2)
                        for u in range(QUAD):
                            pe.matmul(sums[:, s, 0:width], mask[s % 2][:, u, :], x[s][:, u, :],
                                      start=(u == 0), stop=(u == QUAD - 1))
                        for u in range(QUAD):
                            w = S.ex[:, bass.ds(i * (BODY * QUAD) + s * QUAD + u, 1), 0:H].rearrange("p a h -> p (a h)")
                            last = pe.matmul(dens[:, s, 0:H], mask[s % 2][:, u, :], w, start=(u == 0),
                                             stop=(u == QUAD - 1))
                        last.then_inc(summed, 1)


class Representatives:

    SET = 8

    def __init__(self, nc, S, a):
        self.S = S
        self.keys = [a.sb(f"rep_keys{s}", [P, self.SET, P], I32) for s in range(2)]
        self.same = [a.sb(f"rep_same{s}", [P, self.SET, P]) for s in range(2)]
        self.later_mask = a.sb("rep_later_mask", [P, P])
        self.later = a.sb("rep_later", [P, CH])
        self.dummy = a.sb("rep_dummy", [P, 1])
        self.row = a.sb("rep_row", [P, CH])
        self.keys_landed = [a.sem(f"rep_keys_landed{s}") for s in range(2)]
        self.compared, self.counted, self.step = a.sem("rep_compared"), a.sem("rep_counted"), a.sem("rep_step")
        self.masked = a.sem("rep_masked")

    def load(self, sp):
        SET = self.SET
        with sp.Fori(0, CH // (2 * SET)) as i:
            for s in range(2):
                sp.wait_ge(self.compared, i * 2)
                first = i * (2 * SET * P) + s * SET * P
                sp.dma_start(self.keys[s][:].rearrange("p u j -> p (u j)"),
                             row_of(self.S.src_pad[bass.ds(first, SET * P)]).broadcast_to([P, SET * P])
                             ).then_inc(self.keys_landed[s], 16)

    def find(self, dve):
        S, SET, later, row = self.S, self.SET, self.later, self.row
        st = Steps(dve, self.step)
        st(dve.tensor_scalar(self.later_mask[:], S.iota_row[:], S.part_col[:, 0:1], None, ALU.is_gt))
        with dve.Fori(0, CH // (2 * SET)) as i:
            cols = [bass.ds(i * (2 * SET) + s * SET, SET) for s in range(2)]
            for s in range(2):
                dve.wait_ge(self.keys_landed[s], i * 16 + 16)
                dve.wait_ge(self.counted, i * 2)
                dve.tensor_tensor(self.same[s][:], self.keys[s][:],
                                  S.src_c[:, cols[s]].unsqueeze(2).broadcast_to([P, SET, P]),
                                  ALU.is_equal).then_inc(self.compared, 1)
            for s in range(2):
                dve.wait_ge(self.compared, i * 2 + s + 1)
                dve.tensor_tensor(self.same[s][:], self.same[s][:],
                                  self.later_mask[:].unsqueeze(1).broadcast_to([P, SET, P]),
                                  ALU.mult).then_inc(self.masked, 1)
            for s in range(2):
                dve.wait_ge(self.masked, i * 2 + s + 1)
                dve.tensor_reduce(later[:, cols[s]], self.same[s][:], AX.X, ALU.max).then_inc(self.counted, 1)
        dve.wait_ge(self.counted, CH // SET)
        st(dve.tensor_scalar(self.dummy[:], S.part_col[:], float(N), None, ALU.add))
        st(dve.tensor_scalar(row[:], S.src_c[:], self.dummy[:, 0:1], None, ALU.subtract))
        st(dve.tensor_tensor(later[:], row[:], later[:], ALU.mult))
        st(dve.tensor_tensor(row[:], S.src_c[:], later[:], ALU.subtract))
        dve.tensor_copy(S.row_rep[:], row[:])


def layernorm_stats(nc, S, tag, x, eps=1e-5):
    with stage(nc, tag) as a:
        stats = a.sb("stats", [TP, NT, 6])
        mv = a.sb("mv", [TP, NT, 2])
        counted, var_ready, root_ready, step_s = a.sem("counted"), a.sem("var_ready"), a.sem("root_ready"), a.sem("step")
        with nc.Block() as block:
            @block.vector
            def _(dve):
                with dve.Fori(0, NG) as i:
                    for u in range(GROUP):
                        t = i * GROUP + u
                        dve.bn_stats(stats[:, bass.ds(t, 1), :].rearrange("p a s -> p (a s)"),
                                     x[:, bass.ds(t, 1), :].rearrange("p a d -> p (a d)")).then_inc(counted, 1)
                dve.wait_ge(counted, NT)
                for t in range(NT):
                    last = dve.bn_aggr(mv[:, t, :], stats[:, t, :])
                    last.then_inc(counted, 1)
                dve.wait_ge(counted, 2 * NT)
                dve.tensor_scalar(S.ln_r[:], mv[:, :, 1], eps, None, ALU.add).then_inc(var_ready, 1)
                dve.wait_ge(root_ready, 1)
                st = Steps(dve, step_s)
                st(dve.reciprocal(S.ln_r[:], S.ln_r[:]))
                dve.scalar_tensor_tensor(S.ln_b[:], mv[:, :, 0], -1.0, S.ln_r[:], ALU.mult, ALU.mult)

            @block.scalar
            def _(act):
                act.wait_ge(var_ready, 1)
                nc.scalar.activation(S.ln_r[:], S.ln_r[:], ACT.Sqrt).then_inc(root_ready, 1)


def col(ap, t):
    return ap[:, bass.ds(t, 1)]


def tile(ap, t):
    return ap[:, bass.ds(t, 1), :].rearrange("p a d -> p (a d)")


def mix0(nc, g, S, w_conv, bn_gamma, bn_beta, w_dw, pw_blocks, w_res, b_res, pool_work):
    C6 = 6
    with stage(nc, "m0_") as a:
        h = a.sb("h", [P, C6, N])
        affine = a.sb("affine", [P, C6, 2])
        pw = a.sb("pw", [P, C6, P])
        wres = a.sb("wres", [P, 4, D])
        bres = a.sb("bres", [TP, D])
        group_ones = a.sb("group_ones", [P, P])
        weights_in = a.sem("weights_in")

        with stage(nc, "m0a_") as b:
            wconv = b.sb("wconv", [P, 2, C6 * P])
            dw = b.sb("dw", [P, C6])
            gb = b.sb("gb", [P, 2, C6])
            sq_junk = b.sb("sq_junk", [TP, D])
            ss, m, lo, hi, pick, sc, sr, sb_ = (b.sb(n, [TP, NT]) for n in (
                "ss", "m", "lo", "hi", "pick", "sc", "sr", "sb"))
            xm = [b.sb(f"xm{s}", [TP, D]) for s in range(2)]
            xt = [b.sb(f"xt{s}", [P, 2, TP]) for s in range(2)]
            stats = b.sb("stats", [P, C6, 7, 6])
            mv = b.sb("mv", [P, C6, 2])
            turn_ps = b.ps("turn", [P, 2, 512])
            conv_ps = b.ps("conv", [P, 2, 2, 512])
            squared, step_s, roots, logs = b.sem("squared"), b.sem("step"), b.sem("roots"), b.sem("logs")
            scaled, turned, turn_copied = b.sem("scaled"), b.sem("turned"), b.sem("turn_copied")
            conv_done, conv_copied, bn_step, bn_root = (
                b.sem("conv_done"), b.sem("conv_copied"), b.sem("bn_step"), b.sem("bn_root"))
            affine_ready, zeroed, root_asked = b.sem("affine_ready"), b.sem("zeroed"), b.sem("root_asked")
            WIDTHS = [448] * 6 + [N - 6 * 448]
            with nc.Block() as block:
                @block.sync
                def _(sp):
                    sp.dma_start(wconv[:], w_conv.rearrange("(k p) c -> p k c", p=P)).then_inc(weights_in, 16)
                    for n, x in enumerate((bn_gamma, bn_beta)):
                        sp.dma_start(gb[:, n, :], x.rearrange("(c p) -> p c", p=P),
                                     allow_slow_non_contiguous=True).then_inc(weights_in, 16)
                    sp.dma_start(dw[:], w_dw.rearrange("(c p) -> p c", p=P),
                                 allow_slow_non_contiguous=True).then_inc(weights_in, 16)
                    sp.dma_start(wres[:], w_res.rearrange("(k p) c -> p k c", p=P)).then_inc(weights_in, 16)
                    sp.dma_start(bres[:], spread(b_res, TP)).then_inc(weights_in, 16)
                    sp.wait_ge(zeroed, 1)
                    for q in range(4):
                        sp.dma_start(pw[32 * q:32 * q + 32, :, 32 * q:32 * q + 32], pw_blocks[q]).then_inc(weights_in, 16)

                @block.scalar
                def _(act):
                    with act.Fori(0, NG) as i:
                        for u in range(GROUP):
                            t = i * GROUP + u
                            act.wait_ge(squared, i * GROUP + u)
                            nc.scalar.activation(sq_junk[:], tile(S.x, t), ACT.Square, scale=col(S.ln_r, t),
                                                 bias=col(S.ln_b, t), accum_out=col(ss, t)).then_inc(squared, 1)
                    act.wait_ge(root_asked, 1)
                    nc.scalar.activation(m[:], ss[:], ACT.Sqrt).then_inc(roots, 1)
                    act.wait_ge(root_asked, 2)
                    nc.scalar.activation(lo[:], lo[:], ACT.Ln).then_inc(logs, 1)
                    nc.scalar.activation(hi[:], hi[:], ACT.Ln).then_inc(logs, 1)

                    def copy(i, u):
                        act.wait_ge(turned, ready(i, u, PIPE))
                        act.wait_ge(conv_done, freed(i, u, 2, PIPE))
                        nc.scalar.copy(xt[u % 2][:], turn_ps[:, u % 2, 0:2 * TP].rearrange("p (k n) -> p k n", k=2)
                                       ).then_inc(turn_copied, 1)

                    pipeline(act, (0, copy))
                    act.wait_ge(bn_root, 1)
                    nc.scalar.activation(affine[:, :, 0], affine[:, :, 0], ACT.Sqrt).then_inc(bn_root, 1)
                    act.wait_ge(affine_ready, 1)
                    for c in range(C6):
                        nc.scalar.activation(h[:, c, :], h[:, c, :], ACT.Relu, scale=affine[:, c, 0:1],
                                             bias=affine[:, c, 1:2])

                @block.vector
                def _(dve):
                    st = Steps(dve, step_s)
                    dve.memset(pw[:], 0.0).then_inc(zeroed, 1)
                    st(dve.memset(group_ones[:], 0.0))
                    for q in range(4):
                        dve.memset(group_ones[32 * q:32 * q + 32, 32 * q:32 * q + 32], 1.0)
                    dve.wait_ge(squared, NT)
                    dve.tensor_scalar(ss[:], ss[:], MIN_NORM * MIN_NORM, None, ALU.max).then_inc(root_asked, 1)
                    dve.wait_ge(roots, 1)
                    st(dve.reciprocal(sc[:], m[:]))
                    st(dve.tensor_scalar(m[:], m[:], MAXNORM, None, ALU.min))
                    st(dve.tensor_scalar(lo[:], m[:], -1.0, 1.0, ALU.mult, ALU.add))
                    dve.tensor_scalar(hi[:], m[:], 1.0, None, ALU.add).then_inc(root_asked, 1)
                    st(dve.tensor_tensor(sr[:], m[:], m[:], ALU.mult))
                    st(dve.tensor_scalar(sb_[:], sr[:], 1.0 / 7, 1.0 / 5, ALU.mult, ALU.add))
                    st(dve.tensor_tensor(sb_[:], sb_[:], sr[:], ALU.mult))
                    st(dve.tensor_scalar(sb_[:], sb_[:], 1.0 / 3, None, ALU.add))
                    st(dve.tensor_tensor(sb_[:], sb_[:], sr[:], ALU.mult))
                    st(dve.scalar_tensor_tensor(sb_[:], sb_[:], 1.0, m[:], ALU.add, ALU.mult))
                    st(dve.tensor_scalar(pick[:], m[:], 0.0625, None, ALU.is_lt))
                    dve.wait_ge(logs, 2)
                    st(dve.tensor_tensor(hi[:], hi[:], lo[:], ALU.subtract))
                    st(dve.tensor_scalar(hi[:], hi[:], 0.5, None, ALU.mult))
                    st(dve.tensor_tensor(sb_[:], sb_[:], hi[:], ALU.subtract))
                    st(dve.tensor_tensor(sb_[:], sb_[:], pick[:], ALU.mult))
                    st(dve.tensor_tensor(hi[:], hi[:], sb_[:], ALU.add))
                    st(dve.tensor_tensor(sc[:], sc[:], hi[:], ALU.mult))
                    st(dve.tensor_tensor(sr[:], S.ln_r[:], sc[:], ALU.mult))
                    st(dve.tensor_tensor(sb_[:], S.ln_b[:], sc[:], ALU.mult))

                    def log_map(i, u):
                        t = i * PIPE + u
                        dve.wait_ge(turned, freed(i, u, 2, PIPE))
                        dve.tensor_scalar(xm[u % 2][:], tile(S.x, t), col(sr, t), col(sb_, t), ALU.mult,
                                          ALU.add).then_inc(scaled, 1)

                    def keep(i, u):
                        dve.wait_ge(conv_done, ready(i, u, PIPE))
                        dve.tensor_copy(h[:, :, bass.ds((i * PIPE + u) * TP, TP)].rearrange("p (b c) n -> p b c n", b=2),
                                        conv_ps[:, u % 2, :, 0:3 * TP].rearrange("p b (c n) -> p b c n", c=3)
                                        ).then_inc(conv_copied, 1)

                    pipeline(dve, (0, log_map), (2, keep))
                    dve.wait_ge(conv_copied, NT)
                    for c in range(C6):
                        for w, width in enumerate(WIDTHS):
                            last = dve.bn_stats(stats[:, c, w, :], h[:, c, 448 * w:448 * w + width])
                    bn = Steps(dve, bn_step)
                    bn(last)
                    for c in range(C6):
                        last = dve.bn_aggr(mv[:, c, :], stats[:, c].rearrange("p w s -> p (w s)"))
                    bn(last)
                    dve.tensor_scalar(affine[:, :, 0], mv[:, :, 1], 1e-5, None, ALU.add).then_inc(bn_root, 1)
                    dve.wait_ge(bn_root, 2)
                    dve.wait_ge(weights_in, 160)
                    bn(dve.reciprocal(affine[:, :, 0], affine[:, :, 0]))
                    bn(dve.tensor_tensor(affine[:, :, 0], affine[:, :, 0], gb[:, 0, :], ALU.mult))
                    bn(dve.tensor_tensor(affine[:, :, 1], mv[:, :, 0], affine[:, :, 0], ALU.mult))
                    dve.tensor_tensor(affine[:, :, 1], gb[:, 1, :], affine[:, :, 1],
                                      ALU.subtract).then_inc(affine_ready, 1)
                    for c in range(C6):
                        dve.tensor_scalar(pw[:, c, :], pw[:, c, :], dw[:, c:c + 1], None, ALU.mult)

                @block.tensor
                def _(pe):
                    pe.wait_ge(weights_in, 160)

                    def turn(i, u):
                        pe.wait_ge(scaled, ready(i, u, PIPE))
                        pe.wait_ge(turn_copied, freed(i, u, 2, PIPE))
                        for k in range(2):
                            last = pe.transpose(turn_ps[:, u % 2, k * TP:(k + 1) * TP],
                                                xm[u % 2][:, k * P:(k + 1) * P], S.ident[0:TP, 0:TP])
                        last.then_inc(turned, 1)

                    def convolve(i, u):
                        pe.wait_ge(turn_copied, ready(i, u, PIPE))
                        pe.wait_ge(conv_copied, freed(i, u, 2, PIPE))
                        for c in range(C6):
                            for k in range(2):
                                last = pe.matmul(conv_ps[:, u % 2, c // 3, (c % 3) * TP:(c % 3 + 1) * TP],
                                                 wconv[:, k, c * P:(c + 1) * P], xt[u % 2][:, k, :],
                                                 start=(k == 0), stop=(k == 1))
                        last.then_inc(conv_done, 1)

                    pipeline(pe, (0, turn), (1, convolve))

        with stage(nc, "m0b_") as b:
            t_sq = b.sb("t_sq", [P, C6, TP])
            cat = [b.sb(f"cat{s}", [P, 3, 4, TP]) for s in range(2)]
            cat_sq = b.sb("cat_sq", [P, 3, 4, TP])
            n1, r1, n2, r2 = (b.sb(n, [P, TP]) for n in ("n1", "r1", "n2", "r2"))
            rq, rk, vv, o = (b.sb(n, [P, 4, TP]) for n in ("rq", "rk", "vv", "o"))
            o_sq = t_sq[:, 0:4, :]
            rv = cat_sq[:, 0]
            ss3, f3, ss4, f4 = (b.sb(n, [TP, NT]) for n in ("ss3", "f3", "ss4", "f4"))
            junk = t_sq[0:TP].rearrange("p c n -> p (c n)")[:, 0:D]
            norm_ps = b.ps("norm", [P, 2, 512])
            point_ps = b.ps("point", [P, 2, 512])
            ksum_ps = b.ps("ksum", [P, 512])
            proj_ps = b.ps("proj", [TP, 512])
            n3_ps = b.ps("n3", [TP, 512])
            names = ("t_squared", "n1_mm", "n1_in", "n1_root", "t_made", "point_mm", "point_copied", "cat_squared",
                     "n2_mm", "n2_in", "n2_root", "rk_made", "cat_used", "k_summed", "o_made", "o_squared", "n3_mm", "n3_copied",
                     "proj_mm", "proj_copied", "step1", "step2", "step3", "f3_in", "f3_root", "f3_done", "sq4", "biased", "f4_root", "f4_in", "f4_step")
            (t_squared, n1_mm, n1_in, n1_root, t_made, point_mm, point_copied, cat_squared, n2_mm, n2_in, n2_root,
             rk_made, cat_used, k_summed, o_made, o_squared, n3_mm, n3_copied, proj_mm, proj_copied, step1, step2, step3, f3_in, f3_root,
             f3_done, sq4, biased, f4_root, f4_in, f4_step) = (b.sem(n) for n in names)
            with nc.Block() as block:
                @block.gpsimd
                def _(pool):
                    pool_work(pool)

                @block.scalar
                def _(act):
                    def tap(i, u):
                        act.wait_ge(n1_mm, freed(i, u, 1, PIPE))
                        act.wait_ge(n3_mm, i * PIPE + max(u - 2, 0))
                        nc.scalar.activation(t_sq[:], h[:, :, bass.ds((i * PIPE + u) * TP, TP)],
                                             ACT.Square).then_inc(t_squared, 1)

                    def tap_root(i, u):
                        act.wait_ge(n1_in, ready(i, u, PIPE))
                        nc.scalar.activation(n1[:], n1[:], ACT.Sqrt).then_inc(n1_root, 1)

                    def point(i, u):
                        act.wait_ge(point_mm, ready(i, u, PIPE))
                        for c, n in ((0, 2), (2, 1), (3, 1), (4, 2)):
                            nc.scalar.copy(cat[u % 2][:, c // 2, 2 + c % 2:2 + c % 2 + n, :].rearrange("p c n -> p (c n)"),
                                           point_ps[:, c // 3, (c % 3) * TP:(c % 3 + n) * TP]).then_inc(point_copied, 1)
                        act.wait_ge(t_made, ready(i, u, PIPE))
                        act.wait_ge(point_copied, i * (4 * PIPE) + 4 * (u + 1))
                        act.wait_ge(n2_mm, freed(i, u, 1, PIPE))
                        act.wait_ge(step2, (i * PIPE + u) * 6)
                        nc.scalar.activation(cat_sq[:], cat[u % 2][:], ACT.Square).then_inc(cat_squared, 1)

                    def point_root(i, u):
                        act.wait_ge(n2_in, ready(i, u, PIPE))
                        nc.scalar.activation(n2[:], n2[:], ACT.Sqrt).then_inc(n2_root, 1)

                    def attend(i, u):
                        t = i * PIPE + u
                        act.wait_ge(o_made, ready(i, u, PIPE))
                        act.wait_ge(n3_mm, freed(i, u, 1, PIPE))
                        act.wait_ge(n1_mm, capped(i * PIPE + u + 3))
                        nc.scalar.activation(o_sq, o[:], ACT.Square).then_inc(o_squared, 1)

                    def results(i, u):
                        t = i * PIPE + u
                        act.wait_ge(proj_mm, ready(i, u, PIPE))
                        nc.scalar.copy(tile(S.fx, t), proj_ps[:, 0:D]).then_inc(proj_copied, 1)
                        act.wait_ge(n3_mm, ready(i, u, PIPE))
                        nc.scalar.copy(col(ss3, t), n3_ps[:, 0:1]).then_inc(n3_copied, 1)

                    pipeline(act, (0, tap), (1, point), (2, attend), (0, tap_root), (2, results), (1, point_root))
                    act.wait_ge(f3_in, 1)
                    nc.scalar.activation(f3[:], ss3[:], ACT.Sqrt).then_inc(f3_root, 1)
                    with act.Fori(0, NG) as i:
                        for u in range(GROUP):
                            t = i * GROUP + u
                            act.wait_ge(biased, ready(i, u))
                            act.wait_ge(sq4, i * GROUP + u)
                            nc.scalar.activation(junk, tile(S.fx, t), ACT.Square, accum_out=col(ss4, t)).then_inc(sq4, 1)
                    act.wait_ge(f4_in, 1)
                    nc.scalar.activation(ss4[:], ss4[:], ACT.Sqrt).then_inc(f4_root, 1)
                    act.wait_ge(f4_root, 1)
                    nc.scalar.activation(f4[:], ss4[:], ACT.Tanh).then_inc(f4_root, 1)

                @block.vector
                def _(dve):
                    def over(x, m):
                        return x[:].unsqueeze(1).broadcast_to([P, m, TP])

                    def tap(i, u):
                        dve.wait_ge(n1_mm, ready(i, u, PIPE))
                        dve.tensor_scalar(n1[:], norm_ps[:, 0, 0:TP], MIN_NORM * MIN_NORM, None, ALU.max).then_inc(n1_in, 1)
                        dve.wait_ge(n1_root, ready(i, u, PIPE))
                        after(dve, dve.reciprocal(r1[:], n1[:]), step1, (i * PIPE + u) * 2 + 1)
                        after(dve, dve.scalar_tensor_tensor(r1[:], n1[:], ATANH_MAX, r1[:], ALU.min, ALU.mult),
                              step1, (i * PIPE + u) * 2 + 2)
                        dve.wait_ge(cat_squared, freed(i, u, 2, PIPE))
                        hv = h[:, :, bass.ds((i * PIPE + u) * TP, TP)].rearrange("p (r c) n -> p r c n", r=3)
                        for r in range(3):
                            ins = dve.tensor_tensor(cat[u % 2][:, r, 0:2, :], hv[:, r], over(r1, 2), ALU.mult)
                        ins.then_inc(t_made, 1)

                    def point(i, u):
                        c = cat[u % 2]
                        base = (i * PIPE + u) * 6
                        dve.wait_ge(n2_mm, ready(i, u, PIPE))
                        dve.tensor_scalar(n2[:], norm_ps[:, 1, 0:TP], MIN_NORM * MIN_NORM, None, ALU.max).then_inc(n2_in, 1)
                        dve.wait_ge(n2_root, ready(i, u, PIPE))
                        after(dve, dve.reciprocal(r2[:], n2[:]), step2, base + 1)
                        after(dve, dve.scalar_tensor_tensor(r2[:], n2[:], ATANH_MAX, r2[:], ALU.min, ALU.mult),
                              step2, base + 2)
                        dve.wait_ge(k_summed, freed(i, u, 1, PIPE))
                        dve.scalar_tensor_tensor(rk[:], c[:, 1], 0.0, over(r2, 4), ALU.max, ALU.mult).then_inc(rk_made, 1)
                        dve.tensor_tensor(vv[:], c[:, 2], over(r2, 4), ALU.mult).then_inc(step2, 1)
                        dve.scalar_tensor_tensor(rq[:], c[:, 0], 0.0, over(r2, 4), ALU.max, ALU.mult).then_inc(cat_used, 1)
                        dve.wait_ge(step2, base + 3)
                        after(dve, dve.tensor_scalar(rv, vv[:], 1e-15, None, ALU.add), step2, base + 4)
                        after(dve, dve.reciprocal(rv, rv), step2, base + 5)
                        dve.tensor_tensor(vv[:], vv[:], rv, ALU.mult).then_inc(step2, 1)

                    def attend(i, u):
                        dve.wait_ge(cat_used, ready(i, u, PIPE))
                        dve.wait_ge(step2, (i * PIPE + u) * 6 + 6)
                        dve.wait_ge(k_summed, ready(i, u, PIPE))
                        dve.wait_ge(proj_mm, freed(i, u, 1, PIPE))
                        dve.wait_ge(o_squared, freed(i, u, 1, PIPE))
                        after(dve, dve.tensor_tensor(o[:].rearrange("p a n -> p (a n)"), rq[:].rearrange("p a n -> p (a n)"),
                                                     ksum_ps[:, 0:4 * TP], ALU.mult), step3, i * PIPE + u + 1)
                        dve.tensor_tensor(o[:], o[:], vv[:], ALU.mult).then_inc(o_made, 1)

                    pipeline(dve, (2, attend), (0, tap), (1, point))
                    st = Steps(dve, f4_step)
                    dve.wait_ge(n3_copied, NT)
                    dve.tensor_scalar(ss3[:], ss3[:], MIN_NORM * MIN_NORM, None, ALU.max).then_inc(f3_in, 1)
                    dve.wait_ge(f3_root, 1)
                    st(dve.reciprocal(ss3[:], f3[:]))
                    st(dve.scalar_tensor_tensor(f3[:], f3[:], ATANH_MAX, ss3[:], ALU.min, ALU.mult))
                    dve.wait_ge(proj_copied, NT)
                    with dve.Fori(0, NG) as i:
                        for u in range(GROUP):
                            t = i * GROUP + u
                            dve.scalar_tensor_tensor(tile(S.fx, t), tile(S.fx, t), col(f3, t), bres[:], ALU.mult,
                                                     ALU.add).then_inc(biased, 1)
                    dve.wait_ge(sq4, NT)
                    dve.tensor_scalar(ss4[:], ss4[:], MIN_NORM * MIN_NORM, None, ALU.max).then_inc(f4_in, 1)
                    dve.wait_ge(f4_root, 2)
                    st(dve.reciprocal(ss4[:], ss4[:]))
                    st(dve.scalar_tensor_tensor(f4[:], f4[:], MAXNORM, ss4[:], ALU.min, ALU.mult))
                    with dve.Fori(0, NG) as i:
                        for u in range(GROUP):
                            t = i * GROUP + u
                            dve.tensor_scalar(tile(S.fx, t), tile(S.fx, t), col(f4, t), None, ALU.mult)

                @block.tensor
                def _(pe):
                    def tap(i, u):
                        pe.wait_ge(t_squared, ready(i, u, PIPE))
                        pe.wait_ge(n1_in, freed(i, u, 1, PIPE))
                        for k in range(C6):
                            last = pe.matmul(norm_ps[:, 0, 0:TP], S.ones[:], t_sq[:, k, :],
                                             start=(k == 0), stop=(k == C6 - 1))
                        last.then_inc(n1_mm, 1)

                    def point(i, u):
                        c = cat[u % 2]
                        pe.wait_ge(t_made, ready(i, u, PIPE))
                        pe.wait_ge(point_copied, i * (4 * PIPE) + 4 * u)
                        for k in range(C6):
                            last = pe.matmul(point_ps[:, k // 3, (k % 3) * TP:(k % 3 + 1) * TP], pw[:, k, :],
                                             c[:, k // 2, k % 2, :], start=True, stop=True)
                        last.then_inc(point_mm, 1)

                    def norm(i, u):
                        pe.wait_ge(cat_squared, ready(i, u, PIPE))
                        pe.wait_ge(n2_in, freed(i, u, 1, PIPE))
                        for k in range(12):
                            last = pe.matmul(norm_ps[:, 1, 0:TP], S.ones[:], cat_sq[:, k // 4, k % 4, :],
                                             start=(k == 0), stop=(k == 11))
                        last.then_inc(n2_mm, 1)

                    def sum_keys(i, u):
                        pe.wait_ge(rk_made, ready(i, u, PIPE))
                        pe.wait_ge(o_made, freed(i, u, 1, PIPE))
                        pe.matmul(ksum_ps[:, 0:4 * TP], group_ones[:], rk[:].rearrange("p a n -> p (a n)"),
                                  start=True, stop=True).then_inc(k_summed, 1)

                    def attend(i, u):
                        pe.wait_ge(o_made, ready(i, u, PIPE))
                        pe.wait_ge(proj_copied, freed(i, u, 1, PIPE))
                        for k in range(4):
                            last = pe.matmul(proj_ps[:, 0:D], o[:, k, :], wres[:, k, :], start=(k == 0), stop=(k == 3))
                        last.then_inc(proj_mm, 1)
                        pe.wait_ge(o_squared, ready(i, u, PIPE))
                        pe.wait_ge(n3_copied, freed(i, u, 1, PIPE))
                        for k in range(4):
                            last = pe.matmul(n3_ps[:, 0:1], o_sq[:, k, :], S.ones[:, 0:1], start=(k == 0), stop=(k == 3))
                        last.then_inc(n3_mm, 1)

                    pipeline(pe, (1, point), (0, tap), (2, attend), (1, norm), (1, sum_keys))


def load_nodes(nc, g, S, x):
    S.x = g.sb("x", [TP, NT, D])
    S.fx_rows = nc.dram_tensor("fx_rows", [N, D], F32, kind="Internal").ap()
    S.ln_r, S.ln_b = g.sb("ln_r", [TP, NT]), g.sb("ln_b", [TP, NT])
    loaded = g.sem("x_loaded")
    with nc.Block() as block:
        @block.sync
        def _(sp):
            sp.dma_start(S.x[:], tiles_of(x)).then_inc(loaded, 16)
            sp.wait_ge(loaded, 16)


def slot_uses(i, u):
    return i * ((GROUP + 1) // 2 if u % 2 == 0 else GROUP // 2) + u // 2


def load_projection(nc, keep, a, W, W_T, q, k, H, width, chunks):
    OC = width // P
    w = keep.sb("w", [P, chunks, 2, width])
    wqk = keep.sb("wqk", [P, chunks, 2, 2, H])
    w_t = [a.sb(f"w_t{r}", [P, OC, chunks * P]) for r in range(2)]
    qk = a.sb("qk", [P, OC, 2, H])
    wqk_ps = a.ps("wqk_ps", [P, 512])
    loaded, multiplied = a.sem("w_loaded"), a.sem("wqk_multiplied")
    with nc.Block() as block:
        @block.sync
        def _(sp):
            sp.dma_start(qk[:, :, 0, :], q.rearrange("(c p) h -> p c h", p=P),
                         allow_slow_non_contiguous=True).then_inc(loaded, 16)
            sp.dma_start(qk[:, :, 1, :], k.rearrange("(c p) h -> p c h", p=P),
                         allow_slow_non_contiguous=True).then_inc(loaded, 16)
            for r in range(2):
                sp.dma_start(w_t[r][:], W_T[r].rearrange("(c p) i -> p c i", p=P)).then_inc(loaded, 16)
                sp.dma_start(w[:, :, r, :], W[r].rearrange("(c p) o -> p c o", p=P)).then_inc(loaded, 16)

        @block.tensor
        def _(pe):
            pe.wait_ge(loaded, 96)
            for c in range(chunks):
                for r in range(2):
                    at = (c * 2 + r) * 2 * H
                    for o in range(OC):
                        last = pe.matmul(wqk_ps[:, at:at + 2 * H], w_t[r][:, o, c * P:(c + 1) * P],
                                         qk[:, o].rearrange("p s h -> p (s h)"), start=(o == 0), stop=(o == OC - 1))
            last.then_inc(multiplied, 1)

        @block.vector
        def _(dve):
            dve.wait_ge(multiplied, 1)
            dve.tensor_copy(wqk[:].rearrange("p c r s h -> p (c r s h)"), wqk_ps[:, 0:chunks * 4 * H])
    return w, wqk


class Projector:

    def __init__(self, nc, S, a, w, wqk, width, H, table, k_tab, const=None):
        self.nc, self.w, self.wqk, self.width, self.H, self.const = nc, w, wqk, width, H, const
        self.S, self.table, self.k_tab = S, table, k_tab
        self.out = [a.sb(f"proj_out{s}", [TP, 2, width]) for s in range(2)]
        self.k = [a.sb(f"proj_k{s}", [TP, 2, H]) for s in range(2)]
        self.ps = a.ps("proj_ps", [TP, 2, 512])
        self.qk_ps = a.ps("proj_qk_ps", [TP, 512])
        self.done, self.copied = a.sem("proj_done"), a.sem("proj_copied")
        self.stored = [a.sem(f"proj_stored{s}") for s in range(2)]
        self.DMAS = 3

    def multiply(self, pe, i, u, chunks):
        pe.wait_ge(self.copied, i * (3 * PIPE) + 3 * u)
        n = len(chunks)
        for r in range(2):
            for c, x in enumerate(chunks):
                pe.matmul(self.ps[:, r, 0:self.width], x, self.w[:, c, r, :], start=(c == 0),
                          stop=(c == n - 1 and self.const is None))
            if self.const is not None:
                pe.matmul(self.ps[:, r, 0:self.width], self.const[2], self.const[0][0:1, r, :], start=False, stop=True)
        for c, x in enumerate(chunks):
            last = pe.matmul(self.qk_ps[:, 0:4 * self.H], x, self.wqk[:, c].rearrange("p r s h -> p (r s h)"),
                             start=(c == 0), stop=(c == n - 1 and self.const is None))
        if self.const is not None:
            last = pe.matmul(self.qk_ps[:, 0:4 * self.H], self.const[2], self.const[1][0:1, :], start=False, stop=True)
        last.then_inc(self.done, 1)

    def copy(self, act, i, u):
        s = u % 2
        act.wait_ge(self.done, ready(i, u, PIPE))
        act.wait_ge(self.stored[s], (i * (PIPE // 2) + u // 2) * (16 * self.DMAS))
        self.nc.scalar.copy(self.out[s][:], self.ps[:, :, 0:self.width]).then_inc(self.copied, 1)
        both = self.qk_ps[:, 0:4 * self.H].rearrange("p (r s h) -> p r s h", r=2, s=2)
        at = self.S.q_node[:, bass.ds(i * PIPE + u, 1), 0:2 * self.H].rearrange("p a (r h) -> p (a r) h", r=2)
        self.nc.scalar.copy(at, both[:, :, 0]).then_inc(self.copied, 1)
        self.nc.scalar.copy(self.k[s][:], both[:, :, 1]).then_inc(self.copied, 1)

    def store(self, sp, i, u):
        s = u % 2
        t = i * PIPE + u
        rows = bass.ds(t * TP, TP)
        sp.wait_ge(self.copied, i * (3 * PIPE) + 3 * u + 3)
        for r in range(2):
            sp.dma_start(self.table[r * N:(r + 1) * N, :][rows, :], self.out[s][:, r, :]).then_inc(self.stored[s], 16)
        sp.dma_start(self.k_tab.rearrange("(r n) h -> n r h", r=2)[rows], self.k[s][:],
                     allow_slow_non_contiguous=True).then_inc(self.stored[s], 16)

    def finish(self, sp):
        for s in range(2):
            uses = (NT + 1 - s) // 2
            sp.wait_ge(self.stored[s], uses * 16 * self.DMAS)


def gnn_first(nc, S, query, gate_w1, gate_b1, gate_w2, gate_b2, W, W_T, q, k):
    width = HEADS * HID
    with stage(nc, "g1_") as a:
        w = a.sb("w4", [P, 4, 2, width])
        wqk = a.sb("wqk4", [P, 4, 2, 2, HEADS])
        const_row = a.sb("const_row", [1, 2, width])
        const_qk = a.sb("const_qk", [1, 4 * HEADS])
        qcol = a.sb("qcol", [P, 2])
        gw1, gw2 = a.sb("gw1", [P, 4, D]), a.sb("gw2", [P, 2, D])
        gb = a.sb("gb", [P, 2, 2])
        gconst = a.sb("gconst", [P, 2])
        with stage(nc, "g1w_") as b:
            w6, wqk6 = load_projection(nc, b, b, W, W_T, q, k, HEADS, width, 6)
            row_ps, gate_ps = b.ps("row_ps", [1, 3, 512]), b.ps("gate_ps", [P, 512])
            loaded, multiplied = b.sem("loaded"), b.sem("multiplied")
            with nc.Block() as block:
                @block.sync
                def _(sp):
                    sp.dma_start(qcol[:], query[0].rearrange("(k p) -> p k", p=P),
                                 allow_slow_non_contiguous=True).then_inc(loaded, 16)
                    sp.dma_start(gw1[:], gate_w1.rearrange("(k p) c -> p k c", p=P)).then_inc(loaded, 16)
                    sp.dma_start(gw2[:], gate_w2.rearrange("(k p) c -> p k c", p=P)).then_inc(loaded, 16)
                    for n, x in enumerate((gate_b1, gate_b2)):
                        sp.dma_start(gb[:, n, :], x.rearrange("(k p) -> p k", p=P),
                                     allow_slow_non_contiguous=True).then_inc(loaded, 16)

                @block.tensor
                def _(pe):
                    pe.wait_ge(loaded, 80)
                    for r in range(2):
                        for c in range(2):
                            pe.matmul(row_ps[:, r, :], qcol[:, c:c + 1], w6[:, 2 + c, r, :], start=(c == 0), stop=(c == 1))
                    for c in range(2):
                        pe.matmul(row_ps[:, 2, 0:4 * HEADS], qcol[:, c:c + 1],
                                  wqk6[:, 2 + c].rearrange("p r s h -> p (r s h)"), start=(c == 0), stop=(c == 1))
                    for o in range(2):
                        for c in range(2):
                            last = pe.matmul(gate_ps[:, o:o + 1], gw1[:, 2 + c, o * P:(o + 1) * P], qcol[:, c:c + 1],
                                             start=(c == 0), stop=(c == 1))
                    last.then_inc(multiplied, 1)

                @block.vector
                def _(dve):
                    dve.wait_ge(loaded, 80)
                    dve.tensor_copy(w[:, 0:2], w6[:, 0:2])
                    dve.tensor_copy(wqk[:, 0:2], wqk6[:, 0:2])
                    for c in range(2):
                        dve.tensor_scalar(w[:, 2 + c], w6[:, 4 + c], qcol[:, c:c + 1], None, ALU.mult)
                        dve.tensor_scalar(wqk[:, 2 + c], wqk6[:, 4 + c], qcol[:, c:c + 1], None, ALU.mult)
                    dve.wait_ge(multiplied, 1)
                    dve.tensor_copy(const_row[:], row_ps[:, 0:2, :])
                    dve.tensor_copy(const_qk[:], row_ps[:, 2, 0:4 * HEADS])
                    dve.tensor_tensor(gconst[:], gate_ps[:, 0:2], gb[:, 0, :], ALU.add)

        with stage(nc, "g1t_") as b:
            proj = Projector(nc, S, b, w, wqk, width, HEADS, S.table, S.k_tab,
                             const=(const_row, const_qk, S.ones[0:1, 0:TP]))
            xn = [b.sb(f"xn{s}", [TP, D]) for s in range(2)]
            xt = [b.sb(f"xt{s}", [P, 2, TP]) for s in range(PIPE)]
            x0 = [b.sb(f"x0{s}", [P, 2, TP]) for s in range(PIPE)]
            gh, gate = b.sb("gh", [P, 2, TP]), b.sb("gate", [P, 2, TP])
            turn_ps = b.ps("turn", [P, 512])
            gate_ps = b.ps("gate_ps", [P, 2, 512])
            normed, turned, turn_copied, hidden_mm, hidden, gate_mm, gated, x0_made = (
                b.sem(n) for n in ("normed", "turned", "turn_copied", "hidden_mm", "hidden", "gate_mm", "gated", "x0_made"))
            x0_stored = [b.sem(f"x0_stored{s}") for s in range(PIPE)]
            with nc.Block() as block:
                @block.vector
                def _(dve):
                    def norm(i, u):
                        t = i * PIPE + u
                        dve.wait_ge(turned, freed(i, u, 2, PIPE))
                        dve.tensor_scalar(xn[u % 2][:], tile(S.x, t), col(S.ln_r, t), col(S.ln_b, t), ALU.mult,
                                          ALU.add).then_inc(normed, 1)

                    def gate_it(i, u):
                        dve.wait_ge(gated, i * (2 * PIPE) + 2 * u + 2)
                        dve.wait_ge(proj.done, freed(i, u, PIPE, PIPE))
                        dve.wait_ge(x0_stored[u % PIPE], (i + u // PIPE) * 16)
                        dve.tensor_tensor(x0[u % PIPE][:], gate[:], xt[u % PIPE][:], ALU.mult).then_inc(x0_made, 1)

                    pipeline(dve, (0, norm), (1, gate_it))

                @block.scalar
                def _(act):
                    def turn(i, u):
                        act.wait_ge(turned, ready(i, u, PIPE))
                        act.wait_ge(proj.done, freed(i, u, PIPE, PIPE))
                        nc.scalar.copy(xt[u % PIPE][:], turn_ps[:, 0:2 * TP].rearrange("p (k n) -> p k n", k=2)
                                       ).then_inc(turn_copied, 1)

                    def gate_it(i, u):
                        act.wait_ge(hidden_mm, ready(i, u, PIPE))
                        for o in range(2):
                            nc.scalar.activation(gh[:, o, :], gate_ps[:, 0, o * TP:(o + 1) * TP], ACT.Relu,
                                                 bias=gconst[:, o:o + 1]).then_inc(hidden, 1)
                        act.wait_ge(gate_mm, ready(i, u, PIPE))
                        act.wait_ge(x0_made, freed(i, u, 1, PIPE))
                        for o in range(2):
                            nc.scalar.activation(gate[:, o, :], gate_ps[:, 1, o * TP:(o + 1) * TP], ACT.Sigmoid,
                                                 bias=gb[:, 1, o:o + 1]).then_inc(gated, 1)

                    pipeline(act, (0, turn), (0, gate_it), (1, lambda i, u: proj.copy(act, i, u)))

                @block.tensor
                def _(pe):
                    def turn(i, u):
                        pe.wait_ge(normed, ready(i, u, PIPE))
                        pe.wait_ge(turn_copied, freed(i, u, 1, PIPE))
                        for c in range(2):
                            last = pe.transpose(turn_ps[:, c * TP:(c + 1) * TP], xn[u % 2][:, c * P:(c + 1) * P],
                                                S.ident[0:TP, 0:TP])
                        last.then_inc(turned, 1)

                    def hide(i, u):
                        pe.wait_ge(turn_copied, ready(i, u, PIPE))
                        pe.wait_ge(hidden, i * (2 * PIPE) + 2 * u)
                        for o in range(2):
                            for c in range(2):
                                last = pe.matmul(gate_ps[:, 0, o * TP:(o + 1) * TP], gw1[:, c, o * P:(o + 1) * P],
                                                 xt[u % PIPE][:, c, :], start=(c == 0), stop=(c == 1))
                        last.then_inc(hidden_mm, 1)

                    def gate_it(i, u):
                        pe.wait_ge(hidden, i * (2 * PIPE) + 2 * u + 2)
                        pe.wait_ge(gated, i * (2 * PIPE) + 2 * u)
                        for o in range(2):
                            for c in range(2):
                                last = pe.matmul(gate_ps[:, 1, o * TP:(o + 1) * TP], gw2[:, c, o * P:(o + 1) * P],
                                                 gh[:, c, :], start=(c == 0), stop=(c == 1))
                        last.then_inc(gate_mm, 1)

                    def project(i, u):
                        pe.wait_ge(x0_made, ready(i, u, PIPE))
                        proj.multiply(pe, i, u, [x0[u % PIPE][:, 0, :], x0[u % PIPE][:, 1, :], xt[u % PIPE][:, 0, :], xt[u % PIPE][:, 1, :]])

                    pipeline(pe, (0, turn), (0, hide), (1, project), (0, gate_it))

                @block.sync
                def _(sp):
                    def store(i, u):
                        t = i * PIPE + u
                        sp.wait_ge(x0_made, ready(i, u, PIPE))
                        sp.dma_start(S.x0_t[bass.ds(t, 1)].rearrange("a p k n -> (a p) k n"),
                                     x0[u % PIPE][:]).then_inc(x0_stored[u % PIPE], 16)
                        proj.store(sp, i, u)

                    pipeline(sp, (0, store))
                    proj.finish(sp)
                    for s in range(PIPE):
                        sp.wait_ge(x0_stored[s], 16 * ((NT + PIPE - 1 - s) // PIPE))


def gnn_nodes(nc, S, tag, width, H, bias, residual=False, wqk=None, next_H=None, k_tab=None, out_w=None,
              out_b=None):
    CHUNKS = width // P
    last_layer = out_w is not None
    with stage(nc, tag) as a:
        if last_layer:
            ow, ob = a.sb("ow", [P, D]), a.sb("ob", [1, D])
            x0 = [a.sb(f"x0{s}", [P, 2, TP]) for s in range(2)]
            x0_landed = [a.sem(f"x0_landed{s}") for s in range(2)]
            junk = a.sb("junk", [TP, D])
        else:
            k_out = [a.sb(f"k_out{s}", [TP, 2, next_H]) for s in range(2)]
            stored = [a.sem(f"stored{s}") for s in range(2)]
        bias_row = a.sb("bias_row", [TP, width])
        den = [a.sb(f"den{s}", [TP, H]) for s in range(2)]
        h = [a.sb(f"h{s}", [TP, width]) for s in range(2)]
        ht = [a.sb(f"ht{s}", [P, CHUNKS, TP]) for s in range(2)]
        turn_ps = a.ps("turn", [P, 2, 512])
        out_ps = a.ps("out_ps", [TP, 2, 512])
        preload = a.sem("preload")
        dstep, h_made, turned, turn_copied, kept, out_mm, out_copied, biased = (
            a.sem(n) for n in ("dstep", "h_made", "turned", "turn_copied", "kept", "out_mm",
                               "out_copied", "biased"))
        sp_go = a.sem("sp_go")

        def turned_rows(t):
            return S.h_t[:, :, bass.ds(t * TP, TP)]

        with nc.Block() as block:
            @block.sync
            def _(sp):
                sp.dma_start(bias_row[:], spread(bias, TP)).then_inc(preload, 16)
                if last_layer:
                    sp.dma_start(ow[:], out_w).then_inc(preload, 16)
                    sp.dma_start(ob[:], row_of(out_b)).then_inc(preload, 16)

                def load(i, u):
                    t = i * GROUP + u
                    if last_layer:
                        sp.wait_ge(out_mm, freed(i, u, 2))
                        sp.dma_start(x0[u % 2][:], S.x0_t[bass.ds(t, 1)].rearrange("a p k n -> (a p) k n")
                                     ).then_inc(x0_landed[u % 2], 16)

                def store(i, u):
                    if not last_layer:
                        sp.wait_ge(out_copied, i * (2 * GROUP) + 2 * u + 2)
                        sp.sem_inc(sp_go, 1)
                        sp.dma_start(k_tab.rearrange("(r n) h -> n r h", r=2)[bass.ds((i * GROUP + u) * TP, TP)],
                                     k_out[u % 2][:], allow_slow_non_contiguous=True).then_inc(stored[u % 2], 16)

                with sp.Fori(0, NG) as i:
                    stagger(i, load, nothing, nothing, store)
                if not last_layer:
                    for s in range(2):
                        sp.wait_ge(stored[s], 16 * NG * ((GROUP + 1 - s) // 2))

            @block.vector
            def _(dve):
                def finish(i, u):
                    s, t = u % 2, i * GROUP + u
                    base = (i * GROUP + u) * 3
                    rows = tile(S.agg, t)
                    after(dve, dve.tensor_scalar(den[s][:], rows[:, width:width + H], 1e-16, None, ALU.add), dstep, base + 1)
                    after(dve, dve.reciprocal(den[s][:], den[s][:]), dstep, base + 2)
                    dve.wait_ge(turned, freed(i, u, 2))
                    after(dve, dve.tensor_tensor(h[s][:].rearrange("p (h w) -> p h w", h=H),
                                                 rows[:, 0:width].rearrange("p (h w) -> p h w", h=H),
                                                 den[s][:].unsqueeze(2).broadcast_to([TP, H, width // H]), ALU.mult),
                          dstep, base + 3)
                    after(dve, dve.tensor_tensor(h[s][:], h[s][:], bias_row[:], ALU.add), biased, i * GROUP + u + 1)
                    dve.tensor_scalar(h[s][:], h[s][:], 0.0, None, ALU.max).then_inc(h_made, 1)

                def add(i, u):
                    if residual:
                        dve.wait_ge(turned, ready(i, u))
                        dve.wait_ge(kept, freed(i, u, 2))
                        dve.wait_ge(out_mm, freed(i, u, 2))
                        dve.tensor_tensor(ht[u % 2][:], turn_ps[:, u % 2, 0:CHUNKS * TP].rearrange(
                            "p (k n) -> p k n", k=CHUNKS), turned_rows(i * GROUP + u), ALU.add).then_inc(turn_copied, 1)

                dve.wait_ge(preload, 48 if last_layer else 16)
                with dve.Fori(0, NG) as i:
                    stagger(i, finish, nothing, add)

            @block.tensor
            def _(pe):
                def turn(i, u):
                    s = u % 2
                    pe.wait_ge(h_made, ready(i, u))
                    pe.wait_ge(turn_copied, freed(i, u, 2))
                    for c in range(CHUNKS):
                        last = pe.transpose(turn_ps[:, s, c * TP:(c + 1) * TP], h[s][:, c * P:(c + 1) * P],
                                            S.ident[0:TP, 0:TP])
                    last.then_inc(turned, 1)

                def project(i, u):
                    s = u % 2
                    pe.wait_ge(turn_copied, ready(i, u))
                    pe.wait_ge(out_copied, i * (2 * GROUP) + 2 * max(u - 1, 0))
                    if last_layer:
                        pe.wait_ge(x0_landed[s], (slot_uses(i, u) + 1) * 16)
                        pe.matmul(out_ps[:, s, 0:D], ht[s][:, 0, :], ow[:], start=True, stop=False)
                        pe.matmul(out_ps[:, s, 0:D], S.ones[0:1, 0:TP], ob[:], start=False, stop=False)
                        for c in range(2):
                            last = pe.matmul(out_ps[:, s, c * P:(c + 1) * P], x0[s][:, c, :], S.ident[:],
                                             start=False, stop=(c == 1))
                    else:
                        for c in range(CHUNKS):
                            last = pe.matmul(out_ps[:, s, 0:4 * next_H], ht[s][:, c, :],
                                             wqk[:, c].rearrange("p r s h -> p (r s h)"), start=(c == 0),
                                             stop=(c == CHUNKS - 1))
                    last.then_inc(out_mm, 1)

                pe.wait_ge(preload, 48 if last_layer else 16)
                with pe.Fori(0, NG) as i:
                    stagger(i, nothing, turn, project)

            @block.scalar
            def _(act):
                def copy(i, u):
                    s = u % 2
                    if not residual:
                        act.wait_ge(turned, ready(i, u))
                        act.wait_ge(out_mm, freed(i, u, 2))
                        act.wait_ge(kept, freed(i, u, 2))
                        nc.scalar.copy(ht[s][:], turn_ps[:, s, 0:CHUNKS * TP].rearrange("p (k n) -> p k n", k=CHUNKS)
                                       ).then_inc(turn_copied, 1)
                    act.wait_ge(turn_copied, ready(i, u))
                    if last_layer:
                        act.sem_inc(kept, 1)
                    else:
                        nc.scalar.copy(turned_rows(i * GROUP + u), ht[s][:]).then_inc(kept, 1)

                def results(i, u):
                    s, t = u % 2, i * GROUP + u
                    act.wait_ge(out_mm, ready(i, u))
                    if last_layer:
                        act.wait_ge(out_copied, i * (2 * GROUP) + 2 * u)
                        nc.scalar.copy(tile(S.gout, t), out_ps[:, s, 0:D]).then_inc(out_copied, 1)
                        nc.scalar.activation(junk[:], out_ps[:, s, 0:D], ACT.Square,
                                             accum_out=col(S.gss, t)).then_inc(out_copied, 1)
                    else:
                        both = out_ps[:, s, 0:4 * next_H].rearrange("p (r s h) -> p r s h", r=2, s=2)
                        at = S.q_node[:, bass.ds(t, 1), 0:2 * next_H].rearrange("p a (r h) -> p (a r) h", r=2)
                        nc.scalar.copy(at, both[:, :, 0]).then_inc(out_copied, 1)
                        act.wait_ge(stored[s], slot_uses(i, u) * 16)
                        nc.scalar.copy(k_out[s][:], both[:, :, 1]).then_inc(out_copied, 1)

                with act.Fori(0, NG) as i:
                    stagger(i, copy, results)


def project_rows(nc, S, tag, w, width, table, H, k_tab, q_at, with_representatives=False):
    CHUNKS = 4
    with stage(nc, tag) as a:
        keys = KeyGather(nc, S, a, H, k_tab, q_at)
        rep = Representatives(nc, S, a) if with_representatives else None
        ht = [a.sb(f"ht{s}", [P, CHUNKS, TP]) for s in range(2)]
        out = [a.sb(f"out{s}", [TP, 2, width]) for s in range(2)]
        ps = [a.ps(f"rows{s}", [TP, 2, 512]) for s in range(2)]
        picked, multiplied, copied = a.sem("picked"), a.sem("multiplied"), a.sem("copied")
        stored = [a.sem(f"stored{s}") for s in range(2)]
        with nc.Block() as block:
            @block.gpsimd
            def _(pool):
                keys(pool)

            if rep is not None:
                @block.sync
                def _(sp):
                    rep.load(sp)

                @block.vector
                def _(dve):
                    rep.find(dve)

            @block.scalar
            def _(act):
                def pick(i, u):
                    act.wait_ge(multiplied, freed(i, u, 2))
                    nc.scalar.copy(ht[u % 2][:], S.h_t[:, :, bass.ds((i * GROUP + u) * TP, TP)]).then_inc(picked, 1)

                def copy(i, u):
                    s = u % 2
                    act.wait_ge(multiplied, ready(i, u))
                    act.wait_ge(stored[s], slot_uses(i, u) * 32)
                    nc.scalar.copy(out[s][:], ps[s][:, :, 0:width]).then_inc(copied, 1)

                def store(i, u):
                    act.wait_ge(copied, ready(i, u))
                    for r in range(2):
                        act.dma_start(table[r * N:(r + 1) * N, :][bass.ds((i * GROUP + u) * TP, TP), :],
                                      out[u % 2][:, r, :]).then_inc(stored[u % 2], 16)

                with act.Fori(0, NG) as i:
                    stagger(i, pick, copy, store)
                for s in range(2):
                    act.wait_ge(stored[s], 32 * NG * ((GROUP + 1 - s) // 2))

            @block.tensor
            def _(pe):
                with pe.Fori(0, NG) as i:
                    for u in range(GROUP):
                        s = u % 2
                        pe.wait_ge(picked, ready(i, u))
                        pe.wait_ge(copied, freed(i, u, 2))
                        for r in range(2):
                            for c in range(CHUNKS):
                                last = pe.matmul(ps[s][:, r, 0:width], ht[s][:, c, :], w[:, c, r, :], start=(c == 0),
                                                 stop=(c == CHUNKS - 1))
                        last.then_inc(multiplied, 1)


def gnn0(nc, g, S, A):
    dram = lambda name, shape: nc.dram_tensor(name, shape, F32, kind="Internal").ap()
    S.table = dram("table", [2 * N, HEADS * HID])
    S.table3 = dram("table3", [2 * N, HID])
    S.k_tab, S.k_tab3 = dram("k_tab", [2 * N, HEADS]), dram("k_tab3", [2 * N, 1])
    S.x0_t = dram("x0_t", [NT, P, 2, TP])
    S.gss = g.sb("gss", [TP, NT])
    with stage(nc, "gn_") as a:
        S.ex = a.sb("ex", [P, VISITS * QUAD, HEADS])
        S.k_edge = S.ex[:, 0:CH, :]
        S.q_node = a.sb("q_node", [TP, NT, 2 * HEADS])
        W512 = HEADS * HID
        gnn_first(nc, S, A["L0_gnn_query"], A["L0_gnn_gate_w1"], A["L0_gnn_gate_b1"], A["L0_gnn_gate_w2"],
                  A["L0_gnn_gate_b2"], A["W1"], A["W1_T"], A["L0_gnn_q1"], A["L0_gnn_k1"])
        with stage(nc, "kg1_") as b:
            S.fx = b.sb("fx", [TP, NT, D])
            mix0(nc, g, S, A["conv_w"], A["bn_gamma"], A["bn_beta"], A["dw_w"], A["pw_w"], A["res_w"],
                 A["L0_mix_b_res"], KeyGather(nc, S, b, HEADS, S.k_tab, S.q_at))
            fx_stored = b.sem("fx_stored")
            with nc.Block() as block:
                @block.sync
                def _(sp):
                    sp.dma_start(tiles_of(S.fx_rows), S.fx[:]).then_inc(fx_stored, 16)
                    sp.wait_ge(fx_stored, 16)
        visits(nc, a, S)
        S.h_t = a.sb("h_t", [P, W512 // P, N])
        S.gout = S.h_t[0:TP].rearrange("p c n -> p (c n)")[:, 0:NT * D].rearrange("p (t d) -> p t d", d=D)
        for layer in (1, 2):
            edge_softmax(nc, S, f"s{layer}_", S.q_at, HEADS)
            n = layer + 1
            next_H, next_width = (HEADS, W512) if layer == 1 else (1, HID)
            table, k_tab, q_at = (S.table, S.k_tab, S.q_at) if layer == 1 else (S.table3, S.k_tab3, S.q_at3)
            with stage(nc, f"w{n}_") as b:
                S.agg = b.sb("agg", [TP, NT, W512 + HEADS])
                edge_tiles(nc, S, f"a{layer}_", S.table, W512, HEADS)
                with stage(nc, f"w{n}t_") as c:
                    w, wqk = load_projection(nc, b, c, A[f"W{n}"], A[f"W{n}_T"], A[f"L0_gnn_q{n}"], A[f"L0_gnn_k{n}"],
                                             next_H, next_width, W512 // P)
                gnn_nodes(nc, S, f"n{layer}_", W512, HEADS, A[f"L0_gnn_b{layer}"], residual=(layer == 2),
                          wqk=wqk, next_H=next_H, k_tab=k_tab)
                project_rows(nc, S, f"p{n}_", w, next_width, table, next_H, k_tab, q_at,
                             with_representatives=(layer == 2))
        edge_softmax(nc, S, "s3_", S.q_at3, 1)
        with stage(nc, "w4_") as b:
            S.agg = b.sb("agg", [TP, NT, HID + 1])
            edge_tiles(nc, S, "a3_", S.table3, HID, 1)
            gnn_nodes(nc, S, "n3_", HID, 1, A["L0_gnn_b3"], out_w=A["L0_gnn_proj_w"], out_b=A["L0_gnn_proj_b"])
        add_gnn0(nc, S)


def add_gnn0(nc, S):
    with stage(nc, "c0_") as a:
        fx, fx_landed = a.sb("fx", [TP, NT, D]), a.sem("fx_landed")
        root, asked, step_s, scaled = a.sem("root"), a.sem("asked"), a.sem("step"), a.sem("scaled")
        with nc.Block() as block:
            @block.sync
            def _(sp):
                sp.dma_start(fx[:], tiles_of(S.fx_rows)).then_inc(fx_landed, 16)

            @block.scalar
            def _(act):
                act.wait_ge(asked, 1)
                nc.scalar.activation(S.gss[:], S.gss[:], ACT.Sqrt).then_inc(root, 1)

            @block.vector
            def _(dve):
                dve.tensor_scalar(S.gss[:], S.gss[:], 1e-24, None, ALU.max).then_inc(asked, 1)
                dve.wait_ge(root, 1)
                st = Steps(dve, step_s)
                st(dve.reciprocal(S.gss[:], S.gss[:]))
                dve.wait_ge(fx_landed, 16)
                with dve.Fori(0, NG) as i:
                    for u in range(GROUP):
                        t = i * GROUP + u
                        dve.scalar_tensor_tensor(tile(S.x, t), tile(S.gout, t), col(S.gss, t), tile(S.x, t), ALU.mult,
                                                 ALU.add).then_inc(scaled, 1)
                        dve.wait_ge(scaled, ready(i, u))
                        dve.tensor_tensor(tile(S.x, t), tile(S.x, t), tile(fx, t), ALU.add)


EXPERTS = 8
FF = 1024
CAP = -(-5 * N // (4 * EXPERTS))
SLOTS = 4 * P
FLT_MAX = 3.4028234663852886e38


def moe(nc, S, gate_w, gate_b, w1, b1, w2, b2):
    EX = EXPERTS
    buf = nc.dram_tensor("expert_in", [EX * SLOTS, D], F32, kind="Internal").ap()
    ybuf = nc.dram_tensor("expert_out", [EX * SLOTS, D], F32, kind="Internal").ap()
    with stage(nc, "mo_") as a:
        row_in, row_out = a.sb("row_in", [TP, NT], I32), a.sb("row_out", [TP, NT], I32)
        weight = a.sb("weight", [TP, NT])
        with stage(nc, "mor_") as b:
            gw, gb = b.sb("gw", [P, 2, EX]), b.sb("gb", [TP, EX])
            xl = [b.sb(f"xl{s}", [TP, D]) for s in range(2)]
            xt = [b.sb(f"xt{s}", [P, 2, TP]) for s in range(2)]
            logit = b.sb("logit", [TP, NT, EX])
            one_hot, cand, prefix, total, scan = (b.sb(n, [TP, NT, EX]) for n in
                                                  ("one_hot", "cand", "prefix", "total", "scan"))
            until = b.sb("until", [TP, TP])
            ones_t = b.sb("ones_t", [TP, NT])
            top, den, best, pos, kept, idx = (b.sb(n, [TP, NT]) for n in ("top", "den", "best", "pos", "kept", "idx"))
            turn_ps, logit_ps = b.ps("turn", [P, 2, 512]), b.ps("logit_ps", [TP, 512])
            pre_ps, tot_ps = b.ps("pre", [TP, 512]), b.ps("tot", [TP, 512])
            zeros, zeros_set = b.sb("zeros_wide", [P, 512]), b.sem("zeros_set")
            loaded, zeroed, normed, turned, turn_copied, logit_mm, logit_in, shifted, exped, hot, summed, step_s = (
                b.sem(n) for n in ("loaded", "zeroed", "normed", "turned", "turn_copied", "logit_mm", "logit_in",
                                   "shifted", "exped", "hot", "summed", "step"))
            with nc.Block() as block:
                @block.sync
                def _(sp):
                    sp.dma_start(gw[:], gate_w.rearrange("(k p) e -> p k e", p=P)).then_inc(loaded, 16)
                    sp.dma_start(gb[:], spread(gate_b, TP)).then_inc(loaded, 16)
                    rows = buf.rearrange("(p r) d -> p (r d)", p=P)
                    sp.wait_ge(zeros_set, 1)
                    for c in range(0, EX * SLOTS * D // P, 512):
                        sp.dma_start(rows[:, c:c + 512], zeros[:]).then_inc(zeroed, 16)
                    sp.wait_ge(zeroed, 16 * (EX * SLOTS * D // P // 512))

                @block.vector
                def _(dve):
                    dve.memset(zeros[:], 0.0).then_inc(zeros_set, 1)
                    dve.wait_ge(loaded, 32)
                    with dve.Fori(0, NG) as i:
                        for u in range(GROUP):
                            t = i * GROUP + u
                            dve.wait_ge(turned, freed(i, u, 2))
                            dve.tensor_scalar(xl[u % 2][:], tile(S.x, t), col(S.ln_r, t), col(S.ln_b, t), ALU.mult,
                                              ALU.add).then_inc(normed, 1)
                            dve.wait_ge(logit_mm, ready(i, u))
                            dve.tensor_tensor(tile(logit, t), logit_ps[:, 0:EX], gb[:], ALU.add).then_inc(logit_in, 1)
                    dve.wait_ge(logit_in, NT)
                    st = Steps(dve, step_s)

                    def wide(x):
                        return x[:].unsqueeze(2).broadcast_to([TP, NT, EX])

                    st(dve.tensor_reduce(top[:], logit[:], AX.X, ALU.max))
                    dve.tensor_tensor(logit[:], logit[:], wide(top), ALU.subtract).then_inc(shifted, 1)
                    dve.wait_ge(exped, 1)
                    st(dve.tensor_reduce(den[:], logit[:], AX.X, ALU.add))
                    st(dve.reciprocal(den[:], den[:]))
                    st(dve.tensor_tensor(logit[:], logit[:], wide(den), ALU.mult))
                    st(dve.tensor_reduce(best[:], logit[:], AX.X, ALU.max))
                    st(dve.tensor_tensor(one_hot[:], logit[:], wide(best), ALU.is_equal))
                    expert_no = S.iota_row[0:TP, 0:EX].unsqueeze(1).broadcast_to([TP, NT, EX])
                    st(dve.scalar_tensor_tensor(cand[:], expert_no, float(-EX), one_hot[:], ALU.add, ALU.mult))
                    st(dve.tensor_reduce(idx[:], cand[:], AX.X, ALU.min))
                    st(dve.tensor_scalar(idx[:], idx[:], float(EX), None, ALU.add))
                    st(dve.tensor_tensor(one_hot[:], expert_no, wide(idx), ALU.is_equal))
                    dve.tensor_scalar(until[:], S.iota_row[0:TP, 0:TP], S.part_col[0:TP, 0:1], None,
                                      ALU.is_ge).then_inc(hot, 1)
                    st(dve.memset(ones_t[:], 1.0))
                    dve.wait_ge(summed, 1)
                    st(dve.tensor_copy(prefix[:].rearrange("p t e -> p (t e)"), pre_ps[:, 0:NT * EX]))
                    st(dve.tensor_copy(total[:].rearrange("p t e -> p (t e)"), tot_ps[:, 0:NT * EX]))
                    for e in range(EX):
                        last = dve.tensor_tensor_scan(scan[:, :, e], ones_t[:], total[:, :, e], 0.0, ALU.mult, ALU.add)
                    st(last)
                    st(dve.tensor_tensor(scan[:], scan[:], total[:], ALU.subtract))
                    st(dve.tensor_tensor(scan[:], scan[:], prefix[:], ALU.add))
                    st(dve.tensor_tensor(scan[:], scan[:], one_hot[:], ALU.mult))
                    st(dve.tensor_reduce(pos[:], scan[:], AX.X, ALU.add))
                    st(dve.tensor_scalar(pos[:], pos[:], -1.0, None, ALU.add))
                    st(dve.tensor_scalar(kept[:], pos[:], float(CAP), None, ALU.is_lt))
                    st(dve.tensor_tensor(weight[:], best[:], kept[:], ALU.mult))
                    st(dve.tensor_scalar(pos[:], pos[:], float(CAP - 1), None, ALU.min))
                    st(dve.scalar_tensor_tensor(pos[:], idx[:], float(SLOTS), pos[:], ALU.mult, ALU.add))
                    st(dve.tensor_copy(row_out[:], pos[:]))
                    st(dve.scalar_tensor_tensor(pos[:], pos[:], float(-SKIP), kept[:], ALU.add, ALU.mult))
                    st(dve.tensor_scalar(pos[:], pos[:], float(SKIP), None, ALU.add))
                    dve.tensor_copy(row_in[:], pos[:])

                @block.scalar
                def _(act):
                    with act.Fori(0, NG) as i:
                        for u in range(GROUP):
                            act.wait_ge(turned, ready(i, u))
                            act.wait_ge(logit_mm, freed(i, u, 2))
                            nc.scalar.copy(xt[u % 2][:], turn_ps[:, u % 2, 0:2 * TP].rearrange("p (k n) -> p k n", k=2)
                                           ).then_inc(turn_copied, 1)
                    act.wait_ge(shifted, 1)
                    nc.scalar.activation(logit[:], logit[:], ACT.Exp).then_inc(exped, 1)

                @block.tensor
                def _(pe):
                    pe.wait_ge(loaded, 32)
                    with pe.Fori(0, NG) as i:
                        for u in range(GROUP):
                            pe.wait_ge(normed, ready(i, u))
                            pe.wait_ge(turn_copied, freed(i, u, 2))
                            for c in range(2):
                                last = pe.transpose(turn_ps[:, u % 2, c * TP:(c + 1) * TP], xl[u % 2][:, c * P:(c + 1) * P],
                                                    S.ident[0:TP, 0:TP])
                            last.then_inc(turned, 1)
                            pe.wait_ge(turn_copied, ready(i, u))
                            pe.wait_ge(logit_in, freed(i, u, 1))
                            for c in range(2):
                                last = pe.matmul(logit_ps[:, 0:EX], xt[u % 2][:, c, :], gw[:, c, :], start=(c == 0),
                                                 stop=(c == 1))
                            last.then_inc(logit_mm, 1)
                    pe.wait_ge(hot, 1)
                    hots = one_hot[:].rearrange("p t e -> p (t e)")
                    pe.matmul(pre_ps[:, 0:NT * EX], until[:], hots, start=True, stop=True)
                    pe.matmul(tot_ps[:, 0:NT * EX], S.ones[0:TP, 0:TP], hots, start=True, stop=True).then_inc(summed, 1)

        with stage(nc, "mod_") as b:
            xl = [b.sb(f"xl{s}", [TP, D]) for s in range(2)]
            at = [b.sb(f"at{s}", [TP, 1], I32) for s in range(2)]
            normed, pool_go = b.sem("normed"), b.sem("pool_go")
            scattered = b.borrow(S.pool_dma[0:2])
            with nc.Block() as block:
                @block.vector
                def _(dve):
                    with dve.Fori(0, NG) as i:
                        for u in range(GROUP):
                            t, s = i * GROUP + u, u % 2
                            dve.wait_ge(scattered[s], slot_uses(i, u) * 16)
                            dve.tensor_copy(at[s][:], col(row_in, t)).then_inc(normed, 1)
                            dve.tensor_scalar(xl[s][:], tile(S.x, t), col(S.ln_r, t), col(S.ln_b, t), ALU.mult,
                                              ALU.add).then_inc(normed, 1)

                @block.gpsimd
                def _(pool):
                    with pool.Fori(0, NG) as i:
                        for u in range(GROUP):
                            s = u % 2
                            pool.wait_ge(normed, i * (2 * GROUP) + 2 * u + 2)
                            pool.sem_inc(pool_go, 1)
                            pool.indirect_dma_start(buf, bass.IndirectOffsetOnAxis(ap=at[s][:, 0:1], axis=0), xl[s][:],
                                                    None, bounds_check=EX * SLOTS - 1, oob_is_err=False
                                                    ).then_inc(scattered[s], 16)
                    for s in range(2):
                        pool.wait_ge(scattered[s], 16 * NG * (3 - s))

        with stage(nc, "moe_") as b:
            FC = FF // P
            w1s = [b.sb(f"w1{s}", [P, 2, FF]) for s in range(2)]
            w2s = [b.sb(f"w2{s}", [P, FC, D]) for s in range(2)]
            b1s = [b.sb(f"b1{s}", [P, FC]) for s in range(2)]
            b2s = [b.sb(f"b2{s}", [1, D]) for s in range(2)]
            xs = [b.sb(f"xs{s}", [P, 4, D]) for s in range(2)]
            xt = b.sb("xt", [P, 2, SLOTS])
            hid = b.sb("hid", [P, FC, SLOTS])
            out = [b.sb(f"out{s}", [P, 4, D]) for s in range(2)]
            turn_ps = b.ps("turn", [P, 2, 512])
            hid_ps = b.ps("hid_ps", [P, 2, 512])
            out_ps = b.ps("out_ps", [P, 4, 512])
            w_landed = [b.sem(f"w_landed{s}") for s in range(2)]
            out_mm = [b.sem(f"out_mm{s}") for s in range(2)]
            stored = b.borrow(S.pool_dma[0:2])
            turned, turn_copied, hid_mm, hid_done, out_copied, pool_go = (
                b.sem(n) for n in ("turned", "turn_copied", "hid_mm", "hid_done", "out_copied", "pool_go"))
            with nc.Block() as block:
                @block.sync
                def _(sp):
                    with sp.Fori(0, EX // 2) as i:
                        for s in range(2):
                            e = i * 2 + s
                            one = bass.ds(e, 1)
                            sp.wait_ge(out_mm[s], i * 4)
                            sp.dma_start(xs[s][:], buf[bass.ds(e * SLOTS, SLOTS), :].rearrange("(r p) d -> p r d", p=P)
                                         ).then_inc(w_landed[s], 16)
                            sp.dma_start(w1s[s][:], w1[one].rearrange("a (k p) f -> (a p) k f", p=P)).then_inc(w_landed[s], 16)
                            sp.dma_start(b1s[s][:], b1[one].rearrange("a (k p) -> (a p) k", p=P),
                                         allow_slow_non_contiguous=True).then_inc(w_landed[s], 16)
                            sp.dma_start(b2s[s][:], b2[one]).then_inc(w_landed[s], 16)
                            sp.dma_start(w2s[s][:], w2[one].rearrange("a (k p) f -> (a p) k f", p=P)).then_inc(w_landed[s], 16)

                @block.tensor
                def _(pe):
                    with pe.Fori(0, EX // 2) as i:
                        for s in range(2):
                            pe.wait_ge(w_landed[s], i * 80 + 80)
                            pe.wait_ge(turn_copied, i * 2 + s)
                            for r in range(4):
                                for c in range(2):
                                    last = pe.transpose(turn_ps[:, c, r * P:(r + 1) * P], xs[s][:, r, c * P:(c + 1) * P],
                                                        S.ident[:])
                            last.then_inc(turned, 1)
                            pe.wait_ge(turn_copied, i * 2 + s + 1)
                            for o in range(FC):
                                if o >= 2:
                                    pe.wait_ge(hid_done, i * (2 * FC) + s * FC + o - 1)
                                else:
                                    pe.wait_ge(hid_done, i * (2 * FC) + s * FC)
                                for c in range(2):
                                    last = pe.matmul(hid_ps[:, o % 2, :], w1s[s][:, c, o * P:(o + 1) * P], xt[:, c, :],
                                                     start=(c == 0), stop=(c == 1))
                                last.then_inc(hid_mm, 1)
                            pe.wait_ge(hid_done, i * (2 * FC) + (s + 1) * FC)
                            pe.wait_ge(out_copied, i * 2 + s)
                            for r in range(4):
                                for o in range(FC):
                                    pe.matmul(out_ps[:, r, 0:D], hid[:, o, r * P:(r + 1) * P], w2s[s][:, o, :],
                                              start=(o == 0), stop=False)
                                pe.matmul(out_ps[:, r, 0:D], S.ones[0:1, :], b2s[s][:], start=False, stop=True
                                          ).then_inc(out_mm[s], 1)

                @block.scalar
                def _(act):
                    with act.Fori(0, EX // 2) as i:
                        for s in range(2):
                            for o in range(FC):
                                act.wait_ge(hid_mm, i * (2 * FC) + s * FC + o + 1)
                                act.wait_ge(out_mm[1 - s], (i + s) * 4)
                                nc.scalar.activation(hid[:, o, :], hid_ps[:, o % 2, :], ACT.Relu,
                                                     bias=b1s[s][:, o:o + 1]).then_inc(hid_done, 1)

                @block.vector
                def _(dve):
                    with dve.Fori(0, EX // 2) as i:
                        for s in range(2):
                            dve.wait_ge(turned, i * 2 + s + 1)
                            dve.wait_ge(hid_mm, i * (2 * FC) + s * FC)
                            dve.tensor_copy(xt[:], turn_ps[:]).then_inc(turn_copied, 1)
                            dve.wait_ge(out_mm[s], i * 4 + 4)
                            dve.wait_ge(stored[s], i * 16)
                            dve.tensor_copy(out[s][:], out_ps[:, :, 0:D]).then_inc(out_copied, 1)

                @block.gpsimd
                def _(pool):
                    with pool.Fori(0, EX // 2) as i:
                        for s in range(2):
                            pool.wait_ge(out_copied, i * 2 + s + 1)
                            pool.sem_inc(pool_go, 1)
                            pool.dma_start(ybuf[bass.ds((i * 2 + s) * SLOTS, SLOTS), :].rearrange(
                                "(r p) d -> p r d", p=P), out[s][:]).then_inc(stored[s], 16)
                    for s in range(2):
                        pool.wait_ge(stored[s], 16 * (EX // 2))

        with stage(nc, "mog_") as b:
            y = [b.sb(f"y{s}", [TP, D]) for s in range(PIPE)]
            at = [b.sb(f"at{s}", [TP, 1], I32) for s in range(PIPE)]
            z = [b.sb(f"z{s}", [TP, D]) for s in range(PIPE)]
            mask = [b.sb(f"mask{s}", [TP, 3, D], I32) for s in range(PIPE)]
            limit = b.sb("limit", [TP, 2, D])
            limits, indexed, weighted, masked, replaced, picked, y_used, pool_go, dve_go = (
                b.sem(n) for n in ("limits", "indexed", "weighted", "masked", "replaced", "picked", "y_used", "pool_go", "dve_go"))
            landed = b.borrow(S.pool_dma[0:PIPE])
            with nc.Block() as block:
                @block.scalar
                def _(act):
                    def index(i, u):
                        act.wait_ge(y_used, freed(i, u, PIPE, PIPE))
                        nc.scalar.copy(at[u % PIPE][:], col(row_out, i * PIPE + u)).then_inc(indexed, 1)

                    pipeline(act, (0, index), lag=PIPE - 1)

                @block.gpsimd
                def _(pool):
                    def gather(i, u):
                        s = u % PIPE
                        pool.wait_ge(indexed, ready(i, u, PIPE))
                        pool.sem_inc(pool_go, 1)
                        pool.indirect_dma_start(y[s][:], None, ybuf, bass.IndirectOffsetOnAxis(ap=at[s][:, 0:1], axis=0)
                                                ).then_inc(landed[s], 16)

                    pipeline(pool, (0, gather))

                @block.vector
                def _(dve):
                    dve.memset(limit[:, 0], 1e4).then_inc(limits, 1)
                    dve.memset(limit[:, 1], -1e4).then_inc(limits, 1)
                    dve.wait_ge(limits, 2)

                    def weigh(i, u):
                        t, s = i * PIPE + u, u % PIPE
                        dve.wait_ge(y_used, freed(i, u, PIPE, PIPE))
                        dve.memset(z[s][:], 0.0).then_inc(replaced, 1)
                        dve.wait_ge(landed[s], (i + u // PIPE + 1) * 16)
                        dve.tensor_scalar(y[s][:], y[s][:], col(weight, t), None, ALU.mult).then_inc(weighted, 1)

                    def compare(i, u):
                        s = u % PIPE
                        dve.wait_ge(weighted, ready(i, u, PIPE))
                        dve.tensor_tensor(mask[s][:, 0], y[s][:], y[s][:], ALU.is_equal).then_inc(masked, 1)
                        dve.tensor_scalar(mask[s][:, 1], y[s][:], FLT_MAX, None, ALU.is_gt).then_inc(masked, 1)
                        dve.tensor_scalar(mask[s][:, 2], y[s][:], -FLT_MAX, None, ALU.is_lt).then_inc(masked, 1)

                    def replace(i, u):
                        s = u % PIPE
                        dve.wait_ge(masked, ready(i, u, PIPE) * 3)
                        dve.wait_ge(replaced, ready(i, u, PIPE))
                        for n, value in enumerate((y[s][:], limit[:, 0], limit[:, 1])):
                            if n:
                                dve.wait_ge(picked, (i * PIPE + u) * 3 + n)
                            dve.sem_inc(dve_go, 1)
                            dve.copy_predicated(z[s][:], mask[s][:, n], value).then_inc(picked, 1)

                    def add(i, u):
                        t = i * PIPE + u
                        dve.wait_ge(picked, ready(i, u, PIPE) * 3)
                        dve.tensor_tensor(tile(S.x, t), tile(S.x, t), z[u % PIPE][:], ALU.add).then_inc(y_used, 1)

                    pipeline(dve, (3, add), (2, replace), (1, compare), (0, weigh))


class AttentionWeights:
    pass


def attention_sums(nc, S, a, Wg, Wq, bq, Wk, bk, Wv, bv, Wo, bo):
    S.support = nc.dram_tensor("support", [N, D], F32, kind="Internal").ap()
    wg, wq, wo = (a.sb(n, [P, 2, D]) for n in ("wg", "wq", "wo"))
    wkv, bkv = a.sb("wkv", [P, 2, 2, D]), a.sb("bkv", [1, 2 * D])
    bqc, bor = a.sb("bqc", [P, 2]), a.sb("bor", [1, D])
    group_ones = a.sb("group_ones", [P, P])
    kv_block, k_block = a.sb("kv_block", [P, 2, P]), a.sb("k_block", [P, 2, P])
    loaded = a.sem("loaded")

    with stage(nc, "lak_") as b:
        xn = [b.sb(f"xn{s}", [TP, D]) for s in range(2)]
        xt = [b.sb(f"xt{s}", [P, 2, TP]) for s in range(2)]
        low = b.sb("low", [TP, D])
        kp = [b.sb(f"kp{s}", [TP, D]) for s in range(2)]
        v = [b.sb(f"v{s}", [TP, 2, P + 1]) for s in range(2)]
        sup = [b.sb(f"sup{s}", [TP, D]) for s in range(2)]
        ksum = b.sb("ksum", [P, 2])
        turn_ps, kv_ps, sup_ps = b.ps("turn", [P, 512]), b.ps("kv", [TP, 2, 512]), b.ps("sup_ps", [TP, 512])
        sum_ps = b.ps("sum", [P, 2, 512])
        (normed, turned, turn_copied, kv_mm, low_made, exped, k_made, v_made, sup_mm, sup_copied, summed, init,
         step_s) = (b.sem(n) for n in ("normed", "turned", "turn_copied", "kv_mm", "low_made", "exped", "k_made",
                                       "v_made", "sup_mm", "sup_copied", "summed", "init", "step"))
        stored = [b.sem(f"stored{s}") for s in range(2)]
        with nc.Block() as block:
            @block.sync
            def _(sp):
                for to, of in ((wg, Wg), (wq, Wq), (wo, Wo)):
                    sp.dma_start(to[:], of.rearrange("(k p) c -> p k c", p=P)).then_inc(loaded, 16)
                for n, (w, bias) in enumerate(((Wk, bk), (Wv, bv))):
                    sp.dma_start(wkv[:, :, n, :], w.rearrange("(k p) c -> p k c", p=P)).then_inc(loaded, 16)
                    sp.dma_start(bkv[0:1, n * D:(n + 1) * D], row_of(bias)).then_inc(loaded, 16)
                sp.dma_start(bqc[:], bq.rearrange("(k p) -> p k", p=P),
                             allow_slow_non_contiguous=True).then_inc(loaded, 16)
                sp.dma_start(bor[:], row_of(bo)).then_inc(loaded, 16)

                def store(i, u):
                    sp.wait_ge(sup_copied, ready(i, u, PIPE))
                    sp.dma_start(S.support[bass.ds((i * PIPE + u) * TP, TP), :], sup[u % 2][:]
                                 ).then_inc(stored[u % 2], 16)

                pipeline(sp, (0, store))
                for s in range(2):
                    sp.wait_ge(stored[s], 16 * ((NT + 1 - s) // 2))

            @block.vector
            def _(dve):
                st = Steps(dve, step_s)
                st(dve.memset(group_ones[:], 0.0))
                for q in range(4):
                    dve.memset(group_ones[32 * q:32 * q + 32, 32 * q:32 * q + 32], 1.0)
                for s in range(2):
                    dve.memset(v[s][:, :, P:P + 1], 1.0).then_inc(init, 1)
                dve.wait_ge(init, 2)

                def norm(i, u):
                    t, s = i * PIPE + u, u % 2
                    dve.wait_ge(turned, freed(i, u, 2, PIPE))
                    dve.tensor_scalar(xn[s][:], tile(S.x, t), col(S.ln_r, t), col(S.ln_b, t), ALU.mult,
                                      ALU.add).then_inc(normed, 1)

                def feature(i, u):
                    t, s = i * PIPE + u, u % 2
                    dve.wait_ge(kv_mm, ready(i, u, PIPE))
                    dve.wait_ge(exped, freed(i, u, 1, PIPE))
                    dve.tensor_scalar(low[:], kv_ps[:, 0, 0:D], 0.0, None, ALU.min).then_inc(low_made, 1)
                    dve.wait_ge(summed, freed(i, u, 2, PIPE))
                    dve.tensor_copy(v[s][:, :, 0:P], kv_ps[:, 1, 0:D].rearrange("p (c e) -> p c e", c=2)
                                    ).then_inc(v_made, 1)
                    dve.wait_ge(exped, ready(i, u, PIPE))
                    dve.scalar_tensor_tensor(kp[s][:], kv_ps[:, 0, 0:D], 0.0, low[:], ALU.max,
                                             ALU.add).then_inc(k_made, 1)

                pipeline(dve, (0, norm), (1, feature))
                dve.wait_ge(summed, NT + 1)
                for c in range(2):
                    dve.tensor_tensor(kv_block[:, c, :], sum_ps[:, c, 0:P], group_ones[:], ALU.mult)
                    st(dve.tensor_copy(ksum[:, c:c + 1], sum_ps[:, c, P:P + 1]))
                    dve.tensor_scalar(k_block[:, c, :], group_ones[:], ksum[:, c:c + 1], None, ALU.mult)

            @block.scalar
            def _(act):

                def copy(i, u):
                    s = u % 2
                    act.wait_ge(turned, ready(i, u, PIPE))
                    act.wait_ge(sup_mm, freed(i, u, 2, PIPE))
                    nc.scalar.copy(xt[s][:], turn_ps[:, 0:2 * TP].rearrange("p (k n) -> p k n", k=2)
                                   ).then_inc(turn_copied, 1)

                def feature(i, u):
                    s = u % 2
                    act.wait_ge(low_made, ready(i, u, PIPE))
                    act.wait_ge(k_made, freed(i, u, 1, PIPE))
                    nc.scalar.activation(low[:], low[:], ACT.Exp).then_inc(exped, 1)
                    act.wait_ge(sup_mm, ready(i, u, PIPE))
                    act.wait_ge(stored[s], (i * (PIPE // 2) + u // 2) * 16)
                    nc.scalar.copy(sup[s][:], sup_ps[:, 0:D]).then_inc(sup_copied, 1)

                pipeline(act, (0, copy), (1, feature))

            @block.tensor
            def _(pe):
                pe.wait_ge(loaded, 16 * 9)
                for c in range(2):
                    pe.matmul(sum_ps[:, c, 0:P + 1], S.zeros[:, 0:P], S.zeros[:, 0:P + 1], start=True, stop=False)

                def turn(i, u):
                    s = u % 2
                    pe.wait_ge(normed, ready(i, u, PIPE))
                    pe.wait_ge(turn_copied, freed(i, u, 1, PIPE))
                    for c in range(2):
                        last = pe.transpose(turn_ps[:, c * TP:(c + 1) * TP], xn[s][:, c * P:(c + 1) * P],
                                            S.ident[0:TP, 0:TP])
                    last.then_inc(turned, 1)

                def project(i, u):
                    s = u % 2
                    pe.wait_ge(turn_copied, ready(i, u, PIPE))
                    pe.wait_ge(k_made, freed(i, u, 1, PIPE))
                    pe.wait_ge(v_made, freed(i, u, 1, PIPE))
                    for n in range(2):
                        for c in range(2):
                            pe.matmul(kv_ps[:, n, 0:D], xt[s][:, c, :], wkv[:, c, n, :], start=(c == 0), stop=False)
                        last = pe.matmul(kv_ps[:, n, 0:D], S.ones[0:1, 0:TP], bkv[:, n * D:(n + 1) * D],
                                         start=False, stop=True)
                    last.then_inc(kv_mm, 1)
                    pe.wait_ge(sup_copied, freed(i, u, 1, PIPE))
                    for c in range(2):
                        last = pe.matmul(sup_ps[:, 0:D], xt[s][:, c, :], wg[:, c, :], start=(c == 0), stop=(c == 1))
                    last.then_inc(sup_mm, 1)

                def add_up(i, u):
                    s = u % 2
                    pe.wait_ge(k_made, ready(i, u, PIPE))
                    pe.wait_ge(v_made, ready(i, u, PIPE))
                    for c in range(2):
                        last = pe.matmul(sum_ps[:, c, 0:P + 1], kp[s][:, c * P:(c + 1) * P], v[s][:, c, :],
                                         start=False, stop=False)
                    last.then_inc(summed, 1)

                pipeline(pe, (0, turn), (1, project), (2, add_up))
                for c in range(2):
                    last = pe.matmul(sum_ps[:, c, 0:P + 1], S.zeros[:, 0:P], S.zeros[:, 0:P + 1], start=False, stop=True)
                last.then_inc(summed, 1)

    L = AttentionWeights()
    L.wq, L.wo, L.bqc, L.bor, L.kv_block, L.k_block = wq, wo, bqc, bor, kv_block, k_block
    return L


def attention_queries(nc, S, L):
    def make(a):
        xn, xt = a.sb("la_xn", [TP, D]), a.sb("la_xt", [P, 2, TP])
        low, high, qp, rz, o = (a.sb("la_" + n, [P, 2, TP]) for n in ("low", "high", "qp", "rz", "o"))
        turn_ps, q_ps, o_ps, att_ps = (a.ps("la_turn", [P, 512]), a.ps("la_q", [P, 512]), a.ps("la_o_ps", [P, 512]),
                                       a.ps("la_att", [TP, 512]))
        normed, turned, turn_copied, q_mm, low_made, exped, q_made, o_mm, dstep, o_made, att_mm, att_added = (
            a.sem("la_" + n) for n in ("normed", "turned", "turn_copied", "q_mm", "low_made", "exped", "q_made", "o_mm",
                                       "dstep", "o_made", "att_mm", "att_added"))

        def vector(dve, i, part):
            if part == 0:
                dve.wait_ge(att_added, i)
                dve.tensor_scalar(xn[:], tile(S.x, i), col(S.ln_r, i), col(S.ln_b, i), ALU.mult,
                                  ALU.add).then_inc(normed, 1)
            if part == 1:
                dve.wait_ge(q_mm, i + 1)
                for c in range(2):
                    dve.tensor_scalar(low[:, c], q_ps[:, c * TP:(c + 1) * TP], L.bqc[:, c:c + 1], 0.0, ALU.add,
                                      ALU.min).then_inc(low_made, 1)
                    dve.tensor_scalar(high[:, c], q_ps[:, c * TP:(c + 1) * TP], L.bqc[:, c:c + 1], 0.0, ALU.add,
                                      ALU.max).then_inc(low_made, 1)
            if part == 2:
                dve.wait_ge(exped, i + 1)
                dve.tensor_tensor(qp[:], high[:], low[:], ALU.add).then_inc(q_made, 1)
                dve.wait_ge(o_mm, i + 1)
                after(dve, dve.tensor_scalar(rz[:].rearrange("p c n -> p (c n)"), o_ps[:, 2 * TP:4 * TP], 1e-6,
                                             None, ALU.add), dstep, i * 2 + 1)
                after(dve, dve.reciprocal(rz[:], rz[:]), dstep, i * 2 + 2)
                dve.tensor_tensor(o[:].rearrange("p c n -> p (c n)"), o_ps[:, 0:2 * TP],
                                  rz[:].rearrange("p c n -> p (c n)"), ALU.mult).then_inc(o_made, 1)
            if part == 3:
                dve.wait_ge(att_mm, i + 1)
                dve.tensor_tensor(tile(S.y, i), att_ps[:, 0:D], xn[:], ALU.add).then_inc(att_added, 1)

        def scalar(act, i, part):
            if part == 0:
                act.wait_ge(turned, i + 1)
                nc.scalar.copy(xt[:], turn_ps[:, 0:2 * TP].rearrange("p (k n) -> p k n", k=2)).then_inc(turn_copied, 1)
            if part == 1:
                act.wait_ge(low_made, i * 4 + 4)
                nc.scalar.activation(low[:], low[:], ACT.Exp).then_inc(exped, 1)

        def tensor(pe, i, part):
            if part == 0:
                pe.wait_ge(normed, i + 1)
                for c in range(2):
                    last = pe.transpose(turn_ps[:, c * TP:(c + 1) * TP], xn[:, c * P:(c + 1) * P],
                                        S.ident[0:TP, 0:TP])
                last.then_inc(turned, 1)
                pe.wait_ge(turn_copied, i + 1)
                for o_ in range(2):
                    for c in range(2):
                        last = pe.matmul(q_ps[:, o_ * TP:(o_ + 1) * TP], L.wq[:, c, o_ * P:(o_ + 1) * P],
                                         xt[:, c, :], start=(c == 0), stop=(c == 1))
                last.then_inc(q_mm, 1)
            if part == 2:
                pe.wait_ge(q_made, i + 1)
                for n, w in enumerate((L.kv_block, L.k_block)):
                    for c in range(2):
                        at = (2 * n + c) * TP
                        last = pe.matmul(o_ps[:, at:at + TP], w[:, c, :], qp[:, c, :], start=True, stop=True)
                last.then_inc(o_mm, 1)
            if part == 3:
                pe.wait_ge(o_made, i + 1)
                for c in range(2):
                    pe.matmul(att_ps[:, 0:D], o[:, c, :], L.wo[:, c, :], start=(c == 0), stop=False)
                pe.matmul(att_ps[:, 0:D], S.ones[0:1, 0:TP], L.bor[:], start=False, stop=True).then_inc(att_mm, 1)

        return scalar, vector, tensor
    return make


def feed_forward(nc, S, tag, src, gamma, beta, w1, b1, w2, b2, func, out=None, coef=None):
    FC = FF // P
    with stage(nc, tag) as a:
        w1s, w2s = a.sb("w1", [P, 2, FF]), a.sb("w2", [P, FC, D])
        b1s, b2s = a.sb("b1", [P, FC]), a.sb("b2", [1, D])
        xa = [a.sb(f"xa{s}", [TP, D]) for s in range(PIPE)]
        xt = [a.sb(f"xt{s}", [P, 2, TP]) for s in range(2)]
        hid = [a.sb(f"hid{s}", [P, FC, TP]) for s in range(2)]
        res = [a.sb(f"res{s}", [TP, D]) for s in range(2)]
        turn_ps, hid_ps, f_ps = a.ps("turn", [P, 512]), a.ps("hid_ps", [P, 2, 2, 512]), a.ps("f_ps", [TP, 2, 512])
        loaded, normed, dstep, turned, turn_copied, hid_mm, hid_done, f_mm, f_used, base_made = (
            a.sem(n) for n in ("loaded", "normed", "dstep", "turned", "turn_copied", "hid_mm", "hid_done", "f_mm",
                               "f_used", "base_made"))
        stored = [a.sem(f"stored{s}") for s in range(2)]
        affine = gamma is not None
        if affine:
            ga, be = a.sb("ga", [TP, D]), a.sb("be", [TP, D])
        LOADS = 16 * (6 if affine else 4)
        with nc.Block() as block:
            @block.sync
            def _(sp):
                sp.dma_start(w1s[:], w1.rearrange("(k p) f -> p k f", p=P)).then_inc(loaded, 16)
                sp.dma_start(w2s[:], w2.rearrange("(k p) f -> p k f", p=P)).then_inc(loaded, 16)
                sp.dma_start(b1s[:], b1.rearrange("(k p) -> p k", p=P), allow_slow_non_contiguous=True).then_inc(loaded, 16)
                sp.dma_start(b2s[:], row_of(b2)).then_inc(loaded, 16)
                if affine:
                    sp.dma_start(ga[:], spread(gamma, TP)).then_inc(loaded, 16)
                    sp.dma_start(be[:], spread(beta, TP)).then_inc(loaded, 16)
                if out is not None:
                    def store(i, u):
                        sp.wait_ge(f_used, ready(i, u, PIPE))
                        sp.dma_start(out[bass.ds((i * PIPE + u) * TP, TP), :], res[u % 2][:]).then_inc(stored[u % 2], 16)

                    pipeline(sp, (0, store))
                    for s in range(2):
                        sp.wait_ge(stored[s], 16 * ((NT + 1 - s) // 2))

            @block.vector
            def _(dve):
                dve.wait_ge(loaded, LOADS)

                def norm(i, u):
                    t, x = i * PIPE + u, xa[u % PIPE]
                    dve.wait_ge(turned, freed(i, u, PIPE, PIPE))
                    dve.wait_ge(f_used, freed(i, u, PIPE, PIPE))
                    ins = dve.tensor_scalar(x[:], tile(src, t), col(S.ln_r, t), col(S.ln_b, t), ALU.mult, ALU.add)
                    if affine:
                        base = i * (2 * PIPE) + 2 * u
                        after(dve, ins, dstep, base + 1)
                        after(dve, dve.tensor_tensor(x[:], x[:], ga[:], ALU.mult), dstep, base + 2)
                        ins = dve.tensor_tensor(x[:], x[:], be[:], ALU.add)
                    ins.then_inc(normed, 1)

                def add(i, u):
                    t, s = i * PIPE + u, u % 2
                    dve.wait_ge(normed, ready(i, u, PIPE))
                    if out is None:
                        dve.wait_ge(f_mm, ready(i, u, PIPE))
                        dve.tensor_tensor(tile(S.y, t), f_ps[:, s, 0:D], xa[u % PIPE][:], ALU.add).then_inc(f_used, 1)
                    else:
                        dve.wait_ge(stored[s], (i * (PIPE // 2) + u // 2) * 16)
                        dve.tensor_tensor(res[s][:], xa[u % PIPE][:], tile(src, t), ALU.add).then_inc(base_made, 1)
                        dve.wait_ge(f_mm, ready(i, u, PIPE))
                        dve.wait_ge(base_made, ready(i, u, PIPE))
                        dve.scalar_tensor_tensor(res[s][:], f_ps[:, s, 0:D], col(coef, t), res[s][:], ALU.mult,
                                                 ALU.add).then_inc(f_used, 1)

                pipeline(dve, (0, norm), (3, add))

            @block.scalar
            def _(act):
                def copy(i, u):
                    act.wait_ge(turned, ready(i, u, PIPE))
                    act.wait_ge(hid_mm, freed(i, u, 2, PIPE))
                    nc.scalar.copy(xt[u % 2][:], turn_ps[:, 0:2 * TP].rearrange("p (k n) -> p k n", k=2)
                                   ).then_inc(turn_copied, 1)

                def hide(i, u):
                    s = u % 2
                    act.wait_ge(hid_mm, ready(i, u, PIPE))
                    act.wait_ge(f_mm, freed(i, u, 2, PIPE))
                    for o in range(FC):
                        nc.scalar.activation(hid[s][:, o, :], hid_ps[:, s, o // 4, (o % 4) * TP:(o % 4 + 1) * TP], func,
                                             bias=b1s[:, o:o + 1]).then_inc(hid_done, 1)

                pipeline(act, (0, copy), (1, hide))

            @block.tensor
            def _(pe):
                def turn(i, u):
                    pe.wait_ge(normed, ready(i, u, PIPE))
                    pe.wait_ge(turn_copied, freed(i, u, 1, PIPE))
                    for c in range(2):
                        last = pe.transpose(turn_ps[:, c * TP:(c + 1) * TP], xa[u % PIPE][:, c * P:(c + 1) * P],
                                            S.ident[0:TP, 0:TP])
                    last.then_inc(turned, 1)

                def hide(i, u):
                    s = u % 2
                    pe.wait_ge(turn_copied, ready(i, u, PIPE))
                    pe.wait_ge(hid_done, i * (FC * PIPE) + FC * max(u - 1, 0))
                    for o in range(FC):
                        for c in range(2):
                            last = pe.matmul(hid_ps[:, s, o // 4, (o % 4) * TP:(o % 4 + 1) * TP],
                                             w1s[:, c, o * P:(o + 1) * P], xt[s][:, c, :], start=(c == 0), stop=(c == 1))
                    last.then_inc(hid_mm, 1)

                def project(i, u):
                    s = u % 2
                    pe.wait_ge(hid_done, i * (FC * PIPE) + FC * (u + 1))
                    pe.wait_ge(f_used, freed(i, u, 2, PIPE))
                    for o in range(FC):
                        pe.matmul(f_ps[:, s, 0:D], hid[s][:, o, :], w2s[:, o, :], start=(o == 0), stop=False)
                    pe.matmul(f_ps[:, s, 0:D], S.ones[0:1, 0:TP], b2s[:], start=False, stop=True).then_inc(f_mm, 1)

                pe.wait_ge(loaded, LOADS)
                pipeline(pe, (0, turn), (1, hide), (2, project))


def add_l1(nc, S, gamma, beta, bias):
    with stage(nc, "c1_") as a:
        ga, be, bi = (a.sb(n, [TP, D]) for n in ("ga", "be", "bi"))
        rows = [a.sb(f"rows{s}", [TP, 4, D]) for s in range(PIPE)]
        t0 = [a.sb(f"t0{s}", [TP, D]) for s in range(PIPE)]
        loaded, step_s, used = a.sem("loaded"), a.sem("step"), a.sem("used")
        scaled, added, shifted = (a.sem(n) for n in ("scaled", "added", "shifted"))
        landed = [a.sem(f"landed{s}") for s in range(PIPE)]
        with nc.Block() as block:
            @block.sync
            def _(sp):
                for to, of in ((ga, gamma), (be, beta), (bi, bias)):
                    sp.dma_start(to[:], spread(of, TP)).then_inc(loaded, 16)

                def load(i, u):
                    sp.wait_ge(used, freed(i, u, PIPE, PIPE))
                    for n in range(4):
                        sp.dma_start(rows[u % PIPE][:, n, :], S.acc[n][bass.ds((i * PIPE + u) * TP, TP), :]
                                     ).then_inc(landed[u % PIPE], 16)

                pipeline(sp, (0, load), lag=PIPE - 1)

            @block.vector
            def _(dve):
                dve.wait_ge(loaded, 48)
                after(dve, dve.tensor_tensor(be[:], be[:], bi[:], ALU.add), step_s, 1)

                def scale(i, u):
                    t, s = i * PIPE + u, u % PIPE
                    dve.wait_ge(used, freed(i, u, PIPE, PIPE))
                    dve.tensor_scalar(t0[s][:], tile(S.y, t), col(S.ln_r, t), col(S.ln_b, t), ALU.mult,
                                      ALU.add).then_inc(scaled, 1)
                    dve.wait_ge(landed[s], (i + u // PIPE + 1) * 64)
                    dve.tensor_tensor(rows[s][:, 0:2], rows[s][:, 0:2], rows[s][:, 2:4], ALU.add).then_inc(scaled, 1)

                def add(i, u):
                    s = u % PIPE
                    dve.wait_ge(scaled, ready(i, u, PIPE) * 2)
                    dve.tensor_tensor(t0[s][:], t0[s][:], ga[:], ALU.mult).then_inc(added, 1)
                    dve.tensor_tensor(rows[s][:, 0], rows[s][:, 0], rows[s][:, 1], ALU.add).then_inc(added, 1)

                def shift(i, u):
                    t, s = i * PIPE + u, u % PIPE
                    dve.wait_ge(added, ready(i, u, PIPE) * 2)
                    dve.tensor_tensor(t0[s][:], t0[s][:], be[:], ALU.add).then_inc(shifted, 1)
                    dve.tensor_tensor(tile(S.x, t), tile(S.x, t), rows[s][:, 0], ALU.add).then_inc(shifted, 1)

                def finish(i, u):
                    t, s = i * PIPE + u, u % PIPE
                    dve.wait_ge(shifted, ready(i, u, PIPE) * 2)
                    dve.tensor_tensor(tile(S.x, t), tile(S.x, t), t0[s][:], ALU.add).then_inc(used, 1)

                pipeline(dve, (3, finish), (2, shift), (1, add), (0, scale))


KEEP = int(0.5 * N) - 1


def depth_weights(nc, S, wr, br):
    w_dram = nc.dram_tensor("depth_weights", [N], F32, kind="Internal").ap()
    with stage(nc, "dw_") as a:
        wrr, brr = a.sb("wrr", [TP, D]), a.sb("brr", [TP, 1])
        xl, junk = a.sb("xl", [TP, D]), a.sb("junk", [TP, D])
        w, rank = a.sb("weight", [TP, NT]), a.sb("rank", [TP, 4, NT])
        w_rows, big = a.sb("w_rows", [TP, N]), a.sb("big", [TP, N])
        earlier, w_group = a.sb("earlier", [TP, TP]), a.sb("w_group", [TP, GROUP])
        grouped = a.sem("grouped")
        loaded, normed, multiplied, step_s, done, spread_in = (
            a.sem(n) for n in ("loaded", "normed", "multiplied", "step", "done", "spread_in"))
        with nc.Block() as block:
            @block.sync
            def _(sp):
                sp.dma_start(wrr[:], spread(wr.rearrange("d o -> (d o)"), TP)).then_inc(loaded, 16)
                sp.dma_start(brr[:], spread(br, TP)).then_inc(loaded, 16)
                sp.wait_ge(done, 1)
                sp.dma_start(w_dram.rearrange("(t p) -> p t", p=TP), w[:],
                             allow_slow_non_contiguous=True).then_inc(spread_in, 16)
                sp.wait_ge(spread_in, 16)
                sp.dma_start(w_rows[:], spread(w_dram, TP)).then_inc(spread_in, 16)

            @block.vector
            def _(dve):
                dve.wait_ge(loaded, 32)
                with dve.Fori(0, NG) as i:
                    for u in range(GROUP):
                        t = i * GROUP + u
                        after(dve, dve.tensor_scalar(xl[:], tile(S.x, t), col(S.ln_r, t), col(S.ln_b, t), ALU.mult,
                                                     ALU.add), normed, ready(i, u))
                        after(dve, dve.tensor_tensor_reduce(junk[:], xl[:], wrr[:], 1.0, 0.0, ALU.mult, ALU.add,
                                                            w_group[:, u:u + 1]), multiplied, ready(i, u))
                    after(dve, dve.tensor_copy(w[:, bass.ds(i * GROUP, GROUP)], w_group[:]), grouped, i + 1)
                st = Steps(dve, step_s)
                dve.tensor_scalar(w[:], w[:], brr[:, 0:1], None, ALU.add).then_inc(done, 1)
                st(dve.tensor_scalar(earlier[:], S.iota_row[0:TP, 0:TP], S.part_col[0:TP, 0:1], None, ALU.is_lt))
                st(dve.memset(rank[:], 0.0))
                dve.wait_ge(done, 1)
                dve.wait_ge(spread_in, 32)
                for t in range(NT):
                    lo, hi = t * TP, (t + 1) * TP
                    me = w[:, t:t + 1]
                    if lo:
                        st(dve.tensor_scalar(big[:, 0:lo], w_rows[:, 0:lo], me, None, ALU.is_ge, ALU.add,
                                             accum_out=rank[:, 0, t:t + 1]))
                    st(dve.tensor_scalar(big[:, lo:N], w_rows[:, lo:N], me, None, ALU.is_gt, ALU.add,
                                         accum_out=rank[:, 1, t:t + 1]))
                    st(dve.scalar_tensor_tensor(big[:, lo:hi], w_rows[:, lo:hi], me, earlier[:], ALU.is_equal, ALU.mult,
                                                accum_out=rank[:, 2, t:t + 1]))
                st(dve.tensor_tensor(rank[:, 0], rank[:, 0], rank[:, 1], ALU.add))
                st(dve.tensor_tensor(rank[:, 0], rank[:, 0], rank[:, 2], ALU.add))
                st(dve.tensor_scalar(rank[:, 0], rank[:, 0], float(KEEP), None, ALU.is_lt))
                dve.tensor_tensor(S.coef[:], rank[:, 0], w[:], ALU.mult)


def network(nc, A, out):
    with ExitStack() as ctx:
        g = Alloc(nc, ctx)
        S = Shared()
        constants(nc, g, S)
        load_nodes(nc, g, S, A["x"])
        layernorm_stats(nc, S, "l0_", S.x)
        edges(nc, g, S, A["src"], A["dst"], A["edge_type_2"], A["edge_weight"])
        row_starts(nc, g, S)
        gnn0(nc, g, S, A)
        layernorm_stats(nc, S, "l1_", S.x)
        moe(nc, S, A["L0_ffn_gate_w"], A["L0_ffn_gate_b"], A["L0_ffn_w1"], A["L0_ffn_b1"], A["L0_ffn_w2"], A["L0_ffn_b2"])
        layer1(nc, g, S, A, out)


def layer1(nc, g, S, A, out):
    S.y = g.sb("y", [TP, NT, D])
    S.coef = g.sb("coef", [TP, NT])
    layernorm_stats(nc, S, "l2_", S.x)
    M = {k[len("L1_mix_"):]: v for k, v in A.items() if k.startswith("L1_mix_")}
    with stage(nc, "la_") as a:
        L = attention_sums(nc, S, a, A["L1_gnn_weight"], M["Wq"], M["bq"], M["Wk"], M["bk"], M["Wv"], M["bv"], M["Wo"],
                           M["bo"])
        source_sums(nc, S, "a4_", S.support, D, S.ew_c, S.node_dst, S.src_c, S.src_pad, S.row_rep, S.acc,
                    guest=attention_queries(nc, S, L))
    layernorm_stats(nc, S, "l3_", S.y)
    feed_forward(nc, S, "f1_", S.y, M["ln1_g"], M["ln1_b"], M["W1"], M["b1"], M["W2"], M["b2"], ACT.Relu)
    layernorm_stats(nc, S, "l4_", S.y)
    add_l1(nc, S, M["ln2_g"], M["ln2_b"], A["L1_gnn_bias"])
    layernorm_stats(nc, S, "l5_", S.x)
    depth_weights(nc, S, A["L1_ffn_wr"], A["L1_ffn_br"])
    feed_forward(nc, S, "f2_", S.x, None, None, A["L1_ffn_w1"], A["L1_ffn_b1"], A["L1_ffn_w2"], A["L1_ffn_b2"],
                 ACT.Gelu_apprx_tanh, out=out, coef=S.coef)


def lay_out(inputs):
    import numpy as np

    a = {k: np.ascontiguousarray(v) for k, v in inputs.items()}
    perm = np.arange(768).reshape(8, 3, 32).transpose(1, 0, 2).reshape(-1)
    a["conv_w"] = np.ascontiguousarray(a["L0_mix_w_qkv"][perm, :, 2].T)
    a["bn_gamma"] = np.ascontiguousarray(a["L0_mix_bn_gamma"][perm])
    a["bn_beta"] = np.ascontiguousarray(a["L0_mix_bn_beta"][perm])
    a["dw_w"] = np.ascontiguousarray(a["L0_mix_w_dw"][perm, 0, 2])
    a["pw_w"] = np.ascontiguousarray(a["L0_mix_w_pw"][perm, :, 0].reshape(6, 4, 32, 32).transpose(1, 3, 0, 2))
    a["res_w"] = np.ascontiguousarray(a["L0_mix_w_res"][:, :, 0].T)
    for layer in (1, 2, 3):
        a[f"W{layer}"] = a[f"L0_gnn_W{layer}"]
        a[f"W{layer}_T"] = np.ascontiguousarray(a[f"L0_gnn_W{layer}"].transpose(0, 2, 1))
    for name in ("L0_mix_w_qkv", "L0_mix_bn_gamma", "L0_mix_bn_beta", "L0_mix_w_dw", "L0_mix_w_pw", "L0_mix_w_res",
                 "L0_gnn_W1", "L0_gnn_W2", "L0_gnn_W3", "L1_ffn_attention_mask"):
        del a[name]
    return a


def kernel(**inputs):
    import concourse.bacc as bacc
    from concourse.bass_utils import run_bass_kernel_spmd

    nc = bacc.Bacc("TRN2", target_bir_lowering=False, num_devices=1)
    arrays = lay_out(inputs)
    A = {k: nc.dram_tensor(f"in_{k}", v.shape, mybir.dt.from_np(v.dtype), kind="ExternalInput").ap()
         for k, v in arrays.items()}
    out = nc.dram_tensor("out_0", (N, D), F32, kind="ExternalOutput").ap()
    network(nc, A, out)
    r = run_bass_kernel_spmd(nc, [{f"in_{k}": v for k, v in arrays.items()}], core_ids=[0])
    return r.results[0]["out_0"]
```
